# Optimizing a Trainium2 kernel written in Bass

```python
import numpy as np
import jax
import jax.numpy as jnp

def _softmax(x, axis=-1):
    return jax.nn.softmax(x, axis=axis)

def _gelu(x):
    return jax.nn.gelu(x, approximate=True)

def _silu(x):
    return jax.nn.silu(x)

def _sigmoid(x):
    return jax.nn.sigmoid(x)

def _layernorm(x, axis=-1, eps=1e-05):
    m = jnp.mean(x, axis=axis, keepdims=True)
    v = jnp.var(x, axis=axis, keepdims=True)
    return (x - m) / jnp.sqrt(v + eps)

def _scatter_add(tgt, idx, src, axis=0):
    return tgt.at[idx].add(src)

def _segment_sum(src, seg, n):
    return jax.ops.segment_sum(src, seg, n)
kernel_name = 'mk_seq_postln_d2_jaxref_r4_04b8f1'

def setup_inputs(seed: int=0):
    np.random.seed(seed)
    _w = jnp.asarray

    def _L0_attn_setup():
        import jax, jax.numpy as jnp
        import numpy as np
        B, S, HID = (4, 1024, 512)
        H, NB = (16, 4)
        D = HID // H
        EPS = 1e-06

        def elu_plus_one(x):
            return jax.nn.elu(x) + 1.0

        def _reference_tuple_inner(hidden_states, Wq, Wk, Wv, Wo, bank_weights, memories, memory_norms):
            b, s, _ = hidden_states.shape

            def proj(W):
                return (hidden_states @ W.T).reshape(b, s, H, D).transpose(0, 2, 1, 3)
            q, k, v = (proj(Wq), proj(Wk), proj(Wv))
            sigma_q = elu_plus_one(q)
            a_unnorm = jnp.einsum('bhsd,nhde->nbhse', sigma_q, memories)
            norm = jnp.einsum('bhsd,nhd->nbhs', sigma_q, memory_norms)
            a = a_unnorm / jnp.clip(norm, EPS, None)[..., None]
            active = (memory_norms.sum(axis=(1, 2)) >= EPS).astype(a.dtype)
            a = a * active[:, None, None, None, None]
            weights = jax.nn.softmax(bank_weights, axis=-1)
            combined = jnp.einsum('nbhse,hn->bhse', a, weights)
            sigma_k = elu_plus_one(k)
            mem0, norm0 = (memories[0], memory_norms[0])
            retr = jnp.einsum('bhsd,hde->bhse', sigma_k, mem0)
            knorm = jnp.clip(jnp.einsum('bhsd,hd->bhs', sigma_k, norm0), EPS, None)
            delta_v = v - retr / knorm[..., None]
            mem_update = jnp.einsum('bhsd,bhse->hde', sigma_k, delta_v) / (b * s)
            new_mem0 = jax.lax.stop_gradient(mem0 + mem_update)
            new_norm0 = jax.lax.stop_gradient(norm0 + sigma_k.sum(axis=(0, 2)) / b)
            out = combined.transpose(0, 2, 1, 3).reshape(b, s, HID) @ Wo.T
            return (out, new_mem0, new_norm0)
        key = jax.random.key(seed)
        ks = jax.random.split(key, 8)
        return {'hidden_states': jax.random.normal(ks[0], (B, S, HID), jnp.float32), 'Wq': jax.random.normal(ks[1], (HID, HID), jnp.float32) * 0.02, 'Wk': jax.random.normal(ks[2], (HID, HID), jnp.float32) * 0.02, 'Wv': jax.random.normal(ks[3], (HID, HID), jnp.float32) * 0.02, 'Wo': jax.random.normal(ks[4], (HID, HID), jnp.float32) * 0.02, 'bank_weights': jax.random.normal(ks[5], (H, NB), jnp.float32) * 0.02, 'memories': jax.random.uniform(ks[6], (NB, H, D, D), jnp.float32), 'memory_norms': jax.random.uniform(ks[7], (NB, H, D), jnp.float32)}
    _L0_attn_in = _L0_attn_setup()

    def _L0_ffn_setup():
        import jax, jax.numpy as jnp
        import numpy as np
        B, S, D, F, E, SH, K = (2, 512, 512, 256, 16, 2, 2)

        def _experts_all(x, g, gb, w1, b1, w2, b2):
            y = jax.nn.gelu(jnp.einsum('bsd,edf->bsef', x, g) + gb, approximate=False)
            y = y * (jnp.einsum('bsd,edf->bsef', x, w1) + b1)
            return jnp.einsum('bsef,efd->bsed', y, w2) + b2
        key = jax.random.key(seed)
        ks = jax.random.split(key, 8)
        std = 0.02
        mk = lambda k, sh: jax.random.normal(k, sh, jnp.float32) * std
        return {'x': jax.random.normal(ks[0], (B, S, D), jnp.float32), 'wa': mk(ks[1], (D, E)), 'rg': mk(ks[2], (E, D, F)), 'rgb': jnp.zeros((E, F), jnp.float32), 'rw1': mk(ks[3], (E, D, F)), 'rb1': jnp.zeros((E, F), jnp.float32), 'rw2': mk(ks[4], (E, F, D)), 'rb2': jnp.zeros((E, D), jnp.float32), 'sg': mk(ks[5], (SH, D, F)), 'sgb': jnp.zeros((SH, F), jnp.float32), 'sw1': mk(ks[6], (SH, D, F)), 'sb1': jnp.zeros((SH, F), jnp.float32), 'sw2': mk(ks[7], (SH, F, D)), 'sb2': jnp.zeros((SH, D), jnp.float32)}
    _L0_ffn_in = _L0_ffn_setup()

    def _L1_attn_setup():
        import jax, jax.numpy as jnp
        import numpy as np
        B, S, D = (4, 1024, 512)
        H, F = (16, 64)
        DH = D // H
        key = jax.random.key(seed)
        ks = jax.random.split(key, 12)
        std = 0.02
        inp = {'x': jax.random.normal(ks[0], (B, S, D), jnp.float32), 'qw': jax.random.normal(ks[1], (D, D), jnp.float32) * std, 'qb': jnp.zeros((D,), jnp.float32), 'kw': jax.random.normal(ks[2], (D, D), jnp.float32) * std, 'kb': jnp.zeros((D,), jnp.float32), 'vw': jax.random.normal(ks[3], (D, D), jnp.float32) * std, 'vb': jnp.zeros((D,), jnp.float32), 'fw1': jax.random.normal(ks[4], (DH, F), jnp.float32) * std, 'fb1': jnp.zeros((F,), jnp.float32), 'fw2': jax.random.normal(ks[5], (F, F), jnp.float32) * std, 'fb2': jnp.zeros((F,), jnp.float32), 'ow': jax.random.normal(ks[6], (D, D), jnp.float32) * std, 'ob': jnp.zeros((D,), jnp.float32)}
        return inp
    _L1_attn_in = _L1_attn_setup()

    def _L1_ffn_setup():
        import jax, jax.numpy as jnp
        import numpy as np
        E, K, H, F = (64, 6, 512, 192)
        G, KG = (8, 4)
        SHARED_F = 192
        SCALE = 2.5
        T = 2 * 256
        CAP = 2 * (T * K // E)

        def _grouped_topk(logits, bias):
            scores = jax.nn.sigmoid(logits.astype(jnp.float32))
            scores_b = scores + bias[None, :]
            gs = scores_b.reshape(-1, G, E // G)
            group_scores = jnp.sum(jax.lax.top_k(gs, 2)[0], axis=-1)
            gidx = jax.lax.top_k(group_scores, KG)[1]
            rows = jnp.arange(group_scores.shape[0])[:, None]
            group_mask = jnp.zeros_like(group_scores).at[rows, gidx].set(1.0)
            score_mask = jnp.repeat(group_mask, E // G, axis=-1) > 0
            tmp = jnp.where(score_mask, scores_b, -jnp.inf)
            topk_ids = jax.lax.top_k(tmp, K)[1]
            topk_w = jnp.take_along_axis(scores, topk_ids, axis=-1)
            topk_w = topk_w / jnp.sum(topk_w, axis=-1, keepdims=True)
            return (topk_w * SCALE, topk_ids)

        def _routed_moe(x, topk_w, topk_ids, w_gate, w_up, w_down):
            Tn = x.shape[0]
            flat_e = topk_ids.reshape(-1)
            order = jnp.argsort(flat_e)
            se = flat_e[order]
            pos = jnp.arange(Tn * K) - jnp.searchsorted(se, se, side='left')
            tok = order // K
            valid = pos < CAP
            slot = jnp.where(valid, pos, CAP)
            buf = jnp.zeros((E, CAP + 1, H), x.dtype).at[se, slot].set(x[tok])[:, :CAP]
            h = jax.nn.silu(jnp.einsum('ech,ehf->ecf', buf, w_gate)) * jnp.einsum('ech,ehf->ecf', buf, w_up)
            out = jnp.einsum('ecf,efh->ech', h, w_down)
            gathered = out[se, jnp.minimum(pos, CAP - 1)] * valid.astype(x.dtype)[:, None]
            w = topk_w.reshape(-1)[order].astype(x.dtype)[:, None]
            return jax.ops.segment_sum(gathered * w, tok, num_segments=Tn)
        key = jax.random.key(seed)
        ks = jax.random.split(key, 9)
        s = 0.02
        return dict(hidden_states=jax.random.normal(ks[0], (2, 256, H), jnp.float32), gate_w=jax.random.normal(ks[1], (H, E), jnp.float32) * s, bias=jax.random.normal(ks[2], (E,), jnp.float32) * s, w_gate=jax.random.normal(ks[3], (E, H, F), jnp.float32) * s, w_up=jax.random.normal(ks[4], (E, H, F), jnp.float32) * s, w_down=jax.random.normal(ks[5], (E, F, H), jnp.float32) * s, ws_gate=jax.random.normal(ks[6], (H, SHARED_F), jnp.float32) * s, ws_up=jax.random.normal(ks[7], (H, SHARED_F), jnp.float32) * s, ws_down=jax.random.normal(ks[8], (SHARED_F, H), jnp.float32) * s)
    _L1_ffn_in = _L1_ffn_setup()
    _d = {'L0_attn_hidden_states': _L0_attn_in['hidden_states'], 'L0_attn_Wq': _L0_attn_in['Wq'], 'L0_attn_Wk': _L0_attn_in['Wk'], 'L0_attn_Wv': _L0_attn_in['Wv'], 'L0_attn_Wo': _L0_attn_in['Wo'], 'L0_attn_bank_weights': _L0_attn_in['bank_weights'], 'L0_attn_memories': _L0_attn_in['memories'], 'L0_attn_memory_norms': _L0_attn_in['memory_norms'], 'L0_ffn_wa': _L0_ffn_in['wa'], 'L0_ffn_rg': _L0_ffn_in['rg'], 'L0_ffn_rgb': _L0_ffn_in['rgb'], 'L0_ffn_rw1': _L0_ffn_in['rw1'], 'L0_ffn_rb1': _L0_ffn_in['rb1'], 'L0_ffn_rw2': _L0_ffn_in['rw2'], 'L0_ffn_rb2': _L0_ffn_in['rb2'], 'L0_ffn_sg': _L0_ffn_in['sg'], 'L0_ffn_sgb': _L0_ffn_in['sgb'], 'L0_ffn_sw1': _L0_ffn_in['sw1'], 'L0_ffn_sb1': _L0_ffn_in['sb1'], 'L0_ffn_sw2': _L0_ffn_in['sw2'], 'L0_ffn_sb2': _L0_ffn_in['sb2'], 'L1_attn_qw': _L1_attn_in['qw'], 'L1_attn_qb': _L1_attn_in['qb'], 'L1_attn_kw': _L1_attn_in['kw'], 'L1_attn_kb': _L1_attn_in['kb'], 'L1_attn_vw': _L1_attn_in['vw'], 'L1_attn_vb': _L1_attn_in['vb'], 'L1_attn_fw1': _L1_attn_in['fw1'], 'L1_attn_fb1': _L1_attn_in['fb1'], 'L1_attn_fw2': _L1_attn_in['fw2'], 'L1_attn_fb2': _L1_attn_in['fb2'], 'L1_attn_ow': _L1_attn_in['ow'], 'L1_attn_ob': _L1_attn_in['ob'], 'L1_ffn_gate_w': _L1_ffn_in['gate_w'], 'L1_ffn_bias': _L1_ffn_in['bias'], 'L1_ffn_w_gate': _L1_ffn_in['w_gate'], 'L1_ffn_w_up': _L1_ffn_in['w_up'], 'L1_ffn_w_down': _L1_ffn_in['w_down'], 'L1_ffn_ws_gate': _L1_ffn_in['ws_gate'], 'L1_ffn_ws_up': _L1_ffn_in['ws_up'], 'L1_ffn_ws_down': _L1_ffn_in['ws_down']}
    _x0 = _d['L0_attn_hidden_states']
    _d['L0_attn_hidden_states'] = jax.random.normal(jax.random.fold_in(jax.random.key(seed), 1), (1, 2048, 512), dtype=_x0.dtype)
    del _x0
    return _d

def reference(L0_attn_hidden_states, L0_attn_Wq, L0_attn_Wk, L0_attn_Wv, L0_attn_Wo, L0_attn_bank_weights, L0_attn_memories, L0_attn_memory_norms, L0_ffn_wa, L0_ffn_rg, L0_ffn_rgb, L0_ffn_rw1, L0_ffn_rb1, L0_ffn_rw2, L0_ffn_rb2, L0_ffn_sg, L0_ffn_sgb, L0_ffn_sw1, L0_ffn_sb1, L0_ffn_sw2, L0_ffn_sb2, L1_attn_qw, L1_attn_qb, L1_attn_kw, L1_attn_kb, L1_attn_vw, L1_attn_vb, L1_attn_fw1, L1_attn_fb1, L1_attn_fw2, L1_attn_fb2, L1_attn_ow, L1_attn_ob, L1_ffn_gate_w, L1_ffn_bias, L1_ffn_w_gate, L1_ffn_w_up, L1_ffn_w_down, L1_ffn_ws_gate, L1_ffn_ws_up, L1_ffn_ws_down):

    def _L0_attn_ref(hidden_states, Wq, Wk, Wv, Wo, bank_weights, memories, memory_norms):
        import jax, jax.numpy as jnp
        import numpy as np
        B, S, HID = (4, 1024, 512)
        H, NB = (16, 4)
        D = HID // H
        EPS = 1e-06

        def elu_plus_one(x):
            return jax.nn.elu(x) + 1.0

        def _reference_tuple_inner(hidden_states, Wq, Wk, Wv, Wo, bank_weights, memories, memory_norms):
            b, s, _ = hidden_states.shape

            def proj(W):
                return (hidden_states @ W.T).reshape(b, s, H, D).transpose(0, 2, 1, 3)
            q, k, v = (proj(Wq), proj(Wk), proj(Wv))
            sigma_q = elu_plus_one(q)
            a_unnorm = jnp.einsum('bhsd,nhde->nbhse', sigma_q, memories)
            norm = jnp.einsum('bhsd,nhd->nbhs', sigma_q, memory_norms)
            a = a_unnorm / jnp.clip(norm, EPS, None)[..., None]
            active = (memory_norms.sum(axis=(1, 2)) >= EPS).astype(a.dtype)
            a = a * active[:, None, None, None, None]
            weights = jax.nn.softmax(bank_weights, axis=-1)
            combined = jnp.einsum('nbhse,hn->bhse', a, weights)
            sigma_k = elu_plus_one(k)
            mem0, norm0 = (memories[0], memory_norms[0])
            retr = jnp.einsum('bhsd,hde->bhse', sigma_k, mem0)
            knorm = jnp.clip(jnp.einsum('bhsd,hd->bhs', sigma_k, norm0), EPS, None)
            delta_v = v - retr / knorm[..., None]
            mem_update = jnp.einsum('bhsd,bhse->hde', sigma_k, delta_v) / (b * s)
            new_mem0 = jax.lax.stop_gradient(mem0 + mem_update)
            new_norm0 = jax.lax.stop_gradient(norm0 + sigma_k.sum(axis=(0, 2)) / b)
            out = combined.transpose(0, 2, 1, 3).reshape(b, s, HID) @ Wo.T
            return (out, new_mem0, new_norm0)
        return _reference_tuple_inner(hidden_states, Wq, Wk, Wv, Wo, bank_weights, memories, memory_norms)[0]

    def _L0_ffn_ref(x, wa, rg, rgb, rw1, rb1, rw2, rb2, sg, sgb, sw1, sb1, sw2, sb2):
        import jax, jax.numpy as jnp
        import numpy as np
        B, S, D, F, E, SH, K = (2, 512, 512, 256, 16, 2, 2)

        def _experts_all(x, g, gb, w1, b1, w2, b2):
            y = jax.nn.gelu(jnp.einsum('bsd,edf->bsef', x, g) + gb, approximate=False)
            y = y * (jnp.einsum('bsd,edf->bsef', x, w1) + b1)
            return jnp.einsum('bsef,efd->bsed', y, w2) + b2
        aff = jax.nn.sigmoid(jnp.einsum('bsd,de->bse', x, wa))
        topk_p, topk_i = jax.lax.top_k(aff, K)
        topk_p = topk_p / jnp.sum(topk_p, axis=-1, keepdims=True)
        combine = jnp.sum(jax.nn.one_hot(topk_i, E, dtype=x.dtype) * topk_p[..., None], axis=2)
        routed = jnp.einsum('bsed,bse->bsd', _experts_all(x, rg, rgb, rw1, rb1, rw2, rb2), combine)
        shared = jnp.sum(_experts_all(x, sg, sgb, sw1, sb1, sw2, sb2), axis=2)
        return x + shared + routed

    def _L1_attn_ref(x, qw, qb, kw, kb, vw, vb, fw1, fb1, fw2, fb2, ow, ob):
        import jax, jax.numpy as jnp
        import numpy as np
        B, S, D = (4, 1024, 512)
        H, F = (16, 64)
        DH = D // H
        b, s, _ = x.shape

        def heads(t):
            return t.reshape(b, s, H, DH).transpose(0, 2, 1, 3)
        Q = heads(x @ qw + qb)
        K = heads(x @ kw + kb)
        V = heads(x @ vw + vb)

        def feature_map(t):
            return jax.nn.elu(t @ fw1 + fb1) @ fw2 + fb2
        Qm = feature_map(Q)
        Km = feature_map(K)
        KV = jnp.einsum('bhsf,bhsd->bhfd', Km, V)
        Z = Km.sum(axis=2)
        num = jnp.einsum('bhsf,bhfd->bhsd', Qm, KV)
        den = jnp.einsum('bhsf,bhf->bhs', Qm, Z)[..., None]
        attn = num / jnp.maximum(den, 1e-06)
        out = attn.transpose(0, 2, 1, 3).reshape(b, s, D)
        return out @ ow + ob

    def _L1_ffn_ref(hidden_states, gate_w, bias, w_gate, w_up, w_down, ws_gate, ws_up, ws_down):
        import jax, jax.numpy as jnp
        import numpy as np
        E, K, H, F = (64, 6, 512, 192)
        G, KG = (8, 4)
        SHARED_F = 192
        SCALE = 2.5
        T = 2 * 256
        CAP = 2 * (T * K // E)

        def _grouped_topk(logits, bias):
            scores = jax.nn.sigmoid(logits.astype(jnp.float32))
            scores_b = scores + bias[None, :]
            gs = scores_b.reshape(-1, G, E // G)
            group_scores = jnp.sum(jax.lax.top_k(gs, 2)[0], axis=-1)
            gidx = jax.lax.top_k(group_scores, KG)[1]
            rows = jnp.arange(group_scores.shape[0])[:, None]
            group_mask = jnp.zeros_like(group_scores).at[rows, gidx].set(1.0)
            score_mask = jnp.repeat(group_mask, E // G, axis=-1) > 0
            tmp = jnp.where(score_mask, scores_b, -jnp.inf)
            topk_ids = jax.lax.top_k(tmp, K)[1]
            topk_w = jnp.take_along_axis(scores, topk_ids, axis=-1)
            topk_w = topk_w / jnp.sum(topk_w, axis=-1, keepdims=True)
            return (topk_w * SCALE, topk_ids)

        def _routed_moe(x, topk_w, topk_ids, w_gate, w_up, w_down):
            Tn = x.shape[0]
            flat_e = topk_ids.reshape(-1)
            order = jnp.argsort(flat_e)
            se = flat_e[order]
            pos = jnp.arange(Tn * K) - jnp.searchsorted(se, se, side='left')
            tok = order // K
            valid = pos < CAP
            slot = jnp.where(valid, pos, CAP)
            buf = jnp.zeros((E, CAP + 1, H), x.dtype).at[se, slot].set(x[tok])[:, :CAP]
            h = jax.nn.silu(jnp.einsum('ech,ehf->ecf', buf, w_gate)) * jnp.einsum('ech,ehf->ecf', buf, w_up)
            out = jnp.einsum('ecf,efh->ech', h, w_down)
            gathered = out[se, jnp.minimum(pos, CAP - 1)] * valid.astype(x.dtype)[:, None]
            w = topk_w.reshape(-1)[order].astype(x.dtype)[:, None]
            return jax.ops.segment_sum(gathered * w, tok, num_segments=Tn)
        orig_shape = hidden_states.shape
        x = hidden_states.reshape(-1, H)
        router_logits = x @ gate_w
        topk_w, topk_ids = _grouped_topk(router_logits, bias)
        y = _routed_moe(x, topk_w, topk_ids, w_gate, w_up, w_down)
        shared = jax.nn.silu(x @ ws_gate) * (x @ ws_up) @ ws_down
        return (y + shared).reshape(orig_shape)
    x = L0_attn_hidden_states
    x = _layernorm(x + _L0_attn_ref(x, L0_attn_Wq, L0_attn_Wk, L0_attn_Wv, L0_attn_Wo, L0_attn_bank_weights, L0_attn_memories, L0_attn_memory_norms), axis=-1)
    x = _layernorm(x + _L0_ffn_ref(x, L0_ffn_wa, L0_ffn_rg, L0_ffn_rgb, L0_ffn_rw1, L0_ffn_rb1, L0_ffn_rw2, L0_ffn_rb2, L0_ffn_sg, L0_ffn_sgb, L0_ffn_sw1, L0_ffn_sb1, L0_ffn_sw2, L0_ffn_sb2), axis=-1)
    x = _layernorm(x + _L1_attn_ref(x, L1_attn_qw, L1_attn_qb, L1_attn_kw, L1_attn_kb, L1_attn_vw, L1_attn_vb, L1_attn_fw1, L1_attn_fb1, L1_attn_fw2, L1_attn_fb2, L1_attn_ow, L1_attn_ob), axis=-1)
    x = _layernorm(x + _L1_ffn_ref(x, L1_ffn_gate_w, L1_ffn_bias, L1_ffn_w_gate, L1_ffn_w_up, L1_ffn_w_down, L1_ffn_ws_gate, L1_ffn_ws_up, L1_ffn_ws_down), axis=-1)
    return x

_drawn_inputs = setup_inputs


def setup_inputs(seed=0):
    import zlib

    import numpy as np

    out = dict(_drawn_inputs(seed))
    spreads = {'L0_ffn_rgb': (0.0, 0.8),
     'L0_ffn_rb1': (0.0, 0.8),
     'L0_ffn_rb2': (0.0, 0.1),
     'L0_ffn_sgb': (0.0, 0.8),
     'L0_ffn_sb1': (0.0, 0.8),
     'L0_ffn_sb2': (0.0, 0.1),
     'L1_attn_qb': (0.0, 0.8),
     'L1_attn_kb': (0.0, 0.8),
     'L1_attn_vb': (0.0, 0.1),
     'L1_attn_fb1': (0.0, 0.8),
     'L1_attn_fb2': (0.0, 0.8),
     'L1_attn_ob': (0.0, 0.1)}
    factors = {'L0_attn_Wq': 4.464,
     'L0_attn_bank_weights': 8.0,
     'L0_ffn_rg': 4.281,
     'L0_ffn_rw1': 4.115,
     'L0_ffn_rw2': 4.01,
     'L1_attn_qw': 8.0,
     'L1_attn_kw': 8.0,
     'L1_attn_fw1': 8.0,
     'L1_attn_fw2': 8.0,
     'L1_ffn_gate_w': 2.99,
     'L1_ffn_bias': 5.166,
     'L1_ffn_w_gate': 2.94,
     'L1_ffn_w_up': 2.868,
     'L1_ffn_w_down': 2.896}
    for name, (base, spread) in spreads.items():
        noise = np.random.default_rng([zlib.crc32(name.encode()), seed]).standard_normal(out[name].shape)
        drawn = base * np.exp(spread * noise) if base else spread * noise
        out[name] = jnp.asarray(drawn.astype(out[name].dtype))
    for name, factor in factors.items():
        out[name] = (out[name] * factor).astype(out[name].dtype)
    return out
```

```python
from contextlib import ExitStack

import numpy as np
import concourse.bass as bass
import concourse.mybir as mybir

F32 = mybir.dt.float32
F32R = mybir.dt.float32r
BF16 = mybir.dt.bfloat16
I32 = mybir.dt.int32
U32 = mybir.dt.uint32
ALU = mybir.AluOpType
ACT = mybir.ActivationFunctionType
AX = mybir.AxisListType

P = 128
T = 2048
D = 512
NT = T // P
KD = D // P
CH = 512
NC = T // CH
TC = CH // P
EPS_LN = 1e-5
EPS_MEM = 1e-6


class Core:

    def __init__(self, nc, ctx, io):
        self.nc, self.ctx, self.io = nc, ctx, io
        self.sems = []
        self.bank = [ctx.enter_context(nc.psum_tensor(f"bank{i}", [P, 512], F32)) for i in range(8)]

    def sem(self, name):
        self.sems.append(self.nc.alloc_semaphore(name=name))
        return self.sems[-1]

    def clear_semaphores(self):
        self.nc.clear_and_free_semaphores(self.sems)
        self.nc.all_engine_barrier()
        self.sems = []

    def sb(self, name, shape, dt=F32, ctx=None):
        return (ctx or self.ctx).enter_context(self.nc.sbuf_tensor(name, shape, dt))


def mm3(pe, out, a_hi, a_lo, b_hi, b_lo, start, stop):
    pe.matmul(out, a_hi, b_hi, start=start, stop=False)
    pe.matmul(out, a_hi, b_lo, start=False, stop=False)
    return pe.matmul(out, a_lo, b_hi, start=False, stop=stop)


def setup(k):
    k.ident = k.sb("ident", [P, P])
    k.x = k.sb("resid", [P, NT, D])
    k.neg_half = k.sb("neg_half", [P, NT])
    k.mv = k.sb("mv", [P, NT, 2])
    k.stats = k.sb("stats", [P, 2, 6])
    k.var = k.sb("var", [P, NT])
    k.rstd = k.sb("rstd", [P, NT])
    s_ident0 = k.sem("ident_zeroed")
    with k.nc.Block() as block:
        @block.gpsimd
        def _(pool):
            pool.memset(k.ident[:, :], 0.0).then_inc(s_ident0, 1)
            pool.memset(k.neg_half[:, :], -0.5)
            pool.wait_ge(s_ident0, 1)
            pool.affine_select(out=k.ident[:, :], in_=k.ident[:, :], compare_op=ALU.not_equal, fill=1.0,
                               base=0, pattern=[[-1, P]], channel_multiplier=1)


def ln_stats(k, vec, tile, s_stat, n):
    vec.bn_stats(k.stats[:, n % 2, :], k.x[:, tile, :]).then_inc(s_stat, 1)
    vec.wait_ge(s_stat, 2 * n + 1)
    vec.bn_aggr(k.mv[:, tile, :], k.stats[:, n % 2, :]).then_inc(s_stat, 1)


def ln_rstd(k, pool, t0, n, s_var, s_rstd, done):
    pool.tensor_scalar(k.var[:, t0:t0 + n], k.mv[:, t0:t0 + n, 1], EPS_LN, 0.0, ALU.add, ALU.add).then_inc(s_var, 1)
    pool.wait_ge(s_var, done + 1)
    pool.tensor_tensor(k.rstd[:, t0:t0 + n], k.var[:, t0:t0 + n], k.neg_half[:, t0:t0 + n], ALU.pow).then_inc(s_rstd, 1)


def ln_apply(k, vec, tile):
    return vec.tensor_scalar(k.x[:, tile, :], k.x[:, tile, :], k.mv[:, tile, 0:1], k.rstd[:, tile:tile + 1],
                             ALU.subtract, ALU.mult)


def attention0(k):
    nc, bank, io = k.nc, k.bank, k.io
    NB, G, HG, DH = 4, 4, 4, 32
    with ExitStack() as ctx:
        sb = lambda name, shape, dt=F32: k.sb("a0_" + name, shape, dt, ctx)
        wq_raw, wo_raw = sb("wq_raw", [P, KD, D]), sb("wo_raw", [P, KD, D])
        wq_hi, wq_lo = sb("wq_hi", [P, KD, D], F32R), sb("wq_lo", [P, KD, D], F32R)
        wo_hi, wo_lo = sb("wo_hi", [P, KD, D], F32R), sb("wo_lo", [P, KD, D], F32R)
        mem_raw, nrm_raw = sb("mem_raw", [P, G * NB, DH]), sb("nrm_raw", [P, G * NB])
        mem_hi, mem_lo = sb("mem_hi", [P, G, NB * HG * DH], F32R), sb("mem_lo", [P, G, NB * HG * DH], F32R)
        nrm_f = sb("nrm_f", [P, G * NB, HG])
        nrm_hi, nrm_lo = sb("nrm_hi", [P, G * NB, HG], F32R), sb("nrm_lo", [P, G * NB, HG], F32R)
        head_mask = sb("head_mask", [P, HG])
        nrm_all = sb("nrm_all", [P, NB, D])
        bw = sb("bw", [P, G, NB, HG])
        bmax, bsum = sb("bmax", [P, G, HG]), sb("bsum", [P, G, HG])
        act_n = sb("act_n", [P, NB])
        xt_hi, xt_lo = sb("xt_hi", [P, KD, CH], F32R), sb("xt_lo", [P, KD, CH], F32R)
        ex, rl = sb("ex", [P, 2, CH]), sb("rl", [P, 2, CH])
        sg = sb("sg", [P, 2, CH])
        sg_hi, sg_lo = sb("sg_hi", [P, 2, KD, CH], F32R), sb("sg_lo", [P, 2, KD, CH], F32R)
        rw = sb("rw", [P, 2, TC, G * NB * HG])
        read_n = sb("read_n", [P, 2, NB * HG * DH])
        read_2 = sb("read_2", [P, 2, 2 * HG * DH])
        comb = sb("comb", [P, TC, D])
        ct_hi, ct_lo = sb("ct_hi", [P, 2, KD, P], F32R), sb("ct_lo", [P, 2, KD, P], F32R)

        s_x = [k.sem(f"a0_x_loaded{c}") for c in range(NC)]
        s_wq, s_wo, s_mem, s_nrm = (k.sem("a0_" + n) for n in ("wq_loaded", "wo_loaded", "mem_loaded", "nrm_loaded"))
        s_bw, s_na = k.sem("a0_bw_loaded"), k.sem("a0_norms_loaded")
        s_zero, s_mask = k.sem("a0_mem_zeroed"), k.sem("a0_mask_made")
        s_whi, s_split = k.sem("a0_weight_hi"), k.sem("a0_weights_split")
        s_c = k.sem("a0_vector_chain")
        s_bexp = k.sem("a0_bank_exp")
        s_bsub = k.sem("a0_bank_sub")
        s_tps, s_thi, s_tlo = k.sem("a0_turned"), k.sem("a0_turned_hi"), k.sem("a0_turned_lo")
        s_q, s_qev, s_sg, s_slo = k.sem("a0_q"), k.sem("a0_q_read"), k.sem("a0_sigma"), k.sem("a0_sigma_split")
        s_nb, s_r = k.sem("a0_norms"), k.sem("a0_norms_read")
        s_rw = k.sem("a0_read_weights")
        s_m, s_rn, s_comb = k.sem("a0_reads"), k.sem("a0_reads_weighted"), k.sem("a0_combined")
        s_r2 = k.sem("a0_half_sum")
        s_o, s_res = k.sem("a0_out"), k.sem("a0_residual")
        s_stat, s_var, s_rstd = k.sem("a0_stats"), k.sem("a0_var"), k.sem("a0_rstd")
        s_ln, s_st = k.sem("a0_normed"), k.sem("a0_stored")

        TURNED_X = [[b if c == 0 else 8 * c - 4 + b for b in range(KD)] for c in range(NC)]
        TURNED_O = [[(8 * c + 8 if c + 1 < NC else 8 * c + 4) + j for j in range(TC)] for c in range(NC)]

        def schedule(turn, query, reads, out):
            turn(0)
            query(0)
            for c in range(NC):
                reads(c)
                if c + 1 < NC:
                    turn(c + 1)
                    query(c + 1)
                out(c)

        with nc.Block() as block:
            @block.sync
            def _(sp):
                x_d = io["x"].rearrange("(c j p) d -> c p j d", p=P, j=TC)
                sp.dma_start(k.x[:, 0:TC, :], x_d[0]).then_inc(s_x[0], 16)
                sp.dma_start(wq_raw[:, :, :], io["wq_t"].rearrange("(b p) n -> p b n", p=P)).then_inc(s_wq, 16)
                sp.dma_start(mem_raw[:, :, :], io["mem"].rearrange("p (a e) -> p a e", e=DH)).then_inc(s_mem, 16)
                sp.dma_start(nrm_raw[:, :], io["nrm"]).then_inc(s_nrm, 16)
                sp.dma_start(bw[:, :, :, :].rearrange("p g n h -> p (g n h)"),
                             io["bank_w"].partition_broadcast(P)).then_inc(s_bw, 16)
                sp.dma_start(nrm_all[:, :, :].rearrange("p n d -> p (n d)"),
                             io["norms"].partition_broadcast(P)).then_inc(s_na, 16)
                for c in range(1, NC):
                    sp.dma_start(k.x[:, c * TC:(c + 1) * TC, :], x_d[c]).then_inc(s_x[c], 16)
                sp.dma_start(wo_raw[:, :, :], io["wo_t"].rearrange("(b p) n -> p b n", p=P)).then_inc(s_wo, 16)
                for c in range(NC):
                    sp.wait_ge(s_ln, TC * (c + 1))
                    sp.dma_start(k.rows.rearrange("(c j p) d -> c p j d", p=P, j=TC)[c],
                                 k.x[:, c * TC:(c + 1) * TC, :]).then_inc(s_st, 16)
                sp.wait_ge(s_st, 16 * NC)

            @block.gpsimd
            def _(pool):
                pool.memset(mem_hi[:, :, :].bitcast(F32), 0.0).then_inc(s_zero, 1)
                pool.memset(mem_lo[:, :, :].bitcast(F32), 0.0).then_inc(s_zero, 1)
                pool.memset(head_mask[:, :], 0.0).then_inc(s_zero, 1)
                pool.wait_ge(s_zero, 3)
                for h in range(HG):
                    pool.memset(head_mask[DH * h:DH * h + DH, h:h + 1], 1.0).then_inc(s_mask, 1)

                def reads(c):
                    for v in range(16 * c, 16 * c + 16):
                        j, g = v // G % TC, v % G
                        pool.wait_ge(s_rn, v + 1)
                        if c:
                            pool.wait_ge(s_tps, TURNED_O[c - 1][j] + 1)
                        pool.tensor_tensor(read_2[:, v % 2, :], read_n[:, v % 2, 0:256], read_n[:, v % 2, 256:512],
                                           ALU.add).then_inc(s_r2, 1)
                        pool.wait_ge(s_r2, v + 1)
                        pool.tensor_tensor(comb[:, j, g * P:(g + 1) * P], read_2[:, v % 2, 0:P], read_2[:, v % 2, P:2 * P],
                                           ALU.add).then_inc(s_comb, 1)

                def out(c):
                    pool.wait_ge(s_stat, 2 * TC * (c + 1))
                    ln_rstd(k, pool, c * TC, TC, s_var, s_rstd, c)

                schedule(lambda c: None, lambda c: None, reads, out)

            @block.tensor
            def _(pe):
                def turned_bank(n):
                    if n >= 2:
                        pe.wait_ge(s_tlo, n - 1)
                    return bank[n % 2]

                def turn(c):
                    pe.wait_ge(s_x[c], 16)
                    for b in range(KD):
                        t = turned_bank(TURNED_X[c][b])
                        for j in range(TC):
                            mm = pe.transpose(t[:, j * P:(j + 1) * P], k.x[:, c * TC + j, b * P:(b + 1) * P], k.ident[:, :])
                        mm.then_inc(s_tps, 1)

                def query(c):
                    if c == 0:
                        pe.wait_ge(s_split, 1)
                    pe.wait_ge(s_tlo, TURNED_X[c][KD - 1] + 1)
                    for m in range(KD):
                        u = 4 * c + m
                        if u >= 2:
                            pe.wait_ge(s_qev, u - 1)
                        for b in range(KD):
                            mm = mm3(pe, bank[2 + u % 2][:, :], wq_hi[:, b, m * P:(m + 1) * P], wq_lo[:, b, m * P:(m + 1) * P],
                                     xt_hi[:, b, :], xt_lo[:, b, :], b == 0, b == KD - 1)
                        mm.then_inc(s_q, 1)

                def reads(c):
                    if c == 0:
                        pe.wait_ge(s_split, 2)
                    pe.wait_ge(s_slo, 4 * c + 4)
                    if c:
                        pe.wait_ge(s_r, c)
                    s = c % 2
                    for j in range(TC):
                        for g in range(G):
                            tok = slice(j * P, (j + 1) * P)
                            mm = mm3(pe, bank[7][:, j * 64 + g * 16:j * 64 + g * 16 + 16], sg_hi[:, s, g, tok], sg_lo[:, s, g, tok],
                                     nrm_hi[:, g * NB:(g + 1) * NB, :].rearrange("p n h -> p (n h)"),
                                     nrm_lo[:, g * NB:(g + 1) * NB, :].rearrange("p n h -> p (n h)"), True, True)
                    mm.then_inc(s_nb, 1)
                    for v in range(16 * c, 16 * c + 16):
                        j, g = v // G % TC, v % G
                        tok = slice(j * P, (j + 1) * P)
                        if v >= 2:
                            pe.wait_ge(s_rn, v - 1)
                        mm3(pe, bank[4 + v % 2][:, :], sg_hi[:, s, g, tok], sg_lo[:, s, g, tok],
                            mem_hi[:, g, :], mem_lo[:, g, :], True, True).then_inc(s_m, 1)

                def turn_comb(c, j):
                    pe.wait_ge(s_comb, 16 * c + 4 * j + 4)
                    t = turned_bank(TURNED_O[c][j])
                    for b in range(KD):
                        mm = pe.transpose(t[:, b * P:(b + 1) * P], comb[:, j, b * P:(b + 1) * P], k.ident[:, :])
                    mm.then_inc(s_tps, 1)

                def project(c, j):
                    if c == 0:
                        pe.wait_ge(s_split, 3)
                    pe.wait_ge(s_tlo, TURNED_O[c][j] + 1)
                    if c or j:
                        pe.wait_ge(s_res, 4 * c + j)
                    for b in range(KD):
                        mm = mm3(pe, bank[6][:, :], ct_hi[:, j % 2, b, :], ct_lo[:, j % 2, b, :],
                                 wo_hi[:, b, :], wo_lo[:, b, :], b == 0, b == KD - 1)
                    mm.then_inc(s_o, 1)

                def out(c):
                    turn_comb(c, 0)
                    for j in range(TC):
                        if j + 1 < TC:
                            turn_comb(c, j + 1)
                        project(c, j)

                schedule(turn, query, reads, out)

            @block.scalar
            def _(act):
                act.wait_ge(s_wq, 16)
                act.activation(wq_hi[:, :, :], wq_raw[:, :, :], ACT.Copy).then_inc(s_whi, 1)

                def rest_of_weights():
                    act.wait_ge(s_mem, 16)
                    act.wait_ge(s_zero, 3)
                    for h in range(HG):
                        r = slice(DH * h, DH * h + DH)
                        act.activation(mem_hi[r, :, :].rearrange("p g (n x) -> p (g n) x", n=NB)[:, :, r], mem_raw[r, :, :],
                                       ACT.Copy).then_inc(s_whi, 1)
                    act.wait_ge(s_bsub, 1)
                    act.activation(bw[:, :, :, :], bw[:, :, :, :], ACT.Exp).then_inc(s_bexp, 1)

                def turned_hi(n, dst):
                    act.wait_ge(s_tps, n + 1)
                    act.activation(dst, bank[n % 2][:, :], ACT.Copy).then_inc(s_thi, 1)

                def turn(c):
                    if c:
                        act.wait_ge(s_q, 4 * c)
                    for b in range(KD):
                        turned_hi(TURNED_X[c][b], xt_hi[:, b, :])

                def query(c):
                    for u in range(4 * c, 4 * c + 4):
                        act.wait_ge(s_q, u + 1)
                        if u >= 2:
                            act.wait_ge(s_sg, u - 1)
                        act.activation(ex[:, u % 2, :], bank[2 + u % 2][:, :], ACT.Exp)
                        act.activation(rl[:, u % 2, :], bank[2 + u % 2][:, :], ACT.Relu).then_inc(s_qev, 1)
                    if c == 0:
                        rest_of_weights()
                        act.wait_ge(s_wo, 16)
                        act.activation(wo_hi[:, :, :], wo_raw[:, :, :], ACT.Copy).then_inc(s_whi, 1)

                def out(c):
                    for j in range(TC):
                        if j >= 2 or c:
                            act.wait_ge(s_o, 4 * c + j - 1)
                        turned_hi(TURNED_O[c][j], ct_hi[:, j % 2, :, :].rearrange("p b t -> p (b t)"))

                schedule(turn, query, lambda c: None, out)

            @block.vector
            def _(vec):
                def bank_weights():
                    vec.wait_ge(s_bw, 16)
                    vec.wait_ge(s_na, 16)
                    by_n = lambda a: a[:, :, :, :].rearrange("p g n h -> p g h n")
                    over = lambda a: a[:, :, :].unsqueeze(3).to_broadcast([P, G, HG, NB])
                    vec.tensor_reduce(bmax[:, :, :], by_n(bw), AX.X, ALU.max).then_inc(s_c, 1)
                    vec.tensor_reduce(act_n[:, :], nrm_all[:, :, :], AX.X, ALU.add).then_inc(s_c, 1)
                    vec.wait_ge(s_c, 2)
                    vec.tensor_tensor(by_n(bw), by_n(bw), over(bmax), ALU.subtract).then_inc(s_bsub, 1)
                    vec.tensor_scalar(act_n[:, :], act_n[:, :], EPS_MEM, None, ALU.is_ge).then_inc(s_c, 1)
                    vec.wait_ge(s_bexp, 1)
                    vec.tensor_reduce(bsum[:, :, :], by_n(bw), AX.X, ALU.add).then_inc(s_c, 1)
                    vec.wait_ge(s_c, 4)
                    vec.reciprocal(bsum[:, :, :], bsum[:, :, :]).then_inc(s_c, 1)
                    vec.wait_ge(s_c, 5)
                    vec.tensor_tensor(by_n(bw), by_n(bw), over(bsum), ALU.mult).then_inc(s_c, 1)
                    vec.wait_ge(s_c, 6)
                    vec.tensor_tensor(by_n(bw), by_n(bw), act_n[:, :].unsqueeze(1).unsqueeze(1).to_broadcast([P, G, HG, NB]),
                                      ALU.mult).then_inc(s_c, 1)

                def memories():
                    vec.wait_ge(s_nrm, 16)
                    vec.wait_ge(s_mask, HG)
                    vec.tensor_tensor(nrm_f[:, :, :], nrm_raw[:, :].unsqueeze(2).to_broadcast([P, G * NB, HG]),
                                      head_mask[:, :].unsqueeze(1).to_broadcast([P, G * NB, HG]), ALU.mult).then_inc(s_c, 1)
                    vec.wait_ge(s_c, 8)
                    vec.tensor_copy(nrm_hi[:, :, :], nrm_f[:, :, :]).then_inc(s_c, 1)
                    vec.wait_ge(s_c, 9)
                    vec.tensor_tensor(nrm_lo[:, :, :], nrm_f[:, :, :], nrm_hi[:, :, :], ALU.subtract)
                    vec.wait_ge(s_whi, 1 + HG)
                    for h in range(HG):
                        r = slice(DH * h, DH * h + DH)
                        block_of = lambda a: a[r, :, :].rearrange("p g (n x) -> p (g n) x", n=NB)[:, :, r]
                        last = vec.tensor_tensor(block_of(mem_lo), mem_raw[r, :, :], block_of(mem_hi), ALU.subtract)
                    last.then_inc(s_split, 1)

                def turned_lo(n, src, dst):
                    vec.wait_ge(s_thi, n + 1)
                    vec.tensor_tensor(dst, bank[n % 2][:, :], src, ALU.subtract).then_inc(s_tlo, 1)

                def turn(c):
                    for b in range(KD):
                        turned_lo(TURNED_X[c][b], xt_hi[:, b, :], xt_lo[:, b, :])

                def query(c):
                    if c == 0:
                        vec.wait_ge(s_whi, 1)
                        vec.tensor_tensor(wq_lo[:, :, :], wq_raw[:, :, :], wq_hi[:, :, :], ALU.subtract).then_inc(s_split, 1)
                    for u in range(4 * c, 4 * c + 4):
                        m = u % 4
                        vec.wait_ge(s_qev, u + 1)
                        if c >= 2 and m == 0:
                            vec.wait_ge(s_m, 16 * (c - 1))
                        vec.scalar_tensor_tensor(sg[:, u % 2, :], ex[:, u % 2, :], 1.0, rl[:, u % 2, :], ALU.min, ALU.add)
                        vec.scalar_tensor_tensor(sg_hi[:, c % 2, m, :], ex[:, u % 2, :], 1.0, rl[:, u % 2, :],
                                                 ALU.min, ALU.add).then_inc(s_sg, 1)
                        vec.wait_ge(s_sg, u + 1)
                        vec.tensor_tensor(sg_lo[:, c % 2, m, :], sg[:, u % 2, :], sg_hi[:, c % 2, m, :],
                                          ALU.subtract).then_inc(s_slo, 1)
                    if c == 0:
                        bank_weights()
                        memories()
                        vec.wait_ge(s_whi, 2 + HG)
                        vec.tensor_tensor(wo_lo[:, :, :], wo_raw[:, :, :], wo_hi[:, :, :], ALU.subtract).then_inc(s_split, 1)

                def reads(c):
                    vec.wait_ge(s_nb, c + 1)
                    w = rw[:, c % 2, :, :]
                    vec.tensor_scalar(w, bank[7][:, 0:256].rearrange("p (j a) -> p j a", j=TC), EPS_MEM, None,
                                      ALU.max).then_inc(s_r, 1)
                    vec.wait_ge(s_r, c + 1)
                    vec.reciprocal(w, w).then_inc(s_rw, 1)
                    vec.wait_ge(s_rw, 2 * c + 1)
                    vec.tensor_tensor(w, w, bw[:, :, :, :].rearrange("p g n h -> p (g n h)").unsqueeze(1)
                                      .to_broadcast([P, TC, 64]), ALU.mult).then_inc(s_rw, 1)
                    vec.wait_ge(s_rw, 2 * c + 2)
                    for v in range(16 * c, 16 * c + 16):
                        j, g = v // G % TC, v % G
                        vec.wait_ge(s_m, v + 1)
                        if v >= 2:
                            vec.wait_ge(s_comb, v - 1)
                        vec.tensor_tensor(read_n[:, v % 2, :].rearrange("p (a e) -> p a e", e=DH),
                                          bank[4 + v % 2][:, :].rearrange("p (a e) -> p a e", e=DH),
                                          w[:, j, g * 16:g * 16 + 16].unsqueeze(2).to_broadcast([P, 16, DH]),
                                          ALU.mult).then_inc(s_rn, 1)

                def residual(c, j):
                    tile = c * TC + j
                    vec.wait_ge(s_o, tile + 1)
                    vec.tensor_tensor(k.x[:, tile, :], bank[6][:, :], k.x[:, tile, :], ALU.add).then_inc(s_res, 1)
                    vec.wait_ge(s_res, tile + 1)
                    ln_stats(k, vec, tile, s_stat, tile)

                def normalise(c):
                    vec.wait_ge(s_rstd, c + 1)
                    for tile in range(c * TC, c * TC + TC):
                        ln_apply(k, vec, tile).then_inc(s_ln, 1)

                def out(c):
                    lo = lambda j: turned_lo(TURNED_O[c][j], ct_hi[:, j % 2, :, :].rearrange("p b t -> p (b t)"),
                                             ct_lo[:, j % 2, :, :].rearrange("p b t -> p (b t)"))
                    lo(0)
                    for j in range(TC):
                        if j + 1 < TC:
                            lo(j + 1)
                        residual(c, j)
                    if c:
                        normalise(c - 1)

                schedule(turn, query, reads, out)
                normalise(NC - 1)


FLOOR = -0.498046875


def three_stages(eng, n, first, second, third, between=lambda h, p: None):
    def at(stage, g):
        stage(g // 2, g % 2)

    at(first, 0)
    for g in range(3):
        at(first, g + 1)
        if g:
            at(between, g - 1)
        at(second, g)
        if g:
            at(third, g - 1)
    pairs = (n - 2) // 2
    with eng.Fori(1, pairs) as i:
        first(i + 1, 0)
        between(i, 0)
        second(i, 1)
        third(i, 0)
        first(i + 1, 1)
        between(i, 1)
        second(i + 1, 0)
        third(i, 1)
    for g in range(2 * pairs + 1, n):
        if g + 1 < n:
            at(first, g + 1)
        at(between, g - 1)
        at(second, g)
        at(third, g - 1)
    at(between, n - 1)
    at(third, n - 1)


def started(h):
    return not (isinstance(h, int) and h == 0)


E0 = 16
GRP = 256
NG0 = (2 * T) // GRP + E0 - 1
F0 = 256


def experts0_shared(k):
    nc, bank, io = k.nc, k.bank, k.io
    NS, FB = 2, F0 // P
    NU = NS * FB
    rt = lambda name, shape, dt=F32: k.sb("r0_" + name, shape, dt, k.moe_ctx)
    k.slot = rt("slot", [P, 2, NT], I32)
    k.weight = rt("weight", [P, 2, NT])
    k.token_of = rt("token_of", [P, 2 * NG0], I32)
    k.group_expert = rt("group_expert", [P, NG0], I32)
    k.group_bias = rt("group_bias", [P, NG0, 2 * FB])
    k.comb_aug = rt("comb_aug", [P, NT, E0 + NS])
    with ExitStack() as ctx:
        sb = lambda name, shape, dt=F32: k.sb("s0_" + name, shape, dt, ctx)
        wa_raw = sb("wa_raw", [P, KD, E0])
        wa_hi, wa_lo = sb("wa_hi", [P, KD, E0], F32R), sb("wa_lo", [P, KD, E0], F32R)
        sraw = sb("sraw", [P, 2, 2 * KD * F0])
        w1_hi, w1_lo = sb("w1_hi", [P, NS, 2, KD, F0], F32R), sb("w1_lo", [P, NS, 2, KD, F0], F32R)
        w2_hi, w2_lo = sb("w2_hi", [P, NU, D], F32R), sb("w2_lo", [P, NU, D], F32R)
        gb, ub = sb("gb", [P, NU]), sb("ub", [P, NU])
        rgb, rub = sb("rgb", [P, FB, E0]), sb("rub", [P, FB, E0])
        xt_hi, xt_lo = sb("xt_hi", [P, KD, T], F32R), sb("xt_lo", [P, KD, T], F32R)
        ge = sb("ge", [P, CH])
        hf = sb("hf", [P, 2, CH])
        h_hi, h_lo = sb("h_hi", [P, NU, CH], F32R), sb("h_lo", [P, NU, CH], F32R)
        aff = sb("aff", [P, NT, E0])
        top, arg = sb("top", [P, NT, 8]), sb("arg", [P, NT, 8], U32)
        argf = sb("argf", [P, 2, NT])
        onehot = sb("onehot", [P, 2, NT, E0])
        sel = sb("sel", [P, NT * E0], BF16)
        upper, ones = sb("upper", [P, P], BF16), sb("ones", [P, P], BF16)
        run_a, run_b = sb("run_a", [P, NT, E0]), sb("run_b", [P, NT, E0])
        tot = sb("tot", [P, NT, E0])
        cnt_i = sb("cnt_i", [P, E0], I32)
        groups, ends, start2 = sb("groups", [P, E0]), sb("ends", [P, E0]), sb("start2", [P, E0])
        ones16 = sb("ones16", [P, E0])
        prod = sb("prod", [P, 2 * NT, E0])
        posk, st, fl, pp = (sb(n, [P, 2 * NT]) for n in ("posk", "st", "fl", "pp"))
        fl_i = sb("fl_i", [P, 2 * NT], I32)
        rsum = sb("rsum", [P, NT])
        iota_e, iota_p, iota_s, iota_g = sb("iota_e", [P, E0]), sb("iota_p", [P, P]), sb("iota_s", [P, 2 * NG0]), sb("iota_g", [P, NG0])
        tok = sb("tok", [P, NT])
        at_row = sb("at_row", [P, 2, P], F32R)
        at_col = sb("at_col", [P, 2 * NT, 2 * NG0], F32R)
        by_group = lambda flat: flat[:, 0:NG0 * E0].rearrange("p (g e) -> p g e", e=E0)
        gsel = by_group(onehot[:, :, :, :].rearrange("p k t e -> p (k t e)"))
        gprod = by_group(prod[:, :, :].rearrange("p a e -> p (a e)"))
        gef = sb("gef", [P, NG0])

        s_wa, s_b = k.sem("s0_wa_loaded"), k.sem("s0_bias_loaded")
        s_w1, s_w2 = [k.sem(f"s0_w1_loaded{s}") for s in range(NS)], k.sem("s0_w2_loaded")
        s_whi, s_wlo = k.sem("s0_weight_hi"), k.sem("s0_weight_split")
        s_tps, s_thi, s_tlo = k.sem("s0_turned"), k.sem("s0_turned_hi"), k.sem("s0_turned_lo")
        s_lg, s_aff = k.sem("s0_logits"), k.sem("s0_affinity")
        s_gu, s_ge, s_h, s_hlo = k.sem("s0_gate_up"), k.sem("s0_gelu"), k.sem("s0_hidden"), k.sem("s0_hidden_split")
        s_hh = k.sem("s0_hidden_hi")
        s_dn, s_res = k.sem("s0_down"), k.sem("s0_residual")
        s_const = k.sem("s0_constants")
        s_r = k.sem("s0_route_chain")
        s_sel, s_pre, s_tab = k.sem("s0_selected"), k.sem("s0_prefix"), k.sem("s0_table")
        s_row, s_col = k.sem("s0_rows_made"), k.sem("s0_cols_made")
        s_rowfree = k.sem("s0_rows_used")

        with nc.Block() as block:
            @block.sync
            def _(sp):
                sp.dma_start(wa_raw[:, :, :], io["wa"].rearrange("(b p) n -> p b n", p=P)).then_inc(s_wa, 16)
                for s in range(NS):
                    for a, name in enumerate(("sg", "sw1")):
                        sp.dma_start(sraw[:, s, a * KD * F0:(a + 1) * KD * F0].rearrange("p (b n) -> p b n", b=KD),
                                     io[name][s].rearrange("(b p) n -> p b n", p=P)).then_inc(s_w1[s], 16)
                sp.dma_start(gb[:, :], io["sgb_t"]).then_inc(s_b, 16)
                sp.dma_start(ub[:, :], io["sb1_t"]).then_inc(s_b, 16)
                sp.dma_start(rgb[:, :, :].rearrange("p f e -> p (f e)"), io["rgb_t"]).then_inc(s_b, 16)
                sp.dma_start(rub[:, :, :].rearrange("p f e -> p (f e)"), io["rb1_t"]).then_inc(s_b, 16)
                sp.wait_ge(s_wlo, 2)
                sp.dma_start(sraw[:, 0, :].rearrange("p (u n) -> p u n", n=D),
                             io["sw2"].rearrange("s (f p) n -> p (s f) n", p=P)).then_inc(s_w2, 16)

            @block.gpsimd
            def _(pool):
                pool.memset(upper[:, :], 1.0).then_inc(s_const, 1)
                pool.memset(ones[:, :], 1.0).then_inc(s_const, 1)
                pool.memset(ones16[:, :], 1.0).then_inc(s_const, 1)
                pool.memset(k.comb_aug[:, :, :], 1.0).then_inc(s_const, 1)
                for a, n in ((iota_e, E0), (iota_p, P), (iota_s, 2 * NG0), (iota_g, NG0)):
                    pool.iota(a[:, :], [[1, n]], base=0, channel_multiplier=0,
                              allow_small_or_imprecise_dtypes=True).then_inc(s_const, 1)
                pool.iota(tok[:, :], [[P, NT]], base=0, channel_multiplier=1,
                          allow_small_or_imprecise_dtypes=True).then_inc(s_const, 1)
                pool.wait_ge(s_const, 9)
                pool.affine_select(out=upper[:, :], in_=upper[:, :], compare_op=ALU.is_gt, fill=0.0,
                                   base=0, pattern=[[1, P]], channel_multiplier=-1).then_inc(s_const, 1)

            @block.tensor
            def _(pe):
                def turn(c):
                    for b in range(KD):
                        n = 4 * c + b
                        if n >= 2:
                            pe.wait_ge(s_tlo, n - 1)
                        for j in range(TC):
                            mm = pe.transpose(bank[n % 2][:, j * P:(j + 1) * P], k.x[:, c * TC + j, b * P:(b + 1) * P], k.ident[:, :])
                        mm.then_inc(s_tps, 1)

                def logits(c):
                    pe.wait_ge(s_tlo, 4 * c + 4)
                    for i in range(4 * c, 4 * c + 4):
                        for b in range(KD):
                            t = slice(i * P, (i + 1) * P)
                            mm = mm3(pe, bank[7][:, i * E0:(i + 1) * E0], xt_hi[:, b, t], xt_lo[:, b, t],
                                     wa_hi[:, b, :], wa_lo[:, b, :], b == 0, b == KD - 1)
                    mm.then_inc(s_lg, 1)

                def gate_up(c, u):
                    n = c * NU + u
                    s, f = u // FB, u % FB
                    if c == 0:
                        pe.wait_ge(s_wlo, 2 + s)
                    if n >= 2:
                        pe.wait_ge(s_h, n - 1)
                    fs = slice(f * P, (f + 1) * P)
                    t = slice(c * CH, (c + 1) * CH)
                    for a in range(2):
                        for b in range(KD):
                            mm = mm3(pe, bank[2 + 2 * a + n % 2][:, :], w1_hi[:, s, a, b, fs], w1_lo[:, s, a, b, fs],
                                     xt_hi[:, b, t], xt_lo[:, b, t], b == 0, b == KD - 1)
                    mm.then_inc(s_gu, 1)

                def down(c):
                    if c == 0:
                        pe.wait_ge(s_wlo, 4)
                    pe.wait_ge(s_hlo, NU * c + NU)
                    for i in range(4 * c, 4 * c + 4):
                        if i:
                            pe.wait_ge(s_res, i)
                        t = slice(i % 4 * P, (i % 4 + 1) * P)
                        for u in range(NU):
                            mm = mm3(pe, bank[6][:, :], h_hi[:, u, t], h_lo[:, u, t], w2_hi[:, u, :], w2_lo[:, u, :],
                                     u == 0, u == NU - 1)
                        mm.then_inc(s_dn, 1)

                def prefix():
                    pe.wait_ge(s_sel, 1)
                    pe.matmul(bank[0][:, 0:256], upper[:, :], sel[:, :], start=True, stop=True)
                    pe.matmul(bank[0][:, 256:512], ones[:, :], sel[:, :], start=True, stop=True).then_inc(s_pre, 1)

                def table(n):
                    if n == 0:
                        pe.wait_ge(s_col, 1)
                    for a in range(n * 8, n * 8 + 8):
                        pe.wait_ge(s_row, a + 1)
                        pe.matmul(bank[1][:, 0:2 * NG0], at_row[:, a % 2, :], at_col[:, a, :], start=(a == 0),
                                  stop=(a == 2 * NT - 1)).then_inc(s_rowfree, 1)

                pe.wait_ge(s_const, 10)
                turn(0)
                pe.wait_ge(s_wlo, 1)
                for c in range(NC):
                    if c + 1 < NC:
                        turn(c + 1)
                    logits(c)
                gate_up(0, 0)
                gate_up(0, 1)
                prefix()
                gate_up(0, 2)
                gate_up(0, 3)
                for c in range(NC):
                    for u in range(NU):
                        if c + 1 < NC:
                            if u == 1:
                                down(c)
                            gate_up(c + 1, u)
                        if c == 1 and u:
                            table(u - 1)
                    if c == 1:
                        table(NU - 1)
                down(NC - 1)

            @block.scalar
            def _(act):
                act.wait_ge(s_wa, 16)
                act.activation(wa_hi[:, :, :], wa_raw[:, :, :], ACT.Copy).then_inc(s_whi, 1)
                for n in range(4 * NC):
                    act.wait_ge(s_tps, n + 1)
                    act.activation(xt_hi[:, n % 4, n // 4 * CH:(n // 4 + 1) * CH], bank[n % 2][:, :], ACT.Copy).then_inc(s_thi, 1)
                    if n in (3, 7):
                        s = n // 4
                        act.wait_ge(s_w1[s], 32)
                        act.activation(w1_hi[:, s, :, :, :].rearrange("p a b n -> p (a b n)"), sraw[:, s, :],
                                       ACT.Copy).then_inc(s_whi, 1)
                act.wait_ge(s_lg, NC)
                act.activation(aff[:, :, :].rearrange("p t e -> p (t e)"), bank[7][:, 0:NT * E0], ACT.Sigmoid).then_inc(s_aff, 1)
                act.wait_ge(s_w2, 16)
                act.activation(w2_hi[:, :, :].rearrange("p u n -> p (u n)"), sraw[:, 0, :], ACT.Copy).then_inc(s_whi, 1)
                act.wait_ge(s_b, 64)
                for n in range(NC * NU):
                    act.wait_ge(s_gu, n + 1)
                    if n:
                        act.wait_ge(s_h, n)
                    act.activation(ge[:, :], bank[2 + n % 2][:, :], ACT.Gelu, bias=gb[:, n % NU:n % NU + 1]).then_inc(s_ge, 1)

            @block.vector
            def _(vec):
                done = [0]

                def step(ins):
                    ins.then_inc(s_r, 1)
                    done[0] += 1

                def sync():
                    vec.wait_ge(s_r, done[0])

                def split_lo(n, lo, raw, hi):
                    vec.wait_ge(s_whi, n + 1)
                    vec.tensor_tensor(lo, raw, hi, ALU.subtract).then_inc(s_wlo, 1)

                def hidden(c, u):
                    n = c * NU + u
                    vec.wait_ge(s_ge, n + 1)
                    if c:
                        vec.wait_ge(s_dn, 4 * c)
                    up = bank[4 + n % 2][:, :]
                    if n >= 2:
                        vec.wait_ge(s_hlo, n - 1)
                    hfn = hf[:, n % 2, :]
                    vec.scalar_tensor_tensor(hfn, up, ub[:, u:u + 1], ge[:, :], ALU.add, ALU.mult).then_inc(s_h, 1)
                    vec.wait_ge(s_h, n + 1)
                    vec.tensor_copy(h_hi[:, u, :], hfn).then_inc(s_hh, 1)
                    vec.wait_ge(s_hh, n + 1)
                    vec.tensor_tensor(h_lo[:, u, :], hfn, h_hi[:, u, :], ALU.subtract).then_inc(s_hlo, 1)

                def residual(c):
                    for i in range(4 * c, 4 * c + 4):
                        vec.wait_ge(s_dn, i + 1)
                        vec.scalar_tensor_tensor(k.x[:, i, :], k.x[:, i, :], 2.0, bank[6][:, :], ALU.mult, ALU.add).then_inc(s_res, 1)

                def top2():
                    vec.wait_ge(s_aff, 1)
                    for i in range(NT):
                        step(vec.max(top[:, i, :], aff[:, i, :]))
                    sync()
                    for i in range(NT):
                        step(vec.max_index(arg[:, i, :], top[:, i, :], aff[:, i, :]))
                    sync()
                    step(vec.tensor_copy(argf[:, :, :], arg[:, :, 0:2].rearrange("p t k -> p k t")))
                    vec.wait_ge(s_const, 10)
                    sync()
                    step(vec.tensor_tensor(onehot[:, :, :, :].rearrange("p k t e -> p (k t) e"),
                                           iota_e[:, :].unsqueeze(1).to_broadcast([P, 2 * NT, E0]),
                                           argf[:, :, :].rearrange("p k t -> p (k t)").unsqueeze(2).to_broadcast([P, 2 * NT, E0]),
                                           ALU.is_equal))
                    sync()
                    vec.tensor_tensor(sel[:, :], onehot[:, 0, :, :].rearrange("p t e -> p (t e)"),
                                      onehot[:, 1, :, :].rearrange("p t e -> p (t e)"), ALU.add).then_inc(s_sel, 1)
                    step(vec.tensor_tensor(rsum[:, :], top[:, :, 0], top[:, :, 1], ALU.add))
                    sync()
                    step(vec.reciprocal(rsum[:, :], rsum[:, :]))
                    sync()
                    step(vec.tensor_tensor(k.weight[:, :, :], top[:, :, 0:2].rearrange("p t k -> p k t"),
                                           rsum[:, :].unsqueeze(1).to_broadcast([P, 2, NT]), ALU.mult))
                    sync()
                    step(vec.tensor_tensor(prod[:, :, :], onehot[:, :, :, :].rearrange("p k t e -> p (k t) e"),
                                           k.weight[:, :, :].rearrange("p k t -> p (k t)").unsqueeze(2).to_broadcast([P, 2 * NT, E0]),
                                           ALU.mult))
                    sync()
                    step(vec.tensor_tensor(k.comb_aug[:, :, 0:E0], prod[:, 0:NT, :], prod[:, NT:2 * NT, :], ALU.add))

                def positions():
                    vec.wait_ge(s_pre, 1)
                    flat = lambda a: a[:, :, :].rearrange("p t e -> p (t e)")
                    step(vec.tensor_copy(flat(tot), bank[0][:, 256:512]))
                    step(vec.tensor_copy(flat(run_a), bank[0][:, 256:512]))
                    a, b = run_a, run_b
                    for d in (1, 2, 4, 8):
                        sync()
                        step(vec.tensor_tensor(b[:, d:, :], a[:, d:, :], a[:, :NT - d, :], ALU.add))
                        step(vec.tensor_copy(b[:, :d, :], a[:, :d, :]))
                        a, b = b, a
                    sync()
                    step(vec.tensor_scalar(cnt_i[:, :], a[:, NT - 1, :], 1 / GRP, (GRP - 1) / GRP + FLOOR, ALU.mult, ALU.add))
                    step(vec.tensor_tensor(flat(b), flat(a), flat(tot), ALU.subtract))
                    sync()
                    step(vec.tensor_copy(groups[:, :], cnt_i[:, :]))
                    step(vec.tensor_tensor(flat(b), bank[0][:, 0:256], flat(b), ALU.add))
                    sync()
                    step(vec.tensor_tensor_scan(ends[:, :], ones16[:, :], groups[:, :], 0.0, ALU.mult, ALU.add))
                    step(vec.tensor_tensor(prod[:, :, :].rearrange("p (k t) e -> p k (t e)", k=2),
                                           onehot[:, :, :, :].rearrange("p k t e -> p k (t e)"),
                                           flat(b).unsqueeze(1).to_broadcast([P, 2, NT * E0]), ALU.mult))
                    sync()
                    step(vec.tensor_reduce(posk[:, :], prod[:, :, :], AX.X, ALU.add))
                    step(vec.tensor_tensor(start2[:, :], ends[:, :], groups[:, :], ALU.subtract))
                    sync()
                    step(vec.tensor_scalar(start2[:, :], start2[:, :], float(GRP // P), None, ALU.mult))
                    step(vec.tensor_scalar(fl_i[:, :], posk[:, :], 1 / P, FLOOR, ALU.mult, ALU.add))
                    sync()
                    step(vec.tensor_tensor(prod[:, :, :], onehot[:, :, :, :].rearrange("p k t e -> p (k t) e"),
                                           start2[:, :].unsqueeze(1).to_broadcast([P, 2 * NT, E0]), ALU.mult))
                    step(vec.tensor_copy(fl[:, :], fl_i[:, :]))
                    sync()
                    step(vec.tensor_reduce(st[:, :], prod[:, :, :], AX.X, ALU.add))
                    step(vec.scalar_tensor_tensor(pp[:, :], fl[:, :], -float(P), posk[:, :], ALU.mult, ALU.add))
                    sync()
                    step(vec.tensor_tensor(st[:, :], st[:, :], fl[:, :], ALU.add))
                    sync()
                    step(vec.scalar_tensor_tensor(k.slot[:, :, :].rearrange("p k t -> p (k t)"), st[:, :], float(P), pp[:, :],
                                                  ALU.mult, ALU.add))

                def columns():
                    step(vec.tensor_tensor(at_col[:, :, :], iota_s[:, :].unsqueeze(1).to_broadcast([P, 2 * NT, 2 * NG0]),
                                           st[:, :].unsqueeze(2).to_broadcast([P, 2 * NT, 2 * NG0]), ALU.is_equal))
                    sync()
                    for kk in range(2):
                        last = vec.tensor_tensor(at_col[:, kk * NT:(kk + 1) * NT, :], at_col[:, kk * NT:(kk + 1) * NT, :].bitcast(F32),
                                                 tok[:, :].unsqueeze(2).to_broadcast([P, NT, 2 * NG0]), ALU.mult)
                    last.then_inc(s_col, 1)

                def rows(n):
                    for a in range(8 * n, 8 * n + 8):
                        if a >= 2:
                            vec.wait_ge(s_rowfree, a - 1)
                        vec.tensor_scalar(at_row[:, a % 2, :], iota_p[:, :], pp[:, a:a + 1], None, ALU.is_equal).then_inc(s_row, 1)

                def group_tables():
                    step(vec.tensor_tensor(gsel[:, :, :], iota_g[:, :].unsqueeze(2).to_broadcast([P, NG0, E0]),
                                           ends[:, :].unsqueeze(1).to_broadcast([P, NG0, E0]), ALU.is_ge))
                    sync()
                    step(vec.tensor_reduce(gef[:, :], gsel[:, :, :], AX.X, ALU.add))
                    sync()
                    step(vec.tensor_scalar(gef[:, :], gef[:, :], float(E0 - 1), None, ALU.min))
                    sync()
                    step(vec.tensor_copy(k.group_expert[:, :], gef[:, :]))
                    step(vec.tensor_tensor(gsel[:, :, :], iota_e[:, :].unsqueeze(1).to_broadcast([P, NG0, E0]),
                                           gef[:, :].unsqueeze(2).to_broadcast([P, NG0, E0]), ALU.is_equal))
                    vec.wait_ge(s_b, 64)
                    for a, table in enumerate((rgb, rub)):
                        for f in range(FB):
                            sync()
                            step(vec.tensor_tensor(gprod[:, :, :], gsel[:, :, :], table[:, f, :].unsqueeze(1).to_broadcast([P, NG0, E0]),
                                                   ALU.mult))
                            sync()
                            step(vec.tensor_reduce(k.group_bias[:, :, 2 * a + f], gprod[:, :, :], AX.X, ALU.add))

                split_lo(0, wa_lo[:, :, :], wa_raw[:, :, :], wa_hi[:, :, :])
                for n in range(4 * NC):
                    vec.wait_ge(s_thi, n + 1)
                    t = slice(n // 4 * CH, (n // 4 + 1) * CH)
                    vec.tensor_tensor(xt_lo[:, n % 4, t], bank[n % 2][:, :], xt_hi[:, n % 4, t], ALU.subtract).then_inc(s_tlo, 1)
                    if n in (7, 11):
                        s = (n - 7) // 4
                        split_lo(1 + s, w1_lo[:, s, :, :, :].rearrange("p a b n -> p (a b n)"), sraw[:, s, :],
                                 w1_hi[:, s, :, :, :].rearrange("p a b n -> p (a b n)"))
                top2()
                vec.wait_ge(s_b, 64)
                hidden(0, 0)
                split_lo(3, w2_lo[:, :, :].rearrange("p u n -> p (u n)"), sraw[:, 0, :], w2_hi[:, :, :].rearrange("p u n -> p (u n)"))
                hidden(0, 1)
                positions()
                hidden(0, 2)
                columns()
                hidden(0, 3)
                for c in range(NC):
                    for u in range(NU):
                        if c + 1 < NC:
                            if u == 0:
                                residual(c)
                            hidden(c + 1, u)
                        if c == 1:
                            rows(u)
                    if c == 1:
                        vec.wait_ge(s_rowfree, 2 * NT)
                        step(vec.tensor_copy(k.token_of[:, :], bank[1][:, 0:2 * NG0]))
                    if c == 2:
                        group_tables()
                residual(NC - 1)


def experts0_routed(k):
    nc, bank, io = k.nc, k.bank, k.io
    FB, S = F0 // P, GRP // P
    W = KD * F0
    with ExitStack() as ctx:
        sb = lambda name, shape, dt=F32: k.sb("e0_" + name, shape, dt, ctx)
        raw = [sb(f"raw{p}", [P, 3 * W]) for p in range(2)]
        w_hi = [sb(f"w_hi{p}", [P, 3 * W], F32R) for p in range(2)]
        w_lo = [sb(f"w_lo{p}", [P, 3 * W], F32R) for p in range(2)]
        index = [sb(f"index{p}", [P, S], I32) for p in range(2)]
        bias = [sb(f"bias{p}", [P, 2 * FB]) for p in range(2)]
        xg = [sb(f"xg{p}", [P, S, D]) for p in range(2)]
        xt_hi = [sb(f"xt_hi{p}", [P, KD, GRP], F32R) for p in range(2)]
        xt_lo = [sb(f"xt_lo{p}", [P, KD, GRP], F32R) for p in range(2)]
        ge = [sb(f"ge{p}", [P, FB, GRP]) for p in range(2)]
        hf = [sb(f"hf{p}", [P, FB, GRP]) for p in range(2)]
        h_hi = [sb(f"h_hi{p}", [P, FB, GRP], F32R) for p in range(2)]
        h_lo = [sb(f"h_lo{p}", [P, FB, GRP], F32R) for p in range(2)]
        y = [sb(f"y{p}", [P, S, D]) for p in range(2)]

        two = lambda name: [k.sem(f"e0_{name}{p}") for p in range(2)]
        s_w, s_v, s_g, s_y = two("gate_up_loaded"), two("down_loaded"), two("rows_gathered"), two("results_stored")
        s_go = k.sem("e0_index_seen")
        s_ix, s_bias = k.sem("e0_index"), k.sem("e0_bias")
        s_whi, s_wlo = k.sem("e0_gate_up_hi"), k.sem("e0_gate_up_lo")
        s_vhi, s_vlo = k.sem("e0_down_hi"), k.sem("e0_down_lo")
        s_tps, s_thi, s_tlo = k.sem("e0_turned"), k.sem("e0_turned_hi"), k.sem("e0_turned_lo")
        s_gu, s_ge, s_h, s_hh, s_hlo = (k.sem("e0_" + n) for n in ("gate_up", "gelu", "hidden", "hidden_hi", "hidden_lo"))
        s_dn, s_ysb = k.sem("e0_down"), k.sem("e0_results")
        nothing = lambda h, p: None
        y_rows = k.y0.rearrange("(g s p) d -> g p s d", p=P, s=S)

        with nc.Block() as block:
            @block.sync
            def _(sp):
                def load(h, p):
                    g = 2 * h + p
                    e = sp.value_load(k.group_expert[0:1, bass.ds(g, 1)], min_val=0, max_val=E0 - 1)
                    if started(h):
                        sp.wait_ge(s_wlo, g - 1)
                    for a, name in enumerate(("rg", "rw1")):
                        sp.dma_start(raw[p][:, a * W:(a + 1) * W].rearrange("p (b n) -> p b n", b=KD),
                                     io[name][bass.ds(e, 1)].rearrange("e (b p) n -> p (e b) n", p=P)).then_inc(s_w[p], 16)
                    if started(h):
                        sp.wait_ge(s_vlo, g - 1)
                    sp.dma_start(raw[p][:, 2 * W:].rearrange("p (f n) -> p f n", f=FB),
                                 io["rw2"][bass.ds(e, 1)].rearrange("e (f p) n -> p (e f) n", p=P)).then_inc(s_v[p], 16)

                three_stages(sp, NG0, load, nothing, nothing)

            @block.gpsimd
            def _(pool):
                def gather(h, p):
                    g = 2 * h + p
                    if started(h):
                        pool.wait_ge(s_g[p], 16 * S * h)
                        pool.wait_ge(s_tps, g - 1)
                    pool.tensor_copy(index[p][:, :], k.token_of[:, bass.ds(S * g, S)]).then_inc(s_ix, 1)
                    pool.wait_ge(s_ix, g + 1)
                    pool.sem_inc(s_go, 1)
                    for s in range(S):
                        pool.indirect_dma_start(xg[p][:, s, :], None, k.rows, bass.IndirectOffsetOnAxis(index[p][:, s:s + 1], 0)
                                                ).then_inc(s_g[p], 16)

                three_stages(pool, NG0, gather, nothing, nothing)

            @block.tensor
            def _(pe):
                def turn(h, p):
                    g = 2 * h + p
                    pe.wait_ge(s_g[p], 16 * S * (h + 1))
                    if started(h) or p:
                        pe.wait_ge(s_tlo, g)
                    for b in range(KD):
                        for s in range(S):
                            c = (b % 2 * S + s) * P
                            mm = pe.transpose(bank[b // 2][:, c:c + P], xg[p][:, s, b * P:(b + 1) * P], k.ident[:, :])
                    mm.then_inc(s_tps, 1)

                def gate_up(h, p):
                    g = 2 * h + p
                    pe.wait_ge(s_wlo, g + 1)
                    pe.wait_ge(s_tlo, g + 1)
                    if started(h):
                        pe.wait_ge(s_h, g - 1)
                    for a in range(2):
                        for f in range(FB):
                            for b in range(KD):
                                c = slice(a * W + b * F0 + f * P, a * W + b * F0 + f * P + P)
                                mm = mm3(pe, bank[2 + 2 * a + p][:, f * GRP:(f + 1) * GRP], w_hi[p][:, c], w_lo[p][:, c],
                                         xt_hi[p][:, b, :], xt_lo[p][:, b, :], b == 0, b == KD - 1)
                    mm.then_inc(s_gu, 1)

                def down(h, p):
                    g = 2 * h + p
                    pe.wait_ge(s_hlo, g + 1)
                    pe.wait_ge(s_vlo, g + 1)
                    if started(h) or p:
                        pe.wait_ge(s_ysb, g)
                    for s in range(S):
                        for f in range(FB):
                            t, c = slice(s * P, (s + 1) * P), slice(2 * W + f * D, 2 * W + (f + 1) * D)
                            mm = mm3(pe, bank[6 + s][:, :], h_hi[p][:, f, t], h_lo[p][:, f, t], w_hi[p][:, c], w_lo[p][:, c],
                                     f == 0, f == FB - 1)
                    mm.then_inc(s_dn, 1)

                three_stages(pe, NG0, turn, gate_up, down)

            @block.scalar
            def _(act):
                def split(h, p):
                    g = 2 * h + p
                    act.wait_ge(s_w[p], 32 * (h + 1))
                    if started(h):
                        act.wait_ge(s_gu, g - 1)
                    act.activation(w_hi[p][:, 0:2 * W], raw[p][:, 0:2 * W], ACT.Copy).then_inc(s_whi, 1)
                    act.wait_ge(s_tps, g + 1)
                    for q in range(2):
                        last = act.activation(xt_hi[p][:, 2 * q:2 * q + 2, :].rearrange("p b t -> p (b t)"), bank[q][:, :], ACT.Copy)
                    last.then_inc(s_thi, 1)

                def gelu(h, p):
                    g = 2 * h + p
                    act.wait_ge(s_v[p], 16 * (h + 1))
                    if started(h):
                        act.wait_ge(s_dn, g - 1)
                    act.activation(w_hi[p][:, 2 * W:], raw[p][:, 2 * W:], ACT.Copy).then_inc(s_vhi, 1)
                    act.wait_ge(s_gu, g + 1)
                    act.wait_ge(s_bias, g + 1)
                    if started(h):
                        act.wait_ge(s_h, g - 1)
                    for f in range(FB):
                        last = act.activation(ge[p][:, f, :], bank[2 + p][:, f * GRP:(f + 1) * GRP], ACT.Gelu, bias=bias[p][:, f:f + 1])
                    last.then_inc(s_ge, 1)

                def results(h, p):
                    g = 2 * h + p
                    act.wait_ge(s_dn, g + 1)
                    if started(h):
                        act.wait_ge(s_y[p], 16 * h)
                    for s in range(S):
                        last = act.activation(y[p][:, s, :], bank[6 + s][:, :], ACT.Copy)
                    last.then_inc(s_ysb, 1)
                    act.wait_ge(s_ysb, g + 1)
                    act.dma_start(y_rows[bass.ds(g, 1)].rearrange("g p s d -> p (g s) d"), y[p][:, :, :]).then_inc(s_y[p], 16)

                three_stages(act, NG0, split, gelu, results)
                act.wait_ge(s_y[0], 16 * ((NG0 + 1) // 2))
                act.wait_ge(s_y[1], 16 * (NG0 // 2))

            @block.vector
            def _(vec):
                def split(h, p):
                    g = 2 * h + p
                    if started(h):
                        vec.wait_ge(s_h, g - 1)
                    vec.tensor_copy(bias[p][:, :], k.group_bias[:, bass.ds(g, 1), :].rearrange("p g a -> p (g a)")).then_inc(s_bias, 1)
                    vec.wait_ge(s_whi, g + 1)
                    vec.tensor_tensor(w_lo[p][:, 0:2 * W], raw[p][:, 0:2 * W], w_hi[p][:, 0:2 * W], ALU.subtract).then_inc(s_wlo, 1)
                    vec.wait_ge(s_thi, g + 1)
                    for q in range(2):
                        part = lambda a: a[p][:, 2 * q:2 * q + 2, :].rearrange("p b t -> p (b t)")
                        last = vec.tensor_tensor(part(xt_lo), bank[q][:, :], part(xt_hi), ALU.subtract)
                    last.then_inc(s_tlo, 1)

                def hidden(h, p):
                    g = 2 * h + p
                    vec.wait_ge(s_vhi, g + 1)
                    vec.tensor_tensor(w_lo[p][:, 2 * W:], raw[p][:, 2 * W:], w_hi[p][:, 2 * W:], ALU.subtract).then_inc(s_vlo, 1)
                    vec.wait_ge(s_ge, g + 1)
                    if started(h):
                        vec.wait_ge(s_hlo, g - 1)
                    for f in range(FB):
                        last = vec.scalar_tensor_tensor(hf[p][:, f, :], bank[4 + p][:, f * GRP:(f + 1) * GRP],
                                                        bias[p][:, FB + f:FB + f + 1], ge[p][:, f, :], ALU.add, ALU.mult)
                    last.then_inc(s_h, 1)
                    vec.wait_ge(s_h, g + 1)
                    if started(h):
                        vec.wait_ge(s_dn, g - 1)
                    vec.tensor_copy(h_hi[p][:, :, :], hf[p][:, :, :]).then_inc(s_hh, 1)
                    vec.wait_ge(s_hh, g + 1)
                    vec.tensor_tensor(h_lo[p][:, :, :], hf[p][:, :, :], h_hi[p][:, :, :], ALU.subtract).then_inc(s_hlo, 1)

                three_stages(vec, NG0, split, hidden, nothing)


def combine0(k):
    nc, bank, io = k.nc, k.bank, k.io
    EA = E0 + 2
    with ExitStack() as ctx:
        sb = lambda name, shape, dt=F32: k.sb("c0_" + name, shape, dt, ctx)
        b2 = sb("b2", [EA, D])
        comb_t = sb("comb_t", [EA, 2, P])
        yg = [sb(f"yg{n}", [P, 2, D]) for n in range(4)]
        s_b2 = k.sem("c0_b2_loaded")
        s_g = [k.sem(f"c0_gathered{n}") for n in range(4)]
        s_ct, s_cts, s_bt, s_sum = (k.sem("c0_" + n) for n in ("weights_turned", "weights_copied", "bias_term", "summed"))
        s_used = k.sem("c0_gathered_used")
        s_first = k.sem("c0_first_added")
        s_stat, s_var, s_rstd, s_ln = (k.sem("c0_" + n) for n in ("stats", "var", "rstd", "normed"))
        with nc.Block() as block:
            @block.sync
            def _(sp):
                sp.dma_start(b2[:, :], io["b2"]).then_inc(s_b2, 16)

            @block.gpsimd
            def _(pool):
                def rstd(c):
                    pool.wait_ge(s_stat, 2 * TC * (c + 1))
                    ln_rstd(k, pool, c * TC, TC, s_var, s_rstd, c)

                for i in range(NT):
                    if i >= 4:
                        pool.wait_ge(s_used, i - 3)
                    for kk in range(2):
                        pool.indirect_dma_start(yg[i % 4][:, kk, :], None, k.y0, bass.IndirectOffsetOnAxis(k.slot[:, kk, i:i + 1], 0)
                                                ).then_inc(s_g[i % 4], 16)
                    if i >= 7 and i % 4 == 3:
                        rstd(i // 4 - 1)
                rstd(NC - 1)

            @block.tensor
            def _(pe):
                pe.wait_ge(s_b2, 16)
                for i in range(NT):
                    if i >= 2:
                        pe.wait_ge(s_cts, i - 1)
                        pe.wait_ge(s_sum, i - 1)
                    pe.transpose(bank[i % 2][0:EA, 0:P], k.comb_aug[:, i, :], k.ident[:, :]).then_inc(s_ct, 1)
                    pe.wait_ge(s_cts, i + 1)
                    pe.matmul(bank[2 + i % 2][:, :], comb_t[:, i % 2, :], b2[:, :], start=True, stop=True).then_inc(s_bt, 1)

            @block.scalar
            def _(act):
                for i in range(NT):
                    act.wait_ge(s_ct, i + 1)
                    if i >= 2:
                        act.wait_ge(s_bt, i - 1)
                    act.activation(comb_t[:, i % 2, :], bank[i % 2][0:EA, 0:P], ACT.Copy).then_inc(s_cts, 1)

            @block.vector
            def _(vec):
                def apply(c):
                    vec.wait_ge(s_rstd, c + 1)
                    for i in range(c * TC, c * TC + TC):
                        ln_apply(k, vec, i).then_inc(s_ln, 1)

                for i in range(NT):
                    xi = k.x[:, i, :]
                    vec.wait_ge(s_bt, i + 1)
                    vec.tensor_tensor(xi, bank[2 + i % 2][:, :], xi, ALU.add).then_inc(s_sum, 1)
                    vec.wait_ge(s_g[i % 4], 32 * (i // 4 + 1))
                    vec.wait_ge(s_sum, i + 1)
                    vec.scalar_tensor_tensor(xi, yg[i % 4][:, 0, :], k.weight[:, 0, i:i + 1], xi, ALU.mult, ALU.add).then_inc(s_first, 1)
                    vec.wait_ge(s_first, i + 1)
                    vec.scalar_tensor_tensor(xi, yg[i % 4][:, 1, :], k.weight[:, 1, i:i + 1], xi, ALU.mult, ALU.add).then_inc(s_used, 1)
                    vec.wait_ge(s_used, i + 1)
                    ln_stats(k, vec, i, s_stat, i)
                    if i >= 7 and i % 4 == 3:
                        apply(i // 4 - 1)
                apply(NC - 1)


H1, DH1, FM = 16, 32, 64
NP = H1 // 2
VA = 2 * (DH1 + 1)


def attention1(k):
    with ExitStack() as ctx:
        xt = tuple(k.sb("a1_xt_" + n, [P, KD, T], F32R, ctx) for n in ("hi", "lo"))
        sb = lambda name, shape, dt=F32: k.sb("a1_" + name, shape, dt, ctx)
        w = {"fw1_hi": sb("fw1_hi", [P, 4 * FM], F32R), "fw1_lo": sb("fw1_lo", [P, 4 * FM], F32R),
             "kv": sb("kv", [P, NP, VA]), "vsum": sb("vsum", [P, NP * VA]),
             "m_hi": sb("m_hi", [P, NP, VA], F32R), "m_lo": sb("m_lo", [P, NP, VA], F32R),
             "cq": sb("cq", [P, NP * VA])}
        attention1_keys(k, xt, w)
        attention1_memory(k, w)
        attention1_queries(k, xt, w)


def attention1_keys(k, xt, w):
    nc, bank, io = k.nc, k.bank, k.io
    xt_hi, xt_lo = xt
    fw1_hi, fw1_lo, kv, vsum = w["fw1_hi"], w["fw1_lo"], w["kv"], w["vsum"]
    with ExitStack() as ctx:
        sb = lambda name, shape, dt=F32: k.sb("k1_" + name, shape, dt, ctx)
        raw = sb("raw", [P, KD, D])
        kw_hi, kw_lo = sb("kw_hi", [P, KD, D], F32R), sb("kw_lo", [P, KD, D], F32R)
        vw_hi, vw_lo = sb("vw_hi", [P, KD, D], F32R), sb("vw_lo", [P, KD, D], F32R)
        fw1_raw = sb("fw1_raw", [P, FM])
        kb = sb("kb", [P, KD])
        vb = sb("vb", [P, D])
        fb1 = sb("fb1", [2, FM])
        part = sb("part", [2, 1])
        rest = sb("rest", [2, 1])
        fb_hi, fb_lo = sb("fb_hi", [2, FM], F32R), sb("fb_lo", [2, FM])
        fb_hl = sb("fb_hl", [2, 4, FM], F32R)
        ones_f, ones2 = sb("ones_f", [2, P]), sb("ones2", [2, P], F32R)
        k_hi, k_lo = sb("k_hi", [P, KD, CH], F32R), sb("k_lo", [P, KD, CH], F32R)
        vf = sb("vf", [P, 2, NP * VA])
        v_hi, v_lo = sb("v_hi", [P, 2, NP * VA], F32R), sb("v_lo", [P, 2, NP * VA], F32R)
        ex, gf = sb("ex", [P, 2, CH]), sb("gf", [P, 2, CH])
        g_hi, g_lo = sb("g_hi", [P, 2, 2 * CH], F32R), sb("g_lo", [P, 2, 2 * CH], F32R)

        sem = lambda n: k.sem("k1_" + n)
        s_kw, s_vw, s_fw, s_kb, s_vb, s_fb = (sem(n) for n in ("kw_loaded", "vw_loaded", "fw1_loaded", "kb_loaded", "vb_loaded", "fb1_loaded"))
        s_zero, s_whi, s_wlo = sem("zeroed"), sem("weight_hi"), sem("weight_split")
        s_c = sem("fb1_chain")
        s_tps, s_thi, s_tlo = sem("turned"), sem("turned_hi"), sem("turned_lo")
        s_k, s_khi, s_klo = sem("keys"), sem("keys_hi"), sem("keys_split")
        s_v, s_vf, s_vhi, s_vlo, s_vs = sem("values"), sem("values_read"), sem("values_hi"), sem("values_lo"), sem("values_summed")
        s_g, s_gev, s_gf, s_ghi, s_glo = sem("features"), sem("features_read"), sem("features_made"), sem("features_hi"), sem("features_lo")
        s_kv, s_out = sem("kv_added"), sem("kv_copied")
        heads = lambda a: a.rearrange("p (h e) -> p h e", e=DH1 + 1)

        def schedule(turn, keys, tile):
            turn(0)
            keys(0)
            for c in range(NC):
                for i in range(c * TC, c * TC + TC):
                    tile(i)
                if c + 1 < NC:
                    turn(c + 1)
                    keys(c + 1)

        with nc.Block() as block:
            @block.sync
            def _(sp):
                sp.dma_start(raw[:, :, :], io["kw"].rearrange("(b p) n -> p b n", p=P)).then_inc(s_kw, 16)
                for h in range(4):
                    sp.dma_start(fw1_raw[h * DH1:(h + 1) * DH1, :], io["fw1"]).then_inc(s_fw, 16)
                sp.dma_start(kb[:, :], io["kb_t"]).then_inc(s_kb, 16)
                sp.dma_start(vb[:, :], io["vb"].partition_broadcast(P)).then_inc(s_vb, 16)
                sp.dma_start(fb1[:, :], io["fb1"].partition_broadcast(2)).then_inc(s_fb, 16)
                sp.wait_ge(s_wlo, 1)
                sp.dma_start(raw[:, :, :], io["vw"].rearrange("(b p) n -> p b n", p=P)).then_inc(s_vw, 16)

            @block.gpsimd
            def _(pool):
                pool.memset(fw1_hi[:, :].bitcast(F32), 0.0).then_inc(s_zero, 1)
                pool.memset(fw1_lo[:, :].bitcast(F32), 0.0).then_inc(s_zero, 1)
                pool.memset(part[:, :], 0.0).then_inc(s_zero, 1)
                pool.memset(rest[:, :], 1.0).then_inc(s_zero, 1)
                pool.memset(ones_f[:, :], 1.0).then_inc(s_zero, 1)
                pool.memset(vf[:, :, :], 1.0).then_inc(s_zero, 1)
                pool.memset(kv[:, :, :], 0.0).then_inc(s_zero, 1)
                pool.memset(vsum[:, :], 0.0).then_inc(s_zero, 1)
                pool.wait_ge(s_zero, 8)
                pool.memset(part[0:1, :], 1.0).then_inc(s_zero, 1)
                pool.memset(rest[0:1, :], 0.0).then_inc(s_zero, 1)

                def tile(i):
                    pool.wait_ge(s_vf, i + 1)
                    if i:
                        pool.wait_ge(s_vs, i)
                    pool.tensor_tensor(vsum[:, :], vsum[:, :], vf[:, i % 2, :], ALU.add).then_inc(s_vs, 1)
                    for n in (2 * i, 2 * i + 1):
                        pool.wait_ge(s_ghi, n + 1)
                        part_of = slice((n % 2) * CH, (n % 2 + 1) * CH)
                        pool.tensor_tensor(g_lo[:, i % 2, part_of], gf[:, n % 2, :], g_hi[:, i % 2, part_of].bitcast(F32),
                                           ALU.subtract).then_inc(s_glo, 1)

                schedule(lambda c: None, lambda c: None, tile)

            @block.tensor
            def _(pe):
                def turn(c):
                    for b in range(KD):
                        n = 4 * c + b
                        if n >= 2:
                            pe.wait_ge(s_tlo, n - 1)
                        for j in range(TC):
                            mm = pe.transpose(bank[n % 2][:, j * P:(j + 1) * P], k.x[:, c * TC + j, b * P:(b + 1) * P], k.ident[:, :])
                        mm.then_inc(s_tps, 1)

                def keys(c):
                    if c == 0:
                        pe.wait_ge(s_wlo, 1)
                    pe.wait_ge(s_tlo, 4 * c + 4)
                    for m in range(KD):
                        u = 4 * c + m
                        if u >= 2:
                            pe.wait_ge(s_klo, u - 1)
                        if c and m == 1:
                            pe.wait_ge(s_vf, TC * c)
                        for b in range(KD):
                            mm = mm3(pe, bank[2 + m % 2][:, :], kw_hi[:, b, m * P:(m + 1) * P], kw_lo[:, b, m * P:(m + 1) * P],
                                     xt_hi[:, b, c * CH:(c + 1) * CH], xt_lo[:, b, c * CH:(c + 1) * CH], b == 0, b == KD - 1)
                        mm.then_inc(s_k, 1)

                def sums(i):
                    pe.wait_ge(s_glo, 2 * i + 2)
                    pe.wait_ge(s_vlo, i + 1)
                    for q in range(NP):
                        o = bank[6 + q // 4][:, q % 4 * VA:(q % 4 + 1) * VA]
                        f, v = slice(q * P, (q + 1) * P), slice(q * VA, (q + 1) * VA)
                        first = i == 0 and q % 4 == 0
                        pe.matmul(o, g_hi[:, i % 2, f], v_hi[:, i % 2, v], start=first, stop=False, skip_group_check=True)
                        pe.matmul(o, g_hi[:, i % 2, f], v_lo[:, i % 2, v], start=False, stop=False, skip_group_check=True)
                        mm = pe.matmul(o, g_lo[:, i % 2, f], v_hi[:, i % 2, v], start=False, stop=i == NT - 1, skip_group_check=True)
                    mm.then_inc(s_kv, 1)

                def tile(i):
                    c, j = i // TC, i % TC
                    if i == 0:
                        pe.wait_ge(s_wlo, 3)
                    if j == 0:
                        pe.wait_ge(s_klo, 4 * c + 4)
                    if i:
                        pe.wait_ge(s_vf, i)
                    for b in range(KD):
                        mm = mm3(pe, bank[3][:, :], xt_hi[:, b, i * P:(i + 1) * P], xt_lo[:, b, i * P:(i + 1) * P],
                                 vw_hi[:, b, :], vw_lo[:, b, :], b == 0, b == KD - 1)
                    mm.then_inc(s_v, 1)
                    t = slice(j * P, (j + 1) * P)
                    for n in (2 * i, 2 * i + 1):
                        if i:
                            pe.wait_ge(s_gev, n - 1)
                        for a in range(2):
                            g = 2 * (n % 2) + a
                            o = bank[4 + n % 2][:, a * 256:(a + 1) * 256]
                            mm3(pe, o, k_hi[:, g, t], k_lo[:, g, t], fw1_hi[:, :], fw1_lo[:, :], True, False)
                            mm = pe.matmul(o, ones2[:, :], fb_hl[:, :, :].rearrange("p h f -> p (h f)"), start=False, stop=True)
                        mm.then_inc(s_g, 1)
                    if i:
                        sums(i - 1)

                schedule(turn, keys, tile)
                sums(NT - 1)

            @block.scalar
            def _(act):
                def weight(sem, dst):
                    act.wait_ge(sem, 16)
                    act.activation(dst[:, :, :], raw[:, :, :], ACT.Copy).then_inc(s_whi, 1)

                def turn(c):
                    for b in range(KD):
                        act.wait_ge(s_tps, 4 * c + b + 1)
                        act.activation(xt_hi[:, b, c * CH:(c + 1) * CH], bank[b % 2][:, :], ACT.Copy).then_inc(s_thi, 1)

                def keys(c):
                    if c:
                        act.wait_ge(s_g, 2 * TC * c)
                    for m in range(KD):
                        u = 4 * c + m
                        act.wait_ge(s_k, u + 1)
                        act.activation(k_hi[:, m, :], bank[2 + m % 2][:, :], ACT.Identity, bias=kb[:, m:m + 1]).then_inc(s_khi, 1)
                    if c == 0:
                        weight(s_vw, vw_hi)

                def tile(i):
                    act.wait_ge(s_vf, i + 1)
                    if i >= 2:
                        act.wait_ge(s_kv, i - 1)
                    act.activation(v_hi[:, i % 2, :], vf[:, i % 2, :], ACT.Copy).then_inc(s_vhi, 1)
                    for n in (2 * i, 2 * i + 1):
                        act.wait_ge(s_g, n + 1)
                        if i:
                            act.wait_ge(s_gf, n - 1)
                            act.wait_ge(s_glo, n - 1)
                        act.activation(ex[:, n % 2, :], bank[4 + n % 2][:, :], ACT.Exp)
                        act.activation(gf[:, n % 2, :], bank[4 + n % 2][:, :], ACT.Relu).then_inc(s_gev, 1)
                    for n in (2 * i, 2 * i + 1):
                        act.wait_ge(s_gf, n + 1)
                        act.activation(g_hi[:, i % 2, (n % 2) * CH:(n % 2 + 1) * CH], gf[:, n % 2, :], ACT.Copy).then_inc(s_ghi, 1)

                weight(s_kw, kw_hi)
                act.wait_ge(s_kb, 16)
                schedule(turn, keys, tile)

            @block.vector
            def _(vec):
                def weight(n, raw_, hi, lo):
                    vec.wait_ge(s_whi, n)
                    vec.tensor_tensor(lo[:, :, :], raw_[:, :, :], hi[:, :, :], ALU.subtract).then_inc(s_wlo, 1)

                def feature_weights():
                    vec.wait_ge(s_fw, 64)
                    vec.wait_ge(s_zero, 10)
                    for h in range(4):
                        r, c = slice(h * DH1, (h + 1) * DH1), slice(h * FM, (h + 1) * FM)
                        vec.tensor_copy(fw1_hi[r, c], fw1_raw[r, :]).then_inc(s_c, 1)
                    vec.wait_ge(s_c, 4)
                    for h in range(4):
                        r, c = slice(h * DH1, (h + 1) * DH1), slice(h * FM, (h + 1) * FM)
                        vec.tensor_tensor(fw1_lo[r, c], fw1_raw[r, :], fw1_hi[r, c], ALU.subtract)
                    vec.wait_ge(s_fb, 16)
                    vec.tensor_copy(ones2[:, :], ones_f[:, :])
                    vec.tensor_copy(fb_hi[:, :], fb1[:, :]).then_inc(s_c, 1)
                    vec.wait_ge(s_c, 5)
                    vec.tensor_tensor(fb_lo[:, :], fb1[:, :], fb_hi[:, :], ALU.subtract).then_inc(s_c, 1)
                    vec.wait_ge(s_c, 6)
                    vec.tensor_scalar(fb_lo[:, :], fb_lo[:, :], rest[:, 0:1], None, ALU.mult).then_inc(s_c, 1)
                    vec.wait_ge(s_c, 7)
                    for h in range(4):
                        last = vec.scalar_tensor_tensor(fb_hl[:, h, :], fb_hi[:, :], part[:, 0:1], fb_lo[:, :], ALU.mult, ALU.add)
                    last.then_inc(s_wlo, 1)

                def turn(c):
                    for b in range(KD):
                        vec.wait_ge(s_thi, 4 * c + b + 1)
                        t = slice(c * CH, (c + 1) * CH)
                        vec.tensor_tensor(xt_lo[:, b, t], bank[b % 2][:, :], xt_hi[:, b, t], ALU.subtract).then_inc(s_tlo, 1)

                def keys(c):
                    if c == 0:
                        weight(1, raw, kw_hi, kw_lo)
                    for m in range(KD):
                        u = 4 * c + m
                        vec.wait_ge(s_khi, u + 1)
                        vec.scalar_tensor_tensor(k_lo[:, m, :], bank[2 + m % 2][:, :], kb[:, m:m + 1], k_hi[:, m, :],
                                                 ALU.add, ALU.subtract).then_inc(s_klo, 1)
                    if c == 0:
                        feature_weights()
                        weight(2, raw, vw_hi, vw_lo)
                        vec.wait_ge(s_vb, 16)

                def tile(i):
                    vec.wait_ge(s_v, i + 1)
                    if i >= 2:
                        vec.wait_ge(s_vs, i - 1)
                        vec.wait_ge(s_vlo, i - 1)
                    vec.tensor_tensor(heads(vf[:, i % 2, :])[:, :, 0:DH1], bank[3][:, :].rearrange("p (h e) -> p h e", e=DH1),
                                      vb[:, :].rearrange("p (h e) -> p h e", e=DH1), ALU.add).then_inc(s_vf, 1)
                    vec.wait_ge(s_vhi, i + 1)
                    vec.tensor_tensor(v_lo[:, i % 2, :], vf[:, i % 2, :], v_hi[:, i % 2, :], ALU.subtract).then_inc(s_vlo, 1)
                    for n in (2 * i, 2 * i + 1):
                        vec.wait_ge(s_gev, n + 1)
                        vec.scalar_tensor_tensor(gf[:, n % 2, :], ex[:, n % 2, :], 1.0, gf[:, n % 2, :], ALU.min, ALU.add).then_inc(s_gf, 1)

                schedule(turn, keys, tile)
                vec.wait_ge(s_kv, NT)
                for a in range(2):
                    for h in range(2):
                        r, c = slice(h * FM, (h + 1) * FM), slice(h * (DH1 + 1), (h + 1) * (DH1 + 1))
                        vec.tensor_copy(kv[r, 4 * a:4 * a + 4, c],
                                        bank[6 + a][r, 0:4 * VA].rearrange("p (q v) -> p q v", v=VA)[:, :, c])


def attention1_memory(k, w):
    nc, bank, io = k.nc, k.bank, k.io
    kv, vsum = w["kv"], w["vsum"]
    HV = NP * VA // 2
    with ExitStack() as ctx:
        sb = lambda name, shape, dt=F32: k.sb("m1_" + name, shape, dt, ctx)
        fw2, fw2_t = sb("fw2", [P, P]), sb("fw2_t", [P, P])
        fb2, b = sb("fb2", [P, 1]), sb("b", [P, 1])
        ones, b_cols = sb("ones", [P, P]), sb("b_cols", [P, P])
        sv, kv2, mf = sb("sv", [P, 2, HV]), sb("kv2", [P, NP, VA]), sb("mf", [P, NP * VA])
        sem = lambda n: k.sem("m1_" + n)
        s_zero, s_ld, s_ps, s_b, s_sv, s_kv2, s_m, s_split = (sem(n) for n in
            ("zeroed", "loaded", "products", "bias_made", "value_sum", "kv2_made", "memory", "memory_split"))
        with nc.Block() as block:
            @block.gpsimd
            def _(pool):
                pool.memset(fw2[:, :], 0.0).then_inc(s_zero, 1)
                pool.memset(fw2_t[:, :], 0.0).then_inc(s_zero, 1)
                pool.memset(ones[:, :], 1.0).then_inc(s_zero, 1)
                pool.memset(kv2[:, :, :], 0.0).then_inc(s_zero, 1)

            @block.sync
            def _(sp):
                sp.wait_ge(s_zero, 2)
                for h in range(2):
                    r = slice(h * FM, (h + 1) * FM)
                    sp.dma_start(fw2[r, r], io["fw2"]).then_inc(s_ld, 16)
                    sp.dma_start(fw2_t[r, r], io["fw2_t"]).then_inc(s_ld, 16)
                    sp.dma_start(fb2[r, :], io["fb2"].rearrange("(f o) -> f o", o=1)).then_inc(s_ld, 16)

            @block.tensor
            def _(pe):
                pe.wait_ge(s_ld, 96)
                pe.wait_ge(s_zero, 4)
                flat = lambda a: a[:, :, :].rearrange("p q v -> p (q v)")
                pe.matmul(bank[6][:, 0:2], fw2[:, :], ones[:, 0:2], start=True, stop=True).then_inc(s_ps, 1)
                for a in range(2):
                    pe.matmul(bank[a][:, 0:HV], ones[:, :], vsum[:, a * HV:(a + 1) * HV], start=True, stop=True).then_inc(s_ps, 1)
                    pe.matmul(bank[2 + a][:, 0:HV], fw2[:, :], flat(kv)[:, a * HV:(a + 1) * HV], start=True, stop=True).then_inc(s_ps, 1)
                pe.wait_ge(s_kv2, 4)
                pe.wait_ge(s_b, 2)
                for a in range(2):
                    pe.matmul(bank[4 + a][:, 0:HV], fw2_t[:, :], flat(kv2)[:, a * HV:(a + 1) * HV], start=True, stop=True).then_inc(s_ps, 1)
                    pe.matmul(bank[6 + a][:, 0:HV], b_cols[:, :], flat(kv2)[:, a * HV:(a + 1) * HV], start=True, stop=True).then_inc(s_ps, 1)

            @block.vector
            def _(vec):
                vec.wait_ge(s_ps, 5)
                vec.tensor_tensor(b[:, :], fb2[:, :], bank[6][:, 0:1], ALU.subtract).then_inc(s_b, 1)
                for a in range(2):
                    vec.tensor_copy(sv[:, a, :], bank[a][:, 0:HV]).then_inc(s_sv, 1)
                vec.wait_ge(s_b, 1)
                vec.tensor_scalar(b_cols[:, :], ones[:, :], b[:, 0:1], None, ALU.mult).then_inc(s_b, 1)
                vec.wait_ge(s_sv, 2)
                for a in range(2):
                    for h in range(2):
                        r, c = slice(h * FM, (h + 1) * FM), slice(h * (DH1 + 1), (h + 1) * (DH1 + 1))
                        pairs = lambda t: t.rearrange("p (q v) -> p q v", v=VA)[:, :, c]
                        vec.scalar_tensor_tensor(kv2[r, 4 * a:4 * a + 4, c], pairs(sv[r, a, :]), b[r, 0:1],
                                                 pairs(bank[2 + a][r, 0:HV]), ALU.mult, ALU.add).then_inc(s_kv2, 1)
                vec.wait_ge(s_ps, 9)
                for a in range(2):
                    part = slice(a * HV, (a + 1) * HV)
                    vec.tensor_copy(mf[:, part], bank[4 + a][:, 0:HV]).then_inc(s_m, 1)
                    vec.tensor_copy(w["cq"][:, part], bank[6 + a][:, 0:HV]).then_inc(s_m, 1)
                vec.wait_ge(s_m, 4)
                vec.tensor_copy(w["m_hi"][:, :, :].rearrange("p q v -> p (q v)"), mf[:, :]).then_inc(s_split, 1)
                vec.wait_ge(s_split, 1)
                vec.tensor_tensor(w["m_lo"][:, :, :].rearrange("p q v -> p (q v)"), mf[:, :],
                                  w["m_hi"][:, :, :].rearrange("p q v -> p (q v)"), ALU.subtract)


def attention1_queries(k, xt, w):
    nc, bank, io = k.nc, k.bank, k.io
    xt_hi, xt_lo = xt
    fw1_hi, fw1_lo, m_hi, m_lo, cq = (w[n] for n in ("fw1_hi", "fw1_lo", "m_hi", "m_lo", "cq"))
    HV = NP * VA // 2
    with ExitStack() as ctx:
        sb = lambda name, shape, dt=F32: k.sb("q1_" + name, shape, dt, ctx)
        raw = sb("raw", [P, KD, D])
        qw_hi, qw_lo = sb("qw_hi", [P, KD, D], F32R), sb("qw_lo", [P, KD, D], F32R)
        ow_hi, ow_lo = sb("ow_hi", [P, KD, D], F32R), sb("ow_lo", [P, KD, D], F32R)
        qb, fb1, ob = sb("qb", [P, KD]), sb("fb1", [P, 1]), sb("ob", [P, D])
        q_hi, q_lo = sb("q_hi", [P, 2, CH], F32R), sb("q_lo", [P, 2, CH], F32R)
        ex, gf = sb("ex", [P, 2, CH]), sb("gf", [P, 2, CH])
        g_hi, g_lo = sb("g_hi", [P, NP, CH], F32R), sb("g_lo", [P, NP, CH], F32R)
        num = (w["kv"][:, :, :].rearrange("p q v -> p (q v)"), w["vsum"][:, :])
        den = sb("den", [P, 2, H1])
        at_hi, at_lo = sb("at_hi", [P, 2, D], F32R), sb("at_lo", [P, 2, D], F32R)
        attn = raw

        sem = lambda n: k.sem("q1_" + n)
        s_qw, s_ow, s_small = sem("qw_loaded"), sem("ow_loaded"), sem("biases_loaded")
        s_whi, s_wlo, s_ob = sem("weight_hi"), sem("weight_split"), sem("ob_added")
        s_q, s_qhi, s_qlo = sem("queries"), sem("queries_hi"), sem("queries_split")
        s_g, s_gev, s_gf, s_ghi, s_glo = sem("features"), sem("features_read"), sem("features_made"), sem("features_hi"), sem("features_lo")
        s_n, s_nev, s_den, s_at = sem("num"), sem("num_read"), sem("den"), sem("attn")
        s_tps, s_thi, s_tlo = sem("turned"), sem("turned_hi"), sem("turned_lo")
        s_o, s_res = sem("out"), sem("residual")
        s_stat, s_var, s_rstd, s_ln, s_st = sem("stats"), sem("var"), sem("rstd"), sem("normed"), sem("stored")
        NU = NC * KD

        def schedule(query, features, tiles):
            query(0)
            for c in range(NC):
                for m in range(KD):
                    u = c * KD + m
                    if u + 1 < NU:
                        query(u + 1)
                    features(u)
                tiles(c)

        with nc.Block() as block:
            @block.sync
            def _(sp):
                sp.dma_start(raw[:, :, :], io["qw"].rearrange("(b p) n -> p b n", p=P)).then_inc(s_qw, 16)
                sp.dma_start(qb[:, :], io["qb_t"]).then_inc(s_small, 16)
                for h in range(2):
                    sp.dma_start(fb1[h * FM:(h + 1) * FM, :], io["fb1"].rearrange("(f o) -> f o", o=1)).then_inc(s_small, 16)
                sp.dma_start(ob[:, :], io["ob"].partition_broadcast(P)).then_inc(s_small, 16)
                sp.wait_ge(s_wlo, 1)
                sp.dma_start(raw[:, :, :], io["ow"].rearrange("(b p) n -> p b n", p=P)).then_inc(s_ow, 16)
                for c in range(NC):
                    sp.wait_ge(s_ln, TC * (c + 1))
                    sp.dma_start(k.rows.rearrange("(c j p) d -> c p j d", p=P, j=TC)[c],
                                 k.x[:, c * TC:(c + 1) * TC, :]).then_inc(s_st, 16)
                sp.wait_ge(s_st, 16 * NC)

            @block.gpsimd
            def _(pool):
                pool.wait_ge(s_small, 64)
                for i in range(NT):
                    pool.tensor_tensor(k.x[:, i, :], k.x[:, i, :], ob[:, :], ALU.add).then_inc(s_ob, 1)

                def features(u):
                    for n in (2 * u, 2 * u + 1):
                        pool.wait_ge(s_ghi, n + 1)
                        pool.tensor_tensor(g_lo[:, n % NP, :], gf[:, n % 2, :], g_hi[:, n % NP, :].bitcast(F32),
                                           ALU.subtract).then_inc(s_glo, 1)

                def tiles(c):
                    if c:
                        pool.wait_ge(s_stat, 2 * TC * c)
                        ln_rstd(k, pool, (c - 1) * TC, TC, s_var, s_rstd, c - 1)

                schedule(lambda u: None, features, tiles)
                pool.wait_ge(s_stat, 2 * TC * NC)
                ln_rstd(k, pool, (NC - 1) * TC, TC, s_var, s_rstd, NC - 1)

            @block.tensor
            def _(pe):
                def query(u):
                    c, m = u // KD, u % KD
                    if u == 0:
                        pe.wait_ge(s_wlo, 1)
                    if u >= 2:
                        pe.wait_ge(s_qlo, u - 1)
                    for b in range(KD):
                        mm = mm3(pe, bank[u % 2][:, :], qw_hi[:, b, m * P:(m + 1) * P], qw_lo[:, b, m * P:(m + 1) * P],
                                 xt_hi[:, b, c * CH:(c + 1) * CH], xt_lo[:, b, c * CH:(c + 1) * CH], b == 0, b == KD - 1)
                    mm.then_inc(s_q, 1)

                def features(u):
                    pe.wait_ge(s_qlo, u + 1)
                    for a in range(2):
                        n = 2 * u + a
                        if n >= 2:
                            pe.wait_ge(s_gev, n - 1)
                        f = slice(a * P, (a + 1) * P)
                        mm3(pe, bank[2 + n % 2][:, :], fw1_hi[:, f], fw1_lo[:, f], q_hi[:, u % 2, :], q_lo[:, u % 2, :],
                            True, True).then_inc(s_g, 1)

                def numerator(i):
                    if i % TC == 0:
                        pe.wait_ge(s_glo, NP * (i // TC + 1))
                    if i:
                        pe.wait_ge(s_nev, i)
                    t = slice(i % TC * P, (i % TC + 1) * P)
                    for q in range(NP):
                        mm = mm3(pe, bank[4 + q // 4][:, q % 4 * VA:(q % 4 + 1) * VA], g_hi[:, q, t], g_lo[:, q, t],
                                 m_hi[:, q, :], m_lo[:, q, :], True, True)
                    mm.then_inc(s_n, 1)

                def turn(i):
                    pe.wait_ge(s_at, i + 1)
                    if i:
                        pe.wait_ge(s_tlo, i)
                    for b in range(KD):
                        mm = pe.transpose(bank[6][:, b * P:(b + 1) * P], attn[:, i % 2, b * P:(b + 1) * P], k.ident[:, :])
                    mm.then_inc(s_tps, 1)

                def project(i):
                    if i == 0:
                        pe.wait_ge(s_wlo, 2)
                    pe.wait_ge(s_tlo, i + 1)
                    if i:
                        pe.wait_ge(s_res, i)
                    for b in range(KD):
                        f = slice(b * P, (b + 1) * P)
                        mm = mm3(pe, bank[7][:, :], at_hi[:, i % 2, f], at_lo[:, i % 2, f], ow_hi[:, b, :], ow_lo[:, b, :],
                                 b == 0, b == KD - 1)
                    mm.then_inc(s_o, 1)

                def tiles(c):
                    first, end = c * TC, c * TC + TC
                    numerator(first)
                    numerator(first + 1)
                    turn(first)
                    for i in range(first, end):
                        if i + 2 < end:
                            numerator(i + 2)
                        if i + 1 < end:
                            turn(i + 1)
                        project(i)

                schedule(query, features, tiles)

            @block.scalar
            def _(act):
                def query(u):
                    act.wait_ge(s_q, u + 1)
                    if u >= 2:
                        act.wait_ge(s_g, 2 * u - 2)
                    m = u % KD
                    act.activation(q_hi[:, u % 2, :], bank[u % 2][:, :], ACT.Identity, bias=qb[:, m:m + 1]).then_inc(s_qhi, 1)

                def features(u):
                    for n in (2 * u, 2 * u + 1):
                        act.wait_ge(s_g, n + 1)
                        if n >= 2:
                            act.wait_ge(s_gf, n - 1)
                            act.wait_ge(s_glo, n - 1)
                        act.activation(ex[:, n % 2, :], bank[2 + n % 2][:, :], ACT.Exp, bias=fb1[:, 0:1])
                        act.activation(gf[:, n % 2, :], bank[2 + n % 2][:, :], ACT.Relu, bias=fb1[:, 0:1]).then_inc(s_gev, 1)
                    if u % KD == 0 and u:
                        act.wait_ge(s_n, u)
                    for n in (2 * u, 2 * u + 1):
                        act.wait_ge(s_gf, n + 1)
                        act.activation(g_hi[:, n % NP, :], gf[:, n % 2, :], ACT.Copy).then_inc(s_ghi, 1)

                def tiles(c):
                    if c == 0:
                        act.wait_ge(s_ow, 16)
                        act.activation(ow_hi[:, :, :], raw[:, :, :], ACT.Copy).then_inc(s_whi, 1)
                    for i in range(c * TC, c * TC + TC):
                        act.wait_ge(s_tps, i + 1)
                        if i >= 2:
                            act.wait_ge(s_o, i - 1)
                        act.activation(at_hi[:, i % 2, :], bank[6][:, :], ACT.Copy).then_inc(s_thi, 1)

                act.wait_ge(s_qw, 16)
                act.activation(qw_hi[:, :, :], raw[:, :, :], ACT.Copy).then_inc(s_whi, 1)
                act.wait_ge(s_small, 64)
                schedule(query, features, tiles)

            @block.vector
            def _(vec):
                def query(u):
                    if u == 0:
                        vec.wait_ge(s_whi, 1)
                        vec.tensor_tensor(qw_lo[:, :, :], raw[:, :, :], qw_hi[:, :, :], ALU.subtract).then_inc(s_wlo, 1)
                    vec.wait_ge(s_qhi, u + 1)
                    if u >= 2:
                        vec.wait_ge(s_g, 2 * u - 2)
                    m = u % KD
                    vec.scalar_tensor_tensor(q_lo[:, u % 2, :], bank[u % 2][:, :], qb[:, m:m + 1], q_hi[:, u % 2, :],
                                             ALU.add, ALU.subtract).then_inc(s_qlo, 1)

                def features(u):
                    for n in (2 * u, 2 * u + 1):
                        vec.wait_ge(s_gev, n + 1)
                        vec.scalar_tensor_tensor(gf[:, n % 2, :], ex[:, n % 2, :], 1.0, gf[:, n % 2, :], ALU.min, ALU.add).then_inc(s_gf, 1)

                def divide(i):
                    vec.wait_ge(s_n, i + 1)
                    s = i % 2
                    for a in range(2):
                        part = slice(a * HV, (a + 1) * HV)
                        vec.tensor_tensor(num[s][:, part], bank[4 + a][:, 0:HV], cq[:, part], ALU.add).then_inc(s_den, 1)
                    vec.wait_ge(s_den, 4 * i + 2)
                    nh = num[s].rearrange("p (h e) -> p h e", e=DH1 + 1)
                    vec.tensor_scalar(den[:, s, :], nh[:, :, DH1], 1e-6, None, ALU.max).then_inc(s_nev, 1)
                    vec.wait_ge(s_nev, i + 1)
                    vec.reciprocal(den[:, s, :], den[:, s, :]).then_inc(s_den, 2)
                    vec.wait_ge(s_den, 4 * i + 4)
                    if i >= 2:
                        vec.wait_ge(s_tps, i - 1)
                    vec.tensor_tensor(attn[:, s, :].rearrange("p (h e) -> p h e", e=DH1), nh[:, :, 0:DH1],
                                      den[:, s, :].unsqueeze(2).to_broadcast([P, H1, DH1]), ALU.mult).then_inc(s_at, 1)

                def split(i):
                    vec.wait_ge(s_thi, i + 1)
                    vec.tensor_tensor(at_lo[:, i % 2, :], bank[6][:, :], at_hi[:, i % 2, :], ALU.subtract).then_inc(s_tlo, 1)

                def residual(i):
                    vec.wait_ge(s_o, i + 1)
                    vec.tensor_tensor(k.x[:, i, :], bank[7][:, :], k.x[:, i, :], ALU.add).then_inc(s_res, 1)
                    vec.wait_ge(s_res, i + 1)
                    ln_stats(k, vec, i, s_stat, i)

                def apply(c):
                    vec.wait_ge(s_rstd, c + 1)
                    for i in range(c * TC, c * TC + TC):
                        ln_apply(k, vec, i).then_inc(s_ln, 1)

                def tiles(c):
                    first, end = c * TC, c * TC + TC
                    if c == 0:
                        vec.wait_ge(s_whi, 2)
                        vec.tensor_tensor(ow_lo[:, :, :], raw[:, :, :], ow_hi[:, :, :], ALU.subtract).then_inc(s_wlo, 1)
                        vec.wait_ge(s_ob, NT)
                        vec.wait_ge(s_wlo, 2)
                    divide(first)
                    divide(first + 1)
                    split(first)
                    for i in range(first, end):
                        if i + 2 < end:
                            divide(i + 2)
                        if i + 1 < end:
                            split(i + 1)
                        residual(i)
                    if c:
                        apply(c - 1)

                schedule(query, features, tiles)
                apply(NC - 1)


E1, K1, F1, CAP = 64, 6, 192, 96
G1, KG1 = 8, 4
HF1 = F1 // 2
ROUTED_SCALE = 2.5
BIG = 3e38


def experts1_shared(k):
    nc, bank, io = k.nc, k.bank, k.io
    EG = E1 // G1
    rt = lambda name, shape, dt=F32: k.sb("r1_" + name, shape, dt, k.moe_ctx)
    k.slot = rt("slot", [P, NT, K1], I32)
    k.weight = rt("weight", [P, NT, K1])
    k.token_of = rt("token_of", [CAP, E1], I32)
    with ExitStack() as ctx:
        sb = lambda name, shape, dt=F32: k.sb("s1_" + name, shape, dt, ctx)
        gw_raw = sb("gw_raw", [P, KD, E1])
        gw_hi, gw_lo = sb("gw_hi", [P, KD, E1], F32R), sb("gw_lo", [P, KD, E1], F32R)
        w1_raw, w2_raw = sb("w1_raw", [P, KD, 2 * F1]), sb("w2_raw", [HF1, 2, D])
        w1_hi, w1_lo = sb("w1_hi", [P, KD, 2 * F1], F32R), sb("w1_lo", [P, KD, 2 * F1], F32R)
        w2_hi, w2_lo = sb("w2_hi", [HF1, 2, D], F32R), sb("w2_lo", [HF1, 2, D], F32R)
        bias = sb("bias", [P, E1])
        xt_hi, xt_lo = sb("xt_hi", [P, KD, T], F32R), sb("xt_lo", [P, KD, T], F32R)
        si, up = sb("si", [HF1, CH]), sb("up", [HF1, CH])
        hf = sb("hf", [HF1, 2, CH])
        h_hi, h_lo = sb("h_hi", [HF1, 2, CH], F32R), sb("h_lo", [HF1, 2, CH], F32R)
        ys = sb("ys", [P, D])
        scores = sb("scores", [P, NT, E1])
        biased = sb("biased", [P, NT, E1])
        top_in_group = sb("top_in_group", [P, NT * G1, 8])
        gscore, rank = sb("gscore", [P, NT, G1]), sb("rank", [P, NT, G1])
        lower = sb("lower", [P, G1, G1])
        top, arg = sb("top", [P, NT, 8]), sb("arg", [P, NT, 8], U32)
        argf = sb("argf", [P, NT, K1])
        onehot = sb("onehot", [P, NT, K1, E1])
        prod = sb("prod", [P, NT // 2, K1, E1])
        sel = sb("sel", [P, NT * E1], BF16)
        upper, ones = sb("upper", [P, P], BF16), sb("ones", [P, P], BF16)
        tot, run_b = biased, scores
        run_a = top_in_group[:, :, :].rearrange("p (t g) e -> p t (g e)", g=G1)
        wsum = sb("wsum", [P, NT])
        posk, valid = sb("posk", [P, NT, K1]), sb("valid", [P, NT, K1])
        iota_e, iota_c = sb("iota_e", [P, E1]), sb("iota_c", [P, CAP])
        tok = sb("tok", [P, NT])
        at_row = sb("at_row", [P, 2, CAP], F32R)
        at_col = sb("at_col", [P, 2, K1, E1], F32R)

        sem = lambda n: k.sem("s1_" + n)
        s_gw, s_w1, s_w2, s_b = sem("gate_w_loaded"), sem("w1_loaded"), sem("w2_loaded"), sem("bias_loaded")
        s_whi, s_wlo = sem("weight_hi"), sem("weight_split")
        s_tps, s_thi, s_tlo = sem("turned"), sem("turned_hi"), sem("turned_lo")
        s_lg, s_sc = sem("logits"), sem("scores")
        s_gu, s_act, s_h, s_hh, s_hlo = sem("gate_up"), sem("gate_up_read"), sem("hidden"), sem("hidden_hi"), sem("hidden_split")
        s_dn, s_ys, s_res = sem("down"), sem("down_copied"), sem("residual")
        s_const, s_r = sem("constants"), sem("route_chain")
        s_sel, s_pre, s_tot = sem("selected"), sem("prefix"), sem("totals_copied")
        s_row, s_col, s_used = sem("rows_made"), sem("cols_made"), sem("rows_used")
        s_tab = sem("table_made")
        NU = 2 * NC

        def schedule(gate_up, down, ahead=0):
            gate_up(0)
            gate_up(1)
            for c in range(NC):
                if ahead and c + 1 < NC:
                    gate_up(2 * c + 2)
                down(c)
                for u in range(2 * c + 2 + ahead, min(2 * c + 4, NU)):
                    gate_up(u)

        with nc.Block() as block:
            @block.sync
            def _(sp):
                sp.dma_start(gw_raw[:, :, :], io["gate_w"].rearrange("(b p) n -> p b n", p=P)).then_inc(s_gw, 16)
                sp.dma_start(bias[:, :], io["bias"].partition_broadcast(P)).then_inc(s_b, 16)
                for a, name in enumerate(("ws_gate", "ws_up")):
                    sp.dma_start(w1_raw[:, :, a * F1:(a + 1) * F1], io[name].rearrange("(b p) n -> p b n", p=P)).then_inc(s_w1, 16)
                sp.dma_start(w2_raw[:, :, :], io["ws_down"].rearrange("(f p) n -> p f n", p=HF1)).then_inc(s_w2, 16)

            @block.gpsimd
            def _(pool):
                pool.memset(upper[:, :], 1.0).then_inc(s_const, 1)
                pool.memset(ones[:, :], 1.0).then_inc(s_const, 1)
                pool.memset(lower[:, :, :], 1.0).then_inc(s_const, 1)
                for a, n in ((iota_e, E1), (iota_c, CAP)):
                    pool.iota(a[:, :], [[1, n]], base=0, channel_multiplier=0,
                              allow_small_or_imprecise_dtypes=True).then_inc(s_const, 1)
                pool.iota(tok[:, :], [[P, NT]], base=0, channel_multiplier=1,
                          allow_small_or_imprecise_dtypes=True).then_inc(s_const, 1)
                pool.wait_ge(s_const, 6)
                pool.affine_select(out=upper[:, :], in_=upper[:, :], compare_op=ALU.is_gt, fill=0.0,
                                   base=0, pattern=[[1, P]], channel_multiplier=-1).then_inc(s_const, 1)
                pool.affine_select(out=lower[:, :, :], in_=lower[:, :, :], compare_op=ALU.is_gt, fill=0.0,
                                   base=0, pattern=[[1, G1], [-1, G1]], channel_multiplier=0).then_inc(s_const, 1)

                def gate_up(u):
                    if u >= 2:
                        pool.wait_ge(s_hlo, u - 1)
                    pool.wait_ge(s_act, u + 1)
                    pool.tensor_tensor(hf[:, u % 2, :], si[:, :], up[:, :], ALU.mult).then_inc(s_h, 1)
                    pool.wait_ge(s_hh, u + 1)
                    if u >= 2:
                        pool.wait_ge(s_dn, TC * (u // 2))
                    pool.tensor_tensor(h_lo[:, u % 2, :], hf[:, u % 2, :], h_hi[:, u % 2, :].bitcast(F32), ALU.subtract).then_inc(s_hlo, 1)

                def down(c):
                    for i in range(c * TC, c * TC + TC):
                        pool.wait_ge(s_ys, i + 1)
                        pool.tensor_tensor(k.x[:, i, :], ys[:, :], k.x[:, i, :], ALU.add).then_inc(s_res, 1)

                schedule(gate_up, down)

            @block.tensor
            def _(pe):
                def turn(c):
                    for b in range(KD):
                        n = 4 * c + b
                        if n >= 2:
                            pe.wait_ge(s_tlo, n - 1)
                        for j in range(TC):
                            mm = pe.transpose(bank[n % 2][:, j * P:(j + 1) * P], k.x[:, c * TC + j, b * P:(b + 1) * P], k.ident[:, :])
                        mm.then_inc(s_tps, 1)

                def logits(c):
                    pe.wait_ge(s_tlo, 4 * c + 4)
                    for i in range(4 * c, 4 * c + 4):
                        for b in range(KD):
                            t = slice(i * P, (i + 1) * P)
                            mm = mm3(pe, bank[6 + i // 8][:, i % 8 * E1:(i % 8 + 1) * E1], xt_hi[:, b, t], xt_lo[:, b, t],
                                     gw_hi[:, b, :], gw_lo[:, b, :], b == 0, b == KD - 1)
                    mm.then_inc(s_lg, 1)

                def gate_up(u):
                    c, f = u // 2, u % 2
                    if u == 0:
                        pe.wait_ge(s_wlo, 2)
                    if u >= 2:
                        pe.wait_ge(s_act, u - 1)
                    t = slice(c * CH, (c + 1) * CH)
                    for a in range(2):
                        fs = slice(a * F1 + f * HF1, a * F1 + (f + 1) * HF1)
                        for b in range(KD):
                            mm = mm3(pe, bank[2 + 2 * a + f][0:HF1, :], w1_hi[:, b, fs], w1_lo[:, b, fs],
                                     xt_hi[:, b, t], xt_lo[:, b, t], b == 0, b == KD - 1)
                    mm.then_inc(s_gu, 1)

                def down(c):
                    if c == 0:
                        pe.wait_ge(s_wlo, 3)
                        pe.wait_ge(s_sc, 2)
                    pe.wait_ge(s_hlo, 2 * c + 2)
                    for i in range(4 * c, 4 * c + 4):
                        if i:
                            pe.wait_ge(s_ys, i)
                        t = slice(i % 4 * P, (i % 4 + 1) * P)
                        for f in range(2):
                            mm = mm3(pe, bank[6][:, :], h_hi[:, f, t], h_lo[:, f, t], w2_hi[:, f, :], w2_lo[:, f, :],
                                     f == 0, f == 1)
                        mm.then_inc(s_dn, 1)
                    if c == NC - 2:
                        prefix()

                def prefix():
                    pe.wait_ge(s_sel, 1)
                    for a in range(2):
                        half = sel[:, a * 512:(a + 1) * 512]
                        if a:
                            pe.wait_ge(s_tot, 1)
                        pe.matmul(bank[7][:, :], ones[:, :], half, start=True, stop=True)
                        pe.matmul(bank[a][:, :], upper[:, :], half, start=True, stop=True).then_inc(s_pre, 1)

                def table():
                    pe.wait_ge(s_tot, 2)
                    for n in range(NT * K1):
                        if n % K1 == 0:
                            pe.wait_ge(s_col, n // K1 + 1)
                        pe.wait_ge(s_row, n + 1)
                        pe.matmul(bank[7][0:CAP, 0:E1], at_row[:, n % 2, :], at_col[:, n // K1 % 2, n % K1, :], start=(n == 0),
                                  stop=(n == NT * K1 - 1)).then_inc(s_used, 1)

                pe.wait_ge(s_const, 8)
                turn(0)
                pe.wait_ge(s_wlo, 1)
                for c in range(NC):
                    if c + 1 < NC:
                        turn(c + 1)
                    logits(c)
                schedule(gate_up, down, ahead=1)
                table()

            @block.scalar
            def _(act):
                act.wait_ge(s_gw, 16)
                act.activation(gw_hi[:, :, :], gw_raw[:, :, :], ACT.Copy).then_inc(s_whi, 1)
                for n in range(4 * NC):
                    act.wait_ge(s_tps, n + 1)
                    act.activation(xt_hi[:, n % 4, n // 4 * CH:(n // 4 + 1) * CH], bank[n % 2][:, :], ACT.Copy).then_inc(s_thi, 1)
                    if n == 3:
                        act.wait_ge(s_w1, 32)
                        act.activation(w1_hi[:, :, :], w1_raw[:, :, :], ACT.Copy).then_inc(s_whi, 1)
                    if n == 7:
                        act.wait_ge(s_w2, 16)
                        act.activation(w2_hi[:, :, :], w2_raw[:, :, :], ACT.Copy).then_inc(s_whi, 1)
                for a in range(2):
                    act.wait_ge(s_lg, 2 * a + 2)
                    act.activation(scores[:, 8 * a:8 * a + 8, :].rearrange("p t e -> p (t e)"), bank[6 + a][:, :], ACT.Sigmoid).then_inc(s_sc, 1)

                def gate_up(u):
                    act.wait_ge(s_gu, u + 1)
                    if u:
                        act.wait_ge(s_h, u)
                    act.activation(si[:, :], bank[2 + u % 2][0:HF1, :], ACT.Silu)
                    act.activation(up[:, :], bank[4 + u % 2][0:HF1, :], ACT.Copy).then_inc(s_act, 1)
                    act.wait_ge(s_h, u + 1)
                    if u >= 2:
                        act.wait_ge(s_dn, TC * (u // 2))
                    act.activation(h_hi[:, u % 2, :], hf[:, u % 2, :], ACT.Copy).then_inc(s_hh, 1)

                def down(c):
                    for i in range(c * TC, c * TC + TC):
                        act.wait_ge(s_dn, i + 1)
                        if i:
                            act.wait_ge(s_res, i)
                        act.activation(ys[:, :], bank[6][:, :], ACT.Copy).then_inc(s_ys, 1)

                schedule(gate_up, down)

            @block.vector
            def _(vec):
                done = [0]

                def step(ins):
                    ins.then_inc(s_r, 1)
                    done[0] += 1

                def sync():
                    vec.wait_ge(s_r, done[0])

                def split_lo(n, lo, raw, hi):
                    vec.wait_ge(s_whi, n + 1)
                    vec.tensor_tensor(lo, raw, hi, ALU.subtract).then_inc(s_wlo, 1)

                def choose():
                    vec.wait_ge(s_b, 16)
                    vec.wait_ge(s_sc, 2)
                    step(vec.tensor_tensor(biased[:, :, :], scores[:, :, :], bias[:, :].unsqueeze(1).to_broadcast([P, NT, E1]), ALU.add))
                    sync()
                    by_group = biased[:, :, :].rearrange("p t (g e) -> p (t g) e", g=G1)
                    for n in range(NT * G1):
                        last = vec.max(top_in_group[:, n, :], by_group[:, n, :])
                    step(last)
                    sync()
                    best = top_in_group[:, :, :].rearrange("p (t g) e -> p t g e", g=G1)
                    step(vec.tensor_tensor(gscore[:, :, :], best[:, :, :, 0], best[:, :, :, 1], ALU.add))
                    sync()
                    shape = [P, NT, G1, G1]
                    pairs = lambda n: prod[:, :, :, :].rearrange("p t k e -> p (t k e)")[:, n * NT * G1 * G1:(n + 1) * NT * G1 * G1].rearrange(
                        "p (t g h) -> p t g h", g=G1, h=G1)
                    mine = gscore[:, :, :].unsqueeze(3).to_broadcast(shape)
                    other = gscore[:, :, :].unsqueeze(2).to_broadcast(shape)
                    step(vec.tensor_tensor(pairs(0), other, mine, ALU.is_gt))
                    step(vec.tensor_tensor(pairs(1), other, mine, ALU.is_equal))
                    vec.wait_ge(s_const, 8)
                    sync()
                    step(vec.tensor_tensor(pairs(1), pairs(1), lower[:, :, :].unsqueeze(1).to_broadcast(shape), ALU.mult))
                    sync()
                    step(vec.tensor_tensor(pairs(0), pairs(0), pairs(1), ALU.add))
                    sync()
                    step(vec.tensor_reduce(rank[:, :, :], pairs(0), AX.X, ALU.add))
                    sync()
                    step(vec.tensor_scalar(rank[:, :, :], rank[:, :, :], float(KG1), -BIG, ALU.is_ge, ALU.mult))
                    sync()
                    step(vec.tensor_tensor(biased[:, :, :].rearrange("p t (g e) -> p t g e", g=G1),
                                           biased[:, :, :].rearrange("p t (g e) -> p t g e", g=G1),
                                           rank[:, :, :].unsqueeze(3).to_broadcast([P, NT, G1, EG]), ALU.add))
                    sync()
                    for i in range(NT):
                        step(vec.max(top[:, i, :], biased[:, i, :]))
                    sync()
                    for i in range(NT):
                        step(vec.max_index(arg[:, i, :], top[:, i, :], biased[:, i, :]))
                    sync()
                    step(vec.tensor_copy(argf[:, :, :], arg[:, :, 0:K1]))
                    sync()
                    step(vec.tensor_tensor(onehot[:, :, :, :], iota_e[:, :].unsqueeze(1).unsqueeze(1).to_broadcast([P, NT, K1, E1]),
                                           argf[:, :, :].unsqueeze(3).to_broadcast([P, NT, K1, E1]), ALU.is_equal))
                    sync()
                    with nc.allow_low_precision("counts of 0 or 1"):
                        vec.tensor_reduce(sel[:, :].rearrange("p (t e) -> p t e", e=E1), onehot[:, :, :, :].rearrange("p t k e -> p t e k"),
                                          AX.X, ALU.add).then_inc(s_sel, 1)
                    for half in range(2):
                        t = slice(half * NT // 2, (half + 1) * NT // 2)
                        sync()
                        step(vec.tensor_tensor(prod[:, :, :, :], onehot[:, t, :, :],
                                               scores[:, t, :].unsqueeze(2).to_broadcast([P, NT // 2, K1, E1]), ALU.mult))
                        sync()
                        step(vec.tensor_reduce(k.weight[:, t, :], prod[:, :, :, :], AX.X, ALU.add))
                    sync()
                    step(vec.tensor_reduce(wsum[:, :], k.weight[:, :, :], AX.X, ALU.add))
                    sync()
                    step(vec.reciprocal(wsum[:, :], wsum[:, :]))
                    sync()
                    step(vec.tensor_scalar(wsum[:, :], wsum[:, :], ROUTED_SCALE, None, ALU.mult))
                    sync()
                    step(vec.tensor_tensor(k.weight[:, :, :], k.weight[:, :, :], wsum[:, :].unsqueeze(2).to_broadcast([P, NT, K1]), ALU.mult))

                def positions():
                    for a in range(2):
                        t = slice(8 * a, 8 * a + 8)
                        vec.wait_ge(s_pre, a + 1)
                        whole = bank[7][:, :].rearrange("p (t e) -> p t e", e=E1)
                        step(vec.tensor_copy(run_a[:, t, :], whole))
                        vec.tensor_copy(tot[:, t, :], whole).then_inc(s_tot, 1)
                    a, b = run_a, run_b[:, :, :]
                    for d in (1, 2, 4, 8):
                        sync()
                        step(vec.tensor_tensor(b[:, d:, :], a[:, d:, :], a[:, :NT - d, :], ALU.add))
                        step(vec.tensor_copy(b[:, :d, :], a[:, :d, :]))
                        a, b = b, a
                    vec.wait_ge(s_tot, 2)
                    sync()
                    step(vec.tensor_tensor(b, a, tot[:, :, :], ALU.subtract))
                    sync()
                    for h in range(2):
                        t = slice(8 * h, 8 * h + 8)
                        step(vec.tensor_tensor(b[:, t, :], bank[h][:, :].rearrange("p (t e) -> p t e", e=E1), b[:, t, :], ALU.add))
                    for half in range(2):
                        t = slice(half * NT // 2, (half + 1) * NT // 2)
                        sync()
                        step(vec.tensor_tensor(prod[:, :, :, :], onehot[:, t, :, :],
                                               b[:, t, :].unsqueeze(2).to_broadcast([P, NT // 2, K1, E1]), ALU.mult))
                        sync()
                        step(vec.tensor_reduce(posk[:, t, :], prod[:, :, :, :], AX.X, ALU.add))
                    sync()
                    step(vec.tensor_scalar(valid[:, :, :], posk[:, :, :], float(CAP), None, ALU.is_lt))
                    step(vec.tensor_scalar(argf[:, :, :], argf[:, :, :], float(CAP), None, ALU.mult))
                    sync()
                    step(vec.tensor_tensor(k.weight[:, :, :], k.weight[:, :, :], valid[:, :, :], ALU.mult))
                    step(vec.scalar_tensor_tensor(k.slot[:, :, :], posk[:, :, :], float(CAP - 1), argf[:, :, :], ALU.min, ALU.add))

                def table():
                    for i in range(NT):
                        if i >= 2:
                            vec.wait_ge(s_used, K1 * (i - 1))
                        vec.tensor_scalar(at_col[:, i % 2, :, :], onehot[:, i, :, :], tok[:, i:i + 1], None, ALU.mult).then_inc(s_col, 1)
                        for kk in range(K1):
                            n = K1 * i + kk
                            if n >= 2:
                                vec.wait_ge(s_used, n - 1)
                            vec.tensor_scalar(at_row[:, n % 2, :], iota_c[:, :], posk[:, i, kk:kk + 1], None, ALU.is_equal).then_inc(s_row, 1)
                    vec.wait_ge(s_used, K1 * NT)
                    vec.tensor_copy(k.token_of[:, :], bank[7][0:CAP, 0:E1]).then_inc(s_tab, 1)

                split_lo(0, gw_lo[:, :, :], gw_raw[:, :, :], gw_hi[:, :, :])
                for n in range(4 * NC):
                    vec.wait_ge(s_thi, n + 1)
                    t = slice(n // 4 * CH, (n // 4 + 1) * CH)
                    vec.tensor_tensor(xt_lo[:, n % 4, t], bank[n % 2][:, :], xt_hi[:, n % 4, t], ALU.subtract).then_inc(s_tlo, 1)
                    if n == 7:
                        split_lo(1, w1_lo[:, :, :], w1_raw[:, :, :], w1_hi[:, :, :])
                    if n == 11:
                        split_lo(2, w2_lo[:, :, :], w2_raw[:, :, :], w2_hi[:, :, :])
                choose()
                positions()
                table()


def experts1_routed(k):
    nc, bank, io = k.nc, k.bank, k.io
    with ExitStack() as ctx:
        two = lambda name, shape, dt=F32: [k.sb(f"e1_{name}{p}", shape, dt, ctx) for p in range(2)]
        w1_raw, w1_hi, w1_lo = two("w1_raw", [P, KD, 2 * F1]), two("w1_hi", [P, KD, 2 * F1], F32R), two("w1_lo", [P, KD, 2 * F1], F32R)
        w2_raw, w2_hi, w2_lo = two("w2_raw", [HF1, 2, D]), two("w2_hi", [HF1, 2, D], F32R), two("w2_lo", [HF1, 2, D], F32R)
        index = two("index", [CAP, 1], I32)
        xg = two("xg", [CAP, D])
        xt_hi, xt_lo = two("xt_hi", [P, KD * CAP], F32R), two("xt_lo", [P, KD * CAP], F32R)
        si, hf = two("si", [CAP, F1]), two("hf", [CAP, F1])
        ht_hi, ht_lo = two("ht_hi", [HF1, 2 * CAP], F32R), two("ht_lo", [HF1, 2 * CAP], F32R)
        y = two("y", [CAP, D])

        pair = lambda name: [k.sem(f"e1_{name}{p}") for p in range(2)]
        sem = lambda n: k.sem("e1_" + n)
        s_w, s_v, s_g, s_y = pair("gate_up_loaded"), pair("down_loaded"), pair("rows_gathered"), pair("results_stored")
        s_ix, s_go = sem("index"), sem("index_seen")
        s_whi, s_wlo, s_vhi, s_vlo = sem("gate_up_hi"), sem("gate_up_lo"), sem("down_hi"), sem("down_lo")
        s_tps, s_thi, s_tlo = sem("turned"), sem("turned_hi"), sem("turned_lo")
        s_gu, s_si, s_h = sem("gate_up"), sem("silu"), sem("hidden")
        s_ht, s_hh, s_hlo = sem("hidden_turned"), sem("hidden_hi"), sem("hidden_lo")
        s_dn, s_ysb = sem("down"), sem("results")
        nothing = lambda h, p: None
        y_rows = k.y1.rearrange("(e s) d -> e s d", s=CAP)

        with nc.Block() as block:
            @block.sync
            def _(sp):
                def load(h, p):
                    e = 2 * h + p
                    if started(h):
                        sp.wait_ge(s_wlo, e - 1)
                    sp.dma_start(w1_raw[p][:, :, :].rearrange("p b n -> p (b n)"),
                                 io["w_gate_up"][bass.ds(e, 1)].rearrange("e p n -> p (e n)")).then_inc(s_w[p], 16)
                    if started(h):
                        sp.wait_ge(s_vlo, e - 1)
                    sp.dma_start(w2_raw[p][:, :, :].rearrange("p f n -> p (f n)"),
                                 io["w_down"][bass.ds(e, 1)].rearrange("e p n -> p (e n)")).then_inc(s_v[p], 16)

                three_stages(sp, E1, load, nothing, nothing)

            @block.gpsimd
            def _(pool):
                def gather(h, p):
                    e = 2 * h + p
                    if started(h):
                        pool.wait_ge(s_g[p], 16 * h)
                        pool.wait_ge(s_tps, e - 1)
                    pool.tensor_copy(index[p][:, :], k.token_of[:, bass.ds(e, 1)]).then_inc(s_ix, 1)
                    pool.wait_ge(s_ix, e + 1)
                    pool.sem_inc(s_go, 1)
                    pool.indirect_dma_start(xg[p][:, :], None, k.rows, bass.IndirectOffsetOnAxis(index[p][:, 0:1], 0)
                                            ).then_inc(s_g[p], 16)

                three_stages(pool, E1, gather, nothing, nothing)

            @block.tensor
            def _(pe):
                def turn(h, p):
                    pe.wait_ge(s_g[p], 16 * (h + 1))
                    if started(h):
                        pe.wait_ge(s_tlo, 2 * h + p - 1)
                    for b in range(KD):
                        mm = pe.transpose(bank[p][:, b * CAP:(b + 1) * CAP], xg[p][:, b * P:(b + 1) * P], k.ident[0:CAP, 0:CAP])
                    mm.then_inc(s_tps, 1)

                def gate_up(h, p):
                    e = 2 * h + p
                    pe.wait_ge(s_wlo, e + 1)
                    pe.wait_ge(s_tlo, e + 1)
                    if started(h):
                        pe.wait_ge(s_h, e - 1)
                    for b in range(KD):
                        c = slice(b * CAP, (b + 1) * CAP)
                        mm = mm3(pe, bank[2 + p][0:CAP, 0:2 * F1], xt_hi[p][:, c], xt_lo[p][:, c], w1_hi[p][:, b, :], w1_lo[p][:, b, :],
                                 b == 0, b == KD - 1)
                    mm.then_inc(s_gu, 1)

                def turn_hidden(h, p):
                    pe.wait_ge(s_h, 2 * h + p + 1)
                    if started(h):
                        pe.wait_ge(s_hlo, 2 * h + p - 1)
                    for f in range(2):
                        mm = pe.transpose(bank[4 + p][0:HF1, f * CAP:(f + 1) * CAP], hf[p][:, f * HF1:(f + 1) * HF1], k.ident[0:CAP, 0:CAP])
                    mm.then_inc(s_ht, 1)

                def down(h, p):
                    e = 2 * h + p
                    pe.wait_ge(s_hlo, e + 1)
                    pe.wait_ge(s_vlo, e + 1)
                    if started(h):
                        pe.wait_ge(s_ysb, e - 1)
                    for f in range(2):
                        c = slice(f * CAP, (f + 1) * CAP)
                        mm = mm3(pe, bank[6 + p][0:CAP, :], ht_hi[p][:, c], ht_lo[p][:, c], w2_hi[p][:, f, :], w2_lo[p][:, f, :],
                                 f == 0, f == 1)
                    mm.then_inc(s_dn, 1)

                three_stages(pe, E1, turn, gate_up, down, between=turn_hidden)

            @block.scalar
            def _(act):
                def split(h, p):
                    e = 2 * h + p
                    act.wait_ge(s_w[p], 16 * (h + 1))
                    if started(h):
                        act.wait_ge(s_gu, e - 1)
                    act.activation(w1_hi[p][:, :, :], w1_raw[p][:, :, :], ACT.Copy).then_inc(s_whi, 1)
                    act.wait_ge(s_tps, e + 1)
                    act.activation(xt_hi[p][:, :], bank[p][:, 0:KD * CAP], ACT.Copy).then_inc(s_thi, 1)

                def hidden_hi(h, p):
                    e = 2 * h + p
                    act.wait_ge(s_ht, e + 1)
                    if started(h):
                        act.wait_ge(s_dn, e - 1)
                    act.activation(ht_hi[p][:, :], bank[4 + p][0:HF1, 0:2 * CAP], ACT.Copy).then_inc(s_hh, 1)

                def silu(h, p):
                    e = 2 * h + p
                    act.wait_ge(s_v[p], 16 * (h + 1))
                    if started(h):
                        act.wait_ge(s_dn, e - 1)
                    act.activation(w2_hi[p][:, :, :], w2_raw[p][:, :, :], ACT.Copy).then_inc(s_vhi, 1)
                    act.wait_ge(s_gu, e + 1)
                    if started(h):
                        act.wait_ge(s_h, e - 1)
                    act.activation(si[p][:, :], bank[2 + p][0:CAP, 0:F1], ACT.Silu).then_inc(s_si, 1)

                def results(h, p):
                    e = 2 * h + p
                    act.wait_ge(s_dn, e + 1)
                    if started(h):
                        act.wait_ge(s_y[p], 16 * h)
                    act.activation(y[p][:, :], bank[6 + p][0:CAP, :], ACT.Copy).then_inc(s_ysb, 1)
                    act.wait_ge(s_ysb, e + 1)
                    act.dma_start(y_rows[bass.ds(e, 1)].rearrange("e s d -> s (e d)"), y[p][:, :]).then_inc(s_y[p], 16)

                three_stages(act, E1, split, silu, results, between=hidden_hi)
                act.wait_ge(s_y[0], 16 * (E1 // 2))
                act.wait_ge(s_y[1], 16 * (E1 // 2))

            @block.vector
            def _(vec):
                def split(h, p):
                    e = 2 * h + p
                    vec.wait_ge(s_whi, e + 1)
                    vec.tensor_tensor(w1_lo[p][:, :, :], w1_raw[p][:, :, :], w1_hi[p][:, :, :], ALU.subtract).then_inc(s_wlo, 1)
                    vec.wait_ge(s_thi, e + 1)
                    vec.tensor_tensor(xt_lo[p][:, :], bank[p][:, 0:KD * CAP], xt_hi[p][:, :], ALU.subtract).then_inc(s_tlo, 1)

                def hidden_lo(h, p):
                    vec.wait_ge(s_hh, 2 * h + p + 1)
                    vec.tensor_tensor(ht_lo[p][:, :], bank[4 + p][0:HF1, 0:2 * CAP], ht_hi[p][:, :], ALU.subtract).then_inc(s_hlo, 1)

                def hidden(h, p):
                    e = 2 * h + p
                    vec.wait_ge(s_vhi, e + 1)
                    vec.tensor_tensor(w2_lo[p][:, :, :], w2_raw[p][:, :, :], w2_hi[p][:, :, :], ALU.subtract).then_inc(s_vlo, 1)
                    vec.wait_ge(s_si, e + 1)
                    if started(h):
                        vec.wait_ge(s_ht, e - 1)
                    vec.tensor_tensor(hf[p][:, :], si[p][:, :], bank[2 + p][0:CAP, F1:2 * F1], ALU.mult).then_inc(s_h, 1)

                three_stages(vec, E1, split, hidden, nothing, between=hidden_lo)


def combine1(k):
    nc, io = k.nc, k.io
    NB = 3
    with ExitStack() as ctx:
        yg = [k.sb(f"c1_yg{n}", [P, K1, D], F32, ctx) for n in range(NB)]
        s_g = [k.sem(f"c1_gathered{n}") for n in range(NB)]
        s_sum, s_used = k.sem("c1_summed"), k.sem("c1_gathered_used")
        s_stat, s_var, s_rstd, s_ln, s_st = (k.sem("c1_" + n) for n in ("stats", "var", "rstd", "normed", "stored"))
        with nc.Block() as block:
            @block.sync
            def _(sp):
                for c in range(NC):
                    sp.wait_ge(s_ln, TC * (c + 1))
                    sp.dma_start(io["out"].rearrange("(c j p) d -> c p j d", p=P, j=TC)[c],
                                 k.x[:, c * TC:(c + 1) * TC, :]).then_inc(s_st, 16)
                sp.wait_ge(s_st, 16 * NC)

            @block.gpsimd
            def _(pool):
                def rstd(c):
                    pool.wait_ge(s_stat, 2 * TC * (c + 1))
                    ln_rstd(k, pool, c * TC, TC, s_var, s_rstd, c)

                for i in range(NT):
                    if i >= NB:
                        pool.wait_ge(s_used, i - NB + 1)
                    for kk in range(K1):
                        pool.indirect_dma_start(yg[i % NB][:, kk, :], None, k.y1, bass.IndirectOffsetOnAxis(k.slot[:, i, kk:kk + 1], 0)
                                                ).then_inc(s_g[i % NB], 16)
                    if i >= 7 and i % 4 == 3:
                        rstd(i // 4 - 1)
                rstd(NC - 1)

            @block.vector
            def _(vec):
                def apply(c):
                    vec.wait_ge(s_rstd, c + 1)
                    for i in range(c * TC, c * TC + TC):
                        ln_apply(k, vec, i).then_inc(s_ln, 1)

                for i in range(NT):
                    xi = k.x[:, i, :]
                    vec.wait_ge(s_g[i % NB], 16 * K1 * (i // NB + 1))
                    for kk in range(K1):
                        vec.scalar_tensor_tensor(xi, yg[i % NB][:, kk, :], k.weight[:, i, kk:kk + 1], xi, ALU.mult, ALU.add).then_inc(s_sum, 1)
                        vec.wait_ge(s_sum, K1 * i + kk + 1)
                    vec.sem_inc(s_used, 1)
                    ln_stats(k, vec, i, s_stat, i)
                    if i >= 7 and i % 4 == 3:
                        apply(i // 4 - 1)
                apply(NC - 1)


def two_layers(nc, io):
    with ExitStack() as ctx:
        k = Core(nc, ctx, io)
        k.rows = nc.dram_tensor("rows", (T, D), F32, kind="Internal").ap()
        k.y0 = nc.dram_tensor("results0", (NG0 * GRP, D), F32, kind="Internal").ap()
        k.y1 = nc.dram_tensor("results1", (E1 * CAP, D), F32, kind="Internal").ap()
        setup(k)
        attention0(k)
        with ExitStack() as k.moe_ctx:
            experts0_shared(k)
            experts0_routed(k)
            combine0(k)
        k.clear_semaphores()
        attention1(k)
        k.clear_semaphores()
        with ExitStack() as k.moe_ctx:
            experts1_shared(k)
            experts1_routed(k)
            combine1(k)


def layouts(inputs):
    a = {name: np.asarray(v) for name, v in inputs.items()}
    l0 = lambda n: a["L0_ffn_" + n]
    l1 = lambda n: a["L1_attn_" + n]
    m1 = lambda n: a["L1_ffn_" + n]
    blocks = lambda v: v.reshape(-1, P).T
    expert_blocks = lambda v: v.reshape(E0, F0 // P, P).transpose(2, 1, 0).reshape(P, -1)
    by_row = lambda w, n: w.reshape(E1, -1, n, w.shape[-1])
    names = {
        "x": a["L0_attn_hidden_states"].reshape(T, D),
        "wq_t": a["L0_attn_Wq"].T, "wo_t": a["L0_attn_Wo"].T,
        "mem": a["L0_attn_memories"].reshape(4, 4, 4, 32, 32).transpose(2, 3, 1, 0, 4).reshape(P, -1),
        "nrm": a["L0_attn_memory_norms"].reshape(4, 4, 4, 32).transpose(2, 3, 1, 0).reshape(P, -1),
        "norms": a["L0_attn_memory_norms"].reshape(-1),
        "bank_w": a["L0_attn_bank_weights"].reshape(4, 4, 4).transpose(0, 2, 1).reshape(-1),
        "sgb_t": blocks(l0("sgb")), "sb1_t": blocks(l0("sb1")),
        "rgb_t": expert_blocks(l0("rgb")), "rb1_t": expert_blocks(l0("rb1")),
        "b2": np.concatenate([l0("rb2"), l0("sb2")], 0),
        "kb_t": blocks(l1("kb")), "qb_t": blocks(l1("qb")), "fw2_t": l1("fw2").T,
        "w_gate_up": np.concatenate([by_row(m1("w_gate"), P), by_row(m1("w_up"), P)], 3).transpose(0, 2, 1, 3).reshape(E1, P, -1),
        "w_down": by_row(m1("w_down"), HF1).transpose(0, 2, 1, 3).reshape(E1, HF1, -1),
    }
    for n in ("wa", "sg", "sw1", "sw2", "rg", "rw1", "rw2"):
        names[n] = l0(n)
    for n in ("qw", "kw", "vw", "ow", "vb", "ob", "fw1", "fb1", "fw2", "fb2"):
        names[n] = l1(n)
    for n in ("gate_w", "bias", "ws_gate", "ws_up", "ws_down"):
        names[n] = m1(n)
    return {n: np.ascontiguousarray(v) for n, v in names.items()}


def kernel(**inputs):
    import concourse.bacc as bacc
    from concourse.bass_utils import run_bass_kernel_spmd

    nc = bacc.Bacc("TRN2", target_bir_lowering=False, num_devices=1)
    arrays = {"in_" + n: v for n, v in layouts(inputs).items()}
    io = {n[3:]: nc.dram_tensor(n, v.shape, mybir.dt.from_np(v.dtype), kind="ExternalInput").ap() for n, v in arrays.items()}
    io["out"] = nc.dram_tensor("out", (T, D), F32, kind="ExternalOutput").ap()
    two_layers(nc, io)
    r = run_bass_kernel_spmd(nc, [arrays], core_ids=[0])
    return r.results[0]["out"].reshape(1, T, D)
```

```python
from contextlib import ExitStack

import numpy as np
import concourse.bass as bass
import concourse.mybir as mybir

F32 = mybir.dt.float32
F32R = mybir.dt.float32r
BF16 = mybir.dt.bfloat16
I32 = mybir.dt.int32
U32 = mybir.dt.uint32
ALU = mybir.AluOpType
ACT = mybir.ActivationFunctionType
AX = mybir.AxisListType

P = 128
T = 2048
D = 512
NT = T // P
KD = D // P
CH = 512
NC = T // CH
TC = CH // P
EPS_LN = 1e-5
EPS_MEM = 1e-6


class Core:

    def __init__(self, nc, ctx, io):
        self.nc, self.ctx, self.io = nc, ctx, io
        self.sems = []
        self.bank = [ctx.enter_context(nc.psum_tensor(f"bank{i}", [P, 512], F32)) for i in range(8)]

    def sem(self, name):
        self.sems.append(self.nc.alloc_semaphore(name=name))
        return self.sems[-1]

    def clear_semaphores(self):
        self.nc.clear_and_free_semaphores(self.sems)
        self.nc.all_engine_barrier()
        self.sems = []

    def sb(self, name, shape, dt=F32, ctx=None):
        return (ctx or self.ctx).enter_context(self.nc.sbuf_tensor(name, shape, dt))


def mm3(pe, out, a_hi, a_lo, b_hi, b_lo, start, stop):
    pe.matmul(out, a_hi, b_hi, start=start, stop=False)
    pe.matmul(out, a_hi, b_lo, start=False, stop=False)
    return pe.matmul(out, a_lo, b_hi, start=False, stop=stop)


def setup(k):
    k.ident = k.sb("ident", [P, P])
    k.x = k.sb("resid", [P, NT, D])
    k.neg_half = k.sb("neg_half", [P, NT])
    k.mv = k.sb("mv", [P, NT, 2])
    k.stats = k.sb("stats", [P, 2, 6])
    k.var = k.sb("var", [P, NT])
    k.rstd = k.sb("rstd", [P, NT])
    s_ident0 = k.sem("ident_zeroed")
    with k.nc.Block() as block:
        @block.gpsimd
        def _(pool):
            pool.memset(k.ident[:, :], 0.0).then_inc(s_ident0, 1)
            pool.memset(k.neg_half[:, :], -0.5)
            pool.wait_ge(s_ident0, 1)
            pool.affine_select(out=k.ident[:, :], in_=k.ident[:, :], compare_op=ALU.not_equal, fill=1.0,
                               base=0, pattern=[[-1, P]], channel_multiplier=1)


def ln_stats(k, vec, tile, s_stat, n):
    vec.bn_stats(k.stats[:, n % 2, :], k.x[:, tile, :]).then_inc(s_stat, 1)
    vec.wait_ge(s_stat, 2 * n + 1)
    vec.bn_aggr(k.mv[:, tile, :], k.stats[:, n % 2, :]).then_inc(s_stat, 1)


def ln_rstd(k, pool, t0, n, s_var, s_rstd, done):
    pool.tensor_scalar(k.var[:, t0:t0 + n], k.mv[:, t0:t0 + n, 1], EPS_LN, 0.0, ALU.add, ALU.add).then_inc(s_var, 1)
    pool.wait_ge(s_var, done + 1)
    pool.tensor_tensor(k.rstd[:, t0:t0 + n], k.var[:, t0:t0 + n], k.neg_half[:, t0:t0 + n], ALU.pow).then_inc(s_rstd, 1)


def ln_apply(k, vec, tile):
    return vec.tensor_scalar(k.x[:, tile, :], k.x[:, tile, :], k.mv[:, tile, 0:1], k.rstd[:, tile:tile + 1],
                             ALU.subtract, ALU.mult)


def attention0(k):
    nc, bank, io = k.nc, k.bank, k.io
    NB, G, HG, DH = 4, 4, 4, 32
    with ExitStack() as ctx:
        sb = lambda name, shape, dt=F32: k.sb("a0_" + name, shape, dt, ctx)
        raw = sb("raw", [P, KD, D])
        wq_hi, wq_lo = sb("wq_hi", [P, KD, D], F32R), sb("wq_lo", [P, KD, D], F32R)
        wo_hi, wo_lo = sb("wo_hi", [P, KD, D], F32R), sb("wo_lo", [P, KD, D], F32R)
        mem_raw, nrm_raw = sb("mem_raw", [P, G * NB, DH]), sb("nrm_raw", [P, G * NB])
        mem_hi, mem_lo = sb("mem_hi", [P, G, NB * HG * DH], F32R), sb("mem_lo", [P, G, NB * HG * DH], F32R)
        nrm_f = sb("nrm_f", [P, G * NB, HG])
        nrm_hi, nrm_lo = sb("nrm_hi", [P, G * NB, HG], F32R), sb("nrm_lo", [P, G * NB, HG], F32R)
        head_mask = sb("head_mask", [P, HG])
        ones = sb("ones", [P, P])
        bw = sb("bw", [P, G, NB, HG])
        bmax, bsum = sb("bmax", [P, G, HG]), sb("bsum", [P, G, HG])
        act_n = sb("act_n", [P, NB])
        xt_hi, xt_lo = sb("xt_hi", [P, 2, KD, CH], F32R), sb("xt_lo", [P, 2, KD, CH], F32R)
        ex, rl = sb("ex", [P, 2, CH]), sb("rl", [P, 2, CH])
        sg = sb("sg", [P, 2, CH])
        sg_hi, sg_lo = sb("sg_hi", [P, 2, KD, CH], F32R), sb("sg_lo", [P, 2, KD, CH], F32R)
        rw = sb("rw", [P, 2, TC, G * NB * HG])
        comb, read_n = sb("comb", [P, 2, D]), sb("read_n", [P, 2, NB * HG * DH])
        read_2 = sb("read_2", [P, 2, 2 * HG * DH])
        ct_hi, ct_lo = sb("ct_hi", [P, 2, KD, P], F32R), sb("ct_lo", [P, 2, KD, P], F32R)

        s_x = [k.sem(f"a0_x_loaded{c}") for c in range(NC)]
        s_wq, s_wo, s_mem, s_nrm = (k.sem("a0_" + n) for n in ("wq_loaded", "wo_loaded", "mem_loaded", "nrm_loaded"))
        s_bw, s_ones, s_ns = k.sem("a0_bw_loaded"), k.sem("a0_ones_made"), k.sem("a0_norms_summed")
        s_zero, s_mask = k.sem("a0_mem_zeroed"), k.sem("a0_mask_made")
        s_whi, s_split = k.sem("a0_weight_hi"), k.sem("a0_weights_split")
        s_c = k.sem("a0_vector_chain")
        s_bexp = k.sem("a0_bank_exp")
        s_bsub = k.sem("a0_bank_sub")
        s_tps, s_thi, s_tlo = k.sem("a0_turned"), k.sem("a0_turned_hi"), k.sem("a0_turned_lo")
        s_q, s_qev, s_sg, s_slo = k.sem("a0_q"), k.sem("a0_q_read"), k.sem("a0_sigma"), k.sem("a0_sigma_split")
        s_nb, s_r = k.sem("a0_norms"), k.sem("a0_norms_read")
        s_rw = k.sem("a0_read_weights")
        s_m, s_rn, s_comb = k.sem("a0_reads"), k.sem("a0_reads_weighted"), k.sem("a0_combined")
        s_r2 = k.sem("a0_half_sum")
        s_o, s_res = k.sem("a0_out"), k.sem("a0_residual")
        s_stat, s_var, s_rstd = k.sem("a0_stats"), k.sem("a0_var"), k.sem("a0_rstd")
        s_ln, s_st = k.sem("a0_normed"), k.sem("a0_stored")

        def schedule(turn_x, query, norms, weights, read, turn_comb, project, late_query=False):
            for b in range(KD):
                turn_x(0, b)
            for m in range(KD):
                query(0, m)
            for b in range(KD):
                turn_x(1, b)
            for m in range(KD):
                norms(0, m)
            for i in range(NT):
                c, j = i // TC, i % TC
                if j == 0:
                    weights(c)
                read(4 * i)
                if c + 1 < NC and not late_query:
                    query(c + 1, j)
                read(4 * i + 1)
                if i:
                    turn_comb(i - 1)
                if c + 1 < NC and late_query:
                    query(c + 1, j)
                read(4 * i + 2)
                if c + 2 < NC:
                    turn_x(c + 2, j)
                read(4 * i + 3)
                if i:
                    project(i - 1)
                if c + 1 < NC:
                    norms(c + 1, j)
            turn_comb(NT - 1)
            project(NT - 1)

        idle = lambda *_: None
        turned = []
        schedule(lambda c, b: turned.append(("x", c, b)), idle, idle, idle, idle, lambda i: turned.append(("comb", i)), idle)
        number = {what: n for n, what in enumerate(turned)}

        with nc.Block() as block:
            @block.sync
            def _(sp):
                x_d = io["x"].rearrange("(c j p) d -> c p j d", p=P, j=TC)
                sp.dma_start(k.x[:, 0:TC, :], x_d[0]).then_inc(s_x[0], 16)
                sp.dma_start(mem_raw[:, :, :], io["mem"].rearrange("p (a e) -> p a e", e=DH)).then_inc(s_mem, 16)
                sp.dma_start(nrm_raw[:, :], io["nrm"]).then_inc(s_nrm, 16)
                sp.dma_start(bw[:, :, :, :].rearrange("p g n h -> p (g n h)"),
                             io["bank_w"].partition_broadcast(P)).then_inc(s_bw, 16)
                sp.dma_start(raw[:, :, :], io["wq_t"].rearrange("(b p) n -> p b n", p=P)).then_inc(s_wq, 16)
                for c in range(1, NC):
                    sp.dma_start(k.x[:, c * TC:(c + 1) * TC, :], x_d[c]).then_inc(s_x[c], 16)
                sp.wait_ge(s_split, 1)
                sp.dma_start(raw[:, :, :], io["wo_t"].rearrange("(b p) n -> p b n", p=P)).then_inc(s_wo, 16)
                for c in range(NC):
                    sp.wait_ge(s_ln, TC * (c + 1))
                    sp.dma_start(k.rows.rearrange("(c j p) d -> c p j d", p=P, j=TC)[c],
                                 k.x[:, c * TC:(c + 1) * TC, :]).then_inc(s_st, 16)
                sp.wait_ge(s_st, 16 * NC)

            @block.gpsimd
            def _(pool):
                pool.memset(ones[:, :], 1.0).then_inc(s_ones, 1)
                pool.memset(mem_hi[:, :, :].bitcast(F32), 0.0).then_inc(s_zero, 1)
                pool.memset(mem_lo[:, :, :].bitcast(F32), 0.0).then_inc(s_zero, 1)
                pool.memset(head_mask[:, :], 0.0).then_inc(s_zero, 1)
                pool.wait_ge(s_zero, 3)
                for h in range(HG):
                    pool.memset(head_mask[DH * h:DH * h + DH, h:h + 1], 1.0).then_inc(s_mask, 1)

                def read(v):
                    i, g = v // G, v % G
                    pool.wait_ge(s_rn, v + 1)
                    if i >= 2:
                        pool.wait_ge(s_tps, number["comb", i - 2] + 1)
                    pool.tensor_tensor(read_2[:, v % 2, :], read_n[:, v % 2, 0:256], read_n[:, v % 2, 256:512],
                                       ALU.add).then_inc(s_r2, 1)
                    pool.wait_ge(s_r2, v + 1)
                    pool.tensor_tensor(comb[:, i % 2, g * P:(g + 1) * P], read_2[:, v % 2, 0:P], read_2[:, v % 2, P:2 * P],
                                       ALU.add).then_inc(s_comb, 1)

                def project(i):
                    if i % TC == TC - 1:
                        pool.wait_ge(s_stat, 2 * (i + 1))
                        ln_rstd(k, pool, i - TC + 1, TC, s_var, s_rstd, i // TC)

                schedule(idle, idle, idle, idle, read, idle, project)

            @block.tensor
            def _(pe):
                def turned_bank(n):
                    if n >= 2:
                        pe.wait_ge(s_tlo, n - 1)
                    return bank[n % 2]

                def turn_x(c, b):
                    if b == 0:
                        pe.wait_ge(s_x[c], 16)
                    t = turned_bank(number["x", c, b])
                    for j in range(TC):
                        mm = pe.transpose(t[:, j * P:(j + 1) * P], k.x[:, c * TC + j, b * P:(b + 1) * P], k.ident[:, :])
                    mm.then_inc(s_tps, 1)

                def query(c, m):
                    u, s = 4 * c + m, c % 2
                    if u == 0:
                        pe.wait_ge(s_nrm, 16)
                        pe.wait_ge(s_ones, 1)
                        pe.matmul(bank[7][:, 0:G * NB], ones[:, :], nrm_raw[:, :], start=True, stop=True).then_inc(s_ns, 1)
                        pe.wait_ge(s_split, 1)
                    pe.wait_ge(s_tlo, number["x", c, KD - 1] + 1)
                    if u >= 2:
                        pe.wait_ge(s_qev, u - 1)
                    for b in range(KD):
                        mm = mm3(pe, bank[2 + u % 2][:, :], wq_hi[:, b, m * P:(m + 1) * P], wq_lo[:, b, m * P:(m + 1) * P],
                                 xt_hi[:, s, b, :], xt_lo[:, s, b, :], b == 0, b == KD - 1)
                    mm.then_inc(s_q, 1)

                def norms(c, g):
                    s = c % 2
                    if c == 0:
                        pe.wait_ge(s_split, 2)
                    pe.wait_ge(s_slo, 4 * c + g + 1)
                    if c:
                        pe.wait_ge(s_r, c)
                    elif g == 0:
                        pe.wait_ge(s_c, 2)
                    for j in range(TC):
                        tok = slice(j * P, (j + 1) * P)
                        mm = mm3(pe, bank[7][:, j * 64 + g * 16:j * 64 + g * 16 + 16], sg_hi[:, s, g, tok], sg_lo[:, s, g, tok],
                                 nrm_hi[:, g * NB:(g + 1) * NB, :].rearrange("p n h -> p (n h)"),
                                 nrm_lo[:, g * NB:(g + 1) * NB, :].rearrange("p n h -> p (n h)"), True, True)
                    mm.then_inc(s_nb, 1)

                def read(v):
                    s, j, g = v // 16 % 2, v // G % TC, v % G
                    tok = slice(j * P, (j + 1) * P)
                    if v >= 2:
                        pe.wait_ge(s_rn, v - 1)
                    mm3(pe, bank[4 + v % 2][:, :], sg_hi[:, s, g, tok], sg_lo[:, s, g, tok],
                        mem_hi[:, g, :], mem_lo[:, g, :], True, True).then_inc(s_m, 1)

                def turn_comb(i):
                    pe.wait_ge(s_comb, 4 * i + 4)
                    t = turned_bank(number["comb", i])
                    for b in range(KD):
                        mm = pe.transpose(t[:, b * P:(b + 1) * P], comb[:, i % 2, b * P:(b + 1) * P], k.ident[:, :])
                    mm.then_inc(s_tps, 1)

                def project(i):
                    if i == 0:
                        pe.wait_ge(s_split, 3)
                    pe.wait_ge(s_tlo, number["comb", i] + 1)
                    if i:
                        pe.wait_ge(s_res, i)
                    for b in range(KD):
                        mm = mm3(pe, bank[6][:, :], ct_hi[:, i % 2, b, :], ct_lo[:, i % 2, b, :],
                                 wo_hi[:, b, :], wo_lo[:, b, :], b == 0, b == KD - 1)
                    mm.then_inc(s_o, 1)

                schedule(turn_x, query, norms, idle, read, turn_comb, project)

            @block.scalar
            def _(act):
                def weights_hi():
                    act.wait_ge(s_wq, 16)
                    act.activation(wq_hi[:, :, :], raw[:, :, :], ACT.Copy).then_inc(s_whi, 1)
                    act.wait_ge(s_mem, 16)
                    act.wait_ge(s_zero, 3)
                    for h in range(HG):
                        r = slice(DH * h, DH * h + DH)
                        act.activation(mem_hi[r, :, :].rearrange("p g (n x) -> p (g n) x", n=NB)[:, :, r], mem_raw[r, :, :],
                                       ACT.Copy).then_inc(s_whi, 1)
                    act.wait_ge(s_bsub, 1)
                    act.activation(bw[:, :, :, :], bw[:, :, :, :], ACT.Exp).then_inc(s_bexp, 1)

                def turned_hi(n, dst):
                    act.wait_ge(s_tps, n + 1)
                    act.activation(dst, bank[n % 2][:, :], ACT.Copy).then_inc(s_thi, 1)

                def turn_x(c, b):
                    if c >= 2:
                        act.wait_ge(s_q, 4 * (c - 1))
                    turned_hi(number["x", c, b], xt_hi[:, c % 2, b, :])

                def query(c, m):
                    u = 4 * c + m
                    if u == 0:
                        weights_hi()
                    act.wait_ge(s_q, u + 1)
                    if u >= 2:
                        act.wait_ge(s_sg, u - 1)
                    act.activation(ex[:, u % 2, :], bank[2 + u % 2][:, :], ACT.Exp)
                    act.activation(rl[:, u % 2, :], bank[2 + u % 2][:, :], ACT.Relu).then_inc(s_qev, 1)
                    if u == 3:
                        act.wait_ge(s_wo, 16)
                        act.activation(wo_hi[:, :, :], raw[:, :, :], ACT.Copy).then_inc(s_whi, 1)

                def turn_comb(i):
                    if i >= 2:
                        act.wait_ge(s_o, i - 1)
                    turned_hi(number["comb", i], ct_hi[:, i % 2, :, :].rearrange("p b t -> p (b t)"))

                schedule(turn_x, query, idle, idle, idle, turn_comb, idle)

            @block.vector
            def _(vec):
                def bank_weights():
                    vec.wait_ge(s_bw, 16)
                    vec.wait_ge(s_ns, 1)
                    by_n = lambda a: a[:, :, :, :].rearrange("p g n h -> p g h n")
                    over = lambda a: a[:, :, :].unsqueeze(3).to_broadcast([P, G, HG, NB])
                    vec.tensor_reduce(bmax[:, :, :], by_n(bw), AX.X, ALU.max).then_inc(s_c, 1)
                    vec.tensor_reduce(act_n[:, :], bank[7][:, 0:G * NB].rearrange("p (g n) -> p n g", n=NB), AX.X, ALU.add).then_inc(s_c, 1)
                    vec.wait_ge(s_c, 2)
                    vec.tensor_tensor(by_n(bw), by_n(bw), over(bmax), ALU.subtract).then_inc(s_bsub, 1)
                    vec.tensor_scalar(act_n[:, :], act_n[:, :], EPS_MEM, None, ALU.is_ge).then_inc(s_c, 1)
                    vec.wait_ge(s_bexp, 1)
                    vec.tensor_reduce(bsum[:, :, :], by_n(bw), AX.X, ALU.add).then_inc(s_c, 1)
                    vec.wait_ge(s_c, 4)
                    vec.reciprocal(bsum[:, :, :], bsum[:, :, :]).then_inc(s_c, 1)
                    vec.wait_ge(s_c, 5)
                    vec.tensor_tensor(by_n(bw), by_n(bw), over(bsum), ALU.mult).then_inc(s_c, 1)
                    vec.wait_ge(s_c, 6)
                    vec.tensor_tensor(by_n(bw), by_n(bw), act_n[:, :].unsqueeze(1).unsqueeze(1).to_broadcast([P, G, HG, NB]),
                                      ALU.mult).then_inc(s_c, 1)

                def memories():
                    vec.wait_ge(s_nrm, 16)
                    vec.wait_ge(s_mask, HG)
                    vec.tensor_tensor(nrm_f[:, :, :], nrm_raw[:, :].unsqueeze(2).to_broadcast([P, G * NB, HG]),
                                      head_mask[:, :].unsqueeze(1).to_broadcast([P, G * NB, HG]), ALU.mult).then_inc(s_c, 1)
                    vec.wait_ge(s_c, 8)
                    vec.tensor_copy(nrm_hi[:, :, :], nrm_f[:, :, :]).then_inc(s_c, 1)
                    vec.wait_ge(s_c, 9)
                    vec.tensor_tensor(nrm_lo[:, :, :], nrm_f[:, :, :], nrm_hi[:, :, :], ALU.subtract)
                    vec.wait_ge(s_whi, 1 + HG)
                    for h in range(HG):
                        r = slice(DH * h, DH * h + DH)
                        block_of = lambda a: a[r, :, :].rearrange("p g (n x) -> p (g n) x", n=NB)[:, :, r]
                        last = vec.tensor_tensor(block_of(mem_lo), mem_raw[r, :, :], block_of(mem_hi), ALU.subtract)
                    last.then_inc(s_split, 1)

                def turned_lo(n, src, dst):
                    vec.wait_ge(s_thi, n + 1)
                    vec.tensor_tensor(dst, bank[n % 2][:, :], src, ALU.subtract).then_inc(s_tlo, 1)

                def turn_x(c, b):
                    turned_lo(number["x", c, b], xt_hi[:, c % 2, b, :], xt_lo[:, c % 2, b, :])

                def query(c, m):
                    u = 4 * c + m
                    if u == 0:
                        vec.wait_ge(s_whi, 1)
                        vec.tensor_tensor(wq_lo[:, :, :], raw[:, :, :], wq_hi[:, :, :], ALU.subtract).then_inc(s_split, 1)
                        bank_weights()
                        memories()
                    vec.wait_ge(s_qev, u + 1)
                    if c >= 2 and m == 0:
                        vec.wait_ge(s_m, 16 * (c - 1))
                    vec.scalar_tensor_tensor(sg[:, u % 2, :], ex[:, u % 2, :], 1.0, rl[:, u % 2, :], ALU.min, ALU.add)
                    vec.scalar_tensor_tensor(sg_hi[:, c % 2, m, :], ex[:, u % 2, :], 1.0, rl[:, u % 2, :],
                                             ALU.min, ALU.add).then_inc(s_sg, 1)
                    vec.wait_ge(s_sg, u + 1)
                    vec.tensor_tensor(sg_lo[:, c % 2, m, :], sg[:, u % 2, :], sg_hi[:, c % 2, m, :],
                                      ALU.subtract).then_inc(s_slo, 1)

                def weights(c):
                    vec.wait_ge(s_nb, 4 * (c + 1))
                    w = rw[:, c % 2, :, :]
                    vec.tensor_scalar(w, bank[7][:, 0:256].rearrange("p (j a) -> p j a", j=TC), EPS_MEM, None,
                                      ALU.max).then_inc(s_r, 1)
                    vec.wait_ge(s_r, c + 1)
                    vec.reciprocal(w, w).then_inc(s_rw, 1)
                    vec.wait_ge(s_rw, 2 * c + 1)
                    vec.tensor_tensor(w, w, bw[:, :, :, :].rearrange("p g n h -> p (g n h)").unsqueeze(1)
                                      .to_broadcast([P, TC, 64]), ALU.mult).then_inc(s_rw, 1)
                    vec.wait_ge(s_rw, 2 * c + 2)

                def read(v):
                    c, j, g = v // 16, v // G % TC, v % G
                    vec.wait_ge(s_m, v + 1)
                    if v >= 2:
                        vec.wait_ge(s_comb, v - 1)
                    vec.tensor_tensor(read_n[:, v % 2, :].rearrange("p (a e) -> p a e", e=DH),
                                      bank[4 + v % 2][:, :].rearrange("p (a e) -> p a e", e=DH),
                                      rw[:, c % 2, j, g * 16:g * 16 + 16].unsqueeze(2).to_broadcast([P, 16, DH]),
                                      ALU.mult).then_inc(s_rn, 1)

                def turn_comb(i):
                    if i == 0:
                        vec.wait_ge(s_whi, 2 + HG)
                        vec.tensor_tensor(wo_lo[:, :, :], raw[:, :, :], wo_hi[:, :, :], ALU.subtract).then_inc(s_split, 1)
                    turned_lo(number["comb", i], ct_hi[:, i % 2, :, :].rearrange("p b t -> p (b t)"),
                              ct_lo[:, i % 2, :, :].rearrange("p b t -> p (b t)"))

                def project(i):
                    vec.wait_ge(s_o, i + 1)
                    vec.tensor_tensor(k.x[:, i, :], bank[6][:, :], k.x[:, i, :], ALU.add).then_inc(s_res, 1)
                    vec.wait_ge(s_res, i + 1)
                    ln_stats(k, vec, i, s_stat, i)
                    if i >= TC:
                        normalise(i - TC)

                def normalise(i):
                    vec.wait_ge(s_rstd, i // TC + 1)
                    ln_apply(k, vec, i).then_inc(s_ln, 1)

                schedule(turn_x, query, idle, weights, read, turn_comb, project, late_query=True)
                for i in range(NT - TC, NT):
                    normalise(i)


FLOOR = -0.498046875


def no_work(h, p):
    pass


def three_stages(eng, n, first, second, third, ahead=no_work, between=no_work, prepare=no_work, unroll=2):
    def step(g):
        for stage, item in ((ahead, g + 3), (first, g + 1), (between, g - 1), (prepare, g + 1), (second, g), (third, g - 1)):
            if 0 <= item < n:
                stage(item // unroll, item % unroll)

    rounds = (n - 4) // unroll
    for g in range(-3, unroll + 1):
        step(g)
    with eng.Fori(1, rounds) as i:
        for q in range(unroll):
            at = lambda stage, item: stage(i + item // unroll, item % unroll)
            at(ahead, q + 4)
            at(first, q + 2)
            at(between, q)
            at(prepare, q + 2)
            at(second, q + 1)
            at(third, q)
    for g in range(unroll * rounds + 1, n + 1):
        step(g)


def started(h):
    return not (isinstance(h, int) and h == 0)


E0 = 16
GRP = 256
NG0 = (2 * T) // GRP + E0 - 1
F0 = 256


def experts0_shared(k):
    nc, bank, io = k.nc, k.bank, k.io
    NS, FB = 2, F0 // P
    NU = NS * FB
    rt = lambda name, shape, dt=F32: k.sb("r0_" + name, shape, dt, k.moe_ctx)
    k.slot = rt("slot", [P, 2, NT], I32)
    k.weight = rt("weight", [P, 2, NT])
    k.token_of = rt("token_of", [P, 2 * NG0], I32)
    k.group_expert = rt("group_expert", [P, NG0], I32)
    k.group_bias = rt("group_bias", [P, NG0, 2 * FB])
    k.comb_aug = rt("comb_aug", [P, NT, E0 + NS])
    with ExitStack() as ctx:
        sb = lambda name, shape, dt=F32: k.sb("s0_" + name, shape, dt, ctx)
        wa_raw = sb("wa_raw", [P, KD, E0])
        wa_hi, wa_lo = sb("wa_hi", [P, KD, E0], F32R), sb("wa_lo", [P, KD, E0], F32R)
        sraw = sb("sraw", [P, 2, 2 * KD * F0])
        w1_hi, w1_lo = sb("w1_hi", [P, NS, 2, KD, F0], F32R), sb("w1_lo", [P, NS, 2, KD, F0], F32R)
        w2_hi, w2_lo = sb("w2_hi", [P, NU, D], F32R), sb("w2_lo", [P, NU, D], F32R)
        gb, ub = sb("gb", [P, NU]), sb("ub", [P, NU])
        rgb, rub = sb("rgb", [P, FB, E0]), sb("rub", [P, FB, E0])
        xt_hi, xt_lo = sb("xt_hi", [P, KD, T], F32R), sb("xt_lo", [P, KD, T], F32R)
        ge = sb("ge", [P, CH])
        hf = sb("hf", [P, 2, CH])
        h_hi, h_lo = sb("h_hi", [P, NU, CH], F32R), sb("h_lo", [P, NU, CH], F32R)
        aff = sb("aff", [P, NT, E0])
        top, arg = sb("top", [P, NT, 8]), sb("arg", [P, NT, 8], U32)
        argf = sb("argf", [P, 2, NT])
        onehot = sb("onehot", [P, 2, NT, E0])
        sel = sb("sel", [P, NT * E0], BF16)
        upper, ones = sb("upper", [P, P], BF16), sb("ones", [P, P], BF16)
        run_a, run_b = sb("run_a", [P, NT, E0]), sb("run_b", [P, NT, E0])
        tot = sb("tot", [P, NT, E0])
        cnt_i = sb("cnt_i", [P, E0], I32)
        groups, ends, start2 = sb("groups", [P, E0]), sb("ends", [P, E0]), sb("start2", [P, E0])
        ones16 = sb("ones16", [P, E0])
        prod = sb("prod", [P, 2 * NT, E0])
        posk, st, fl, pp = (sb(n, [P, 2 * NT]) for n in ("posk", "st", "fl", "pp"))
        fl_i = sb("fl_i", [P, 2 * NT], I32)
        rsum = sb("rsum", [P, NT])
        iota_e, iota_p, iota_s, iota_g = sb("iota_e", [P, E0]), sb("iota_p", [P, P]), sb("iota_s", [P, 2 * NG0]), sb("iota_g", [P, NG0])
        tok = sb("tok", [P, NT])
        at_row = sb("at_row", [P, 2, P], F32R)
        at_col = sb("at_col", [P, 2 * NT, 2 * NG0], F32R)
        by_group = lambda flat: flat[:, 0:NG0 * E0].rearrange("p (g e) -> p g e", e=E0)
        gsel = by_group(onehot[:, :, :, :].rearrange("p k t e -> p (k t e)"))
        gprod = by_group(prod[:, :, :].rearrange("p a e -> p (a e)"))
        gef = sb("gef", [P, NG0])

        s_wa, s_b = k.sem("s0_wa_loaded"), k.sem("s0_bias_loaded")
        s_w1, s_w2 = [k.sem(f"s0_w1_loaded{s}") for s in range(NS)], k.sem("s0_w2_loaded")
        s_whi, s_wlo = k.sem("s0_weight_hi"), k.sem("s0_weight_split")
        s_tps, s_thi, s_tlo = k.sem("s0_turned"), k.sem("s0_turned_hi"), k.sem("s0_turned_lo")
        s_lg, s_aff = k.sem("s0_logits"), k.sem("s0_affinity")
        s_gu, s_ge, s_h, s_hlo = k.sem("s0_gate_up"), k.sem("s0_gelu"), k.sem("s0_hidden"), k.sem("s0_hidden_split")
        s_hh = k.sem("s0_hidden_hi")
        s_dn, s_res = k.sem("s0_down"), k.sem("s0_residual")
        s_const = k.sem("s0_constants")
        s_r = k.sem("s0_route_chain")
        s_sel, s_pre, s_tab = k.sem("s0_selected"), k.sem("s0_prefix"), k.sem("s0_table")
        s_row, s_col = k.sem("s0_rows_made"), k.sem("s0_cols_made")
        s_rowfree = k.sem("s0_rows_used")

        with nc.Block() as block:
            @block.sync
            def _(sp):
                sp.dma_start(wa_raw[:, :, :], io["wa"].rearrange("(b p) n -> p b n", p=P)).then_inc(s_wa, 16)
                for s in range(NS):
                    for a, name in enumerate(("sg", "sw1")):
                        sp.dma_start(sraw[:, s, a * KD * F0:(a + 1) * KD * F0].rearrange("p (b n) -> p b n", b=KD),
                                     io[name][s].rearrange("(b p) n -> p b n", p=P)).then_inc(s_w1[s], 16)
                sp.dma_start(gb[:, :], io["sgb_t"]).then_inc(s_b, 16)
                sp.dma_start(ub[:, :], io["sb1_t"]).then_inc(s_b, 16)
                sp.dma_start(rgb[:, :, :].rearrange("p f e -> p (f e)"), io["rgb_t"]).then_inc(s_b, 16)
                sp.dma_start(rub[:, :, :].rearrange("p f e -> p (f e)"), io["rb1_t"]).then_inc(s_b, 16)
                sp.wait_ge(s_wlo, 2)
                sp.dma_start(sraw[:, 0, :].rearrange("p (u n) -> p u n", n=D),
                             io["sw2"].rearrange("s (f p) n -> p (s f) n", p=P)).then_inc(s_w2, 16)

            @block.gpsimd
            def _(pool):
                pool.memset(upper[:, :], 1.0).then_inc(s_const, 1)
                pool.memset(ones[:, :], 1.0).then_inc(s_const, 1)
                pool.memset(ones16[:, :], 1.0).then_inc(s_const, 1)
                pool.memset(k.comb_aug[:, :, :], 1.0).then_inc(s_const, 1)
                for a, n in ((iota_e, E0), (iota_p, P), (iota_s, 2 * NG0), (iota_g, NG0)):
                    pool.iota(a[:, :], [[1, n]], base=0, channel_multiplier=0,
                              allow_small_or_imprecise_dtypes=True).then_inc(s_const, 1)
                pool.iota(tok[:, :], [[P, NT]], base=0, channel_multiplier=1,
                          allow_small_or_imprecise_dtypes=True).then_inc(s_const, 1)
                pool.wait_ge(s_const, 9)
                pool.affine_select(out=upper[:, :], in_=upper[:, :], compare_op=ALU.is_gt, fill=0.0,
                                   base=0, pattern=[[1, P]], channel_multiplier=-1).then_inc(s_const, 1)

            @block.tensor
            def _(pe):
                def turn(c):
                    for b in range(KD):
                        n = 4 * c + b
                        if n >= 2:
                            pe.wait_ge(s_tlo, n - 1)
                        for j in range(TC):
                            mm = pe.transpose(bank[n % 2][:, j * P:(j + 1) * P], k.x[:, c * TC + j, b * P:(b + 1) * P], k.ident[:, :])
                        mm.then_inc(s_tps, 1)

                def logits(c):
                    pe.wait_ge(s_tlo, 4 * c + 4)
                    for i in range(4 * c, 4 * c + 4):
                        for b in range(KD):
                            t = slice(i * P, (i + 1) * P)
                            mm = mm3(pe, bank[7][:, i * E0:(i + 1) * E0], xt_hi[:, b, t], xt_lo[:, b, t],
                                     wa_hi[:, b, :], wa_lo[:, b, :], b == 0, b == KD - 1)
                    mm.then_inc(s_lg, 1)

                def gate_up(c, u):
                    n = c * NU + u
                    s, f = u // FB, u % FB
                    if c == 0:
                        pe.wait_ge(s_wlo, 2 + s)
                    if n >= 2:
                        pe.wait_ge(s_h, n - 1)
                    fs = slice(f * P, (f + 1) * P)
                    t = slice(c * CH, (c + 1) * CH)
                    for a in range(2):
                        for b in range(KD):
                            mm = mm3(pe, bank[2 + 2 * a + n % 2][:, :], w1_hi[:, s, a, b, fs], w1_lo[:, s, a, b, fs],
                                     xt_hi[:, b, t], xt_lo[:, b, t], b == 0, b == KD - 1)
                    mm.then_inc(s_gu, 1)

                def down(c):
                    if c == 0:
                        pe.wait_ge(s_wlo, 4)
                    pe.wait_ge(s_hlo, NU * c + NU)
                    for i in range(4 * c, 4 * c + 4):
                        if i:
                            pe.wait_ge(s_res, i)
                        t = slice(i % 4 * P, (i % 4 + 1) * P)
                        for u in range(NU):
                            mm = mm3(pe, bank[6][:, :], h_hi[:, u, t], h_lo[:, u, t], w2_hi[:, u, :], w2_lo[:, u, :],
                                     u == 0, u == NU - 1)
                        mm.then_inc(s_dn, 1)

                def prefix():
                    pe.wait_ge(s_sel, 1)
                    pe.matmul(bank[0][:, 0:256], upper[:, :], sel[:, :], start=True, stop=True)
                    pe.matmul(bank[0][:, 256:512], ones[:, :], sel[:, :], start=True, stop=True).then_inc(s_pre, 1)

                def table(n):
                    if n == 0:
                        pe.wait_ge(s_col, 1)
                    for a in range(n * 8, n * 8 + 8):
                        pe.wait_ge(s_row, a + 1)
                        pe.matmul(bank[1][:, 0:2 * NG0], at_row[:, a % 2, :], at_col[:, a, :], start=(a == 0),
                                  stop=(a == 2 * NT - 1)).then_inc(s_rowfree, 1)

                pe.wait_ge(s_const, 10)
                turn(0)
                pe.wait_ge(s_wlo, 1)
                for c in range(NC):
                    if c + 1 < NC:
                        turn(c + 1)
                    logits(c)
                gate_up(0, 0)
                gate_up(0, 1)
                prefix()
                gate_up(0, 2)
                gate_up(0, 3)
                for c in range(NC):
                    for u in range(NU):
                        if c + 1 < NC:
                            if u == 1:
                                down(c)
                            gate_up(c + 1, u)
                        if c == 1 and u:
                            table(u - 1)
                    if c == 1:
                        table(NU - 1)
                down(NC - 1)

            @block.scalar
            def _(act):
                act.wait_ge(s_wa, 16)
                act.activation(wa_hi[:, :, :], wa_raw[:, :, :], ACT.Copy).then_inc(s_whi, 1)
                for n in range(4 * NC):
                    act.wait_ge(s_tps, n + 1)
                    act.activation(xt_hi[:, n % 4, n // 4 * CH:(n // 4 + 1) * CH], bank[n % 2][:, :], ACT.Copy).then_inc(s_thi, 1)
                    if n in (3, 7):
                        s = n // 4
                        act.wait_ge(s_w1[s], 32)
                        act.activation(w1_hi[:, s, :, :, :].rearrange("p a b n -> p (a b n)"), sraw[:, s, :],
                                       ACT.Copy).then_inc(s_whi, 1)
                act.wait_ge(s_lg, NC)
                act.activation(aff[:, :, :].rearrange("p t e -> p (t e)"), bank[7][:, 0:NT * E0], ACT.Sigmoid).then_inc(s_aff, 1)
                act.wait_ge(s_w2, 16)
                act.activation(w2_hi[:, :, :].rearrange("p u n -> p (u n)"), sraw[:, 0, :], ACT.Copy).then_inc(s_whi, 1)
                act.wait_ge(s_b, 64)
                for n in range(NC * NU):
                    act.wait_ge(s_gu, n + 1)
                    if n:
                        act.wait_ge(s_h, n)
                    act.activation(ge[:, :], bank[2 + n % 2][:, :], ACT.Gelu, bias=gb[:, n % NU:n % NU + 1]).then_inc(s_ge, 1)

            @block.vector
            def _(vec):
                done = [0]

                def step(ins):
                    ins.then_inc(s_r, 1)
                    done[0] += 1

                def sync():
                    vec.wait_ge(s_r, done[0])

                def split_lo(n, lo, raw, hi):
                    vec.wait_ge(s_whi, n + 1)
                    vec.tensor_tensor(lo, raw, hi, ALU.subtract).then_inc(s_wlo, 1)

                def hidden(c, u):
                    n = c * NU + u
                    vec.wait_ge(s_ge, n + 1)
                    if c:
                        vec.wait_ge(s_dn, 4 * c)
                    up = bank[4 + n % 2][:, :]
                    if n >= 2:
                        vec.wait_ge(s_hlo, n - 1)
                    hfn = hf[:, n % 2, :]
                    vec.scalar_tensor_tensor(hfn, up, ub[:, u:u + 1], ge[:, :], ALU.add, ALU.mult).then_inc(s_h, 1)
                    vec.wait_ge(s_h, n + 1)
                    vec.tensor_copy(h_hi[:, u, :], hfn).then_inc(s_hh, 1)
                    vec.wait_ge(s_hh, n + 1)
                    vec.tensor_tensor(h_lo[:, u, :], hfn, h_hi[:, u, :], ALU.subtract).then_inc(s_hlo, 1)

                def residual(c):
                    for i in range(4 * c, 4 * c + 4):
                        vec.wait_ge(s_dn, i + 1)
                        vec.scalar_tensor_tensor(k.x[:, i, :], k.x[:, i, :], 2.0, bank[6][:, :], ALU.mult, ALU.add).then_inc(s_res, 1)

                def top2():
                    vec.wait_ge(s_aff, 1)
                    for i in range(NT):
                        step(vec.max(top[:, i, :], aff[:, i, :]))
                    sync()
                    for i in range(NT):
                        step(vec.max_index(arg[:, i, :], top[:, i, :], aff[:, i, :]))
                    sync()
                    step(vec.tensor_copy(argf[:, :, :], arg[:, :, 0:2].rearrange("p t k -> p k t")))
                    vec.wait_ge(s_const, 10)
                    sync()
                    step(vec.tensor_tensor(onehot[:, :, :, :].rearrange("p k t e -> p (k t) e"),
                                           iota_e[:, :].unsqueeze(1).to_broadcast([P, 2 * NT, E0]),
                                           argf[:, :, :].rearrange("p k t -> p (k t)").unsqueeze(2).to_broadcast([P, 2 * NT, E0]),
                                           ALU.is_equal))
                    sync()
                    vec.tensor_tensor(sel[:, :], onehot[:, 0, :, :].rearrange("p t e -> p (t e)"),
                                      onehot[:, 1, :, :].rearrange("p t e -> p (t e)"), ALU.add).then_inc(s_sel, 1)
                    step(vec.tensor_tensor(rsum[:, :], top[:, :, 0], top[:, :, 1], ALU.add))
                    sync()
                    step(vec.reciprocal(rsum[:, :], rsum[:, :]))
                    sync()
                    step(vec.tensor_tensor(k.weight[:, :, :], top[:, :, 0:2].rearrange("p t k -> p k t"),
                                           rsum[:, :].unsqueeze(1).to_broadcast([P, 2, NT]), ALU.mult))
                    sync()
                    step(vec.tensor_tensor(prod[:, :, :], onehot[:, :, :, :].rearrange("p k t e -> p (k t) e"),
                                           k.weight[:, :, :].rearrange("p k t -> p (k t)").unsqueeze(2).to_broadcast([P, 2 * NT, E0]),
                                           ALU.mult))
                    sync()
                    step(vec.tensor_tensor(k.comb_aug[:, :, 0:E0], prod[:, 0:NT, :], prod[:, NT:2 * NT, :], ALU.add))

                def positions():
                    vec.wait_ge(s_pre, 1)
                    flat = lambda a: a[:, :, :].rearrange("p t e -> p (t e)")
                    step(vec.tensor_copy(flat(tot), bank[0][:, 256:512]))
                    step(vec.tensor_copy(flat(run_a), bank[0][:, 256:512]))
                    a, b = run_a, run_b
                    for d in (1, 2, 4, 8):
                        sync()
                        step(vec.tensor_tensor(b[:, d:, :], a[:, d:, :], a[:, :NT - d, :], ALU.add))
                        step(vec.tensor_copy(b[:, :d, :], a[:, :d, :]))
                        a, b = b, a
                    sync()
                    step(vec.tensor_scalar(cnt_i[:, :], a[:, NT - 1, :], 1 / GRP, (GRP - 1) / GRP + FLOOR, ALU.mult, ALU.add))
                    step(vec.tensor_tensor(flat(b), flat(a), flat(tot), ALU.subtract))
                    sync()
                    step(vec.tensor_copy(groups[:, :], cnt_i[:, :]))
                    step(vec.tensor_tensor(flat(b), bank[0][:, 0:256], flat(b), ALU.add))
                    sync()
                    step(vec.tensor_tensor_scan(ends[:, :], ones16[:, :], groups[:, :], 0.0, ALU.mult, ALU.add))
                    step(vec.tensor_tensor(prod[:, :, :].rearrange("p (k t) e -> p k (t e)", k=2),
                                           onehot[:, :, :, :].rearrange("p k t e -> p k (t e)"),
                                           flat(b).unsqueeze(1).to_broadcast([P, 2, NT * E0]), ALU.mult))
                    sync()
                    step(vec.tensor_reduce(posk[:, :], prod[:, :, :], AX.X, ALU.add))
                    step(vec.tensor_tensor(start2[:, :], ends[:, :], groups[:, :], ALU.subtract))
                    sync()
                    step(vec.tensor_scalar(start2[:, :], start2[:, :], float(GRP // P), None, ALU.mult))
                    step(vec.tensor_scalar(fl_i[:, :], posk[:, :], 1 / P, FLOOR, ALU.mult, ALU.add))
                    sync()
                    step(vec.tensor_tensor(prod[:, :, :], onehot[:, :, :, :].rearrange("p k t e -> p (k t) e"),
                                           start2[:, :].unsqueeze(1).to_broadcast([P, 2 * NT, E0]), ALU.mult))
                    step(vec.tensor_copy(fl[:, :], fl_i[:, :]))
                    sync()
                    step(vec.tensor_reduce(st[:, :], prod[:, :, :], AX.X, ALU.add))
                    step(vec.scalar_tensor_tensor(pp[:, :], fl[:, :], -float(P), posk[:, :], ALU.mult, ALU.add))
                    sync()
                    step(vec.tensor_tensor(st[:, :], st[:, :], fl[:, :], ALU.add))
                    sync()
                    step(vec.scalar_tensor_tensor(k.slot[:, :, :].rearrange("p k t -> p (k t)"), st[:, :], float(P), pp[:, :],
                                                  ALU.mult, ALU.add))

                def columns():
                    step(vec.tensor_tensor(at_col[:, :, :], iota_s[:, :].unsqueeze(1).to_broadcast([P, 2 * NT, 2 * NG0]),
                                           st[:, :].unsqueeze(2).to_broadcast([P, 2 * NT, 2 * NG0]), ALU.is_equal))
                    sync()
                    for kk in range(2):
                        last = vec.tensor_tensor(at_col[:, kk * NT:(kk + 1) * NT, :], at_col[:, kk * NT:(kk + 1) * NT, :].bitcast(F32),
                                                 tok[:, :].unsqueeze(2).to_broadcast([P, NT, 2 * NG0]), ALU.mult)
                    last.then_inc(s_col, 1)

                def rows(n):
                    for a in range(8 * n, 8 * n + 8):
                        if a >= 2:
                            vec.wait_ge(s_rowfree, a - 1)
                        vec.tensor_scalar(at_row[:, a % 2, :], iota_p[:, :], pp[:, a:a + 1], None, ALU.is_equal).then_inc(s_row, 1)

                def group_tables():
                    step(vec.tensor_tensor(gsel[:, :, :], iota_g[:, :].unsqueeze(2).to_broadcast([P, NG0, E0]),
                                           ends[:, :].unsqueeze(1).to_broadcast([P, NG0, E0]), ALU.is_ge))
                    sync()
                    step(vec.tensor_reduce(gef[:, :], gsel[:, :, :], AX.X, ALU.add))
                    sync()
                    step(vec.tensor_scalar(gef[:, :], gef[:, :], float(E0 - 1), None, ALU.min))
                    sync()
                    step(vec.tensor_copy(k.group_expert[:, :], gef[:, :]))
                    step(vec.tensor_tensor(gsel[:, :, :], iota_e[:, :].unsqueeze(1).to_broadcast([P, NG0, E0]),
                                           gef[:, :].unsqueeze(2).to_broadcast([P, NG0, E0]), ALU.is_equal))
                    vec.wait_ge(s_b, 64)
                    for a, table in enumerate((rgb, rub)):
                        for f in range(FB):
                            sync()
                            step(vec.tensor_tensor(gprod[:, :, :], gsel[:, :, :], table[:, f, :].unsqueeze(1).to_broadcast([P, NG0, E0]),
                                                   ALU.mult))
                            sync()
                            step(vec.tensor_reduce(k.group_bias[:, :, 2 * a + f], gprod[:, :, :], AX.X, ALU.add))

                split_lo(0, wa_lo[:, :, :], wa_raw[:, :, :], wa_hi[:, :, :])
                for n in range(4 * NC):
                    vec.wait_ge(s_thi, n + 1)
                    t = slice(n // 4 * CH, (n // 4 + 1) * CH)
                    vec.tensor_tensor(xt_lo[:, n % 4, t], bank[n % 2][:, :], xt_hi[:, n % 4, t], ALU.subtract).then_inc(s_tlo, 1)
                    if n in (7, 11):
                        s = (n - 7) // 4
                        split_lo(1 + s, w1_lo[:, s, :, :, :].rearrange("p a b n -> p (a b n)"), sraw[:, s, :],
                                 w1_hi[:, s, :, :, :].rearrange("p a b n -> p (a b n)"))
                top2()
                vec.wait_ge(s_b, 64)
                hidden(0, 0)
                split_lo(3, w2_lo[:, :, :].rearrange("p u n -> p (u n)"), sraw[:, 0, :], w2_hi[:, :, :].rearrange("p u n -> p (u n)"))
                hidden(0, 1)
                positions()
                hidden(0, 2)
                columns()
                hidden(0, 3)
                for c in range(NC):
                    for u in range(NU):
                        if c + 1 < NC:
                            if u == 0:
                                residual(c)
                            hidden(c + 1, u)
                        if c == 1:
                            rows(u)
                    if c == 1:
                        vec.wait_ge(s_rowfree, 2 * NT)
                        step(vec.tensor_copy(k.token_of[:, :], bank[1][:, 0:2 * NG0]))
                    if c == 2:
                        group_tables()
                residual(NC - 1)


def experts0_routed(k):
    nc, bank, io = k.nc, k.bank, k.io
    FB, S = F0 // P, GRP // P
    W = KD * F0
    with ExitStack() as ctx:
        sb = lambda name, shape, dt=F32: k.sb("e0_" + name, shape, dt, ctx)
        raw = [sb(f"raw{p}", [P, 3 * W]) for p in range(2)]
        w_hi = [sb(f"w_hi{p}", [P, 3 * W], F32R) for p in range(2)]
        w_lo = [sb(f"w_lo{p}", [P, 3 * W], F32R) for p in range(2)]
        index = [sb(f"index{p}", [P, S], I32) for p in range(2)]
        bias = [sb(f"bias{p}", [P, 2 * FB]) for p in range(2)]
        xg = [sb(f"xg{p}", [P, S, D]) for p in range(2)]
        xt_hi = [sb(f"xt_hi{p}", [P, KD, GRP], F32R) for p in range(2)]
        xt_lo = [sb(f"xt_lo{p}", [P, KD, GRP], F32R) for p in range(2)]
        ge = [sb(f"ge{p}", [P, FB, GRP]) for p in range(2)]
        hf = [sb(f"hf{p}", [P, FB, GRP]) for p in range(2)]
        h_hi = [sb(f"h_hi{p}", [P, FB, GRP], F32R) for p in range(2)]
        h_lo = [sb(f"h_lo{p}", [P, FB, GRP], F32R) for p in range(2)]
        y = [sb(f"y{p}", [P, S, D]) for p in range(2)]

        two = lambda name: [k.sem(f"e0_{name}{p}") for p in range(2)]
        s_w, s_v, s_g, s_y = two("gate_up_loaded"), two("down_loaded"), two("rows_gathered"), two("results_stored")
        s_go = k.sem("e0_index_seen")
        s_ix, s_bias = k.sem("e0_index"), k.sem("e0_bias")
        s_whi, s_wlo = k.sem("e0_gate_up_hi"), k.sem("e0_gate_up_lo")
        s_vhi, s_vlo = k.sem("e0_down_hi"), k.sem("e0_down_lo")
        s_tps, s_thi, s_tlo = k.sem("e0_turned"), k.sem("e0_turned_hi"), k.sem("e0_turned_lo")
        s_gu, s_ge, s_h, s_hh, s_hlo = (k.sem("e0_" + n) for n in ("gate_up", "gelu", "hidden", "hidden_hi", "hidden_lo"))
        s_dn, s_ysb = k.sem("e0_down"), k.sem("e0_results")
        nothing = lambda h, p: None
        y_rows = k.y0.rearrange("(g s p) d -> g p s d", p=P, s=S)

        with nc.Block() as block:
            @block.sync
            def _(sp):
                def load(h, p):
                    g = 2 * h + p
                    e = sp.value_load(k.group_expert[0:1, bass.ds(g, 1)], min_val=0, max_val=E0 - 1)
                    if started(h):
                        sp.wait_ge(s_wlo, g - 1)
                    for a, name in enumerate(("rg", "rw1")):
                        sp.dma_start(raw[p][:, a * W:(a + 1) * W].rearrange("p (b n) -> p b n", b=KD),
                                     io[name][bass.ds(e, 1)].rearrange("e (b p) n -> p (e b) n", p=P)).then_inc(s_w[p], 16)
                    if started(h):
                        sp.wait_ge(s_vlo, g - 1)
                    sp.dma_start(raw[p][:, 2 * W:].rearrange("p (f n) -> p f n", f=FB),
                                 io["rw2"][bass.ds(e, 1)].rearrange("e (f p) n -> p (e f) n", p=P)).then_inc(s_v[p], 16)

                three_stages(sp, NG0, load, nothing, nothing)

            @block.gpsimd
            def _(pool):
                def gather(h, p):
                    g = 2 * h + p
                    if started(h):
                        pool.wait_ge(s_g[p], 16 * S * h)
                        pool.wait_ge(s_tps, g - 1)
                    pool.tensor_copy(index[p][:, :], k.token_of[:, bass.ds(S * g, S)]).then_inc(s_ix, 1)
                    pool.wait_ge(s_ix, g + 1)
                    pool.sem_inc(s_go, 1)
                    for s in range(S):
                        pool.indirect_dma_start(xg[p][:, s, :], None, k.rows, bass.IndirectOffsetOnAxis(index[p][:, s:s + 1], 0)
                                                ).then_inc(s_g[p], 16)

                three_stages(pool, NG0, gather, nothing, nothing)

            @block.tensor
            def _(pe):
                def turn(h, p):
                    g = 2 * h + p
                    pe.wait_ge(s_g[p], 16 * S * (h + 1))
                    if started(h) or p:
                        pe.wait_ge(s_tlo, g)
                    for b in range(KD):
                        for s in range(S):
                            c = (b % 2 * S + s) * P
                            mm = pe.transpose(bank[b // 2][:, c:c + P], xg[p][:, s, b * P:(b + 1) * P], k.ident[:, :])
                    mm.then_inc(s_tps, 1)

                def gate_up(h, p):
                    g = 2 * h + p
                    pe.wait_ge(s_wlo, g + 1)
                    pe.wait_ge(s_tlo, g + 1)
                    if started(h):
                        pe.wait_ge(s_h, g - 1)
                    for a in range(2):
                        for f in range(FB):
                            for b in range(KD):
                                c = slice(a * W + b * F0 + f * P, a * W + b * F0 + f * P + P)
                                mm = mm3(pe, bank[2 + 2 * a + p][:, f * GRP:(f + 1) * GRP], w_hi[p][:, c], w_lo[p][:, c],
                                         xt_hi[p][:, b, :], xt_lo[p][:, b, :], b == 0, b == KD - 1)
                    mm.then_inc(s_gu, 1)

                def down(h, p):
                    g = 2 * h + p
                    pe.wait_ge(s_hlo, g + 1)
                    pe.wait_ge(s_vlo, g + 1)
                    if started(h) or p:
                        pe.wait_ge(s_ysb, g)
                    for s in range(S):
                        for f in range(FB):
                            t, c = slice(s * P, (s + 1) * P), slice(2 * W + f * D, 2 * W + (f + 1) * D)
                            mm = mm3(pe, bank[6 + s][:, :], h_hi[p][:, f, t], h_lo[p][:, f, t], w_hi[p][:, c], w_lo[p][:, c],
                                     f == 0, f == FB - 1)
                    mm.then_inc(s_dn, 1)

                three_stages(pe, NG0, turn, gate_up, down)

            @block.scalar
            def _(act):
                def split(h, p):
                    g = 2 * h + p
                    act.wait_ge(s_w[p], 32 * (h + 1))
                    if started(h):
                        act.wait_ge(s_gu, g - 1)
                    act.activation(w_hi[p][:, 0:2 * W], raw[p][:, 0:2 * W], ACT.Copy).then_inc(s_whi, 1)
                    act.wait_ge(s_tps, g + 1)
                    for q in range(2):
                        last = act.activation(xt_hi[p][:, 2 * q:2 * q + 2, :].rearrange("p b t -> p (b t)"), bank[q][:, :], ACT.Copy)
                    last.then_inc(s_thi, 1)

                def gelu(h, p):
                    g = 2 * h + p
                    act.wait_ge(s_v[p], 16 * (h + 1))
                    if started(h):
                        act.wait_ge(s_dn, g - 1)
                    act.activation(w_hi[p][:, 2 * W:], raw[p][:, 2 * W:], ACT.Copy).then_inc(s_vhi, 1)
                    act.wait_ge(s_gu, g + 1)
                    act.wait_ge(s_bias, g + 1)
                    if started(h):
                        act.wait_ge(s_h, g - 1)
                    for f in range(FB):
                        last = act.activation(ge[p][:, f, :], bank[2 + p][:, f * GRP:(f + 1) * GRP], ACT.Gelu, bias=bias[p][:, f:f + 1])
                    last.then_inc(s_ge, 1)

                def results(h, p):
                    g = 2 * h + p
                    act.wait_ge(s_dn, g + 1)
                    if started(h):
                        act.wait_ge(s_y[p], 16 * h)
                    for s in range(S):
                        last = act.activation(y[p][:, s, :], bank[6 + s][:, :], ACT.Copy)
                    last.then_inc(s_ysb, 1)
                    act.wait_ge(s_ysb, g + 1)
                    act.dma_start(y_rows[bass.ds(g, 1)].rearrange("g p s d -> p (g s) d"), y[p][:, :, :]).then_inc(s_y[p], 16)

                three_stages(act, NG0, split, gelu, results)
                act.wait_ge(s_y[0], 16 * ((NG0 + 1) // 2))
                act.wait_ge(s_y[1], 16 * (NG0 // 2))

            @block.vector
            def _(vec):
                def split(h, p):
                    g = 2 * h + p
                    if started(h):
                        vec.wait_ge(s_h, g - 1)
                    vec.tensor_copy(bias[p][:, :], k.group_bias[:, bass.ds(g, 1), :].rearrange("p g a -> p (g a)")).then_inc(s_bias, 1)
                    vec.wait_ge(s_whi, g + 1)
                    vec.tensor_tensor(w_lo[p][:, 0:2 * W], raw[p][:, 0:2 * W], w_hi[p][:, 0:2 * W], ALU.subtract).then_inc(s_wlo, 1)
                    vec.wait_ge(s_thi, g + 1)
                    for q in range(2):
                        part = lambda a: a[p][:, 2 * q:2 * q + 2, :].rearrange("p b t -> p (b t)")
                        last = vec.tensor_tensor(part(xt_lo), bank[q][:, :], part(xt_hi), ALU.subtract)
                    last.then_inc(s_tlo, 1)

                def hidden(h, p):
                    g = 2 * h + p
                    vec.wait_ge(s_vhi, g + 1)
                    vec.tensor_tensor(w_lo[p][:, 2 * W:], raw[p][:, 2 * W:], w_hi[p][:, 2 * W:], ALU.subtract).then_inc(s_vlo, 1)
                    vec.wait_ge(s_ge, g + 1)
                    if started(h):
                        vec.wait_ge(s_hlo, g - 1)
                    for f in range(FB):
                        last = vec.scalar_tensor_tensor(hf[p][:, f, :], bank[4 + p][:, f * GRP:(f + 1) * GRP],
                                                        bias[p][:, FB + f:FB + f + 1], ge[p][:, f, :], ALU.add, ALU.mult)
                    last.then_inc(s_h, 1)
                    vec.wait_ge(s_h, g + 1)
                    if started(h):
                        vec.wait_ge(s_dn, g - 1)
                    vec.tensor_copy(h_hi[p][:, :, :], hf[p][:, :, :]).then_inc(s_hh, 1)
                    vec.wait_ge(s_hh, g + 1)
                    vec.tensor_tensor(h_lo[p][:, :, :], hf[p][:, :, :], h_hi[p][:, :, :], ALU.subtract).then_inc(s_hlo, 1)

                three_stages(vec, NG0, split, hidden, nothing)


def combine0(k):
    nc, bank, io = k.nc, k.bank, k.io
    EA = E0 + 2
    with ExitStack() as ctx:
        sb = lambda name, shape, dt=F32: k.sb("c0_" + name, shape, dt, ctx)
        b2 = sb("b2", [EA, D])
        comb_t = sb("comb_t", [EA, 2, P])
        yg = [sb(f"yg{n}", [P, 2, D]) for n in range(4)]
        s_b2 = k.sem("c0_b2_loaded")
        s_g = [k.sem(f"c0_gathered{n}") for n in range(4)]
        s_ct, s_cts, s_bt, s_sum = (k.sem("c0_" + n) for n in ("weights_turned", "weights_copied", "bias_term", "summed"))
        s_used = k.sem("c0_gathered_used")
        s_first = k.sem("c0_first_added")
        s_stat, s_var, s_rstd, s_ln = (k.sem("c0_" + n) for n in ("stats", "var", "rstd", "normed"))
        with nc.Block() as block:
            @block.sync
            def _(sp):
                sp.dma_start(b2[:, :], io["b2"]).then_inc(s_b2, 16)

            @block.gpsimd
            def _(pool):
                def rstd(c):
                    pool.wait_ge(s_stat, 2 * TC * (c + 1))
                    ln_rstd(k, pool, c * TC, TC, s_var, s_rstd, c)

                for i in range(NT):
                    if i >= 4:
                        pool.wait_ge(s_used, i - 3)
                    for kk in range(2):
                        pool.indirect_dma_start(yg[i % 4][:, kk, :], None, k.y0, bass.IndirectOffsetOnAxis(k.slot[:, kk, i:i + 1], 0)
                                                ).then_inc(s_g[i % 4], 16)
                    if i >= 7 and i % 4 == 3:
                        rstd(i // 4 - 1)
                rstd(NC - 1)

            @block.tensor
            def _(pe):
                pe.wait_ge(s_b2, 16)
                for i in range(NT):
                    if i >= 2:
                        pe.wait_ge(s_cts, i - 1)
                        pe.wait_ge(s_sum, i - 1)
                    pe.transpose(bank[i % 2][0:EA, 0:P], k.comb_aug[:, i, :], k.ident[:, :]).then_inc(s_ct, 1)
                    pe.wait_ge(s_cts, i + 1)
                    pe.matmul(bank[2 + i % 2][:, :], comb_t[:, i % 2, :], b2[:, :], start=True, stop=True).then_inc(s_bt, 1)

            @block.scalar
            def _(act):
                for i in range(NT):
                    act.wait_ge(s_ct, i + 1)
                    if i >= 2:
                        act.wait_ge(s_bt, i - 1)
                    act.activation(comb_t[:, i % 2, :], bank[i % 2][0:EA, 0:P], ACT.Copy).then_inc(s_cts, 1)

            @block.vector
            def _(vec):
                def apply(c):
                    vec.wait_ge(s_rstd, c + 1)
                    for i in range(c * TC, c * TC + TC):
                        ln_apply(k, vec, i).then_inc(s_ln, 1)

                for i in range(NT):
                    xi = k.x[:, i, :]
                    vec.wait_ge(s_bt, i + 1)
                    vec.tensor_tensor(xi, bank[2 + i % 2][:, :], xi, ALU.add).then_inc(s_sum, 1)
                    vec.wait_ge(s_g[i % 4], 32 * (i // 4 + 1))
                    vec.wait_ge(s_sum, i + 1)
                    vec.scalar_tensor_tensor(xi, yg[i % 4][:, 0, :], k.weight[:, 0, i:i + 1], xi, ALU.mult, ALU.add).then_inc(s_first, 1)
                    vec.wait_ge(s_first, i + 1)
                    vec.scalar_tensor_tensor(xi, yg[i % 4][:, 1, :], k.weight[:, 1, i:i + 1], xi, ALU.mult, ALU.add).then_inc(s_used, 1)
                    vec.wait_ge(s_used, i + 1)
                    ln_stats(k, vec, i, s_stat, i)
                    if i >= 7 and i % 4 == 3:
                        apply(i // 4 - 1)
                apply(NC - 1)


H1, DH1, FM = 16, 32, 64
NP = H1 // 2
VA = 2 * (DH1 + 1)


def attention1(k):
    with ExitStack() as ctx:
        xt = tuple(k.sb("a1_xt_" + n, [P, KD, T], F32R, ctx) for n in ("hi", "lo"))
        sb = lambda name, shape, dt=F32: k.sb("a1_" + name, shape, dt, ctx)
        w = {"fw1_hi": sb("fw1_hi", [P, 4 * FM], F32R), "fw1_lo": sb("fw1_lo", [P, 4 * FM], F32R),
             "kv": sb("kv", [P, NP, VA]), "vsum": sb("vsum", [P, NP * VA]),
             "m_hi": sb("m_hi", [P, NP, VA], F32R), "m_lo": sb("m_lo", [P, NP, VA], F32R),
             "cq": sb("cq", [P, NP * VA])}
        attention1_keys(k, xt, w)
        attention1_memory(k, w)
        attention1_queries(k, xt, w)


def attention1_keys(k, xt, w):
    nc, bank, io = k.nc, k.bank, k.io
    xt_hi, xt_lo = xt
    fw1_hi, fw1_lo, kv, vsum = w["fw1_hi"], w["fw1_lo"], w["kv"], w["vsum"]
    CK, TK = 2 * P, 2
    with ExitStack() as ctx:
        sb = lambda name, shape, dt=F32: k.sb("k1_" + name, shape, dt, ctx)
        raw = sb("raw", [P, KD, D])
        kw_hi, kw_lo = sb("kw_hi", [P, KD, D], F32R), sb("kw_lo", [P, KD, D], F32R)
        vw_hi, vw_lo = sb("vw_hi", [P, KD, D], F32R), sb("vw_lo", [P, KD, D], F32R)
        fw1_raw = sb("fw1_raw", [P, FM])
        kb = sb("kb", [P, KD])
        vb = sb("vb", [P, D])
        fb1 = sb("fb1", [2, FM])
        part = sb("part", [2, 1])
        rest = sb("rest", [2, 1])
        fb_hi, fb_lo = sb("fb_hi", [2, FM], F32R), sb("fb_lo", [2, FM])
        fb_hl = sb("fb_hl", [2, 4, FM], F32R)
        ones_f, ones2 = sb("ones_f", [2, P]), sb("ones2", [2, P], F32R)
        k_hi, k_lo = sb("k_hi", [P, 2, KD, CK], F32R), sb("k_lo", [P, 2, KD, CK], F32R)
        vf = sb("vf", [P, 2, NP * VA])
        v_hi, v_lo = sb("v_hi", [P, 2, NP * VA], F32R), sb("v_lo", [P, 2, NP * VA], F32R)
        ex, gf = sb("ex", [P, 2, CH]), sb("gf", [P, 2, CH])
        g_hi, g_lo = sb("g_hi", [P, 2, 2 * CH], F32R), sb("g_lo", [P, 2, 2 * CH], F32R)

        sem = lambda n: k.sem("k1_" + n)
        s_kw, s_vw, s_fw, s_kb, s_vb, s_fb = (sem(n) for n in ("kw_loaded", "vw_loaded", "fw1_loaded", "kb_loaded", "vb_loaded", "fb1_loaded"))
        s_zero, s_whi, s_wlo = sem("zeroed"), sem("weight_hi"), sem("weight_split")
        s_c = sem("fb1_chain")
        s_tps, s_thi, s_tlo = sem("turned"), sem("turned_hi"), sem("turned_lo")
        s_k, s_khi, s_klo = sem("keys"), sem("keys_hi"), sem("keys_split")
        s_v, s_vf, s_vhi, s_vlo, s_vs = sem("values"), sem("values_read"), sem("values_hi"), sem("values_lo"), sem("values_summed")
        s_g, s_gev, s_gf, s_ghi, s_glo = sem("features"), sem("features_read"), sem("features_made"), sem("features_hi"), sem("features_lo")
        s_kv, s_out = sem("kv_added"), sem("kv_copied")
        heads = lambda a: a.rearrange("p (h e) -> p h e", e=DH1 + 1)

        def schedule(turn, keys, tile, before_tile=lambda i: None, after_tile=lambda i: None):
            for n in range(4):
                turn(n)
            keys(0)
            keys(1)
            for i in range(NT):
                if i + 4 < NT:
                    turn(i + 4)
                if i + 2 < NT:
                    keys(i + 2)
                if i:
                    before_tile(i - 1)
                tile(i)
                if i:
                    after_tile(i - 1)
            before_tile(NT - 1)
            after_tile(NT - 1)

        with nc.Block() as block:
            @block.sync
            def _(sp):
                sp.dma_start(raw[:, :, :], io["kw"].rearrange("(b p) n -> p b n", p=P)).then_inc(s_kw, 16)
                for h in range(4):
                    sp.dma_start(fw1_raw[h * DH1:(h + 1) * DH1, :], io["fw1"]).then_inc(s_fw, 16)
                sp.dma_start(kb[:, :], io["kb_t"]).then_inc(s_kb, 16)
                sp.dma_start(vb[:, :], io["vb"].partition_broadcast(P)).then_inc(s_vb, 16)
                sp.dma_start(fb1[:, :], io["fb1"].partition_broadcast(2)).then_inc(s_fb, 16)
                sp.wait_ge(s_wlo, 1)
                sp.dma_start(raw[:, :, :], io["vw"].rearrange("(b p) n -> p b n", p=P)).then_inc(s_vw, 16)

            @block.gpsimd
            def _(pool):
                pool.memset(fw1_hi[:, :].bitcast(F32), 0.0).then_inc(s_zero, 1)
                pool.memset(fw1_lo[:, :].bitcast(F32), 0.0).then_inc(s_zero, 1)
                pool.memset(part[:, :], 0.0).then_inc(s_zero, 1)
                pool.memset(rest[:, :], 1.0).then_inc(s_zero, 1)
                pool.memset(ones_f[:, :], 1.0).then_inc(s_zero, 1)
                pool.memset(vf[:, :, :], 1.0).then_inc(s_zero, 1)
                pool.memset(kv[:, :, :], 0.0).then_inc(s_zero, 1)
                pool.memset(vsum[:, :], 0.0).then_inc(s_zero, 1)
                pool.wait_ge(s_zero, 8)
                pool.memset(part[0:1, :], 1.0).then_inc(s_zero, 1)
                pool.memset(rest[0:1, :], 0.0).then_inc(s_zero, 1)

                def tile(i):
                    pool.wait_ge(s_vf, i + 1)
                    if i:
                        pool.wait_ge(s_vs, i)
                    pool.tensor_tensor(vsum[:, :], vsum[:, :], vf[:, i % 2, :], ALU.add).then_inc(s_vs, 1)

                def tile_end(i):
                    for n in (2 * i, 2 * i + 1):
                        pool.wait_ge(s_ghi, n + 1)
                        part_of = slice((n % 2) * CH, (n % 2 + 1) * CH)
                        pool.tensor_tensor(g_lo[:, i % 2, part_of], gf[:, n % 2, :], g_hi[:, i % 2, part_of].bitcast(F32),
                                           ALU.subtract).then_inc(s_glo, 1)

                schedule(lambda n: None, lambda n: None, tile, tile_end)

            @block.tensor
            def _(pe):
                def turn(n):
                    c, half = n // 2, n % 2
                    if n >= 2:
                        pe.wait_ge(s_tlo, n - 1)
                    for b in range(2):
                        for j in range(TK):
                            o = (b * TK + j) * P
                            f = slice((2 * half + b) * P, (2 * half + b + 1) * P)
                            mm = pe.transpose(bank[n % 2][:, o:o + P], k.x[:, c * TK + j, f], k.ident[:, :])
                    mm.then_inc(s_tps, 1)

                def keys(n):
                    c, half = n // 2, n % 2
                    if n == 0:
                        pe.wait_ge(s_wlo, 1)
                    pe.wait_ge(s_tlo, 2 * c + 2)
                    if n:
                        pe.wait_ge(s_klo, n)
                    for q in range(2):
                        m = slice((2 * half + q) * P, (2 * half + q + 1) * P)
                        for b in range(KD):
                            mm = mm3(pe, bank[2][:, q * CK:(q + 1) * CK], kw_hi[:, b, m], kw_lo[:, b, m],
                                     xt_hi[:, b, c * CK:(c + 1) * CK], xt_lo[:, b, c * CK:(c + 1) * CK], b == 0, b == KD - 1)
                    mm.then_inc(s_k, 1)

                def sums(i):
                    pe.wait_ge(s_glo, 2 * i + 2)
                    pe.wait_ge(s_vlo, i + 1)
                    for q in range(NP):
                        o = bank[6 + q // 4][:, q % 4 * VA:(q % 4 + 1) * VA]
                        f, v = slice(q * P, (q + 1) * P), slice(q * VA, (q + 1) * VA)
                        first = i == 0 and q % 4 == 0
                        pe.matmul(o, g_hi[:, i % 2, f], v_hi[:, i % 2, v], start=first, stop=False, skip_group_check=True)
                        pe.matmul(o, g_hi[:, i % 2, f], v_lo[:, i % 2, v], start=False, stop=False, skip_group_check=True)
                        mm = pe.matmul(o, g_lo[:, i % 2, f], v_hi[:, i % 2, v], start=False, stop=i == NT - 1, skip_group_check=True)
                    mm.then_inc(s_kv, 1)

                def tile(i):
                    c, j = i // TK, i % TK
                    if i == 0:
                        pe.wait_ge(s_wlo, 3)
                    if j == 0:
                        pe.wait_ge(s_klo, 2 * c + 2)
                    if i:
                        pe.wait_ge(s_vf, i)
                    for b in range(KD):
                        mm = mm3(pe, bank[3][:, :], xt_hi[:, b, i * P:(i + 1) * P], xt_lo[:, b, i * P:(i + 1) * P],
                                 vw_hi[:, b, :], vw_lo[:, b, :], b == 0, b == KD - 1)
                    mm.then_inc(s_v, 1)
                    t = slice(j * P, (j + 1) * P)
                    for n in (2 * i, 2 * i + 1):
                        if i:
                            pe.wait_ge(s_gev, n - 1)
                        for a in range(2):
                            g = 2 * (n % 2) + a
                            o = bank[4 + n % 2][:, a * 256:(a + 1) * 256]
                            mm3(pe, o, k_hi[:, c % 2, g, t], k_lo[:, c % 2, g, t], fw1_hi[:, :], fw1_lo[:, :], True, False)
                            mm = pe.matmul(o, ones2[:, :], fb_hl[:, :, :].rearrange("p h f -> p (h f)"), start=False, stop=True)
                        mm.then_inc(s_g, 1)

                schedule(turn, keys, tile, after_tile=sums)

            @block.scalar
            def _(act):
                def weight(sem, dst):
                    act.wait_ge(sem, 16)
                    act.activation(dst[:, :, :], raw[:, :, :], ACT.Copy).then_inc(s_whi, 1)

                def turn(n):
                    c, half = n // 2, n % 2
                    act.wait_ge(s_tps, n + 1)
                    act.activation(xt_hi[:, 2 * half:2 * half + 2, c * CK:(c + 1) * CK], bank[n % 2][:, :].rearrange("p (b t) -> p b t", b=2),
                                   ACT.Copy).then_inc(s_thi, 1)
                    if n == 1:
                        weight(s_kw, kw_hi)
                        act.wait_ge(s_kb, 16)

                def keys(n):
                    c, half = n // 2, n % 2
                    act.wait_ge(s_k, n + 1)
                    if n % 2 == 0 and c >= 2:
                        act.wait_ge(s_g, 2 * TK * (c - 1))
                    for q in range(2):
                        m = 2 * half + q
                        act.activation(k_hi[:, c % 2, m, :], bank[2][:, q * CK:(q + 1) * CK], ACT.Identity, bias=kb[:, m:m + 1]).then_inc(s_khi, 1)
                    if n == 1:
                        weight(s_vw, vw_hi)

                def tile(i):
                    act.wait_ge(s_vf, i + 1)
                    if i >= 2:
                        act.wait_ge(s_kv, i - 1)
                    act.activation(v_hi[:, i % 2, :], vf[:, i % 2, :], ACT.Copy).then_inc(s_vhi, 1)
                    for n in (2 * i, 2 * i + 1):
                        act.wait_ge(s_g, n + 1)
                        if i:
                            act.wait_ge(s_gf, n - 1)
                            act.wait_ge(s_glo, n - 1)
                        act.activation(ex[:, n % 2, :], bank[4 + n % 2][:, :], ACT.Exp)
                        act.activation(gf[:, n % 2, :], bank[4 + n % 2][:, :], ACT.Relu).then_inc(s_gev, 1)

                def tile_end(i):
                    if i >= 2:
                        act.wait_ge(s_kv, i - 1)
                    for n in (2 * i, 2 * i + 1):
                        act.wait_ge(s_gf, n + 1)
                        act.activation(g_hi[:, i % 2, (n % 2) * CH:(n % 2 + 1) * CH], gf[:, n % 2, :], ACT.Copy).then_inc(s_ghi, 1)

                schedule(turn, keys, tile, tile_end)

            @block.vector
            def _(vec):
                def weight(n, raw_, hi, lo):
                    vec.wait_ge(s_whi, n)
                    vec.tensor_tensor(lo[:, :, :], raw_[:, :, :], hi[:, :, :], ALU.subtract).then_inc(s_wlo, 1)

                def feature_weights():
                    vec.wait_ge(s_fw, 64)
                    vec.wait_ge(s_zero, 10)
                    for h in range(4):
                        r, c = slice(h * DH1, (h + 1) * DH1), slice(h * FM, (h + 1) * FM)
                        vec.tensor_copy(fw1_hi[r, c], fw1_raw[r, :]).then_inc(s_c, 1)
                    vec.wait_ge(s_c, 4)
                    for h in range(4):
                        r, c = slice(h * DH1, (h + 1) * DH1), slice(h * FM, (h + 1) * FM)
                        vec.tensor_tensor(fw1_lo[r, c], fw1_raw[r, :], fw1_hi[r, c], ALU.subtract)
                    vec.wait_ge(s_fb, 16)
                    vec.tensor_copy(ones2[:, :], ones_f[:, :])
                    vec.tensor_copy(fb_hi[:, :], fb1[:, :]).then_inc(s_c, 1)
                    vec.wait_ge(s_c, 5)
                    vec.tensor_tensor(fb_lo[:, :], fb1[:, :], fb_hi[:, :], ALU.subtract).then_inc(s_c, 1)
                    vec.wait_ge(s_c, 6)
                    vec.tensor_scalar(fb_lo[:, :], fb_lo[:, :], rest[:, 0:1], None, ALU.mult).then_inc(s_c, 1)
                    vec.wait_ge(s_c, 7)
                    for h in range(4):
                        last = vec.scalar_tensor_tensor(fb_hl[:, h, :], fb_hi[:, :], part[:, 0:1], fb_lo[:, :], ALU.mult, ALU.add)
                    last.then_inc(s_wlo, 1)

                def turn(n):
                    c, half = n // 2, n % 2
                    vec.wait_ge(s_thi, n + 1)
                    part = lambda a: a[:, 2 * half:2 * half + 2, c * CK:(c + 1) * CK]
                    vec.tensor_tensor(part(xt_lo), bank[n % 2][:, :].rearrange("p (b t) -> p b t", b=2), part(xt_hi), ALU.subtract).then_inc(s_tlo, 1)
                    if n == 1:
                        weight(1, raw, kw_hi, kw_lo)

                def keys(n):
                    c, half = n // 2, n % 2
                    if n % 2 == 0 and c >= 2:
                        vec.wait_ge(s_g, 2 * TK * (c - 1))
                    vec.wait_ge(s_khi, 2 * n + 2)
                    for q in range(2):
                        m = 2 * half + q
                        last = vec.scalar_tensor_tensor(k_lo[:, c % 2, m, :], bank[2][:, q * CK:(q + 1) * CK], kb[:, m:m + 1], k_hi[:, c % 2, m, :],
                                                        ALU.add, ALU.subtract)
                    last.then_inc(s_klo, 1)
                    if n == 1:
                        feature_weights()
                        weight(2, raw, vw_hi, vw_lo)
                        vec.wait_ge(s_vb, 16)

                def tile(i):
                    vec.wait_ge(s_v, i + 1)
                    if i >= 2:
                        vec.wait_ge(s_vs, i - 1)
                        vec.wait_ge(s_vlo, i - 1)
                    vec.tensor_tensor(heads(vf[:, i % 2, :])[:, :, 0:DH1], bank[3][:, :].rearrange("p (h e) -> p h e", e=DH1),
                                      vb[:, :].rearrange("p (h e) -> p h e", e=DH1), ALU.add).then_inc(s_vf, 1)
                    vec.wait_ge(s_vhi, i + 1)
                    vec.tensor_tensor(v_lo[:, i % 2, :], vf[:, i % 2, :], v_hi[:, i % 2, :], ALU.subtract).then_inc(s_vlo, 1)
                    for n in (2 * i, 2 * i + 1):
                        vec.wait_ge(s_gev, n + 1)
                        vec.scalar_tensor_tensor(gf[:, n % 2, :], ex[:, n % 2, :], 1.0, gf[:, n % 2, :], ALU.min, ALU.add).then_inc(s_gf, 1)

                schedule(turn, keys, tile)
                vec.wait_ge(s_kv, NT)
                for a in range(2):
                    for h in range(2):
                        r, c = slice(h * FM, (h + 1) * FM), slice(h * (DH1 + 1), (h + 1) * (DH1 + 1))
                        vec.tensor_copy(kv[r, 4 * a:4 * a + 4, c],
                                        bank[6 + a][r, 0:4 * VA].rearrange("p (q v) -> p q v", v=VA)[:, :, c])


def attention1_memory(k, w):
    nc, bank, io = k.nc, k.bank, k.io
    kv, vsum = w["kv"], w["vsum"]
    HV = NP * VA // 2
    with ExitStack() as ctx:
        sb = lambda name, shape, dt=F32: k.sb("m1_" + name, shape, dt, ctx)
        fw2, fw2_t = sb("fw2", [P, P]), sb("fw2_t", [P, P])
        fb2, b = sb("fb2", [P, 1]), sb("b", [P, 1])
        ones, b_cols = sb("ones", [P, P]), sb("b_cols", [P, P])
        sv, kv2, mf = sb("sv", [P, 2, HV]), sb("kv2", [P, NP, VA]), sb("mf", [P, NP * VA])
        sem = lambda n: k.sem("m1_" + n)
        s_zero, s_ld, s_ps, s_b, s_sv, s_kv2, s_m, s_split = (sem(n) for n in
            ("zeroed", "loaded", "products", "bias_made", "value_sum", "kv2_made", "memory", "memory_split"))
        with nc.Block() as block:
            @block.gpsimd
            def _(pool):
                pool.memset(fw2[:, :], 0.0).then_inc(s_zero, 1)
                pool.memset(fw2_t[:, :], 0.0).then_inc(s_zero, 1)
                pool.memset(ones[:, :], 1.0).then_inc(s_zero, 1)
                pool.memset(kv2[:, :, :], 0.0).then_inc(s_zero, 1)

            @block.sync
            def _(sp):
                sp.wait_ge(s_zero, 2)
                for h in range(2):
                    r = slice(h * FM, (h + 1) * FM)
                    sp.dma_start(fw2[r, r], io["fw2"]).then_inc(s_ld, 16)
                    sp.dma_start(fw2_t[r, r], io["fw2_t"]).then_inc(s_ld, 16)
                    sp.dma_start(fb2[r, :], io["fb2"].rearrange("(f o) -> f o", o=1)).then_inc(s_ld, 16)

            @block.tensor
            def _(pe):
                pe.wait_ge(s_ld, 96)
                pe.wait_ge(s_zero, 4)
                flat = lambda a: a[:, :, :].rearrange("p q v -> p (q v)")
                pe.matmul(bank[6][:, 0:2], fw2[:, :], ones[:, 0:2], start=True, stop=True).then_inc(s_ps, 1)
                for a in range(2):
                    pe.matmul(bank[a][:, 0:HV], ones[:, :], vsum[:, a * HV:(a + 1) * HV], start=True, stop=True).then_inc(s_ps, 1)
                    pe.matmul(bank[2 + a][:, 0:HV], fw2[:, :], flat(kv)[:, a * HV:(a + 1) * HV], start=True, stop=True).then_inc(s_ps, 1)
                pe.wait_ge(s_kv2, 4)
                pe.wait_ge(s_b, 2)
                for a in range(2):
                    pe.matmul(bank[4 + a][:, 0:HV], fw2_t[:, :], flat(kv2)[:, a * HV:(a + 1) * HV], start=True, stop=True).then_inc(s_ps, 1)
                    pe.matmul(bank[6 + a][:, 0:HV], b_cols[:, :], flat(kv2)[:, a * HV:(a + 1) * HV], start=True, stop=True).then_inc(s_ps, 1)

            @block.vector
            def _(vec):
                vec.wait_ge(s_ps, 5)
                vec.tensor_tensor(b[:, :], fb2[:, :], bank[6][:, 0:1], ALU.subtract).then_inc(s_b, 1)
                for a in range(2):
                    vec.tensor_copy(sv[:, a, :], bank[a][:, 0:HV]).then_inc(s_sv, 1)
                vec.wait_ge(s_b, 1)
                vec.tensor_scalar(b_cols[:, :], ones[:, :], b[:, 0:1], None, ALU.mult).then_inc(s_b, 1)
                vec.wait_ge(s_sv, 2)
                for a in range(2):
                    for h in range(2):
                        r, c = slice(h * FM, (h + 1) * FM), slice(h * (DH1 + 1), (h + 1) * (DH1 + 1))
                        pairs = lambda t: t.rearrange("p (q v) -> p q v", v=VA)[:, :, c]
                        vec.scalar_tensor_tensor(kv2[r, 4 * a:4 * a + 4, c], pairs(sv[r, a, :]), b[r, 0:1],
                                                 pairs(bank[2 + a][r, 0:HV]), ALU.mult, ALU.add).then_inc(s_kv2, 1)
                vec.wait_ge(s_ps, 9)
                for a in range(2):
                    part = slice(a * HV, (a + 1) * HV)
                    vec.tensor_copy(mf[:, part], bank[4 + a][:, 0:HV]).then_inc(s_m, 1)
                    vec.tensor_copy(w["cq"][:, part], bank[6 + a][:, 0:HV]).then_inc(s_m, 1)
                vec.wait_ge(s_m, 4)
                vec.tensor_copy(w["m_hi"][:, :, :].rearrange("p q v -> p (q v)"), mf[:, :]).then_inc(s_split, 1)
                vec.wait_ge(s_split, 1)
                vec.tensor_tensor(w["m_lo"][:, :, :].rearrange("p q v -> p (q v)"), mf[:, :],
                                  w["m_hi"][:, :, :].rearrange("p q v -> p (q v)"), ALU.subtract)


def attention1_queries(k, xt, w):
    nc, bank, io = k.nc, k.bank, k.io
    xt_hi, xt_lo = xt
    fw1_hi, fw1_lo, m_hi, m_lo, cq = (w[n] for n in ("fw1_hi", "fw1_lo", "m_hi", "m_lo", "cq"))
    HV = NP * VA // 2
    CQ = 256
    NQ, TQ = T // CQ, CQ // P
    NU = NQ * KD
    with ExitStack() as ctx:
        sb = lambda name, shape, dt=F32: k.sb("q1_" + name, shape, dt, ctx)
        raw = sb("raw", [P, KD, D])
        qw_hi, qw_lo = sb("qw_hi", [P, KD, D], F32R), sb("qw_lo", [P, KD, D], F32R)
        ow_hi, ow_lo = sb("ow_hi", [P, KD, D], F32R), sb("ow_lo", [P, KD, D], F32R)
        qb, fb1, ob = sb("qb", [P, KD]), sb("fb1", [P, 1]), sb("ob", [P, D])
        q_hi, q_lo = sb("q_hi", [P, 2, CQ], F32R), sb("q_lo", [P, 2, CQ], F32R)
        ex, gf = sb("ex", [P, 2, 2 * CQ]), sb("gf", [P, 2, 2 * CQ])
        g_hi, g_lo = sb("g_hi", [P, 2, NP * CQ], F32R), sb("g_lo", [P, 2, NP * CQ], F32R)
        num = (w["kv"][:, :, :].rearrange("p q v -> p (q v)"), w["vsum"][:, :])
        den = sb("den", [P, 2, H1])
        at_hi, at_lo = sb("at_hi", [P, 2, D], F32R), sb("at_lo", [P, 2, D], F32R)
        attn = raw

        sem = lambda n: k.sem("q1_" + n)
        s_qw, s_ow, s_small = sem("qw_loaded"), sem("ow_loaded"), sem("biases_loaded")
        s_whi, s_wlo, s_ob = sem("weight_hi"), sem("weight_split"), sem("ob_added")
        s_q, s_qhi, s_qlo = sem("queries"), sem("queries_hi"), sem("queries_split")
        s_g, s_gev, s_gf, s_ghi, s_glo = sem("features"), sem("features_read"), sem("features_made"), sem("features_hi"), sem("features_lo")
        s_n, s_nev, s_den, s_at = sem("num"), sem("num_read"), sem("den"), sem("attn")
        s_tps, s_thi, s_tlo = sem("turned"), sem("turned_hi"), sem("turned_lo")
        s_o, s_res = sem("out"), sem("residual")
        s_stat, s_var, s_rstd, s_ln, s_st = sem("stats"), sem("var"), sem("rstd"), sem("normed"), sem("stored")

        def schedule(query, features, features_hi, numerator, turn, project):
            query(0)
            for u in range(NU + KD + 1):
                if u + 1 < NU:
                    query(u + 1)
                if u < NU:
                    features(u)
                if 1 <= u <= NU:
                    features_hi(u - 1)
                i = TQ * (u // KD - 1)
                work = {1: ((numerator, i),), 2: ((numerator, i + 1), (turn, i)),
                        3: ((project, i), (turn, i + 1)), 0: ((project, i - 1),)}[u % KD]
                for stage, tile in work:
                    if tile >= 0:
                        stage(tile)

        with nc.Block() as block:
            @block.sync
            def _(sp):
                sp.dma_start(raw[:, :, :], io["qw"].rearrange("(b p) n -> p b n", p=P)).then_inc(s_qw, 16)
                sp.dma_start(qb[:, :], io["qb_t"]).then_inc(s_small, 16)
                for h in range(2):
                    sp.dma_start(fb1[h * FM:(h + 1) * FM, :], io["fb1"].rearrange("(f o) -> f o", o=1)).then_inc(s_small, 16)
                sp.dma_start(ob[:, :], io["ob"].partition_broadcast(P)).then_inc(s_small, 16)
                sp.wait_ge(s_wlo, 1)
                sp.dma_start(raw[:, :, :], io["ow"].rearrange("(b p) n -> p b n", p=P)).then_inc(s_ow, 16)
                for c in range(NC):
                    sp.wait_ge(s_ln, TC * (c + 1))
                    sp.dma_start(k.rows.rearrange("(c j p) d -> c p j d", p=P, j=TC)[c],
                                 k.x[:, c * TC:(c + 1) * TC, :]).then_inc(s_st, 16)
                sp.wait_ge(s_st, 16 * NC)

            @block.gpsimd
            def _(pool):
                pool.wait_ge(s_small, 64)
                for i in range(NT):
                    pool.tensor_tensor(k.x[:, i, :], k.x[:, i, :], ob[:, :], ALU.add).then_inc(s_ob, 1)

                def features_lo(u):
                    c, m = u // KD, u % KD
                    f = slice(2 * m * CQ, (2 * m + 2) * CQ)
                    pool.wait_ge(s_ghi, u + 1)
                    pool.tensor_tensor(g_lo[:, c % 2, f], gf[:, u % 2, :], g_hi[:, c % 2, f].bitcast(F32), ALU.subtract).then_inc(s_glo, 1)

                def project(i):
                    if i % TC == TC - 1:
                        pool.wait_ge(s_stat, 2 * (i + 1))
                        ln_rstd(k, pool, i - TC + 1, TC, s_var, s_rstd, i // TC)

                idle = lambda n: None
                schedule(idle, idle, features_lo, idle, idle, project)

            @block.tensor
            def _(pe):
                def query(u):
                    c, m = u // KD, u % KD
                    t = slice(c * CQ, (c + 1) * CQ)
                    if u == 0:
                        pe.wait_ge(s_wlo, 1)
                    if u >= 2:
                        pe.wait_ge(s_qlo, u - 1)
                    for b in range(KD):
                        mm = mm3(pe, bank[u % 2][:, 0:CQ], qw_hi[:, b, m * P:(m + 1) * P], qw_lo[:, b, m * P:(m + 1) * P],
                                 xt_hi[:, b, t], xt_lo[:, b, t], b == 0, b == KD - 1)
                    mm.then_inc(s_q, 1)

                def features(u):
                    pe.wait_ge(s_qlo, u + 1)
                    if u >= 2:
                        pe.wait_ge(s_gev, u - 1)
                    for a in range(2):
                        f = slice(a * P, (a + 1) * P)
                        mm = mm3(pe, bank[2 + u % 2][:, a * CQ:(a + 1) * CQ], fw1_hi[:, f], fw1_lo[:, f], q_hi[:, u % 2, :], q_lo[:, u % 2, :],
                                 True, True)
                    mm.then_inc(s_g, 1)

                def numerator(i):
                    c = i // TQ
                    if i % TQ == 0:
                        pe.wait_ge(s_glo, KD * (c + 1))
                    if i:
                        pe.wait_ge(s_nev, i)
                    for q in range(NP):
                        t = slice(q * CQ + i % TQ * P, q * CQ + (i % TQ + 1) * P)
                        mm = mm3(pe, bank[4 + q // 4][:, q % 4 * VA:(q % 4 + 1) * VA], g_hi[:, c % 2, t], g_lo[:, c % 2, t],
                                 m_hi[:, q, :], m_lo[:, q, :], True, True)
                    mm.then_inc(s_n, 1)

                def turn(i):
                    pe.wait_ge(s_at, i + 1)
                    if i:
                        pe.wait_ge(s_tlo, i)
                    for b in range(KD):
                        mm = pe.transpose(bank[6][:, b * P:(b + 1) * P], attn[:, i % 2, b * P:(b + 1) * P], k.ident[:, :])
                    mm.then_inc(s_tps, 1)

                def project(i):
                    if i == 0:
                        pe.wait_ge(s_wlo, 2)
                    pe.wait_ge(s_tlo, i + 1)
                    if i:
                        pe.wait_ge(s_res, i)
                    for b in range(KD):
                        f = slice(b * P, (b + 1) * P)
                        mm = mm3(pe, bank[7][:, :], at_hi[:, i % 2, f], at_lo[:, i % 2, f], ow_hi[:, b, :], ow_lo[:, b, :],
                                 b == 0, b == KD - 1)
                    mm.then_inc(s_o, 1)

                schedule(query, features, lambda u: None, numerator, turn, project)

            @block.scalar
            def _(act):
                def query(u):
                    m = u % KD
                    act.wait_ge(s_q, u + 1)
                    if u >= 2:
                        act.wait_ge(s_g, u - 1)
                    act.activation(q_hi[:, u % 2, :], bank[u % 2][:, 0:CQ], ACT.Identity, bias=qb[:, m:m + 1]).then_inc(s_qhi, 1)

                def features(u):
                    act.wait_ge(s_g, u + 1)
                    if u >= 2:
                        act.wait_ge(s_gf, u - 1)
                        act.wait_ge(s_glo, u - 1)
                    act.activation(ex[:, u % 2, :], bank[2 + u % 2][:, :], ACT.Exp, bias=fb1[:, 0:1])
                    act.activation(gf[:, u % 2, :], bank[2 + u % 2][:, :], ACT.Relu, bias=fb1[:, 0:1]).then_inc(s_gev, 1)

                def features_hi(u):
                    c, m = u // KD, u % KD
                    act.wait_ge(s_gf, u + 1)
                    if c >= 2:
                        act.wait_ge(s_n, TQ * (c - 1))
                    act.activation(g_hi[:, c % 2, 2 * m * CQ:(2 * m + 2) * CQ], gf[:, u % 2, :], ACT.Copy).then_inc(s_ghi, 1)

                def turn(i):
                    act.wait_ge(s_tps, i + 1)
                    if i >= 2:
                        act.wait_ge(s_o, i - 1)
                    act.activation(at_hi[:, i % 2, :], bank[6][:, :], ACT.Copy).then_inc(s_thi, 1)

                def numerator(i):
                    if i == 0:
                        act.wait_ge(s_ow, 16)
                        act.activation(ow_hi[:, :, :], raw[:, :, :], ACT.Copy).then_inc(s_whi, 1)

                act.wait_ge(s_qw, 16)
                act.activation(qw_hi[:, :, :], raw[:, :, :], ACT.Copy).then_inc(s_whi, 1)
                act.wait_ge(s_small, 64)
                schedule(query, features, features_hi, numerator, turn, lambda i: None)

            @block.vector
            def _(vec):
                def query(u):
                    if u == 0:
                        vec.wait_ge(s_whi, 1)
                        vec.tensor_tensor(qw_lo[:, :, :], raw[:, :, :], qw_hi[:, :, :], ALU.subtract).then_inc(s_wlo, 1)
                    vec.wait_ge(s_qhi, u + 1)
                    if u >= 2:
                        vec.wait_ge(s_g, u - 1)
                    m = u % KD
                    vec.scalar_tensor_tensor(q_lo[:, u % 2, :], bank[u % 2][:, 0:CQ], qb[:, m:m + 1], q_hi[:, u % 2, :],
                                             ALU.add, ALU.subtract).then_inc(s_qlo, 1)

                def features(u):
                    vec.wait_ge(s_gev, u + 1)
                    vec.scalar_tensor_tensor(gf[:, u % 2, :], ex[:, u % 2, :], 1.0, gf[:, u % 2, :], ALU.min, ALU.add).then_inc(s_gf, 1)

                def divide(i):
                    if i == 0:
                        vec.wait_ge(s_whi, 2)
                        vec.tensor_tensor(ow_lo[:, :, :], raw[:, :, :], ow_hi[:, :, :], ALU.subtract).then_inc(s_wlo, 1)
                        vec.wait_ge(s_wlo, 2)
                        vec.wait_ge(s_ob, NT)
                    vec.wait_ge(s_n, i + 1)
                    s = i % 2
                    for a in range(2):
                        part = slice(a * HV, (a + 1) * HV)
                        vec.tensor_tensor(num[s][:, part], bank[4 + a][:, 0:HV], cq[:, part], ALU.add).then_inc(s_den, 1)
                    vec.wait_ge(s_den, 4 * i + 2)
                    nh = num[s].rearrange("p (h e) -> p h e", e=DH1 + 1)
                    vec.tensor_scalar(den[:, s, :], nh[:, :, DH1], 1e-6, None, ALU.max).then_inc(s_nev, 1)
                    vec.wait_ge(s_nev, i + 1)
                    vec.reciprocal(den[:, s, :], den[:, s, :]).then_inc(s_den, 2)
                    vec.wait_ge(s_den, 4 * i + 4)
                    if i >= 2:
                        vec.wait_ge(s_tps, i - 1)
                    vec.tensor_tensor(attn[:, s, :].rearrange("p (h e) -> p h e", e=DH1), nh[:, :, 0:DH1],
                                      den[:, s, :].unsqueeze(2).to_broadcast([P, H1, DH1]), ALU.mult).then_inc(s_at, 1)

                def split(i):
                    vec.wait_ge(s_thi, i + 1)
                    vec.tensor_tensor(at_lo[:, i % 2, :], bank[6][:, :], at_hi[:, i % 2, :], ALU.subtract).then_inc(s_tlo, 1)

                def residual(i):
                    vec.wait_ge(s_o, i + 1)
                    vec.tensor_tensor(k.x[:, i, :], bank[7][:, :], k.x[:, i, :], ALU.add).then_inc(s_res, 1)
                    vec.wait_ge(s_res, i + 1)
                    ln_stats(k, vec, i, s_stat, i)

                def apply(c):
                    vec.wait_ge(s_rstd, c + 1)
                    for i in range(c * TC, c * TC + TC):
                        ln_apply(k, vec, i).then_inc(s_ln, 1)

                def finish(i):
                    residual(i)
                    if i % TC == 1 and i > TC:
                        apply(i // TC - 1)

                schedule(query, features, lambda u: None, divide, split, finish)
                apply(NC - 1)


E1, K1, F1, CAP = 64, 6, 192, 96
G1, KG1 = 8, 4
HF1 = F1 // 2
ROUTED_SCALE = 2.5
BIG = 3e38


def experts1_shared(k):
    nc, bank, io = k.nc, k.bank, k.io
    EG = E1 // G1
    rt = lambda name, shape, dt=F32: k.sb("r1_" + name, shape, dt, k.moe_ctx)
    k.slot = rt("slot", [P, NT, K1], I32)
    k.weight = rt("weight", [P, NT, K1])
    k.token_of = rt("token_of", [CAP, E1], I32)
    with ExitStack() as ctx:
        sb = lambda name, shape, dt=F32: k.sb("s1_" + name, shape, dt, ctx)
        gw_raw = sb("gw_raw", [P, KD, E1])
        gw_hi, gw_lo = sb("gw_hi", [P, KD, E1], F32R), sb("gw_lo", [P, KD, E1], F32R)
        w1_raw, w2_raw = sb("w1_raw", [P, KD, 2 * F1]), sb("w2_raw", [HF1, 2, D])
        w1_hi, w1_lo = sb("w1_hi", [P, KD, 2 * F1], F32R), sb("w1_lo", [P, KD, 2 * F1], F32R)
        w2_hi, w2_lo = sb("w2_hi", [HF1, 2, D], F32R), sb("w2_lo", [HF1, 2, D], F32R)
        bias = sb("bias", [P, E1])
        xt_hi, xt_lo = sb("xt_hi", [P, KD, T], F32R), sb("xt_lo", [P, KD, T], F32R)
        si, up = sb("si", [HF1, CH]), sb("up", [HF1, CH])
        hf = sb("hf", [HF1, 2, CH])
        h_hi, h_lo = sb("h_hi", [HF1, 2, CH], F32R), sb("h_lo", [HF1, 2, CH], F32R)
        ys = sb("ys", [P, D])
        scores = sb("scores", [P, NT, E1])
        biased = sb("biased", [P, NT, E1])
        top_in_group = sb("top_in_group", [P, NT * G1, 8])
        gscore, rank = sb("gscore", [P, NT, G1]), sb("rank", [P, NT, G1])
        lower = sb("lower", [P, G1, G1])
        top, arg = sb("top", [P, NT, 8]), sb("arg", [P, NT, 8], U32)
        argf = sb("argf", [P, NT, K1])
        onehot = sb("onehot", [P, NT, K1, E1])
        prod = sb("prod", [P, NT // 2, K1, E1])
        sel = sb("sel", [P, NT * E1], BF16)
        upper, ones = sb("upper", [P, P], BF16), sb("ones", [P, P], BF16)
        tot, run_b = biased, scores
        run_a = top_in_group[:, :, :].rearrange("p (t g) e -> p t (g e)", g=G1)
        wsum = sb("wsum", [P, NT])
        posk, valid = sb("posk", [P, NT, K1]), sb("valid", [P, NT, K1])
        iota_e, iota_c = sb("iota_e", [P, E1]), sb("iota_c", [P, CAP])
        tok = sb("tok", [P, NT])
        at_row = sb("at_row", [P, 2, CAP], F32R)
        at_col = sb("at_col", [P, 2, K1, E1], F32R)

        sem = lambda n: k.sem("s1_" + n)
        s_gw, s_w1, s_w2, s_b = sem("gate_w_loaded"), sem("w1_loaded"), sem("w2_loaded"), sem("bias_loaded")
        s_whi, s_wlo = sem("weight_hi"), sem("weight_split")
        s_tps, s_thi, s_tlo = sem("turned"), sem("turned_hi"), sem("turned_lo")
        s_lg, s_sc = sem("logits"), sem("scores")
        s_gu, s_act, s_h, s_hh, s_hlo = sem("gate_up"), sem("gate_up_read"), sem("hidden"), sem("hidden_hi"), sem("hidden_split")
        s_dn, s_ys, s_res = sem("down"), sem("down_copied"), sem("residual")
        s_const, s_r = sem("constants"), sem("route_chain")
        s_sel, s_pre, s_tot = sem("selected"), sem("prefix"), sem("totals_copied")
        s_row, s_col, s_used = sem("rows_made"), sem("cols_made"), sem("rows_used")
        s_tab = sem("table_made")
        NU = 2 * NC

        def schedule(gate_up, down, ahead=0):
            gate_up(0)
            gate_up(1)
            for c in range(NC):
                if ahead and c + 1 < NC:
                    gate_up(2 * c + 2)
                down(c)
                for u in range(2 * c + 2 + ahead, min(2 * c + 4, NU)):
                    gate_up(u)

        with nc.Block() as block:
            @block.sync
            def _(sp):
                sp.dma_start(gw_raw[:, :, :], io["gate_w"].rearrange("(b p) n -> p b n", p=P)).then_inc(s_gw, 16)
                sp.dma_start(bias[:, :], io["bias"].partition_broadcast(P)).then_inc(s_b, 16)
                for a, name in enumerate(("ws_gate", "ws_up")):
                    sp.dma_start(w1_raw[:, :, a * F1:(a + 1) * F1], io[name].rearrange("(b p) n -> p b n", p=P)).then_inc(s_w1, 16)
                sp.dma_start(w2_raw[:, :, :], io["ws_down"].rearrange("(f p) n -> p f n", p=HF1)).then_inc(s_w2, 16)

            @block.gpsimd
            def _(pool):
                pool.memset(upper[:, :], 1.0).then_inc(s_const, 1)
                pool.memset(ones[:, :], 1.0).then_inc(s_const, 1)
                pool.memset(lower[:, :, :], 1.0).then_inc(s_const, 1)
                for a, n in ((iota_e, E1), (iota_c, CAP)):
                    pool.iota(a[:, :], [[1, n]], base=0, channel_multiplier=0,
                              allow_small_or_imprecise_dtypes=True).then_inc(s_const, 1)
                pool.iota(tok[:, :], [[P, NT]], base=0, channel_multiplier=1,
                          allow_small_or_imprecise_dtypes=True).then_inc(s_const, 1)
                pool.wait_ge(s_const, 6)
                pool.affine_select(out=upper[:, :], in_=upper[:, :], compare_op=ALU.is_gt, fill=0.0,
                                   base=0, pattern=[[1, P]], channel_multiplier=-1).then_inc(s_const, 1)
                pool.affine_select(out=lower[:, :, :], in_=lower[:, :, :], compare_op=ALU.is_gt, fill=0.0,
                                   base=0, pattern=[[1, G1], [-1, G1]], channel_multiplier=0).then_inc(s_const, 1)

                def gate_up(u):
                    if u >= 2:
                        pool.wait_ge(s_hlo, u - 1)
                    pool.wait_ge(s_act, u + 1)
                    pool.tensor_tensor(hf[:, u % 2, :], si[:, :], up[:, :], ALU.mult).then_inc(s_h, 1)
                    pool.wait_ge(s_hh, u + 1)
                    if u >= 2:
                        pool.wait_ge(s_dn, TC * (u // 2))
                    pool.tensor_tensor(h_lo[:, u % 2, :], hf[:, u % 2, :], h_hi[:, u % 2, :].bitcast(F32), ALU.subtract).then_inc(s_hlo, 1)

                def down(c):
                    for i in range(c * TC, c * TC + TC):
                        pool.wait_ge(s_ys, i + 1)
                        pool.tensor_tensor(k.x[:, i, :], ys[:, :], k.x[:, i, :], ALU.add).then_inc(s_res, 1)

                schedule(gate_up, down)

            @block.tensor
            def _(pe):
                def turn(c):
                    for b in range(KD):
                        n = 4 * c + b
                        if n >= 2:
                            pe.wait_ge(s_tlo, n - 1)
                        for j in range(TC):
                            mm = pe.transpose(bank[n % 2][:, j * P:(j + 1) * P], k.x[:, c * TC + j, b * P:(b + 1) * P], k.ident[:, :])
                        mm.then_inc(s_tps, 1)

                def logits(c):
                    pe.wait_ge(s_tlo, 4 * c + 4)
                    for i in range(4 * c, 4 * c + 4):
                        for b in range(KD):
                            t = slice(i * P, (i + 1) * P)
                            mm = mm3(pe, bank[6 + i // 8][:, i % 8 * E1:(i % 8 + 1) * E1], xt_hi[:, b, t], xt_lo[:, b, t],
                                     gw_hi[:, b, :], gw_lo[:, b, :], b == 0, b == KD - 1)
                    mm.then_inc(s_lg, 1)

                def gate_up(u):
                    c, f = u // 2, u % 2
                    if u == 0:
                        pe.wait_ge(s_wlo, 2)
                    if u >= 2:
                        pe.wait_ge(s_act, u - 1)
                    t = slice(c * CH, (c + 1) * CH)
                    for a in range(2):
                        fs = slice(a * F1 + f * HF1, a * F1 + (f + 1) * HF1)
                        for b in range(KD):
                            mm = mm3(pe, bank[2 + 2 * a + f][0:HF1, :], w1_hi[:, b, fs], w1_lo[:, b, fs],
                                     xt_hi[:, b, t], xt_lo[:, b, t], b == 0, b == KD - 1)
                    mm.then_inc(s_gu, 1)

                def down(c):
                    if c == 0:
                        pe.wait_ge(s_wlo, 3)
                        pe.wait_ge(s_sc, 2)
                    pe.wait_ge(s_hlo, 2 * c + 2)
                    for i in range(4 * c, 4 * c + 4):
                        if i:
                            pe.wait_ge(s_ys, i)
                        t = slice(i % 4 * P, (i % 4 + 1) * P)
                        for f in range(2):
                            mm = mm3(pe, bank[6][:, :], h_hi[:, f, t], h_lo[:, f, t], w2_hi[:, f, :], w2_lo[:, f, :],
                                     f == 0, f == 1)
                        mm.then_inc(s_dn, 1)
                    if c == NC - 2:
                        prefix()

                def prefix():
                    pe.wait_ge(s_sel, 1)
                    for a in range(2):
                        half = sel[:, a * 512:(a + 1) * 512]
                        if a:
                            pe.wait_ge(s_tot, 1)
                        pe.matmul(bank[7][:, :], ones[:, :], half, start=True, stop=True)
                        pe.matmul(bank[a][:, :], upper[:, :], half, start=True, stop=True).then_inc(s_pre, 1)

                def table():
                    pe.wait_ge(s_tot, 2)
                    for n in range(NT * K1):
                        if n % K1 == 0:
                            pe.wait_ge(s_col, n // K1 + 1)
                        pe.wait_ge(s_row, n + 1)
                        pe.matmul(bank[7][0:CAP, 0:E1], at_row[:, n % 2, :], at_col[:, n // K1 % 2, n % K1, :], start=(n == 0),
                                  stop=(n == NT * K1 - 1)).then_inc(s_used, 1)

                pe.wait_ge(s_const, 8)
                turn(0)
                pe.wait_ge(s_wlo, 1)
                for c in range(NC):
                    if c + 1 < NC:
                        turn(c + 1)
                    logits(c)
                schedule(gate_up, down, ahead=1)
                table()

            @block.scalar
            def _(act):
                act.wait_ge(s_gw, 16)
                act.activation(gw_hi[:, :, :], gw_raw[:, :, :], ACT.Copy).then_inc(s_whi, 1)
                for n in range(4 * NC):
                    act.wait_ge(s_tps, n + 1)
                    act.activation(xt_hi[:, n % 4, n // 4 * CH:(n // 4 + 1) * CH], bank[n % 2][:, :], ACT.Copy).then_inc(s_thi, 1)
                    if n == 3:
                        act.wait_ge(s_w1, 32)
                        act.activation(w1_hi[:, :, :], w1_raw[:, :, :], ACT.Copy).then_inc(s_whi, 1)
                    if n == 7:
                        act.wait_ge(s_w2, 16)
                        act.activation(w2_hi[:, :, :], w2_raw[:, :, :], ACT.Copy).then_inc(s_whi, 1)
                for a in range(2):
                    act.wait_ge(s_lg, 2 * a + 2)
                    act.activation(scores[:, 8 * a:8 * a + 8, :].rearrange("p t e -> p (t e)"), bank[6 + a][:, :], ACT.Sigmoid).then_inc(s_sc, 1)

                def gate_up(u):
                    act.wait_ge(s_gu, u + 1)
                    if u:
                        act.wait_ge(s_h, u)
                    act.activation(si[:, :], bank[2 + u % 2][0:HF1, :], ACT.Silu)
                    act.activation(up[:, :], bank[4 + u % 2][0:HF1, :], ACT.Copy).then_inc(s_act, 1)
                    act.wait_ge(s_h, u + 1)
                    if u >= 2:
                        act.wait_ge(s_dn, TC * (u // 2))
                    act.activation(h_hi[:, u % 2, :], hf[:, u % 2, :], ACT.Copy).then_inc(s_hh, 1)

                def down(c):
                    for i in range(c * TC, c * TC + TC):
                        act.wait_ge(s_dn, i + 1)
                        if i:
                            act.wait_ge(s_res, i)
                        act.activation(ys[:, :], bank[6][:, :], ACT.Copy).then_inc(s_ys, 1)

                schedule(gate_up, down)

            @block.vector
            def _(vec):
                done = [0]

                def step(ins):
                    ins.then_inc(s_r, 1)
                    done[0] += 1

                def sync():
                    vec.wait_ge(s_r, done[0])

                def split_lo(n, lo, raw, hi):
                    vec.wait_ge(s_whi, n + 1)
                    vec.tensor_tensor(lo, raw, hi, ALU.subtract).then_inc(s_wlo, 1)

                def choose():
                    vec.wait_ge(s_b, 16)
                    vec.wait_ge(s_sc, 2)
                    step(vec.tensor_tensor(biased[:, :, :], scores[:, :, :], bias[:, :].unsqueeze(1).to_broadcast([P, NT, E1]), ALU.add))
                    sync()
                    by_group = biased[:, :, :].rearrange("p t (g e) -> p (t g) e", g=G1)
                    for n in range(NT * G1):
                        last = vec.max(top_in_group[:, n, :], by_group[:, n, :])
                    step(last)
                    sync()
                    best = top_in_group[:, :, :].rearrange("p (t g) e -> p t g e", g=G1)
                    step(vec.tensor_tensor(gscore[:, :, :], best[:, :, :, 0], best[:, :, :, 1], ALU.add))
                    sync()
                    shape = [P, NT, G1, G1]
                    pairs = lambda n: prod[:, :, :, :].rearrange("p t k e -> p (t k e)")[:, n * NT * G1 * G1:(n + 1) * NT * G1 * G1].rearrange(
                        "p (t g h) -> p t g h", g=G1, h=G1)
                    mine = gscore[:, :, :].unsqueeze(3).to_broadcast(shape)
                    other = gscore[:, :, :].unsqueeze(2).to_broadcast(shape)
                    step(vec.tensor_tensor(pairs(0), other, mine, ALU.is_gt))
                    step(vec.tensor_tensor(pairs(1), other, mine, ALU.is_equal))
                    vec.wait_ge(s_const, 8)
                    sync()
                    step(vec.tensor_tensor(pairs(1), pairs(1), lower[:, :, :].unsqueeze(1).to_broadcast(shape), ALU.mult))
                    sync()
                    step(vec.tensor_tensor(pairs(0), pairs(0), pairs(1), ALU.add))
                    sync()
                    step(vec.tensor_reduce(rank[:, :, :], pairs(0), AX.X, ALU.add))
                    sync()
                    step(vec.tensor_scalar(rank[:, :, :], rank[:, :, :], float(KG1), -BIG, ALU.is_ge, ALU.mult))
                    sync()
                    step(vec.tensor_tensor(biased[:, :, :].rearrange("p t (g e) -> p t g e", g=G1),
                                           biased[:, :, :].rearrange("p t (g e) -> p t g e", g=G1),
                                           rank[:, :, :].unsqueeze(3).to_broadcast([P, NT, G1, EG]), ALU.add))
                    sync()
                    for i in range(NT):
                        step(vec.max(top[:, i, :], biased[:, i, :]))
                    sync()
                    for i in range(NT):
                        step(vec.max_index(arg[:, i, :], top[:, i, :], biased[:, i, :]))
                    sync()
                    step(vec.tensor_copy(argf[:, :, :], arg[:, :, 0:K1]))
                    sync()
                    step(vec.tensor_tensor(onehot[:, :, :, :], iota_e[:, :].unsqueeze(1).unsqueeze(1).to_broadcast([P, NT, K1, E1]),
                                           argf[:, :, :].unsqueeze(3).to_broadcast([P, NT, K1, E1]), ALU.is_equal))
                    sync()
                    with nc.allow_low_precision("counts of 0 or 1"):
                        vec.tensor_reduce(sel[:, :].rearrange("p (t e) -> p t e", e=E1), onehot[:, :, :, :].rearrange("p t k e -> p t e k"),
                                          AX.X, ALU.add).then_inc(s_sel, 1)
                    for half in range(2):
                        t = slice(half * NT // 2, (half + 1) * NT // 2)
                        sync()
                        step(vec.tensor_tensor(prod[:, :, :, :], onehot[:, t, :, :],
                                               scores[:, t, :].unsqueeze(2).to_broadcast([P, NT // 2, K1, E1]), ALU.mult))
                        sync()
                        step(vec.tensor_reduce(k.weight[:, t, :], prod[:, :, :, :], AX.X, ALU.add))
                    sync()
                    step(vec.tensor_reduce(wsum[:, :], k.weight[:, :, :], AX.X, ALU.add))
                    sync()
                    step(vec.reciprocal(wsum[:, :], wsum[:, :]))
                    sync()
                    step(vec.tensor_scalar(wsum[:, :], wsum[:, :], ROUTED_SCALE, None, ALU.mult))
                    sync()
                    step(vec.tensor_tensor(k.weight[:, :, :], k.weight[:, :, :], wsum[:, :].unsqueeze(2).to_broadcast([P, NT, K1]), ALU.mult))

                def positions():
                    for a in range(2):
                        t = slice(8 * a, 8 * a + 8)
                        vec.wait_ge(s_pre, a + 1)
                        whole = bank[7][:, :].rearrange("p (t e) -> p t e", e=E1)
                        step(vec.tensor_copy(run_a[:, t, :], whole))
                        vec.tensor_copy(tot[:, t, :], whole).then_inc(s_tot, 1)
                    a, b = run_a, run_b[:, :, :]
                    for d in (1, 2, 4, 8):
                        sync()
                        step(vec.tensor_tensor(b[:, d:, :], a[:, d:, :], a[:, :NT - d, :], ALU.add))
                        step(vec.tensor_copy(b[:, :d, :], a[:, :d, :]))
                        a, b = b, a
                    vec.wait_ge(s_tot, 2)
                    sync()
                    step(vec.tensor_tensor(b, a, tot[:, :, :], ALU.subtract))
                    sync()
                    for h in range(2):
                        t = slice(8 * h, 8 * h + 8)
                        step(vec.tensor_tensor(b[:, t, :], bank[h][:, :].rearrange("p (t e) -> p t e", e=E1), b[:, t, :], ALU.add))
                    for half in range(2):
                        t = slice(half * NT // 2, (half + 1) * NT // 2)
                        sync()
                        step(vec.tensor_tensor(prod[:, :, :, :], onehot[:, t, :, :],
                                               b[:, t, :].unsqueeze(2).to_broadcast([P, NT // 2, K1, E1]), ALU.mult))
                        sync()
                        step(vec.tensor_reduce(posk[:, t, :], prod[:, :, :, :], AX.X, ALU.add))
                    sync()
                    step(vec.tensor_scalar(valid[:, :, :], posk[:, :, :], float(CAP), None, ALU.is_lt))
                    step(vec.tensor_scalar(argf[:, :, :], argf[:, :, :], float(CAP), None, ALU.mult))
                    sync()
                    step(vec.tensor_tensor(k.weight[:, :, :], k.weight[:, :, :], valid[:, :, :], ALU.mult))
                    step(vec.scalar_tensor_tensor(k.slot[:, :, :], posk[:, :, :], float(CAP - 1), argf[:, :, :], ALU.min, ALU.add))

                def table():
                    for i in range(NT):
                        if i >= 2:
                            vec.wait_ge(s_used, K1 * (i - 1))
                        vec.tensor_scalar(at_col[:, i % 2, :, :], onehot[:, i, :, :], tok[:, i:i + 1], None, ALU.mult).then_inc(s_col, 1)
                        for kk in range(K1):
                            n = K1 * i + kk
                            if n >= 2:
                                vec.wait_ge(s_used, n - 1)
                            vec.tensor_scalar(at_row[:, n % 2, :], iota_c[:, :], posk[:, i, kk:kk + 1], None, ALU.is_equal).then_inc(s_row, 1)
                    vec.wait_ge(s_used, K1 * NT)
                    vec.tensor_copy(k.token_of[:, :], bank[7][0:CAP, 0:E1]).then_inc(s_tab, 1)

                split_lo(0, gw_lo[:, :, :], gw_raw[:, :, :], gw_hi[:, :, :])
                for n in range(4 * NC):
                    vec.wait_ge(s_thi, n + 1)
                    t = slice(n // 4 * CH, (n // 4 + 1) * CH)
                    vec.tensor_tensor(xt_lo[:, n % 4, t], bank[n % 2][:, :], xt_hi[:, n % 4, t], ALU.subtract).then_inc(s_tlo, 1)
                    if n == 7:
                        split_lo(1, w1_lo[:, :, :], w1_raw[:, :, :], w1_hi[:, :, :])
                    if n == 11:
                        split_lo(2, w2_lo[:, :, :], w2_raw[:, :, :], w2_hi[:, :, :])
                choose()
                positions()
                table()


def experts1_routed(k):
    nc, bank, io = k.nc, k.bank, k.io
    with ExitStack() as ctx:
        U = 4
        two = lambda name, shape, dt=F32: [k.sb(f"e1_{name}{p}", shape, dt, ctx) for p in range(2)] * 2
        four = lambda name, shape, dt=F32: [k.sb(f"e1_{name}{p}", shape, dt, ctx) for p in range(U)]
        w1_raw, w1_hi, w1_lo = four("w1_raw", [P, KD, 2 * F1]), two("w1_hi", [P, KD, 2 * F1], F32R), two("w1_lo", [P, KD, 2 * F1], F32R)
        w2_raw, w2_hi, w2_lo = four("w2_raw", [HF1, 2, D]), two("w2_hi", [HF1, 2, D], F32R), two("w2_lo", [HF1, 2, D], F32R)
        index = four("index", [CAP, 1], I32)
        xg = four("xg", [CAP, D])
        xt_hi, xt_lo = two("xt_hi", [P, KD * CAP], F32R), two("xt_lo", [P, KD * CAP], F32R)
        si, hf = two("si", [CAP, F1]), two("hf", [CAP, F1])
        ht_hi, ht_lo = two("ht_hi", [HF1, 2 * CAP], F32R), two("ht_lo", [HF1, 2 * CAP], F32R)
        y = four("y", [CAP, D])

        each = lambda name: [k.sem(f"e1_{name}{p}") for p in range(U)]
        sem = lambda n: k.sem("e1_" + n)
        s_w, s_v, s_g, s_y = each("gate_up_loaded"), each("down_loaded"), each("rows_gathered"), each("results_stored")
        s_ix, s_go = sem("index"), sem("index_seen")
        s_whi, s_wlo, s_vhi, s_vlo = sem("gate_up_hi"), sem("gate_up_lo"), sem("down_hi"), sem("down_lo")
        s_tps, s_thi, s_tlo = sem("turned"), sem("turned_hi"), sem("turned_lo")
        s_gu, s_si, s_h = sem("gate_up"), sem("silu"), sem("hidden")
        s_ht, s_hh, s_hlo = sem("hidden_turned"), sem("hidden_hi"), sem("hidden_lo")
        s_dn, s_ysb = sem("down"), sem("results")
        nothing = lambda h, p: None
        past = lambda h, p, n: not (isinstance(h, int) and U * h + p < n)
        y_rows = k.y1.rearrange("(e s) d -> e s d", s=CAP)

        with nc.Block() as block:
            @block.sync
            def _(sp):
                def load(h, p):
                    e = U * h + p
                    if past(h, p, U):
                        sp.wait_ge(s_wlo, e - U + 1)
                    sp.dma_start(w1_raw[p][:, :, :].rearrange("p b n -> p (b n)"),
                                 io["w_gate_up"][bass.ds(e, 1)].rearrange("e p n -> p (e n)")).then_inc(s_w[p], 16)
                    if past(h, p, U):
                        sp.wait_ge(s_vlo, e - U + 1)
                    sp.dma_start(w2_raw[p][:, :, :].rearrange("p f n -> p (f n)"),
                                 io["w_down"][bass.ds(e, 1)].rearrange("e p n -> p (e n)")).then_inc(s_v[p], 16)

                def store(h, p):
                    e = U * h + p
                    sp.wait_ge(s_ysb, e + 1)
                    sp.dma_start(y_rows[bass.ds(e, 1)].rearrange("e s d -> s (e d)"), y[p][:, :]).then_inc(s_y[p], 16)

                three_stages(sp, E1, nothing, nothing, store, ahead=load, unroll=U)
                for p in range(U):
                    sp.wait_ge(s_y[p], 16 * (E1 // U))

            @block.gpsimd
            def _(pool):
                def gather(h, p):
                    e = U * h + p
                    if past(h, p, U):
                        pool.wait_ge(s_g[p], 16 * h)
                        pool.wait_ge(s_tps, e - U + 1)
                    pool.tensor_copy(index[p][:, :], k.token_of[:, bass.ds(e, 1)]).then_inc(s_ix, 1)
                    pool.wait_ge(s_ix, e + 1)
                    pool.sem_inc(s_go, 1)
                    pool.indirect_dma_start(xg[p][:, :], None, k.rows, bass.IndirectOffsetOnAxis(index[p][:, 0:1], 0)
                                            ).then_inc(s_g[p], 16)

                def down_lo(h, p):
                    e = U * h + p
                    pool.wait_ge(s_vhi, e + 1)
                    pool.tensor_tensor(w2_lo[p][:, :, :], w2_raw[p][:, :, :], w2_hi[p][:, :, :].bitcast(F32), ALU.subtract).then_inc(s_vlo, 1)

                three_stages(pool, E1, nothing, down_lo, nothing, ahead=gather, unroll=U)

            @block.tensor
            def _(pe):
                def turn(h, p):
                    pe.wait_ge(s_g[p], 16 * (h + 1))
                    if past(h, p, 2):
                        pe.wait_ge(s_tlo, U * h + p - 1)
                    for b in range(KD):
                        mm = pe.transpose(bank[p % 2][:, b * CAP:(b + 1) * CAP], xg[p][:, b * P:(b + 1) * P], k.ident[0:CAP, 0:CAP])
                    mm.then_inc(s_tps, 1)

                def gate_up(h, p):
                    e = U * h + p
                    pe.wait_ge(s_wlo, e + 1)
                    pe.wait_ge(s_tlo, e + 1)
                    if past(h, p, 2):
                        pe.wait_ge(s_h, e - 1)
                    for b in range(KD):
                        c = slice(b * CAP, (b + 1) * CAP)
                        mm = mm3(pe, bank[2 + p % 2][0:CAP, 0:2 * F1], xt_hi[p][:, c], xt_lo[p][:, c], w1_hi[p][:, b, :], w1_lo[p][:, b, :],
                                 b == 0, b == KD - 1)
                    mm.then_inc(s_gu, 1)

                def turn_hidden(h, p):
                    pe.wait_ge(s_h, U * h + p + 1)
                    if past(h, p, 2):
                        pe.wait_ge(s_hlo, U * h + p - 1)
                    for f in range(2):
                        mm = pe.transpose(bank[4 + p % 2][0:HF1, f * CAP:(f + 1) * CAP], hf[p][:, f * HF1:(f + 1) * HF1], k.ident[0:CAP, 0:CAP])
                    mm.then_inc(s_ht, 1)

                def down(h, p):
                    e = U * h + p
                    pe.wait_ge(s_hlo, e + 1)
                    pe.wait_ge(s_vlo, e + 1)
                    if past(h, p, 2):
                        pe.wait_ge(s_ysb, e - 1)
                    for f in range(2):
                        c = slice(f * CAP, (f + 1) * CAP)
                        mm = mm3(pe, bank[6 + p % 2][0:CAP, :], ht_hi[p][:, c], ht_lo[p][:, c], w2_hi[p][:, f, :], w2_lo[p][:, f, :],
                                 f == 0, f == 1)
                    mm.then_inc(s_dn, 1)

                three_stages(pe, E1, turn, gate_up, down, between=turn_hidden, unroll=U)

            @block.scalar
            def _(act):
                def turned_hi(h, p):
                    e = U * h + p
                    act.wait_ge(s_tps, e + 1)
                    act.activation(xt_hi[p][:, :], bank[p % 2][:, 0:KD * CAP], ACT.Copy).then_inc(s_thi, 1)

                def weights_hi(h, p):
                    e = U * h + p
                    act.wait_ge(s_w[p], 16 * (h + 1))
                    if past(h, p, 2):
                        act.wait_ge(s_gu, e - 1)
                    act.activation(w1_hi[p][:, :, :], w1_raw[p][:, :, :], ACT.Copy).then_inc(s_whi, 1)

                def hidden_hi(h, p):
                    e = U * h + p
                    act.wait_ge(s_ht, e + 1)
                    if past(h, p, 2):
                        act.wait_ge(s_dn, e - 1)
                    act.activation(ht_hi[p][:, :], bank[4 + p % 2][0:HF1, 0:2 * CAP], ACT.Copy).then_inc(s_hh, 1)

                def silu(h, p):
                    e = U * h + p
                    act.wait_ge(s_v[p], 16 * (h + 1))
                    if past(h, p, 2):
                        act.wait_ge(s_dn, e - 1)
                    act.activation(w2_hi[p][:, :, :], w2_raw[p][:, :, :], ACT.Copy).then_inc(s_vhi, 1)
                    act.wait_ge(s_gu, e + 1)
                    if past(h, p, 2):
                        act.wait_ge(s_h, e - 1)
                    act.activation(si[p][:, :], bank[2 + p % 2][0:CAP, 0:F1], ACT.Silu).then_inc(s_si, 1)

                def results(h, p):
                    e = U * h + p
                    act.wait_ge(s_dn, e + 1)
                    if past(h, p, U):
                        act.wait_ge(s_y[p], 16 * h)
                    act.activation(y[p][:, :], bank[6 + p % 2][0:CAP, :], ACT.Copy).then_inc(s_ysb, 1)

                three_stages(act, E1, turned_hi, silu, results, between=hidden_hi, prepare=weights_hi, unroll=U)

            @block.vector
            def _(vec):
                def weights_lo(h, p):
                    e = U * h + p
                    vec.wait_ge(s_whi, e + 1)
                    vec.tensor_tensor(w1_lo[p][:, :, :], w1_raw[p][:, :, :], w1_hi[p][:, :, :], ALU.subtract).then_inc(s_wlo, 1)

                def turned_lo(h, p):
                    e = U * h + p
                    vec.wait_ge(s_thi, e + 1)
                    vec.tensor_tensor(xt_lo[p][:, :], bank[p % 2][:, 0:KD * CAP], xt_hi[p][:, :], ALU.subtract).then_inc(s_tlo, 1)

                def hidden_lo(h, p):
                    vec.wait_ge(s_hh, U * h + p + 1)
                    vec.tensor_tensor(ht_lo[p][:, :], bank[4 + p % 2][0:HF1, 0:2 * CAP], ht_hi[p][:, :], ALU.subtract).then_inc(s_hlo, 1)

                def hidden(h, p):
                    e = U * h + p
                    vec.wait_ge(s_si, e + 1)
                    if past(h, p, 2):
                        vec.wait_ge(s_ht, e - 1)
                    vec.tensor_tensor(hf[p][:, :], si[p][:, :], bank[2 + p % 2][0:CAP, F1:2 * F1], ALU.mult).then_inc(s_h, 1)

                three_stages(vec, E1, turned_lo, hidden, nothing, between=hidden_lo, prepare=weights_lo, unroll=U)


def combine1(k):
    nc, io = k.nc, k.io
    NB = 3
    with ExitStack() as ctx:
        yg = [k.sb(f"c1_yg{n}", [P, K1, D], F32, ctx) for n in range(NB)]
        s_g = [k.sem(f"c1_gathered{n}") for n in range(NB)]
        s_sum, s_used = k.sem("c1_summed"), k.sem("c1_gathered_used")
        s_stat, s_var, s_rstd, s_ln, s_st = (k.sem("c1_" + n) for n in ("stats", "var", "rstd", "normed", "stored"))
        with nc.Block() as block:
            @block.sync
            def _(sp):
                for c in range(NC):
                    sp.wait_ge(s_ln, TC * (c + 1))
                    sp.dma_start(io["out"].rearrange("(c j p) d -> c p j d", p=P, j=TC)[c],
                                 k.x[:, c * TC:(c + 1) * TC, :]).then_inc(s_st, 16)
                sp.wait_ge(s_st, 16 * NC)

            @block.gpsimd
            def _(pool):
                def rstd(c):
                    pool.wait_ge(s_stat, 2 * TC * (c + 1))
                    ln_rstd(k, pool, c * TC, TC, s_var, s_rstd, c)

                for i in range(NT):
                    if i >= NB:
                        pool.wait_ge(s_used, i - NB + 1)
                    for kk in range(K1):
                        pool.indirect_dma_start(yg[i % NB][:, kk, :], None, k.y1, bass.IndirectOffsetOnAxis(k.slot[:, i, kk:kk + 1], 0)
                                                ).then_inc(s_g[i % NB], 16)
                    if i >= 7 and i % 4 == 3:
                        rstd(i // 4 - 1)
                rstd(NC - 1)

            @block.vector
            def _(vec):
                def apply(c):
                    vec.wait_ge(s_rstd, c + 1)
                    for i in range(c * TC, c * TC + TC):
                        ln_apply(k, vec, i).then_inc(s_ln, 1)

                for i in range(NT):
                    xi = k.x[:, i, :]
                    vec.wait_ge(s_g[i % NB], 16 * K1 * (i // NB + 1))
                    for kk in range(K1):
                        vec.scalar_tensor_tensor(xi, yg[i % NB][:, kk, :], k.weight[:, i, kk:kk + 1], xi, ALU.mult, ALU.add).then_inc(s_sum, 1)
                        vec.wait_ge(s_sum, K1 * i + kk + 1)
                    vec.sem_inc(s_used, 1)
                    ln_stats(k, vec, i, s_stat, i)
                    if i >= 7 and i % 4 == 3:
                        apply(i // 4 - 1)
                apply(NC - 1)


def two_layers(nc, io):
    with ExitStack() as ctx:
        k = Core(nc, ctx, io)
        k.rows = nc.dram_tensor("rows", (T, D), F32, kind="Internal").ap()
        k.y0 = nc.dram_tensor("results0", (NG0 * GRP, D), F32, kind="Internal").ap()
        k.y1 = nc.dram_tensor("results1", (E1 * CAP, D), F32, kind="Internal").ap()
        setup(k)
        attention0(k)
        with ExitStack() as k.moe_ctx:
            experts0_shared(k)
            experts0_routed(k)
            combine0(k)
        k.clear_semaphores()
        attention1(k)
        k.clear_semaphores()
        with ExitStack() as k.moe_ctx:
            experts1_shared(k)
            experts1_routed(k)
            combine1(k)


def layouts(inputs):
    a = {name: np.asarray(v) for name, v in inputs.items()}
    l0 = lambda n: a["L0_ffn_" + n]
    l1 = lambda n: a["L1_attn_" + n]
    m1 = lambda n: a["L1_ffn_" + n]
    blocks = lambda v: v.reshape(-1, P).T
    expert_blocks = lambda v: v.reshape(E0, F0 // P, P).transpose(2, 1, 0).reshape(P, -1)
    by_row = lambda w, n: w.reshape(E1, -1, n, w.shape[-1])
    names = {
        "x": a["L0_attn_hidden_states"].reshape(T, D),
        "wq_t": a["L0_attn_Wq"].T, "wo_t": a["L0_attn_Wo"].T,
        "mem": a["L0_attn_memories"].reshape(4, 4, 4, 32, 32).transpose(2, 3, 1, 0, 4).reshape(P, -1),
        "nrm": a["L0_attn_memory_norms"].reshape(4, 4, 4, 32).transpose(2, 3, 1, 0).reshape(P, -1),
        "bank_w": a["L0_attn_bank_weights"].reshape(4, 4, 4).transpose(0, 2, 1).reshape(-1),
        "sgb_t": blocks(l0("sgb")), "sb1_t": blocks(l0("sb1")),
        "rgb_t": expert_blocks(l0("rgb")), "rb1_t": expert_blocks(l0("rb1")),
        "b2": np.concatenate([l0("rb2"), l0("sb2")], 0),
        "kb_t": blocks(l1("kb")), "qb_t": blocks(l1("qb")), "fw2_t": l1("fw2").T,
        "w_gate_up": np.concatenate([by_row(m1("w_gate"), P), by_row(m1("w_up"), P)], 3).transpose(0, 2, 1, 3).reshape(E1, P, -1),
        "w_down": by_row(m1("w_down"), HF1).transpose(0, 2, 1, 3).reshape(E1, HF1, -1),
    }
    for n in ("wa", "sg", "sw1", "sw2", "rg", "rw1", "rw2"):
        names[n] = l0(n)
    for n in ("qw", "kw", "vw", "ow", "vb", "ob", "fw1", "fb1", "fw2", "fb2"):
        names[n] = l1(n)
    for n in ("gate_w", "bias", "ws_gate", "ws_up", "ws_down"):
        names[n] = m1(n)
    return {n: np.ascontiguousarray(v) for n, v in names.items()}


def kernel(**inputs):
    import concourse.bacc as bacc
    from concourse.bass_utils import run_bass_kernel_spmd

    nc = bacc.Bacc("TRN2", target_bir_lowering=False, num_devices=1)
    arrays = {"in_" + n: v for n, v in layouts(inputs).items()}
    io = {n[3:]: nc.dram_tensor(n, v.shape, mybir.dt.from_np(v.dtype), kind="ExternalInput").ap() for n, v in arrays.items()}
    io["out"] = nc.dram_tensor("out", (T, D), F32, kind="ExternalOutput").ap()
    two_layers(nc, io)
    r = run_bass_kernel_spmd(nc, [arrays], core_ids=[0])
    return r.results[0]["out"].reshape(1, T, D)
```

```python
from contextlib import ExitStack

import numpy as np
import concourse.bass as bass
import concourse.mybir as mybir

F32 = mybir.dt.float32
F32R = mybir.dt.float32r
BF16 = mybir.dt.bfloat16
I32 = mybir.dt.int32
U32 = mybir.dt.uint32
ALU = mybir.AluOpType
ACT = mybir.ActivationFunctionType
AX = mybir.AxisListType

P = 128
T = 2048
D = 512
NT = T // P
KD = D // P
CH = 512
NC = T // CH
TC = CH // P
EPS_LN = 1e-5
EPS_MEM = 1e-6


class Core:

    def __init__(self, nc, ctx, io):
        self.nc, self.ctx, self.io = nc, ctx, io
        self.sems = []
        self.s_rows = nc.alloc_semaphore(name="rows_stored")
        self.bank = [ctx.enter_context(nc.psum_tensor(f"bank{i}", [P, 512], F32)) for i in range(8)]

    def sem(self, name):
        self.sems.append(self.nc.alloc_semaphore(name=name))
        return self.sems[-1]

    def clear_semaphores(self):
        self.nc.clear_and_free_semaphores(self.sems)
        self.nc.all_engine_barrier()
        self.sems = []

    def sb(self, name, shape, dt=F32, ctx=None):
        return (ctx or self.ctx).enter_context(self.nc.sbuf_tensor(name, shape, dt))


def mm3(pe, out, a_hi, a_lo, b_hi, b_lo, start, stop):
    pe.matmul(out, a_hi, b_hi, start=start, stop=False)
    pe.matmul(out, a_hi, b_lo, start=False, stop=False)
    return pe.matmul(out, a_lo, b_hi, start=False, stop=stop)


def setup(k):
    k.ident = k.sb("ident", [P, P])
    k.x = k.sb("resid", [P, NT, D])
    k.neg_half = k.sb("neg_half", [P, NT])
    k.mv = k.sb("mv", [P, NT, 2])
    k.stats = k.sb("stats", [P, 2, 6])
    k.var = k.sb("var", [P, NT])
    k.rstd = k.sb("rstd", [P, NT])
    s_ident0 = k.sem("ident_zeroed")
    with k.nc.Block() as block:
        @block.gpsimd
        def _(pool):
            pool.memset(k.ident[:, :], 0.0).then_inc(s_ident0, 1)
            pool.memset(k.neg_half[:, :], -0.5)
            pool.wait_ge(s_ident0, 1)
            pool.affine_select(out=k.ident[:, :], in_=k.ident[:, :], compare_op=ALU.not_equal, fill=1.0,
                               base=0, pattern=[[-1, P]], channel_multiplier=1)


def ln_stats(k, vec, tile, s_stat, n):
    vec.bn_stats(k.stats[:, n % 2, :], k.x[:, tile, :]).then_inc(s_stat, 1)
    vec.wait_ge(s_stat, 2 * n + 1)
    vec.bn_aggr(k.mv[:, tile, :], k.stats[:, n % 2, :]).then_inc(s_stat, 1)


def ln_rstd(k, pool, t0, n, s_var, s_rstd, done):
    pool.tensor_scalar(k.var[:, t0:t0 + n], k.mv[:, t0:t0 + n, 1], EPS_LN, 0.0, ALU.add, ALU.add).then_inc(s_var, 1)
    pool.wait_ge(s_var, done + 1)
    pool.tensor_tensor(k.rstd[:, t0:t0 + n], k.var[:, t0:t0 + n], k.neg_half[:, t0:t0 + n], ALU.pow).then_inc(s_rstd, 1)


def ln_apply(k, vec, tile):
    return vec.tensor_scalar(k.x[:, tile, :], k.x[:, tile, :], k.mv[:, tile, 0:1], k.rstd[:, tile:tile + 1],
                             ALU.subtract, ALU.mult)


def attention0(k):
    nc, bank, io = k.nc, k.bank, k.io
    NB, G, HG, DH = 4, 4, 4, 32
    with ExitStack() as ctx:
        sb = lambda name, shape, dt=F32: k.sb("a0_" + name, shape, dt, ctx)
        raw = sb("raw", [P, KD, D])
        wq_hi, wq_lo = sb("wq_hi", [P, KD, D], F32R), sb("wq_lo", [P, KD, D], F32R)
        wo_hi, wo_lo = sb("wo_hi", [P, KD, D], F32R), sb("wo_lo", [P, KD, D], F32R)
        mem_raw, nrm_raw = sb("mem_raw", [P, G * NB, DH]), sb("nrm_raw", [P, G * NB])
        mem_hi, mem_lo = sb("mem_hi", [P, G, NB * HG * DH], F32R), sb("mem_lo", [P, G, NB * HG * DH], F32R)
        nrm_f = sb("nrm_f", [P, G * NB, HG])
        nrm_hl = sb("nrm_hl", [P, G, 2, NB * HG], F32R)
        nrm_hi, nrm_lo = nrm_hl[:, :, 0, :], nrm_hl[:, :, 1, :]
        head_mask = sb("head_mask", [P, HG])
        ones = sb("ones", [P, P])
        bw = sb("bw", [P, G, NB, HG])
        bmax, bsum = sb("bmax", [P, G, HG]), sb("bsum", [P, G, HG])
        act_n = sb("act_n", [P, NB])
        xt_hi, xt_lo = sb("xt_hi", [P, 2, KD, CH], F32R), sb("xt_lo", [P, 2, KD, CH], F32R)
        ex, rl = sb("ex", [P, 2, CH]), sb("rl", [P, 2, CH])
        sg = sb("sg", [P, 2, CH])
        sg_hi, sg_lo = sb("sg_hi", [P, 2, KD, CH], F32R), sb("sg_lo", [P, 2, KD, CH], F32R)
        rw = sb("rw", [P, 2, TC, G * NB * HG])
        comb, read_n = sb("comb", [P, 2, D]), sb("read_n", [P, 2, NB * HG * DH])
        read_2 = sb("read_2", [P, 2, 2 * HG * DH])
        ct_hi, ct_lo = sb("ct_hi", [P, 2, KD, P], F32R), sb("ct_lo", [P, 2, KD, P], F32R)

        s_x = [k.sem(f"a0_x_loaded{c}") for c in range(NC)]
        s_wq, s_wo, s_mem, s_nrm = (k.sem("a0_" + n) for n in ("wq_loaded", "wo_loaded", "mem_loaded", "nrm_loaded"))
        s_bw, s_ones, s_ns = k.sem("a0_bw_loaded"), k.sem("a0_ones_made"), k.sem("a0_norms_summed")
        s_zero, s_mask = k.sem("a0_mem_zeroed"), k.sem("a0_mask_made")
        s_whi, s_split = k.sem("a0_weight_hi"), k.sem("a0_weights_split")
        s_c = k.sem("a0_vector_chain")
        s_bexp = k.sem("a0_bank_exp")
        s_bsub = k.sem("a0_bank_sub")
        s_tps, s_thi, s_tlo = k.sem("a0_turned"), k.sem("a0_turned_hi"), k.sem("a0_turned_lo")
        s_q, s_qev, s_sg, s_slo = k.sem("a0_q"), k.sem("a0_q_read"), k.sem("a0_sigma"), k.sem("a0_sigma_split")
        s_nb, s_r = k.sem("a0_norms"), k.sem("a0_norms_read")
        s_rw, s_wl = k.sem("a0_read_weights"), k.sem("a0_norm_parts")
        s_m, s_rn, s_comb = k.sem("a0_reads"), k.sem("a0_reads_weighted"), k.sem("a0_combined")
        s_r2 = k.sem("a0_half_sum")
        s_o, s_res = k.sem("a0_out"), k.sem("a0_residual")
        s_stat, s_var, s_rstd = k.sem("a0_stats"), k.sem("a0_var"), k.sem("a0_rstd")
        s_ln = k.sem("a0_normed")

        def schedule(turn_x, query, norms, weights, read, turn_comb, project, late_query=False):
            for b in range(KD):
                turn_x(0, b)
            for m in range(KD):
                query(0, m)
            for b in range(KD):
                turn_x(1, b)
            for m in range(KD):
                norms(0, m)
            for i in range(NT):
                c, j = i // TC, i % TC
                if j == 0:
                    weights(c)
                read(4 * i)
                if c + 1 < NC and not late_query:
                    query(c + 1, j)
                read(4 * i + 1)
                if i:
                    turn_comb(i - 1)
                if c + 1 < NC and late_query:
                    query(c + 1, j)
                read(4 * i + 2)
                if c + 2 < NC:
                    turn_x(c + 2, j)
                read(4 * i + 3)
                if i:
                    project(i - 1)
                if c + 1 < NC:
                    norms(c + 1, j)
            turn_comb(NT - 1)
            project(NT - 1)

        idle = lambda *_: None
        turned = []
        schedule(lambda c, b: turned.append(("x", c, b)), idle, idle, idle, idle, lambda i: turned.append(("comb", i)), idle)
        number = {what: n for n, what in enumerate(turned)}

        with nc.Block() as block:
            @block.sync
            def _(sp):
                x_d = io["x"].rearrange("(c j p) d -> c p j d", p=P, j=TC)
                sp.dma_start(k.x[:, 0:TC, :], x_d[0]).then_inc(s_x[0], 16)
                sp.dma_start(mem_raw[:, :, :], io["mem"].rearrange("p (a e) -> p a e", e=DH)).then_inc(s_mem, 16)
                sp.dma_start(nrm_raw[:, :], io["nrm"]).then_inc(s_nrm, 16)
                sp.dma_start(bw[:, :, :, :].rearrange("p g n h -> p (g n h)"),
                             io["bank_w"].partition_broadcast(P)).then_inc(s_bw, 16)
                sp.dma_start(raw[:, :, :], io["wq_t"].rearrange("(b p) n -> p b n", p=P)).then_inc(s_wq, 16)
                for c in range(1, NC):
                    sp.dma_start(k.x[:, c * TC:(c + 1) * TC, :], x_d[c]).then_inc(s_x[c], 16)
                sp.wait_ge(s_split, 1)
                sp.dma_start(raw[:, :, :], io["wo_t"].rearrange("(b p) n -> p b n", p=P)).then_inc(s_wo, 16)
                for c in range(NC):
                    sp.wait_ge(s_ln, TC * (c + 1))
                    sp.dma_start(k.rows.rearrange("(c j p) d -> c p j d", p=P, j=TC)[c],
                                 k.x[:, c * TC:(c + 1) * TC, :]).then_inc(k.s_rows, 16)

            @block.gpsimd
            def _(pool):
                pool.memset(ones[:, :], 1.0).then_inc(s_ones, 1)
                pool.memset(mem_hi[:, :, :].bitcast(F32), 0.0).then_inc(s_zero, 1)
                pool.memset(mem_lo[:, :, :].bitcast(F32), 0.0).then_inc(s_zero, 1)
                pool.memset(head_mask[:, :], 0.0).then_inc(s_zero, 1)
                pool.wait_ge(s_zero, 3)
                for h in range(HG):
                    pool.memset(head_mask[DH * h:DH * h + DH, h:h + 1], 1.0).then_inc(s_mask, 1)

                def read(v):
                    i, g = v // G, v % G
                    pool.wait_ge(s_rn, v + 1)
                    if i >= 2:
                        pool.wait_ge(s_tps, number["comb", i - 2] + 1)
                    pool.tensor_tensor(read_2[:, v % 2, :], read_n[:, v % 2, 0:256], read_n[:, v % 2, 256:512],
                                       ALU.add).then_inc(s_r2, 1)
                    pool.wait_ge(s_r2, v + 1)
                    pool.tensor_tensor(comb[:, i % 2, g * P:(g + 1) * P], read_2[:, v % 2, 0:P], read_2[:, v % 2, P:2 * P],
                                       ALU.add).then_inc(s_comb, 1)

                def project(i):
                    if i % TC == TC - 1:
                        pool.wait_ge(s_stat, 2 * (i + 1))
                        ln_rstd(k, pool, i - TC + 1, TC, s_var, s_rstd, i // TC)

                schedule(idle, idle, idle, idle, read, idle, project)

            @block.tensor
            def _(pe):
                def turned_bank(n):
                    if n >= 2:
                        pe.wait_ge(s_tlo, n - 1)
                    return bank[n % 2]

                def turn_x(c, b):
                    if b == 0:
                        pe.wait_ge(s_x[c], 16)
                    t = turned_bank(number["x", c, b])
                    for j in range(TC):
                        mm = pe.transpose(t[:, j * P:(j + 1) * P], k.x[:, c * TC + j, b * P:(b + 1) * P], k.ident[:, :])
                    mm.then_inc(s_tps, 1)

                def query(c, m):
                    u, s = 4 * c + m, c % 2
                    if u == 0:
                        pe.wait_ge(s_nrm, 16)
                        pe.wait_ge(s_ones, 1)
                        pe.matmul(bank[7][:, 0:G * NB], ones[:, :], nrm_raw[:, :], start=True, stop=True).then_inc(s_ns, 1)
                        pe.wait_ge(s_split, 1)
                    pe.wait_ge(s_tlo, number["x", c, KD - 1] + 1)
                    if u >= 2:
                        pe.wait_ge(s_qev, u - 1)
                    for b in range(KD):
                        mm = mm3(pe, bank[2 + u % 2][:, :], wq_hi[:, b, m * P:(m + 1) * P], wq_lo[:, b, m * P:(m + 1) * P],
                                 xt_hi[:, s, b, :], xt_lo[:, s, b, :], b == 0, b == KD - 1)
                    mm.then_inc(s_q, 1)

                def norms(c, g):
                    s = c % 2
                    if c == 0:
                        pe.wait_ge(s_split, 2)
                    pe.wait_ge(s_slo, 4 * c + g + 1)
                    if c:
                        pe.wait_ge(s_r, c)
                    elif g == 0:
                        pe.wait_ge(s_c, 2)
                    for j in range(TC):
                        tok = slice(j * P, (j + 1) * P)
                        o = (j * G + g) * 32
                        pe.matmul(bank[7][:, o:o + 32], sg_hi[:, s, g, tok], nrm_hl[:, g, :, :].rearrange("p l a -> p (l a)"),
                                  start=True, stop=False)
                        mm = pe.matmul(bank[7][:, o:o + 16], sg_lo[:, s, g, tok], nrm_hi[:, g, :], start=False, stop=True)
                    mm.then_inc(s_nb, 1)

                def read(v):
                    s, j, g = v // 16 % 2, v // G % TC, v % G
                    tok = slice(j * P, (j + 1) * P)
                    if v >= 2:
                        pe.wait_ge(s_rn, v - 1)
                    mm3(pe, bank[4 + v % 2][:, :], sg_hi[:, s, g, tok], sg_lo[:, s, g, tok],
                        mem_hi[:, g, :], mem_lo[:, g, :], True, True).then_inc(s_m, 1)

                def turn_comb(i):
                    pe.wait_ge(s_comb, 4 * i + 4)
                    t = turned_bank(number["comb", i])
                    for b in range(KD):
                        mm = pe.transpose(t[:, b * P:(b + 1) * P], comb[:, i % 2, b * P:(b + 1) * P], k.ident[:, :])
                    mm.then_inc(s_tps, 1)

                def project(i):
                    if i == 0:
                        pe.wait_ge(s_split, 3)
                    pe.wait_ge(s_tlo, number["comb", i] + 1)
                    if i:
                        pe.wait_ge(s_res, i)
                    for b in range(KD):
                        mm = mm3(pe, bank[6][:, :], ct_hi[:, i % 2, b, :], ct_lo[:, i % 2, b, :],
                                 wo_hi[:, b, :], wo_lo[:, b, :], b == 0, b == KD - 1)
                    mm.then_inc(s_o, 1)

                schedule(turn_x, query, norms, idle, read, turn_comb, project)

            @block.scalar
            def _(act):
                def weights_hi():
                    act.wait_ge(s_wq, 16)
                    act.activation(wq_hi[:, :, :], raw[:, :, :], ACT.Copy).then_inc(s_whi, 1)
                    act.wait_ge(s_mem, 16)
                    act.wait_ge(s_zero, 3)
                    for h in range(HG):
                        r = slice(DH * h, DH * h + DH)
                        act.activation(mem_hi[r, :, :].rearrange("p g (n x) -> p (g n) x", n=NB)[:, :, r], mem_raw[r, :, :],
                                       ACT.Copy).then_inc(s_whi, 1)
                    act.wait_ge(s_bsub, 1)
                    act.activation(bw[:, :, :, :], bw[:, :, :, :], ACT.Exp).then_inc(s_bexp, 1)

                def turned_hi(n, dst):
                    act.wait_ge(s_tps, n + 1)
                    act.activation(dst, bank[n % 2][:, :], ACT.Copy).then_inc(s_thi, 1)

                def turn_x(c, b):
                    if c >= 2:
                        act.wait_ge(s_q, 4 * (c - 1))
                    turned_hi(number["x", c, b], xt_hi[:, c % 2, b, :])

                def query(c, m):
                    u = 4 * c + m
                    if u == 0:
                        weights_hi()
                    act.wait_ge(s_q, u + 1)
                    if u >= 2:
                        act.wait_ge(s_sg, u - 1)
                    act.activation(ex[:, u % 2, :], bank[2 + u % 2][:, :], ACT.Exp)
                    act.activation(rl[:, u % 2, :], bank[2 + u % 2][:, :], ACT.Relu).then_inc(s_qev, 1)
                    if u == 3:
                        act.wait_ge(s_wo, 16)
                        act.activation(wo_hi[:, :, :], raw[:, :, :], ACT.Copy).then_inc(s_whi, 1)

                def turn_comb(i):
                    if i >= 2:
                        act.wait_ge(s_o, i - 1)
                    turned_hi(number["comb", i], ct_hi[:, i % 2, :, :].rearrange("p b t -> p (b t)"))

                schedule(turn_x, query, idle, idle, idle, turn_comb, idle)

            @block.vector
            def _(vec):
                def bank_weights():
                    vec.wait_ge(s_bw, 16)
                    vec.wait_ge(s_ns, 1)
                    by_n = lambda a: a[:, :, :, :].rearrange("p g n h -> p g h n")
                    over = lambda a: a[:, :, :].unsqueeze(3).to_broadcast([P, G, HG, NB])
                    vec.tensor_reduce(bmax[:, :, :], by_n(bw), AX.X, ALU.max).then_inc(s_c, 1)
                    vec.tensor_reduce(act_n[:, :], bank[7][:, 0:G * NB].rearrange("p (g n) -> p n g", n=NB), AX.X, ALU.add).then_inc(s_c, 1)
                    vec.wait_ge(s_c, 2)
                    vec.tensor_tensor(by_n(bw), by_n(bw), over(bmax), ALU.subtract).then_inc(s_bsub, 1)
                    vec.tensor_scalar(act_n[:, :], act_n[:, :], EPS_MEM, None, ALU.is_ge).then_inc(s_c, 1)
                    vec.wait_ge(s_bexp, 1)
                    vec.tensor_reduce(bsum[:, :, :], by_n(bw), AX.X, ALU.add).then_inc(s_c, 1)
                    vec.wait_ge(s_c, 4)
                    vec.reciprocal(bsum[:, :, :], bsum[:, :, :]).then_inc(s_c, 1)
                    vec.wait_ge(s_c, 5)
                    vec.tensor_tensor(by_n(bw), by_n(bw), over(bsum), ALU.mult).then_inc(s_c, 1)
                    vec.wait_ge(s_c, 6)
                    vec.tensor_tensor(by_n(bw), by_n(bw), act_n[:, :].unsqueeze(1).unsqueeze(1).to_broadcast([P, G, HG, NB]),
                                      ALU.mult).then_inc(s_c, 1)

                def memories():
                    vec.wait_ge(s_nrm, 16)
                    vec.wait_ge(s_mask, HG)
                    vec.tensor_tensor(nrm_f[:, :, :], nrm_raw[:, :].unsqueeze(2).to_broadcast([P, G * NB, HG]),
                                      head_mask[:, :].unsqueeze(1).to_broadcast([P, G * NB, HG]), ALU.mult).then_inc(s_c, 1)
                    vec.wait_ge(s_c, 8)
                    by_group = nrm_f[:, :, :].rearrange("p (g n) h -> p g (n h)", g=G)
                    vec.tensor_copy(nrm_hi, by_group).then_inc(s_c, 1)
                    vec.wait_ge(s_c, 9)
                    vec.tensor_tensor(nrm_lo, by_group, nrm_hi, ALU.subtract)
                    vec.wait_ge(s_whi, 1 + HG)
                    for h in range(HG):
                        r = slice(DH * h, DH * h + DH)
                        block_of = lambda a: a[r, :, :].rearrange("p g (n x) -> p (g n) x", n=NB)[:, :, r]
                        last = vec.tensor_tensor(block_of(mem_lo), mem_raw[r, :, :], block_of(mem_hi), ALU.subtract)
                    last.then_inc(s_split, 1)

                def turned_lo(n, src, dst):
                    vec.wait_ge(s_thi, n + 1)
                    vec.tensor_tensor(dst, bank[n % 2][:, :], src, ALU.subtract).then_inc(s_tlo, 1)

                def turn_x(c, b):
                    turned_lo(number["x", c, b], xt_hi[:, c % 2, b, :], xt_lo[:, c % 2, b, :])

                def query(c, m):
                    u = 4 * c + m
                    if u == 0:
                        vec.wait_ge(s_whi, 1)
                        vec.tensor_tensor(wq_lo[:, :, :], raw[:, :, :], wq_hi[:, :, :], ALU.subtract).then_inc(s_split, 1)
                        bank_weights()
                        memories()
                    vec.wait_ge(s_qev, u + 1)
                    if c >= 2 and m == 0:
                        vec.wait_ge(s_m, 16 * (c - 1))
                    vec.scalar_tensor_tensor(sg[:, u % 2, :], ex[:, u % 2, :], 1.0, rl[:, u % 2, :], ALU.min, ALU.add)
                    vec.scalar_tensor_tensor(sg_hi[:, c % 2, m, :], ex[:, u % 2, :], 1.0, rl[:, u % 2, :],
                                             ALU.min, ALU.add).then_inc(s_sg, 1)
                    vec.wait_ge(s_sg, u + 1)
                    vec.tensor_tensor(sg_lo[:, c % 2, m, :], sg[:, u % 2, :], sg_hi[:, c % 2, m, :],
                                      ALU.subtract).then_inc(s_slo, 1)

                def weights(c):
                    vec.wait_ge(s_nb, 4 * (c + 1))
                    w = rw[:, c % 2, :, :]
                    half = lambda l: bank[7][:, :].rearrange("p (a l b) -> p a l b", l=2, b=16)[:, :, l, :]
                    blocks = w.rearrange("p j (g b) -> p (j g) b", g=G)
                    vec.tensor_copy(blocks, half(1)).then_inc(s_wl, 1)
                    vec.wait_ge(s_wl, 2 * c + 1)
                    vec.tensor_tensor(blocks, half(0), blocks, ALU.add).then_inc(s_r, 1)
                    vec.wait_ge(s_r, c + 1)
                    vec.tensor_scalar(w, w, EPS_MEM, None, ALU.max).then_inc(s_wl, 1)
                    vec.wait_ge(s_wl, 2 * c + 2)
                    vec.reciprocal(w, w).then_inc(s_rw, 1)
                    vec.wait_ge(s_rw, 2 * c + 1)
                    vec.tensor_tensor(w, w, bw[:, :, :, :].rearrange("p g n h -> p (g n h)").unsqueeze(1)
                                      .to_broadcast([P, TC, 64]), ALU.mult).then_inc(s_rw, 1)
                    vec.wait_ge(s_rw, 2 * c + 2)

                def read(v):
                    c, j, g = v // 16, v // G % TC, v % G
                    vec.wait_ge(s_m, v + 1)
                    if v >= 2:
                        vec.wait_ge(s_comb, v - 1)
                    vec.tensor_tensor(read_n[:, v % 2, :].rearrange("p (a e) -> p a e", e=DH),
                                      bank[4 + v % 2][:, :].rearrange("p (a e) -> p a e", e=DH),
                                      rw[:, c % 2, j, g * 16:g * 16 + 16].unsqueeze(2).to_broadcast([P, 16, DH]),
                                      ALU.mult).then_inc(s_rn, 1)

                def turn_comb(i):
                    if i == 0:
                        vec.wait_ge(s_whi, 2 + HG)
                        vec.tensor_tensor(wo_lo[:, :, :], raw[:, :, :], wo_hi[:, :, :], ALU.subtract).then_inc(s_split, 1)
                    turned_lo(number["comb", i], ct_hi[:, i % 2, :, :].rearrange("p b t -> p (b t)"),
                              ct_lo[:, i % 2, :, :].rearrange("p b t -> p (b t)"))

                def project(i):
                    vec.wait_ge(s_o, i + 1)
                    vec.tensor_tensor(k.x[:, i, :], bank[6][:, :], k.x[:, i, :], ALU.add).then_inc(s_res, 1)
                    vec.wait_ge(s_res, i + 1)
                    ln_stats(k, vec, i, s_stat, i)
                    if i >= TC:
                        normalise(i - TC)

                def normalise(i):
                    vec.wait_ge(s_rstd, i // TC + 1)
                    ln_apply(k, vec, i).then_inc(s_ln, 1)

                schedule(turn_x, query, idle, weights, read, turn_comb, project, late_query=True)
                for i in range(NT - TC, NT):
                    normalise(i)


FLOOR = -0.498046875


def no_work(h, p):
    pass


def three_stages(eng, n, first, second, third, ahead=no_work, between=no_work, prepare=no_work, unroll=2):
    def step(g):
        for stage, item in ((ahead, g + 3), (first, g + 1), (between, g - 1), (prepare, g + 1), (second, g), (third, g - 1)):
            if 0 <= item < n:
                stage(item // unroll, item % unroll)

    rounds = (n - 4) // unroll
    for g in range(-3, unroll + 1):
        step(g)
    with eng.Fori(1, rounds) as i:
        for q in range(unroll):
            at = lambda stage, item: stage(i + item // unroll, item % unroll)
            at(ahead, q + 4)
            at(first, q + 2)
            at(between, q)
            at(prepare, q + 2)
            at(second, q + 1)
            at(third, q)
    for g in range(unroll * rounds + 1, n + 1):
        step(g)


def started(h):
    return not (isinstance(h, int) and h == 0)


E0 = 16
GRP = 256
NG0 = (2 * T) // GRP + E0 - 1
F0 = 256


def experts0_shared(k):
    nc, bank, io = k.nc, k.bank, k.io
    NS, FB = 2, F0 // P
    NU = NS * FB
    rt = lambda name, shape, dt=F32: k.sb("r0_" + name, shape, dt, k.moe_ctx)
    k.slot = k.sb("r0_slot", [P, 2, NT], I32, k.table_ctx)
    k.weight = k.sb("r0_weight", [P, 2, NT], F32, k.table_ctx)
    k.token_of = rt("token_of", [P, 2 * NG0], I32)
    k.group_expert = rt("group_expert", [P, NG0], I32)
    k.group_bias = rt("group_bias", [P, NG0, 2 * FB])
    EA = E0 + NS
    with ExitStack() as ctx:
        sb = lambda name, shape, dt=F32: k.sb("s0_" + name, shape, dt, ctx)
        wa_raw = sb("wa_raw", [P, KD, E0])
        sraw = sb("sraw", [P, 2, 2 * KD * F0])
        comb_aug = sb("comb_aug", [P, NT, EA])
        b2 = sraw[0:EA, 1, 0:D]
        comb_t = sraw[0:EA, 1, D:3 * D].rearrange("p (c t) -> p c t", c=2)
        w1_hi, w1_lo = sb("w1_hi", [P, NS, 2, KD, F0], F32R), sb("w1_lo", [P, NS, 2, KD, F0], F32R)
        w2_hi, w2_lo = sb("w2_hi", [P, NU, D], F32R), sb("w2_lo", [P, NU, D], F32R)
        gb, ub = sb("gb", [P, NU]), sb("ub", [P, NU])
        rgb, rub = sb("rgb", [P, FB, E0]), sb("rub", [P, FB, E0])
        xt_hi, xt_lo = sb("xt_hi", [P, KD, T], F32R), sb("xt_lo", [P, KD, T], F32R)
        ge = sb("ge", [P, CH])
        hf = sb("hf", [P, 2, CH])
        h_hi, h_lo = sb("h_hi", [P, NU, CH], F32R), sb("h_lo", [P, NU, CH], F32R)
        aff = sb("aff", [P, NT, E0])
        top, arg = sb("top", [P, NT, 8]), sb("arg", [P, NT, 8], U32)
        argf = sb("argf", [P, 2, NT])
        onehot = sb("onehot", [P, 2, NT, E0])
        sel = sb("sel", [P, NT * E0], BF16)
        upper, ones = sb("upper", [P, P], BF16), sb("ones", [P, P], BF16)
        run_a, run_b = sb("run_a", [P, NT, E0]), sb("run_b", [P, NT, E0])
        tot = sb("tot", [P, NT, E0])
        cnt_i = sb("cnt_i", [P, E0], I32)
        groups, ends, start2 = sb("groups", [P, E0]), sb("ends", [P, E0]), sb("start2", [P, E0])
        ones16 = sb("ones16", [P, E0])
        prod = sb("prod", [P, 2 * NT, E0])
        posk, st, fl, pp = (sb(n, [P, 2 * NT]) for n in ("posk", "st", "fl", "pp"))
        fl_i = sb("fl_i", [P, 2 * NT], I32)
        rsum = sb("rsum", [P, NT])
        iota_e, iota_p, iota_s, iota_g = sb("iota_e", [P, E0]), sb("iota_p", [P, P]), sb("iota_s", [P, 2 * NG0]), sb("iota_g", [P, NG0])
        tok = sb("tok", [P, NT])
        at_row = lambda a: xt_hi[:, a // 4 % 4, a % 4 * P:(a % 4 + 1) * P]
        at_col = sb("at_col", [P, 2 * NT, 2 * NG0], F32R)
        wa_hi, wa_lo = (at_col[:, :, :].rearrange("p a s -> p (a s)")[:, n * KD * P:(n + 1) * KD * P].rearrange("p (b n) -> p b n", b=KD)
                        for n in range(2))
        aff_t = hf[0:E0, :, :]
        by_group = lambda flat: flat[:, 0:NG0 * E0].rearrange("p (g e) -> p g e", e=E0)
        gsel = by_group(onehot[:, :, :, :].rearrange("p k t e -> p (k t e)"))
        gprod = by_group(prod[:, :, :].rearrange("p a e -> p (a e)"))
        gef = sb("gef", [P, NG0])

        s_wa, s_b = k.sem("s0_wa_loaded"), k.sem("s0_bias_loaded")
        s_w1, s_w2 = [k.sem(f"s0_w1_loaded{s}") for s in range(NS)], k.sem("s0_w2_loaded")
        s_whi, s_wlo = k.sem("s0_weight_hi"), k.sem("s0_weight_split")
        s_tps, s_thi, s_tlo = k.sem("s0_turned"), k.sem("s0_turned_hi"), k.sem("s0_turned_lo")
        s_waz, s_lg, s_sig = k.sem("s0_wa_zeroed"), k.sem("s0_logits"), k.sem("s0_sigmoid")
        s_back, s_aff = k.sem("s0_turned_back"), k.sem("s0_affinity")
        s_gu, s_ge, s_h, s_hlo = k.sem("s0_gate_up"), k.sem("s0_gelu"), k.sem("s0_hidden"), k.sem("s0_hidden_split")
        s_hh = k.sem("s0_hidden_hi")
        s_dn, s_res = k.sem("s0_down"), k.sem("s0_residual")
        s_b2, s_ca, s_ct, s_cts = (k.sem("s0_" + n) for n in ("b2_loaded", "comb_made", "comb_turned", "comb_copied"))
        s_const = k.sem("s0_constants")
        s_r = k.sem("s0_route_chain")
        s_sel, s_pre, s_tab = k.sem("s0_selected"), k.sem("s0_prefix"), k.sem("s0_table")
        s_row, s_col = k.sem("s0_rows_made"), k.sem("s0_cols_made")
        s_rowfree = k.sem("s0_rows_used")

        with nc.Block() as block:
            @block.sync
            def _(sp):
                sp.dma_start(wa_raw[:, :, :], io["wa"].rearrange("(b p) n -> p b n", p=P)).then_inc(s_wa, 16)
                for s in range(NS):
                    for a, name in enumerate(("sg", "sw1")):
                        sp.dma_start(sraw[:, s, a * KD * F0:(a + 1) * KD * F0].rearrange("p (b n) -> p b n", b=KD),
                                     io[name][s].rearrange("(b p) n -> p b n", p=P)).then_inc(s_w1[s], 16)
                sp.dma_start(gb[:, :], io["sgb_t"]).then_inc(s_b, 16)
                sp.dma_start(ub[:, :], io["sb1_t"]).then_inc(s_b, 16)
                sp.dma_start(rgb[:, :, :].rearrange("p f e -> p (f e)"), io["rgb_t"]).then_inc(s_b, 16)
                sp.dma_start(rub[:, :, :].rearrange("p f e -> p (f e)"), io["rb1_t"]).then_inc(s_b, 16)
                sp.wait_ge(s_wlo, 2)
                sp.dma_start(sraw[:, 0, :].rearrange("p (u n) -> p u n", n=D),
                             io["sw2"].rearrange("s (f p) n -> p (s f) n", p=P)).then_inc(s_w2, 16)

                sp.wait_ge(s_wlo, 3)
                sp.dma_start(b2, io["b2"]).then_inc(s_b2, 16)
                sp.wait_ge(k.s_rows, 16 * NC)

            @block.gpsimd
            def _(pool):
                pool.memset(wa_hi[:, :, :].bitcast(F32), 0.0).then_inc(s_waz, 1)
                pool.memset(wa_lo[:, :, :].bitcast(F32), 0.0).then_inc(s_waz, 1)
                pool.memset(upper[:, :], 1.0).then_inc(s_const, 1)
                pool.memset(ones[:, :], 1.0).then_inc(s_const, 1)
                pool.memset(ones16[:, :], 1.0).then_inc(s_const, 1)
                pool.memset(comb_aug[:, :, :], 1.0).then_inc(s_const, 1)
                for a, n in ((iota_e, E0), (iota_p, P), (iota_s, 2 * NG0), (iota_g, NG0)):
                    pool.iota(a[:, :], [[1, n]], base=0, channel_multiplier=0,
                              allow_small_or_imprecise_dtypes=True).then_inc(s_const, 1)
                pool.iota(tok[:, :], [[P, NT]], base=0, channel_multiplier=1,
                          allow_small_or_imprecise_dtypes=True).then_inc(s_const, 1)
                pool.wait_ge(s_const, 9)
                pool.affine_select(out=upper[:, :], in_=upper[:, :], compare_op=ALU.is_gt, fill=0.0,
                                   base=0, pattern=[[1, P]], channel_multiplier=-1).then_inc(s_const, 1)

            @block.tensor
            def _(pe):
                def turn(c):
                    for b in range(KD):
                        n = 4 * c + b
                        if n >= 2:
                            pe.wait_ge(s_tlo, n - 1)
                        for j in range(TC):
                            mm = pe.transpose(bank[n % 2][:, j * P:(j + 1) * P], k.x[:, c * TC + j, b * P:(b + 1) * P], k.ident[:, :])
                        mm.then_inc(s_tps, 1)

                def logits(c):
                    pe.wait_ge(s_tlo, 4 * c + 4)
                    if c >= 2:
                        pe.wait_ge(s_sig, c - 1)
                    for b in range(KD):
                        t = slice(c * CH, (c + 1) * CH)
                        mm = mm3(pe, bank[6 + c % 2][:, :], wa_hi[:, b, :], wa_lo[:, b, :], xt_hi[:, b, t], xt_lo[:, b, t], b == 0, b == KD - 1)
                    mm.then_inc(s_lg, 1)

                def affinities_back(c):
                    pe.wait_ge(s_sig, c + 1)
                    for j in range(TC):
                        i = c * TC + j
                        mm = pe.transpose(bank[5][:, i * E0:(i + 1) * E0], aff_t[:, c % 2, j * P:(j + 1) * P], k.ident[0:E0, 0:E0])
                    mm.then_inc(s_back, 1)

                def gate_up(c, u):
                    n = c * NU + u
                    s, f = u // FB, u % FB
                    if c == 0:
                        pe.wait_ge(s_wlo, 2 + s)
                    if n == 1:
                        pe.wait_ge(s_aff, 1)
                    if n >= 2:
                        pe.wait_ge(s_h, n - 1)
                    fs = slice(f * P, (f + 1) * P)
                    t = slice(c * CH, (c + 1) * CH)
                    for a in range(2):
                        for b in range(KD):
                            mm = mm3(pe, bank[2 + 2 * a + n % 2][:, :], w1_hi[:, s, a, b, fs], w1_lo[:, s, a, b, fs],
                                     xt_hi[:, b, t], xt_lo[:, b, t], b == 0, b == KD - 1)
                    mm.then_inc(s_gu, 1)

                def turn_comb(c):
                    if c == 0:
                        pe.wait_ge(s_ca, 1)
                    else:
                        pe.wait_ge(s_col, 1)
                        pe.wait_ge(s_cts, c)
                    for j in range(TC):
                        mm = pe.transpose(bank[0 if c else 1][0:EA, j * P:(j + 1) * P], comb_aug[:, c * TC + j, :], k.ident[:, :])
                    mm.then_inc(s_ct, 1)

                def down(c):
                    if c == 0:
                        pe.wait_ge(s_wlo, 4)
                        pe.wait_ge(s_b2, 16)
                    pe.wait_ge(s_cts, c + 1)
                    pe.wait_ge(s_hlo, NU * c + NU)
                    for i in range(4 * c, 4 * c + 4):
                        if i >= 2:
                            pe.wait_ge(s_res, i - 1)
                        t = slice(i % 4 * P, (i % 4 + 1) * P)
                        for u in range(NU):
                            mm3(pe, bank[6 + i % 2][:, :], h_hi[:, u, t], h_lo[:, u, t], w2_hi[:, u, :], w2_lo[:, u, :],
                                u == 0, False)
                        mm = pe.matmul(bank[6 + i % 2][:, :], comb_t[:, c % 2, t], b2, start=False, stop=True)
                        mm.then_inc(s_dn, 1)

                def prefix():
                    pe.wait_ge(s_sel, 1)
                    pe.wait_ge(s_const, 10)
                    pe.matmul(bank[0][:, 0:256], upper[:, :], sel[:, :], start=True, stop=True)
                    pe.matmul(bank[0][:, 256:512], ones[:, :], sel[:, :], start=True, stop=True).then_inc(s_pre, 1)

                def table(n):
                    if n == 0:
                        pe.wait_ge(s_col, 1)
                    pe.wait_ge(s_row, 2 * n + 2)
                    for a in range(n * 8, n * 8 + 8):
                        pe.matmul(bank[1][:, 0:2 * NG0], at_row(a), at_col[:, a, :], start=(a == 0),
                                  stop=(a == 2 * NT - 1)).then_inc(s_rowfree, 1)

                turn(0)
                pe.wait_ge(s_wlo, 1)
                for c in range(NC):
                    if c + 1 < NC:
                        turn(c + 1)
                    logits(c)
                    if c:
                        affinities_back(c - 1)
                affinities_back(NC - 1)
                gate_up(0, 0)
                gate_up(0, 1)
                prefix()
                gate_up(0, 2)
                gate_up(0, 3)
                for c in range(NC):
                    if c == 0:
                        turn_comb(0)
                    for u in range(NU):
                        if c + 1 < NC:
                            if u == 1:
                                down(c)
                                turn_comb(c + 1)
                            gate_up(c + 1, u)
                        if c == 1 and u:
                            table(u - 1)
                    if c == 1:
                        table(NU - 1)
                down(NC - 1)

            @block.scalar
            def _(act):
                act.wait_ge(s_wa, 16)
                act.wait_ge(s_waz, 2)
                act.activation(wa_hi[:, :, 0:E0], wa_raw[:, :, :], ACT.Copy).then_inc(s_whi, 1)

                def sigmoid(c):
                    act.wait_ge(s_lg, c + 1)
                    if c >= 2:
                        act.wait_ge(s_back, c - 1)
                    act.activation(aff_t[:, c % 2, :], bank[6 + c % 2][0:E0, :], ACT.Sigmoid).then_inc(s_sig, 1)

                for n in range(4 * NC):
                    act.wait_ge(s_tps, n + 1)
                    act.activation(xt_hi[:, n % 4, n // 4 * CH:(n // 4 + 1) * CH], bank[n % 2][:, :], ACT.Copy).then_inc(s_thi, 1)
                    if n in (3, 7):
                        s = n // 4
                        act.wait_ge(s_w1[s], 32)
                        act.activation(w1_hi[:, s, :, :, :].rearrange("p a b n -> p (a b n)"), sraw[:, s, :],
                                       ACT.Copy).then_inc(s_whi, 1)
                    if n % 4 == 3 and n > 3:
                        sigmoid(n // 4 - 1)
                sigmoid(NC - 1)
                act.wait_ge(s_back, NC)
                act.activation(aff[:, :, :].rearrange("p t e -> p (t e)"), bank[5][:, 0:NT * E0], ACT.Copy).then_inc(s_aff, 1)
                act.wait_ge(s_w2, 16)
                act.activation(w2_hi[:, :, :].rearrange("p u n -> p (u n)"), sraw[:, 0, :], ACT.Copy).then_inc(s_whi, 1)
                act.wait_ge(s_b, 64)

                def copy_comb(c):
                    act.wait_ge(s_wlo, 3)
                    act.wait_ge(s_ct, c + 1)
                    if c >= 2:
                        act.wait_ge(s_dn, TC * (c - 1))
                    act.activation(comb_t[:, c % 2, :], bank[0 if c else 1][0:EA, :], ACT.Copy).then_inc(s_cts, 1)

                for n in range(NC * NU):
                    if n % NU == 1 and n > NU:
                        copy_comb(n // NU)
                    if n == NU:
                        copy_comb(0)
                    act.wait_ge(s_gu, n + 1)
                    if n:
                        act.wait_ge(s_h, n)
                    act.activation(ge[:, :], bank[2 + n % 2][:, :], ACT.Gelu, bias=gb[:, n % NU:n % NU + 1]).then_inc(s_ge, 1)

            @block.vector
            def _(vec):
                done = [0]

                def step(ins):
                    ins.then_inc(s_r, 1)
                    done[0] += 1

                def sync():
                    vec.wait_ge(s_r, done[0])

                def split_lo(n, lo, raw, hi):
                    vec.wait_ge(s_whi, n + 1)
                    vec.tensor_tensor(lo, raw, hi, ALU.subtract).then_inc(s_wlo, 1)

                def hidden(c, u):
                    n = c * NU + u
                    vec.wait_ge(s_ge, n + 1)
                    if c:
                        vec.wait_ge(s_dn, 4 * c)
                    up = bank[4 + n % 2][:, :]
                    if n >= 2:
                        vec.wait_ge(s_hlo, n - 1)
                    hfn = hf[:, n % 2, :]
                    vec.scalar_tensor_tensor(hfn, up, ub[:, u:u + 1], ge[:, :], ALU.add, ALU.mult).then_inc(s_h, 1)
                    vec.wait_ge(s_h, n + 1)
                    vec.tensor_copy(h_hi[:, u, :], hfn).then_inc(s_hh, 1)
                    vec.wait_ge(s_hh, n + 1)
                    vec.tensor_tensor(h_lo[:, u, :], hfn, h_hi[:, u, :], ALU.subtract).then_inc(s_hlo, 1)

                def residual(c):
                    if c == 0:
                        vec.wait_ge(k.s_rows, 16 * NC)
                    for i in range(4 * c, 4 * c + 4):
                        vec.wait_ge(s_dn, i + 1)
                        vec.scalar_tensor_tensor(k.x[:, i, :], k.x[:, i, :], 2.0, bank[6 + i % 2][:, :],
                                                 ALU.mult, ALU.add).then_inc(s_res, 1)

                def top2():
                    vec.wait_ge(s_aff, 1)
                    for i in range(NT):
                        step(vec.max(top[:, i, :], aff[:, i, :]))
                    sync()
                    for i in range(NT):
                        step(vec.max_index(arg[:, i, :], top[:, i, :], aff[:, i, :]))
                    sync()
                    step(vec.tensor_copy(argf[:, :, :], arg[:, :, 0:2].rearrange("p t k -> p k t")))
                    vec.wait_ge(s_const, 10)
                    sync()
                    step(vec.tensor_tensor(onehot[:, :, :, :].rearrange("p k t e -> p (k t) e"),
                                           iota_e[:, :].unsqueeze(1).to_broadcast([P, 2 * NT, E0]),
                                           argf[:, :, :].rearrange("p k t -> p (k t)").unsqueeze(2).to_broadcast([P, 2 * NT, E0]),
                                           ALU.is_equal))
                    sync()
                    vec.tensor_tensor(sel[:, :], onehot[:, 0, :, :].rearrange("p t e -> p (t e)"),
                                      onehot[:, 1, :, :].rearrange("p t e -> p (t e)"), ALU.add).then_inc(s_sel, 1)
                    step(vec.tensor_tensor(rsum[:, :], top[:, :, 0], top[:, :, 1], ALU.add))
                    sync()
                    step(vec.reciprocal(rsum[:, :], rsum[:, :]))
                    sync()
                    step(vec.tensor_tensor(k.weight[:, :, :], top[:, :, 0:2].rearrange("p t k -> p k t"),
                                           rsum[:, :].unsqueeze(1).to_broadcast([P, 2, NT]), ALU.mult))
                    sync()
                    step(vec.tensor_tensor(prod[:, :, :], onehot[:, :, :, :].rearrange("p k t e -> p (k t) e"),
                                           k.weight[:, :, :].rearrange("p k t -> p (k t)").unsqueeze(2).to_broadcast([P, 2 * NT, E0]),
                                           ALU.mult))
                    sync()
                    vec.tensor_tensor(comb_aug[:, :, 0:E0], prod[:, 0:NT, :], prod[:, NT:2 * NT, :], ALU.add).then_inc(s_ca, 1)
                    vec.wait_ge(s_ca, 1)

                def positions():
                    vec.wait_ge(s_pre, 1)
                    flat = lambda a: a[:, :, :].rearrange("p t e -> p (t e)")
                    step(vec.tensor_copy(flat(tot), bank[0][:, 256:512]))
                    step(vec.tensor_copy(flat(run_a), bank[0][:, 256:512]))
                    a, b = run_a, run_b
                    for d in (1, 2, 4, 8):
                        sync()
                        step(vec.tensor_tensor(b[:, d:, :], a[:, d:, :], a[:, :NT - d, :], ALU.add))
                        step(vec.tensor_copy(b[:, :d, :], a[:, :d, :]))
                        a, b = b, a
                    sync()
                    step(vec.tensor_scalar(cnt_i[:, :], a[:, NT - 1, :], 1 / GRP, (GRP - 1) / GRP + FLOOR, ALU.mult, ALU.add))
                    step(vec.tensor_tensor(flat(b), flat(a), flat(tot), ALU.subtract))
                    sync()
                    step(vec.tensor_copy(groups[:, :], cnt_i[:, :]))
                    step(vec.tensor_tensor(flat(b), bank[0][:, 0:256], flat(b), ALU.add))
                    sync()
                    step(vec.tensor_tensor_scan(ends[:, :], ones16[:, :], groups[:, :], 0.0, ALU.mult, ALU.add))
                    step(vec.tensor_tensor(prod[:, :, :].rearrange("p (k t) e -> p k (t e)", k=2),
                                           onehot[:, :, :, :].rearrange("p k t e -> p k (t e)"),
                                           flat(b).unsqueeze(1).to_broadcast([P, 2, NT * E0]), ALU.mult))
                    sync()
                    step(vec.tensor_reduce(posk[:, :], prod[:, :, :], AX.X, ALU.add))
                    step(vec.tensor_tensor(start2[:, :], ends[:, :], groups[:, :], ALU.subtract))
                    sync()
                    step(vec.tensor_scalar(start2[:, :], start2[:, :], float(GRP // P), None, ALU.mult))
                    step(vec.tensor_scalar(fl_i[:, :], posk[:, :], 1 / P, FLOOR, ALU.mult, ALU.add))
                    sync()
                    step(vec.tensor_tensor(prod[:, :, :], onehot[:, :, :, :].rearrange("p k t e -> p (k t) e"),
                                           start2[:, :].unsqueeze(1).to_broadcast([P, 2 * NT, E0]), ALU.mult))
                    step(vec.tensor_copy(fl[:, :], fl_i[:, :]))
                    sync()
                    step(vec.tensor_reduce(st[:, :], prod[:, :, :], AX.X, ALU.add))
                    step(vec.scalar_tensor_tensor(pp[:, :], fl[:, :], -float(P), posk[:, :], ALU.mult, ALU.add))
                    sync()
                    step(vec.tensor_tensor(st[:, :], st[:, :], fl[:, :], ALU.add))
                    sync()
                    step(vec.scalar_tensor_tensor(k.slot[:, :, :].rearrange("p k t -> p (k t)"), st[:, :], float(P), pp[:, :],
                                                  ALU.mult, ALU.add))

                def columns():
                    step(vec.tensor_tensor(at_col[:, :, :], iota_s[:, :].unsqueeze(1).to_broadcast([P, 2 * NT, 2 * NG0]),
                                           st[:, :].unsqueeze(2).to_broadcast([P, 2 * NT, 2 * NG0]), ALU.is_equal))
                    sync()
                    for kk in range(2):
                        last = vec.tensor_tensor(at_col[:, kk * NT:(kk + 1) * NT, :], at_col[:, kk * NT:(kk + 1) * NT, :].bitcast(F32),
                                                 tok[:, :].unsqueeze(2).to_broadcast([P, NT, 2 * NG0]), ALU.mult)
                    last.then_inc(s_col, 1)

                def rows(n):
                    if n == 0:
                        vec.wait_ge(s_gu, NU)
                    if n >= 2:
                        vec.wait_ge(s_rowfree, 8 * (n - 1))
                    shape = [P, 4, P]
                    for a in (8 * n, 8 * n + 4):
                        vec.tensor_tensor(xt_hi[:, a // 4 % 4, 0:CH].rearrange("p (r s) -> p r s", r=4),
                                          iota_p[:, :].unsqueeze(1).to_broadcast(shape), pp[:, a:a + 4].unsqueeze(2).to_broadcast(shape),
                                          ALU.is_equal).then_inc(s_row, 1)

                def group_tables():
                    step(vec.tensor_tensor(gsel[:, :, :], iota_g[:, :].unsqueeze(2).to_broadcast([P, NG0, E0]),
                                           ends[:, :].unsqueeze(1).to_broadcast([P, NG0, E0]), ALU.is_ge))
                    sync()
                    step(vec.tensor_reduce(gef[:, :], gsel[:, :, :], AX.X, ALU.add))
                    sync()
                    step(vec.tensor_scalar(gef[:, :], gef[:, :], float(E0 - 1), None, ALU.min))
                    sync()
                    step(vec.tensor_copy(k.group_expert[:, :], gef[:, :]))
                    step(vec.tensor_tensor(gsel[:, :, :], iota_e[:, :].unsqueeze(1).to_broadcast([P, NG0, E0]),
                                           gef[:, :].unsqueeze(2).to_broadcast([P, NG0, E0]), ALU.is_equal))
                    vec.wait_ge(s_b, 64)
                    for a, table in enumerate((rgb, rub)):
                        for f in range(FB):
                            sync()
                            step(vec.tensor_tensor(gprod[:, :, :], gsel[:, :, :], table[:, f, :].unsqueeze(1).to_broadcast([P, NG0, E0]),
                                                   ALU.mult))
                            sync()
                            step(vec.tensor_reduce(k.group_bias[:, :, 2 * a + f], gprod[:, :, :], AX.X, ALU.add))

                split_lo(0, wa_lo[:, :, 0:E0], wa_raw[:, :, :], wa_hi[:, :, 0:E0])
                for n in range(4 * NC):
                    vec.wait_ge(s_thi, n + 1)
                    t = slice(n // 4 * CH, (n // 4 + 1) * CH)
                    vec.tensor_tensor(xt_lo[:, n % 4, t], bank[n % 2][:, :], xt_hi[:, n % 4, t], ALU.subtract).then_inc(s_tlo, 1)
                    if n in (7, 11):
                        s = (n - 7) // 4
                        split_lo(1 + s, w1_lo[:, s, :, :, :].rearrange("p a b n -> p (a b n)"), sraw[:, s, :],
                                 w1_hi[:, s, :, :, :].rearrange("p a b n -> p (a b n)"))
                top2()
                vec.wait_ge(s_b, 64)
                hidden(0, 0)
                split_lo(3, w2_lo[:, :, :].rearrange("p u n -> p (u n)"), sraw[:, 0, :], w2_hi[:, :, :].rearrange("p u n -> p (u n)"))
                hidden(0, 1)
                positions()
                hidden(0, 2)
                columns()
                hidden(0, 3)
                for c in range(NC):
                    for u in range(NU):
                        if c + 1 < NC:
                            if u == 0:
                                residual(c)
                            hidden(c + 1, u)
                        if c == 1:
                            rows(u)
                    if c == 1:
                        vec.wait_ge(s_rowfree, 2 * NT)
                        step(vec.tensor_copy(k.token_of[:, :], bank[1][:, 0:2 * NG0]))
                    if c == 2:
                        group_tables()
                residual(NC - 1)


def experts0_routed(k):
    nc, bank, io = k.nc, k.bank, k.io
    FB, S = F0 // P, GRP // P
    W = KD * F0
    with ExitStack() as ctx:
        sb = lambda name, shape, dt=F32: k.sb("e0_" + name, shape, dt, ctx)
        raw = [sb(f"raw{p}", [P, 3 * W]) for p in range(2)]
        w_hi = [sb(f"w_hi{p}", [P, 3 * W], F32R) for p in range(2)]
        w_lo = [sb(f"w_lo{p}", [P, 3 * W], F32R) for p in range(2)]
        index = [sb(f"index{p}", [P, S], I32) for p in range(2)]
        bias = [sb(f"bias{p}", [P, 2 * FB]) for p in range(2)]
        xg = [sb(f"xg{p}", [P, S, D]) for p in range(2)]
        xt_hi = [sb(f"xt_hi{p}", [P, KD, GRP], F32R) for p in range(2)]
        xt_lo = [sb(f"xt_lo{p}", [P, KD, GRP], F32R) for p in range(2)]
        ge = [sb(f"ge{p}", [P, FB, GRP]) for p in range(2)]
        hf = [sb(f"hf{p}", [P, FB, GRP]) for p in range(2)]
        h_hi = [sb(f"h_hi{p}", [P, FB, GRP], F32R) for p in range(2)]
        h_lo = [sb(f"h_lo{p}", [P, FB, GRP], F32R) for p in range(2)]
        y = [sb(f"y{p}", [P, S, D]) for p in range(2)]

        two = lambda name: [k.sem(f"e0_{name}{p}") for p in range(2)]
        s_w, s_v, s_g, s_y = two("gate_up_loaded"), two("down_loaded"), two("rows_gathered"), two("results_stored")
        s_go = k.sem("e0_index_seen")
        s_ix, s_bias = k.sem("e0_index"), k.sem("e0_bias")
        s_whi, s_wlo = k.sem("e0_gate_up_hi"), k.sem("e0_gate_up_lo")
        s_vhi, s_vlo = k.sem("e0_down_hi"), k.sem("e0_down_lo")
        s_tps, s_thi, s_tlo = k.sem("e0_turned"), k.sem("e0_turned_hi"), k.sem("e0_turned_lo")
        s_gu, s_ge, s_h, s_hh, s_hlo = (k.sem("e0_" + n) for n in ("gate_up", "gelu", "hidden", "hidden_hi", "hidden_lo"))
        s_dn, s_ysb = k.sem("e0_down"), k.sem("e0_results")
        nothing = lambda h, p: None
        y_rows = k.y0.rearrange("(g s p) d -> g p s d", p=P, s=S)

        with nc.Block() as block:
            @block.sync
            def _(sp):
                def load(h, p):
                    g = 2 * h + p
                    e = sp.value_load(k.group_expert[0:1, bass.ds(g, 1)], min_val=0, max_val=E0 - 1)
                    if started(h):
                        sp.wait_ge(s_wlo, g - 1)
                    for a, name in enumerate(("rg", "rw1")):
                        sp.dma_start(raw[p][:, a * W:(a + 1) * W].rearrange("p (b n) -> p b n", b=KD),
                                     io[name][bass.ds(e, 1)].rearrange("e (b p) n -> p (e b) n", p=P)).then_inc(s_w[p], 16)
                    if started(h):
                        sp.wait_ge(s_vlo, g - 1)
                    sp.dma_start(raw[p][:, 2 * W:].rearrange("p (f n) -> p f n", f=FB),
                                 io["rw2"][bass.ds(e, 1)].rearrange("e (f p) n -> p (e f) n", p=P)).then_inc(s_v[p], 16)

                three_stages(sp, NG0, load, nothing, nothing)

            @block.gpsimd
            def _(pool):
                def gather(h, p):
                    g = 2 * h + p
                    if started(h):
                        pool.wait_ge(s_g[p], 16 * S * h)
                        pool.wait_ge(s_tps, g - 1)
                    pool.tensor_copy(index[p][:, :], k.token_of[:, bass.ds(S * g, S)]).then_inc(s_ix, 1)
                    pool.wait_ge(s_ix, g + 1)
                    pool.sem_inc(s_go, 1)
                    for s in range(S):
                        pool.indirect_dma_start(xg[p][:, s, :], None, k.rows, bass.IndirectOffsetOnAxis(index[p][:, s:s + 1], 0)
                                                ).then_inc(s_g[p], 16)

                three_stages(pool, NG0, gather, nothing, nothing)

            @block.tensor
            def _(pe):
                def turn(h, p):
                    g = 2 * h + p
                    pe.wait_ge(s_g[p], 16 * S * (h + 1))
                    if started(h) or p:
                        pe.wait_ge(s_tlo, g)
                    for b in range(KD):
                        for s in range(S):
                            c = (b % 2 * S + s) * P
                            mm = pe.transpose(bank[b // 2][:, c:c + P], xg[p][:, s, b * P:(b + 1) * P], k.ident[:, :])
                    mm.then_inc(s_tps, 1)

                def gate_up(h, p):
                    g = 2 * h + p
                    pe.wait_ge(s_wlo, g + 1)
                    pe.wait_ge(s_tlo, g + 1)
                    if started(h):
                        pe.wait_ge(s_h, g - 1)
                    for a in range(2):
                        for f in range(FB):
                            for b in range(KD):
                                c = slice(a * W + b * F0 + f * P, a * W + b * F0 + f * P + P)
                                mm = mm3(pe, bank[2 + 2 * a + p][:, f * GRP:(f + 1) * GRP], w_hi[p][:, c], w_lo[p][:, c],
                                         xt_hi[p][:, b, :], xt_lo[p][:, b, :], b == 0, b == KD - 1)
                    mm.then_inc(s_gu, 1)

                def down(h, p):
                    g = 2 * h + p
                    pe.wait_ge(s_hlo, g + 1)
                    pe.wait_ge(s_vlo, g + 1)
                    if started(h) or p:
                        pe.wait_ge(s_ysb, g)
                    for s in range(S):
                        for f in range(FB):
                            t, c = slice(s * P, (s + 1) * P), slice(2 * W + f * D, 2 * W + (f + 1) * D)
                            mm = mm3(pe, bank[6 + s][:, :], h_hi[p][:, f, t], h_lo[p][:, f, t], w_hi[p][:, c], w_lo[p][:, c],
                                     f == 0, f == FB - 1)
                    mm.then_inc(s_dn, 1)

                three_stages(pe, NG0, turn, gate_up, down)

            @block.scalar
            def _(act):
                def split(h, p):
                    g = 2 * h + p
                    act.wait_ge(s_w[p], 32 * (h + 1))
                    if started(h):
                        act.wait_ge(s_gu, g - 1)
                    act.activation(w_hi[p][:, 0:2 * W], raw[p][:, 0:2 * W], ACT.Copy).then_inc(s_whi, 1)
                    act.wait_ge(s_tps, g + 1)
                    for q in range(2):
                        last = act.activation(xt_hi[p][:, 2 * q:2 * q + 2, :].rearrange("p b t -> p (b t)"), bank[q][:, :], ACT.Copy)
                    last.then_inc(s_thi, 1)

                def gelu(h, p):
                    g = 2 * h + p
                    act.wait_ge(s_v[p], 16 * (h + 1))
                    if started(h):
                        act.wait_ge(s_dn, g - 1)
                    act.activation(w_hi[p][:, 2 * W:], raw[p][:, 2 * W:], ACT.Copy).then_inc(s_vhi, 1)
                    act.wait_ge(s_gu, g + 1)
                    act.wait_ge(s_bias, g + 1)
                    if started(h):
                        act.wait_ge(s_h, g - 1)
                    for f in range(FB):
                        last = act.activation(ge[p][:, f, :], bank[2 + p][:, f * GRP:(f + 1) * GRP], ACT.Gelu, bias=bias[p][:, f:f + 1])
                    last.then_inc(s_ge, 1)

                def results(h, p):
                    g = 2 * h + p
                    act.wait_ge(s_dn, g + 1)
                    if started(h):
                        act.wait_ge(s_y[p], 16 * h)
                    for s in range(S):
                        last = act.activation(y[p][:, s, :], bank[6 + s][:, :], ACT.Copy)
                    last.then_inc(s_ysb, 1)
                    act.wait_ge(s_ysb, g + 1)
                    act.dma_start(y_rows[bass.ds(g, 1)].rearrange("g p s d -> p (g s) d"), y[p][:, :, :]).then_inc(s_y[p], 16)

                three_stages(act, NG0, split, gelu, results)
                act.wait_ge(s_y[0], 16 * ((NG0 + 1) // 2))
                act.wait_ge(s_y[1], 16 * (NG0 // 2))

            @block.vector
            def _(vec):
                def split(h, p):
                    g = 2 * h + p
                    if started(h):
                        vec.wait_ge(s_h, g - 1)
                    vec.tensor_copy(bias[p][:, :], k.group_bias[:, bass.ds(g, 1), :].rearrange("p g a -> p (g a)")).then_inc(s_bias, 1)
                    vec.wait_ge(s_whi, g + 1)
                    vec.tensor_tensor(w_lo[p][:, 0:2 * W], raw[p][:, 0:2 * W], w_hi[p][:, 0:2 * W], ALU.subtract).then_inc(s_wlo, 1)
                    vec.wait_ge(s_thi, g + 1)
                    for q in range(2):
                        part = lambda a: a[p][:, 2 * q:2 * q + 2, :].rearrange("p b t -> p (b t)")
                        last = vec.tensor_tensor(part(xt_lo), bank[q][:, :], part(xt_hi), ALU.subtract)
                    last.then_inc(s_tlo, 1)

                def hidden(h, p):
                    g = 2 * h + p
                    vec.wait_ge(s_vhi, g + 1)
                    vec.tensor_tensor(w_lo[p][:, 2 * W:], raw[p][:, 2 * W:], w_hi[p][:, 2 * W:], ALU.subtract).then_inc(s_vlo, 1)
                    vec.wait_ge(s_ge, g + 1)
                    if started(h):
                        vec.wait_ge(s_hlo, g - 1)
                    for f in range(FB):
                        last = vec.scalar_tensor_tensor(hf[p][:, f, :], bank[4 + p][:, f * GRP:(f + 1) * GRP],
                                                        bias[p][:, FB + f:FB + f + 1], ge[p][:, f, :], ALU.add, ALU.mult)
                    last.then_inc(s_h, 1)
                    vec.wait_ge(s_h, g + 1)
                    if started(h):
                        vec.wait_ge(s_dn, g - 1)
                    vec.tensor_copy(h_hi[p][:, :, :], hf[p][:, :, :]).then_inc(s_hh, 1)
                    vec.wait_ge(s_hh, g + 1)
                    vec.tensor_tensor(h_lo[p][:, :, :], hf[p][:, :, :], h_hi[p][:, :, :], ALU.subtract).then_inc(s_hlo, 1)

                three_stages(vec, NG0, split, hidden, nothing)


H1, DH1, FM = 16, 32, 64
NP = H1 // 2
VA = 2 * (DH1 + 1)


def attention1(k):
    with ExitStack() as ctx:
        xt = tuple(k.sb("a1_xt_" + n, [P, KD, T], F32R, ctx) for n in ("hi", "lo"))
        sb = lambda name, shape, dt=F32: k.sb("a1_" + name, shape, dt, ctx)
        w = {"fw1_hi": sb("fw1_hi", [P, 4 * FM], F32R), "fw1_lo": sb("fw1_lo", [P, 4 * FM], F32R),
             "kv": sb("kv", [P, NP, VA]), "vsum": sb("vsum", [P, NP * VA]),
             "raw": sb("raw", [P, KD, D]),
             "fw2": sb("fw2", [P, P]), "fw2_t": sb("fw2_t", [P, P]),
             "fb2": sb("fb2", [P, 1]), "qb": sb("qb", [P, KD]), "fb1": sb("fb1", [P, 1]),
             "s_qw": k.sem("a1_qw_loaded"), "s_small": k.sem("a1_small_loaded")}
        attention1_keys(k, xt, w)
        attention1_queries(k, xt, w)


def attention1_keys(k, xt, w):
    nc, bank, io = k.nc, k.bank, k.io
    xt_hi, xt_lo = xt
    fw1_hi, fw1_lo, kv, vsum = w["fw1_hi"], w["fw1_lo"], w["kv"], w["vsum"]
    CK, TK = 2 * P, 2
    with ExitStack() as ctx:
        sb = lambda name, shape, dt=F32: k.sb("k1_" + name, shape, dt, ctx)
        raw = w["raw"]
        kw_hi, kw_lo = sb("kw_hi", [P, KD, D], F32R), sb("kw_lo", [P, KD, D], F32R)
        vw_hi, vw_lo = sb("vw_hi", [P, KD, D], F32R), sb("vw_lo", [P, KD, D], F32R)
        fw1_raw = sb("fw1_raw", [P, FM])
        kb = sb("kb", [P, KD])
        vb = sb("vb", [P, D])
        fb1 = sb("fb1", [2, FM])
        part = sb("part", [2, 1])
        rest = sb("rest", [2, 1])
        fb_hi, fb_lo = sb("fb_hi", [2, FM], F32R), sb("fb_lo", [2, FM])
        fb_hl = sb("fb_hl", [2, 4, FM], F32R)
        ones_f, ones2 = sb("ones_f", [2, P]), sb("ones2", [2, P], F32R)
        k_hi, k_lo = sb("k_hi", [P, 2, KD, CK], F32R), sb("k_lo", [P, 2, KD, CK], F32R)
        vf = sb("vf", [P, NP * VA])
        v_hl = sb("v_hl", [P, 2, NP, 2, VA], F32R)
        v_hi, v_lo = v_hl[:, :, :, 0, :], v_hl[:, :, :, 1, :]
        SUMS = [(1, 6, 7)[q // 3] for q in range(NP)]
        sum_of = lambda q, l: slice(q % 3 * 2 * VA + l * VA, q % 3 * 2 * VA + (l + 1) * VA)
        yg = [sb(f"yg{n}", [P, 2, D]) for n in range(2)]
        ex, gf = sb("ex", [P, 2, CH]), sb("gf", [P, 2, CH])
        g_hi, g_lo = sb("g_hi", [P, 2, 2 * CH], F32R), sb("g_lo", [P, 2, 2 * CH], F32R)

        sem = lambda n: k.sem("k1_" + n)
        s_kw, s_vw, s_fw, s_kb, s_vb, s_fb = (sem(n) for n in ("kw_loaded", "vw_loaded", "fw1_loaded", "kb_loaded", "vb_loaded", "fb1_loaded"))
        s_zero, s_whi, s_wlo = sem("zeroed"), sem("weight_hi"), sem("weight_split")
        s_c = sem("fb1_chain")
        s_tps, s_thi, s_tlo = sem("turned"), sem("turned_hi"), sem("turned_lo")
        s_k, s_khi, s_klo = sem("keys"), sem("keys_hi"), sem("keys_split")
        s_v, s_vf, s_vhi, s_vlo, s_vs = sem("values"), sem("values_read"), sem("values_hi"), sem("values_lo"), sem("values_summed")
        s_g, s_gev, s_gf, s_ghi, s_glo = sem("features"), sem("features_read"), sem("features_made"), sem("features_hi"), sem("features_lo")
        s_kv, s_out = sem("kv_added"), sem("kv_copied")
        landing = lambda i: {2: ex, 3: gf}.get(i, yg[i % 2])
        s_gt = [sem(f"results_gathered{n}") for n in range(4)]
        gathered = lambda i: s_gt[i if i in (2, 3) else i % 2]
        users_before = lambda i: 1 if i < 4 else i // 2
        s_first, s_used, s_stat, s_var, s_rstd, s_ln = (sem(n) for n in ("first_added", "results_used", "stats", "var", "rstd", "normed"))
        heads = lambda a: a.rearrange("p (h e) -> p h e", e=DH1 + 1)

        idle = lambda n: None

        def schedule(turn=idle, keys=idle, tile=idle, before_tile=idle, after_tile=idle, combine=idle, rstd=idle, normalise=idle):
            for c in range(3):
                combine(2 * c)
                combine(2 * c + 1)
                rstd(c)
                normalise(c)
                if c < 2:
                    turn(2 * c)
                    turn(2 * c + 1)
            keys(0)
            keys(1)
            for i in range(NT):
                if i + 6 < NT:
                    combine(i + 6)
                    if i % 2:
                        rstd((i + 5) // 2)
                if i + 4 < NT:
                    turn(i + 4)
                if i + 2 < NT:
                    keys(i + 2)
                if i % 2 and i + 6 < NT:
                    normalise((i + 5) // 2)
                if i:
                    before_tile(i - 1)
                tile(i)
                if i:
                    after_tile(i - 1)
            before_tile(NT - 1)
            after_tile(NT - 1)

        with nc.Block() as block:
            @block.sync
            def _(sp):
                sp.dma_start(raw[:, :, :], io["kw"].rearrange("(b p) n -> p b n", p=P)).then_inc(s_kw, 16)
                for h in range(4):
                    sp.dma_start(fw1_raw[h * DH1:(h + 1) * DH1, :], io["fw1"]).then_inc(s_fw, 16)
                sp.dma_start(kb[:, :], io["kb_t"]).then_inc(s_kb, 16)
                sp.dma_start(vb[:, :], io["vb"].partition_broadcast(P)).then_inc(s_vb, 16)
                sp.dma_start(fb1[:, :], io["fb1"].partition_broadcast(2)).then_inc(s_fb, 16)
                sp.wait_ge(s_wlo, 1)
                sp.dma_start(raw[:, :, :], io["vw"].rearrange("(b p) n -> p b n", p=P)).then_inc(s_vw, 16)
                sp.wait_ge(s_zero, 12)
                for h in range(2):
                    r = slice(h * FM, (h + 1) * FM)
                    sp.dma_start(w["fw2"][r, r], io["fw2"]).then_inc(w["s_small"], 16)
                    sp.dma_start(w["fw2_t"][r, r], io["fw2_t"]).then_inc(w["s_small"], 16)
                    sp.dma_start(w["fb2"][r, :], io["fb2"].rearrange("(f o) -> f o", o=1)).then_inc(w["s_small"], 16)
                    sp.dma_start(w["fb1"][r, :], io["fb1"].rearrange("(f o) -> f o", o=1)).then_inc(w["s_small"], 16)
                sp.dma_start(w["qb"][:, :], io["qb_t"]).then_inc(w["s_small"], 16)
                sp.wait_ge(s_wlo, 3)
                sp.dma_start(raw[:, :, :], io["qw"].rearrange("(b p) n -> p b n", p=P)).then_inc(w["s_qw"], 16)

            @block.gpsimd
            def _(pool):
                def gather(i):
                    for kk in range(2):
                        pool.indirect_dma_start(landing(i)[:, kk, :], None, k.y0, bass.IndirectOffsetOnAxis(k.slot[:, kk, i:i + 1], 0)
                                                ).then_inc(gathered(i), 16)

                for i in range(4):
                    gather(i)
                pool.memset(fw1_hi[:, :].bitcast(F32), 0.0).then_inc(s_zero, 1)
                pool.memset(fw1_lo[:, :].bitcast(F32), 0.0).then_inc(s_zero, 1)
                pool.memset(part[:, :], 0.0).then_inc(s_zero, 1)
                pool.memset(rest[:, :], 1.0).then_inc(s_zero, 1)
                pool.memset(ones_f[:, :], 1.0).then_inc(s_zero, 1)
                pool.memset(vf[:, :], 1.0).then_inc(s_zero, 1)
                pool.memset(kv[:, :, :], 0.0).then_inc(s_zero, 1)
                pool.memset(vsum[:, :], 0.0).then_inc(s_zero, 1)
                pool.wait_ge(s_zero, 8)
                pool.memset(part[0:1, :], 1.0).then_inc(s_zero, 1)
                pool.memset(rest[0:1, :], 0.0).then_inc(s_zero, 1)
                pool.memset(w["fw2"][:, :], 0.0).then_inc(s_zero, 1)
                pool.memset(w["fw2_t"][:, :], 0.0).then_inc(s_zero, 1)

                def combine(i):
                    if 4 <= i + 1 < NT:
                        pool.wait_ge(s_used, i - 2 if i < 5 else i)
                        gather(i + 1)

                def rstd(c):
                    pool.wait_ge(s_stat, 2 * TK * (c + 1))
                    ln_rstd(k, pool, c * TK, TK, s_var, s_rstd, c)

                def tile(i):
                    pool.wait_ge(s_vf, i + 1)
                    if i:
                        pool.wait_ge(s_vs, i)
                    pool.tensor_tensor(vsum[:, :], vsum[:, :], vf[:, :], ALU.add).then_inc(s_vs, 1)

                def tile_end(i):
                    for n in (2 * i, 2 * i + 1):
                        pool.wait_ge(s_ghi, n + 1)
                        part_of = slice((n % 2) * CH, (n % 2 + 1) * CH)
                        pool.tensor_tensor(g_lo[:, i % 2, part_of], gf[:, n % 2, :], g_hi[:, i % 2, part_of].bitcast(F32),
                                           ALU.subtract).then_inc(s_glo, 1)

                schedule(tile=tile, before_tile=tile_end, combine=combine, rstd=rstd)

            @block.tensor
            def _(pe):
                def turn(n):
                    c, half = n // 2, n % 2
                    if half == 0:
                        pe.wait_ge(s_ln, TK * (c + 1))
                    if n:
                        pe.wait_ge(s_tlo, n)
                    for b in range(2):
                        for j in range(TK):
                            o = (b * TK + j) * P
                            f = slice((2 * half + b) * P, (2 * half + b + 1) * P)
                            mm = pe.transpose(bank[0][:, o:o + P], k.x[:, c * TK + j, f], k.ident[:, :])
                    mm.then_inc(s_tps, 1)

                def keys(n):
                    c, half = n // 2, n % 2
                    if n == 0:
                        pe.wait_ge(s_wlo, 1)
                    pe.wait_ge(s_tlo, 2 * c + 2)
                    if n:
                        pe.wait_ge(s_klo, n)
                    for q in range(2):
                        m = slice((2 * half + q) * P, (2 * half + q + 1) * P)
                        for b in range(KD):
                            mm = mm3(pe, bank[2][:, q * CK:(q + 1) * CK], kw_hi[:, b, m], kw_lo[:, b, m],
                                     xt_hi[:, b, c * CK:(c + 1) * CK], xt_lo[:, b, c * CK:(c + 1) * CK], b == 0, b == KD - 1)
                    mm.then_inc(s_k, 1)

                def sums(i):
                    pe.wait_ge(s_glo, 2 * i + 2)
                    pe.wait_ge(s_vlo, i + 1)
                    for q in range(NP):
                        o, f = bank[SUMS[q]], slice(q * P, (q + 1) * P)
                        both = slice(sum_of(q, 0).start, sum_of(q, 1).stop)
                        pe.matmul(o[:, both], g_hi[:, i % 2, f], v_hl[:, i % 2, q, :, :].rearrange("p l v -> p (l v)"),
                                  start=i == 0 and q % 3 == 0, stop=False, skip_group_check=True)
                        mm = pe.matmul(o[:, sum_of(q, 0)], g_lo[:, i % 2, f], v_hi[:, i % 2, q, :], start=False, stop=i == NT - 1,
                                       skip_group_check=True)
                    mm.then_inc(s_kv, 1)

                def tile(i):
                    c, j = i // TK, i % TK
                    if i == 0:
                        pe.wait_ge(s_wlo, 3)
                    if j == 0:
                        pe.wait_ge(s_klo, 2 * c + 2)
                    if i:
                        pe.wait_ge(s_vf, i)
                    for b in range(KD):
                        mm = mm3(pe, bank[3][:, :], xt_hi[:, b, i * P:(i + 1) * P], xt_lo[:, b, i * P:(i + 1) * P],
                                 vw_hi[:, b, :], vw_lo[:, b, :], b == 0, b == KD - 1)
                    mm.then_inc(s_v, 1)
                    t = slice(j * P, (j + 1) * P)
                    for n in (2 * i, 2 * i + 1):
                        if i:
                            pe.wait_ge(s_gev, n - 1)
                        for a in range(2):
                            g = 2 * (n % 2) + a
                            o = bank[4 + n % 2][:, a * 256:(a + 1) * 256]
                            mm3(pe, o, k_hi[:, c % 2, g, t], k_lo[:, c % 2, g, t], fw1_hi[:, :], fw1_lo[:, :], True, False)
                            mm = pe.matmul(o, ones2[:, :], fb_hl[:, :, :].rearrange("p h f -> p (h f)"), start=False, stop=True)
                        mm.then_inc(s_g, 1)

                schedule(turn, keys, tile, after_tile=sums)

            @block.scalar
            def _(act):
                def weight(sem, dst):
                    act.wait_ge(sem, 16)
                    act.activation(dst[:, :, :], raw[:, :, :], ACT.Copy).then_inc(s_whi, 1)

                def turn(n):
                    c, half = n // 2, n % 2
                    act.wait_ge(s_tps, n + 1)
                    act.activation(xt_hi[:, 2 * half:2 * half + 2, c * CK:(c + 1) * CK], bank[0][:, :].rearrange("p (b t) -> p b t", b=2),
                                   ACT.Copy).then_inc(s_thi, 1)
                    if n == 1:
                        weight(s_kw, kw_hi)
                        act.wait_ge(s_kb, 16)

                def keys(n):
                    c, half = n // 2, n % 2
                    act.wait_ge(s_k, n + 1)
                    if n % 2 == 0 and c >= 2:
                        act.wait_ge(s_g, 2 * TK * (c - 1))
                    for q in range(2):
                        m = 2 * half + q
                        act.activation(k_hi[:, c % 2, m, :], bank[2][:, q * CK:(q + 1) * CK], ACT.Identity, bias=kb[:, m:m + 1]).then_inc(s_khi, 1)
                    if n == 1:
                        weight(s_vw, vw_hi)

                def tile(i):
                    act.wait_ge(s_vf, i + 1)
                    if i >= 2:
                        act.wait_ge(s_kv, i - 1)
                    act.activation(v_hi[:, i % 2, :, :], vf[:, :].rearrange("p (q v) -> p q v", v=VA), ACT.Copy).then_inc(s_vhi, 1)
                    for n in (2 * i, 2 * i + 1):
                        act.wait_ge(s_g, n + 1)
                        if i:
                            act.wait_ge(s_gf, n - 1)
                            act.wait_ge(s_glo, n - 1)
                        act.activation(ex[:, n % 2, :], bank[4 + n % 2][:, :], ACT.Exp)
                        act.activation(gf[:, n % 2, :], bank[4 + n % 2][:, :], ACT.Relu).then_inc(s_gev, 1)

                def tile_end(i):
                    if i >= 2:
                        act.wait_ge(s_kv, i - 1)
                    for n in (2 * i, 2 * i + 1):
                        act.wait_ge(s_gf, n + 1)
                        act.activation(g_hi[:, i % 2, (n % 2) * CH:(n % 2 + 1) * CH], gf[:, n % 2, :], ACT.Copy).then_inc(s_ghi, 1)

                schedule(turn, keys, tile, before_tile=tile_end)

            @block.vector
            def _(vec):
                def weight(n, raw_, hi, lo):
                    vec.wait_ge(s_whi, n)
                    vec.tensor_tensor(lo[:, :, :], raw_[:, :, :], hi[:, :, :], ALU.subtract).then_inc(s_wlo, 1)

                def feature_weights():
                    vec.wait_ge(s_fw, 64)
                    vec.wait_ge(s_zero, 10)
                    for h in range(4):
                        r, c = slice(h * DH1, (h + 1) * DH1), slice(h * FM, (h + 1) * FM)
                        vec.tensor_copy(fw1_hi[r, c], fw1_raw[r, :]).then_inc(s_c, 1)
                    vec.wait_ge(s_c, 4)
                    for h in range(4):
                        r, c = slice(h * DH1, (h + 1) * DH1), slice(h * FM, (h + 1) * FM)
                        vec.tensor_tensor(fw1_lo[r, c], fw1_raw[r, :], fw1_hi[r, c], ALU.subtract)
                    vec.wait_ge(s_fb, 16)
                    vec.tensor_copy(ones2[:, :], ones_f[:, :])
                    vec.tensor_copy(fb_hi[:, :], fb1[:, :]).then_inc(s_c, 1)
                    vec.wait_ge(s_c, 5)
                    vec.tensor_tensor(fb_lo[:, :], fb1[:, :], fb_hi[:, :], ALU.subtract).then_inc(s_c, 1)
                    vec.wait_ge(s_c, 6)
                    vec.tensor_scalar(fb_lo[:, :], fb_lo[:, :], rest[:, 0:1], None, ALU.mult).then_inc(s_c, 1)
                    vec.wait_ge(s_c, 7)
                    for h in range(4):
                        last = vec.scalar_tensor_tensor(fb_hl[:, h, :], fb_hi[:, :], part[:, 0:1], fb_lo[:, :], ALU.mult, ALU.add)
                    last.then_inc(s_wlo, 1)

                def turn(n):
                    c, half = n // 2, n % 2
                    vec.wait_ge(s_thi, n + 1)
                    part = lambda a: a[:, 2 * half:2 * half + 2, c * CK:(c + 1) * CK]
                    vec.tensor_tensor(part(xt_lo), bank[0][:, :].rearrange("p (b t) -> p b t", b=2), part(xt_hi), ALU.subtract).then_inc(s_tlo, 1)
                    if n == 1:
                        weight(1, raw, kw_hi, kw_lo)

                def keys(n):
                    c, half = n // 2, n % 2
                    if n % 2 == 0 and c >= 2:
                        vec.wait_ge(s_g, 2 * TK * (c - 1))
                    vec.wait_ge(s_khi, 2 * n + 2)
                    for q in range(2):
                        m = 2 * half + q
                        last = vec.scalar_tensor_tensor(k_lo[:, c % 2, m, :], bank[2][:, q * CK:(q + 1) * CK], kb[:, m:m + 1], k_hi[:, c % 2, m, :],
                                                        ALU.add, ALU.subtract)
                    last.then_inc(s_klo, 1)
                    if n == 1:
                        feature_weights()
                        weight(2, raw, vw_hi, vw_lo)
                        vec.wait_ge(s_vb, 16)

                def tile(i):
                    vec.wait_ge(s_v, i + 1)
                    if i:
                        vec.wait_ge(s_vs, i)
                        vec.wait_ge(s_vlo, i)
                    vec.tensor_tensor(heads(vf[:, :])[:, :, 0:DH1], bank[3][:, :].rearrange("p (h e) -> p h e", e=DH1),
                                      vb[:, :].rearrange("p (h e) -> p h e", e=DH1), ALU.add).then_inc(s_vf, 1)
                    vec.wait_ge(s_vhi, i + 1)
                    vec.tensor_tensor(v_lo[:, i % 2, :, :], vf[:, :].rearrange("p (q v) -> p q v", v=VA), v_hi[:, i % 2, :, :],
                                      ALU.subtract).then_inc(s_vlo, 1)
                    for n in (2 * i, 2 * i + 1):
                        vec.wait_ge(s_gev, n + 1)
                        vec.scalar_tensor_tensor(gf[:, n % 2, :], ex[:, n % 2, :], 1.0, gf[:, n % 2, :], ALU.min, ALU.add).then_inc(s_gf, 1)

                def combine(i):
                    xi, y = k.x[:, i, :], landing(i)
                    vec.wait_ge(gathered(i), 32 * users_before(i))
                    vec.scalar_tensor_tensor(xi, y[:, 0, :], k.weight[:, 0, i:i + 1], xi, ALU.mult, ALU.add).then_inc(s_first, 1)
                    vec.wait_ge(s_first, i + 1)
                    vec.scalar_tensor_tensor(xi, y[:, 1, :], k.weight[:, 1, i:i + 1], xi, ALU.mult, ALU.add).then_inc(s_used, 1)
                    vec.wait_ge(s_used, i + 1)
                    ln_stats(k, vec, i, s_stat, i)

                def normalise(c):
                    vec.wait_ge(s_rstd, c + 1)
                    for i in range(c * TK, c * TK + TK):
                        ln_apply(k, vec, i).then_inc(s_ln, 1)

                schedule(turn, keys, tile, combine=combine, normalise=normalise)
                vec.wait_ge(s_kv, NT)
                for lo in range(2):
                    for q in range(NP):
                        for h in range(2):
                            r, c = slice(h * FM, (h + 1) * FM), slice(h * (DH1 + 1), (h + 1) * (DH1 + 1))
                            src = bank[SUMS[q]][r, sum_of(q, lo)][:, c]
                            if lo == 0:
                                last = vec.tensor_copy(kv[r, q, c], src)
                            else:
                                vec.tensor_tensor(kv[r, q, c], kv[r, q, c], src, ALU.add)
                    if lo == 0:
                        last.then_inc(s_out, 1)
                        vec.wait_ge(s_out, 1)


def attention1_queries(k, xt, w):
    nc, bank, io = k.nc, k.bank, k.io
    xt_hi, xt_lo = xt
    fw1_hi, fw1_lo = w["fw1_hi"], w["fw1_lo"]
    HV = NP * VA // 2
    CQ = 256
    NQ, TQ = T // CQ, CQ // P
    NU = NQ * KD
    with ExitStack() as ctx:
        sb = lambda name, shape, dt=F32: k.sb("q1_" + name, shape, dt, ctx)
        raw, fw2, fw2_t, fb2 = w["raw"], w["fw2"], w["fw2_t"], w["fb2"]
        kv, vsum, qb, fb1 = w["kv"], w["vsum"], w["qb"], w["fb1"]
        b_vec, b_cols, ones = sb("b_vec", [P, 1]), sb("b_cols", [P, P]), sb("ones", [P, P])
        kv2 = sb("kv2", [P, NP, VA])
        m_hi, m_lo, cq = sb("m_hi", [P, NP, VA], F32R), sb("m_lo", [P, NP, VA], F32R), sb("cq", [P, NP * VA])
        qw_hi, qw_lo = sb("qw_hi", [P, KD, D], F32R), sb("qw_lo", [P, KD, D], F32R)
        ow_hi, ow_lo = sb("ow_hi", [P, KD, D], F32R), sb("ow_lo", [P, KD, D], F32R)
        ob = sb("ob", [P, D])
        q_hi, q_lo = sb("q_hi", [P, 2, CQ], F32R), sb("q_lo", [P, 2, CQ], F32R)
        ex, gf = sb("ex", [P, 2, 2 * CQ]), sb("gf", [P, 2, 2 * CQ])
        g_hi, g_lo = sb("g_hi", [P, 2, NP * CQ], F32R), sb("g_lo", [P, 2, NP * CQ], F32R)
        num = (w["kv"][:, :, :].rearrange("p q v -> p (q v)"), w["vsum"][:, :])
        den = sb("den", [P, 2, H1])
        at_hi, at_lo = sb("at_hi", [P, 2, D], F32R), sb("at_lo", [P, 2, D], F32R)
        attn = raw

        sem = lambda n: k.sem("q1_" + n)
        s_qw, s_small, s_ow, s_obl = w["s_qw"], w["s_small"], sem("ow_loaded"), sem("ob_loaded")
        s_zero, s_ps, s_b, s_kv2, s_m = (sem(n) for n in ("zeroed", "memory_products", "bias_made", "kv2_made", "memory"))
        s_kv2p = sem("kv2_first_part")
        s_whi, s_wlo, s_ob = sem("weight_hi"), sem("weight_split"), sem("ob_added")
        s_q, s_qhi, s_qlo = sem("queries"), sem("queries_hi"), sem("queries_split")
        s_g, s_gev, s_gf, s_ghi, s_glo = sem("features"), sem("features_read"), sem("features_made"), sem("features_hi"), sem("features_lo")
        s_n, s_nev, s_den, s_at = sem("num"), sem("num_read"), sem("den"), sem("attn")
        s_tps, s_thi, s_tlo = sem("turned"), sem("turned_hi"), sem("turned_lo")
        s_o, s_res = sem("out"), sem("residual")
        s_stat, s_var, s_rstd, s_ln = sem("stats"), sem("var"), sem("rstd"), sem("normed")

        flat = lambda a: a[:, :, :].rearrange("p q v -> p (q v)")

        def schedule(query, features, features_hi, numerator, turn, project):
            query(0)
            for u in range(NU + KD + 1):
                if u + 1 < NU:
                    query(u + 1)
                if u < NU:
                    features(u)
                if 1 <= u <= NU:
                    features_hi(u - 1)
                i = TQ * (u // KD - 1)
                work = {1: ((numerator, i),), 2: ((numerator, i + 1), (turn, i)),
                        3: ((project, i), (turn, i + 1)), 0: ((project, i - 1),)}[u % KD]
                for stage, tile in work:
                    if tile >= 0:
                        stage(tile)

        with nc.Block() as block:
            @block.sync
            def _(sp):
                sp.dma_start(ob[:, :], io["ob"].partition_broadcast(P)).then_inc(s_obl, 16)
                sp.wait_ge(s_wlo, 1)
                sp.dma_start(raw[:, :, :], io["ow"].rearrange("(b p) n -> p b n", p=P)).then_inc(s_ow, 16)
                for c in range(NC):
                    sp.wait_ge(s_ln, TC * (c + 1))
                    sp.dma_start(k.rows.rearrange("(c j p) d -> c p j d", p=P, j=TC)[c],
                                 k.x[:, c * TC:(c + 1) * TC, :]).then_inc(k.s_rows, 16)

            @block.gpsimd
            def _(pool):
                pool.memset(ones[:, :], 1.0).then_inc(s_zero, 1)
                pool.memset(kv2[:, :, :], 0.0).then_inc(s_zero, 1)
                pool.wait_ge(s_obl, 16)

                def numerator(i):
                    pool.tensor_tensor(k.x[:, i, :], k.x[:, i, :], ob[:, :], ALU.add).then_inc(s_ob, 1)

                def features_lo(u):
                    c, m = u // KD, u % KD
                    f = slice(2 * m * CQ, (2 * m + 2) * CQ)
                    pool.wait_ge(s_ghi, u + 1)
                    pool.tensor_tensor(g_lo[:, c % 2, f], gf[:, u % 2, :], g_hi[:, c % 2, f].bitcast(F32), ALU.subtract).then_inc(s_glo, 1)

                def project(i):
                    if i % TC == TC - 1:
                        pool.wait_ge(s_stat, 2 * (i + 1))
                        ln_rstd(k, pool, i - TC + 1, TC, s_var, s_rstd, i // TC)

                idle = lambda n: None
                schedule(idle, idle, features_lo, numerator, idle, project)

            @block.tensor
            def _(pe):
                def query(u):
                    c, m = u // KD, u % KD
                    t = slice(c * CQ, (c + 1) * CQ)
                    if u == 0:
                        pe.wait_ge(s_wlo, 1)
                    if u >= 2:
                        pe.wait_ge(s_qlo, u - 1)
                    for b in range(KD):
                        mm = mm3(pe, bank[u % 2][:, 0:CQ], qw_hi[:, b, m * P:(m + 1) * P], qw_lo[:, b, m * P:(m + 1) * P],
                                 xt_hi[:, b, t], xt_lo[:, b, t], b == 0, b == KD - 1)
                    mm.then_inc(s_q, 1)

                def features(u):
                    pe.wait_ge(s_qlo, u + 1)
                    if u >= 2:
                        pe.wait_ge(s_gev, u - 1)
                    for a in range(2):
                        f = slice(a * P, (a + 1) * P)
                        mm = mm3(pe, bank[2 + u % 2][:, a * CQ:(a + 1) * CQ], fw1_hi[:, f], fw1_lo[:, f], q_hi[:, u % 2, :], q_lo[:, u % 2, :],
                                 True, True)
                    mm.then_inc(s_g, 1)

                def numerator(i):
                    c = i // TQ
                    if i == 0:
                        pe.wait_ge(s_m, 6)
                    if i % TQ == 0:
                        pe.wait_ge(s_glo, KD * (c + 1))
                    if i:
                        pe.wait_ge(s_nev, i)
                    for q in range(NP):
                        t = slice(q * CQ + i % TQ * P, q * CQ + (i % TQ + 1) * P)
                        mm = mm3(pe, bank[4 + q // 4][:, q % 4 * VA:(q % 4 + 1) * VA], g_hi[:, c % 2, t], g_lo[:, c % 2, t],
                                 m_hi[:, q, :], m_lo[:, q, :], True, True)
                    mm.then_inc(s_n, 1)

                def turn(i):
                    pe.wait_ge(s_at, i + 1)
                    if i:
                        pe.wait_ge(s_tlo, i)
                    for b in range(KD):
                        mm = pe.transpose(bank[6][:, b * P:(b + 1) * P], attn[:, i % 2, b * P:(b + 1) * P], k.ident[:, :])
                    mm.then_inc(s_tps, 1)

                def project(i):
                    if i == 0:
                        pe.wait_ge(s_wlo, 2)
                    pe.wait_ge(s_tlo, i + 1)
                    if i:
                        pe.wait_ge(s_res, i)
                    for b in range(KD):
                        f = slice(b * P, (b + 1) * P)
                        mm = mm3(pe, bank[7][:, :], at_hi[:, i % 2, f], at_lo[:, i % 2, f], ow_hi[:, b, :], ow_lo[:, b, :],
                                 b == 0, b == KD - 1)
                    mm.then_inc(s_o, 1)

                def memory_in():
                    pe.wait_ge(s_small, 16 * 9)
                    pe.wait_ge(s_zero, 2)
                    pe.matmul(bank[6][:, HV:HV + 2], fw2[:, :], ones[:, 0:2], start=True, stop=True).then_inc(s_ps, 1)
                    for a in range(2):
                        pe.matmul(bank[4 + a][:, 0:HV], ones[:, :], vsum[:, a * HV:(a + 1) * HV], start=True, stop=True).then_inc(s_ps, 1)
                        pe.matmul(bank[6 + a][:, 0:HV], fw2[:, :], flat(kv)[:, a * HV:(a + 1) * HV], start=True, stop=True).then_inc(s_ps, 1)

                def memory_out():
                    pe.wait_ge(s_kv2, 4)
                    pe.wait_ge(s_b, 2)
                    for a in range(2):
                        pe.matmul(bank[4 + a][:, 0:HV], fw2_t[:, :], flat(kv2)[:, a * HV:(a + 1) * HV], start=True, stop=True).then_inc(s_ps, 1)
                        pe.matmul(bank[6 + a][:, 0:HV], b_cols[:, :], flat(kv2)[:, a * HV:(a + 1) * HV], start=True, stop=True).then_inc(s_ps, 1)

                def query_and_memory(u):
                    query(u)
                    if u == 0:
                        memory_out()

                memory_in()
                schedule(query_and_memory, features, lambda u: None, numerator, turn, project)

            @block.scalar
            def _(act):
                def query(u):
                    m = u % KD
                    act.wait_ge(s_q, u + 1)
                    if u >= 2:
                        act.wait_ge(s_g, u - 1)
                    act.activation(q_hi[:, u % 2, :], bank[u % 2][:, 0:CQ], ACT.Identity, bias=qb[:, m:m + 1]).then_inc(s_qhi, 1)

                def features(u):
                    act.wait_ge(s_g, u + 1)
                    if u >= 2:
                        act.wait_ge(s_gf, u - 1)
                        act.wait_ge(s_glo, u - 1)
                    act.activation(ex[:, u % 2, :], bank[2 + u % 2][:, :], ACT.Exp, bias=fb1[:, 0:1])
                    act.activation(gf[:, u % 2, :], bank[2 + u % 2][:, :], ACT.Relu, bias=fb1[:, 0:1]).then_inc(s_gev, 1)

                def features_hi(u):
                    c, m = u // KD, u % KD
                    act.wait_ge(s_gf, u + 1)
                    if c >= 2:
                        act.wait_ge(s_n, TQ * (c - 1))
                    act.activation(g_hi[:, c % 2, 2 * m * CQ:(2 * m + 2) * CQ], gf[:, u % 2, :], ACT.Copy).then_inc(s_ghi, 1)

                def turn(i):
                    act.wait_ge(s_tps, i + 1)
                    if i >= 2:
                        act.wait_ge(s_o, i - 1)
                    act.activation(at_hi[:, i % 2, :], bank[6][:, :], ACT.Copy).then_inc(s_thi, 1)

                def numerator(i):
                    if i == 0:
                        act.wait_ge(s_ow, 16)
                        act.activation(ow_hi[:, :, :], raw[:, :, :], ACT.Copy).then_inc(s_whi, 1)

                act.wait_ge(s_qw, 16)
                act.activation(qw_hi[:, :, :], raw[:, :, :], ACT.Copy).then_inc(s_whi, 1)
                act.wait_ge(s_small, 16 * 9)
                schedule(query, features, features_hi, numerator, turn, lambda i: None)

            @block.vector
            def _(vec):
                def memory_sums():
                    vec.wait_ge(s_ps, 5)
                    vec.tensor_tensor(b_vec[:, :], fb2[:, :], bank[6][:, HV:HV + 1], ALU.subtract).then_inc(s_b, 1)
                    vec.wait_ge(s_b, 1)
                    vec.tensor_scalar(b_cols[:, :], ones[:, :], b_vec[:, 0:1], None, ALU.mult).then_inc(s_b, 1)
                    pairs = lambda t, c: t.rearrange("p (q v) -> p q v", v=VA)[:, :, c]
                    for a in range(2):
                        for h in range(2):
                            r, c = slice(h * FM, (h + 1) * FM), slice(h * (DH1 + 1), (h + 1) * (DH1 + 1))
                            vec.tensor_scalar(kv2[r, 4 * a:4 * a + 4, c], pairs(bank[4 + a][r, 0:HV], c), b_vec[r, 0:1], None,
                                              ALU.mult).then_inc(s_kv2p, 1)
                    for a in range(2):
                        for h in range(2):
                            r, c = slice(h * FM, (h + 1) * FM), slice(h * (DH1 + 1), (h + 1) * (DH1 + 1))
                            vec.wait_ge(s_kv2p, 2 * a + h + 1)
                            vec.tensor_tensor(kv2[r, 4 * a:4 * a + 4, c], kv2[r, 4 * a:4 * a + 4, c], pairs(bank[6 + a][r, 0:HV], c),
                                              ALU.add).then_inc(s_kv2, 1)

                def memory():
                    vec.wait_ge(s_ps, 9)
                    for a in range(2):
                        part = slice(a * HV, (a + 1) * HV)
                        vec.tensor_copy(cq[:, part], bank[6 + a][:, 0:HV]).then_inc(s_m, 1)
                        vec.tensor_copy(flat(m_hi)[:, part], bank[4 + a][:, 0:HV]).then_inc(s_m, 1)
                    vec.wait_ge(s_m, 4)
                    for a in range(2):
                        part = slice(a * HV, (a + 1) * HV)
                        vec.tensor_tensor(flat(m_lo)[:, part], bank[4 + a][:, 0:HV], flat(m_hi)[:, part], ALU.subtract).then_inc(s_m, 1)

                def query(u):
                    if u == 0:
                        vec.wait_ge(s_zero, 2)
                        vec.wait_ge(s_whi, 1)
                        vec.tensor_tensor(qw_lo[:, :, :], raw[:, :, :], qw_hi[:, :, :], ALU.subtract).then_inc(s_wlo, 1)
                        memory_sums()
                    if u == 1:
                        memory()
                    vec.wait_ge(s_qhi, u + 1)
                    if u >= 2:
                        vec.wait_ge(s_g, u - 1)
                    m = u % KD
                    vec.scalar_tensor_tensor(q_lo[:, u % 2, :], bank[u % 2][:, 0:CQ], qb[:, m:m + 1], q_hi[:, u % 2, :],
                                             ALU.add, ALU.subtract).then_inc(s_qlo, 1)

                def features(u):
                    vec.wait_ge(s_gev, u + 1)
                    vec.scalar_tensor_tensor(gf[:, u % 2, :], ex[:, u % 2, :], 1.0, gf[:, u % 2, :], ALU.min, ALU.add).then_inc(s_gf, 1)

                def divide(i):
                    if i == 0:
                        vec.wait_ge(s_whi, 2)
                        vec.tensor_tensor(ow_lo[:, :, :], raw[:, :, :], ow_hi[:, :, :], ALU.subtract).then_inc(s_wlo, 1)
                        vec.wait_ge(s_wlo, 2)
                    vec.wait_ge(s_n, i + 1)
                    s = i % 2
                    for a in range(2):
                        part = slice(a * HV, (a + 1) * HV)
                        vec.tensor_tensor(num[s][:, part], bank[4 + a][:, 0:HV], cq[:, part], ALU.add).then_inc(s_den, 1)
                    vec.wait_ge(s_den, 4 * i + 2)
                    nh = num[s].rearrange("p (h e) -> p h e", e=DH1 + 1)
                    vec.tensor_scalar(den[:, s, :], nh[:, :, DH1], 1e-6, None, ALU.max).then_inc(s_nev, 1)
                    vec.wait_ge(s_nev, i + 1)
                    vec.reciprocal(den[:, s, :], den[:, s, :]).then_inc(s_den, 2)
                    vec.wait_ge(s_den, 4 * i + 4)
                    if i >= 2:
                        vec.wait_ge(s_tps, i - 1)
                    vec.tensor_tensor(attn[:, s, :].rearrange("p (h e) -> p h e", e=DH1), nh[:, :, 0:DH1],
                                      den[:, s, :].unsqueeze(2).to_broadcast([P, H1, DH1]), ALU.mult).then_inc(s_at, 1)

                def split(i):
                    vec.wait_ge(s_thi, i + 1)
                    vec.tensor_tensor(at_lo[:, i % 2, :], bank[6][:, :], at_hi[:, i % 2, :], ALU.subtract).then_inc(s_tlo, 1)

                def residual(i):
                    vec.wait_ge(s_o, i + 1)
                    vec.wait_ge(s_ob, i + 1)
                    vec.tensor_tensor(k.x[:, i, :], bank[7][:, :], k.x[:, i, :], ALU.add).then_inc(s_res, 1)
                    vec.wait_ge(s_res, i + 1)
                    ln_stats(k, vec, i, s_stat, i)

                def apply(c):
                    vec.wait_ge(s_rstd, c + 1)
                    for i in range(c * TC, c * TC + TC):
                        ln_apply(k, vec, i).then_inc(s_ln, 1)

                def finish(i):
                    residual(i)
                    if i % TC == 1 and i > TC:
                        apply(i // TC - 1)

                schedule(query, features, lambda u: None, divide, split, finish)
                apply(NC - 1)


E1, K1, F1, CAP = 64, 6, 192, 96
G1, KG1 = 8, 4
HF1 = F1 // 2
ROUTED_SCALE = 2.5
BIG = 3e38


def experts1_shared(k):
    nc, bank, io = k.nc, k.bank, k.io
    EG = E1 // G1
    rt = lambda name, shape, dt=F32: k.sb("r1_" + name, shape, dt, k.moe_ctx)
    k.slot = rt("slot", [P, NT, K1], I32)
    k.weight = rt("weight", [P, NT, K1])
    k.token_of = rt("token_of", [CAP, E1], I32)
    k.w1_first = rt("w1_first", [P, KD, 2 * F1])
    k.s_w1_first = k.sem("e1_gate_up_loaded0")
    with ExitStack() as ctx:
        sb = lambda name, shape, dt=F32: k.sb("s1_" + name, shape, dt, ctx)
        gw_hi, gw_lo = sb("gw_hi", [P, KD, P], F32R), sb("gw_lo", [P, KD, P], F32R)
        w1_raw = k.w1_first
        w1_hi, w1_lo = sb("w1_hi", [P, KD, 2 * F1], F32R), sb("w1_lo", [P, KD, 2 * F1], F32R)
        w2_hi, w2_lo = sb("w2_hi", [HF1, 2, D], F32R), sb("w2_lo", [HF1, 2, D], F32R)
        bias = sb("bias", [P, E1])
        xt_hi, xt_lo = sb("xt_hi", [P, KD, T], F32R), sb("xt_lo", [P, KD, T], F32R)
        si, up = sb("si", [HF1, CH]), sb("up", [HF1, CH])
        hf = sb("hf", [HF1, 2, CH])
        h_hi, h_lo = sb("h_hi", [HF1, 2, CH], F32R), sb("h_lo", [HF1, 2, CH], F32R)
        ys = sb("ys", [P, D])
        scores = sb("scores", [P, NT, E1])
        biased = sb("biased", [P, NT, E1])
        top_in_group = sb("top_in_group", [P, NT * G1, 8])
        gscore, rank = sb("gscore", [P, NT, G1]), sb("rank", [P, NT, G1])
        lower = sb("lower", [P, G1, G1])
        top, arg = sb("top", [P, NT, 8]), sb("arg", [P, NT, 8], U32)
        argf = sb("argf", [P, NT, K1])
        onehot = sb("onehot", [P, NT, K1, E1])
        prod = sb("prod", [P, NT // 2, K1, E1])
        flat = lambda a: a[:, :, :, :].rearrange("p t k e -> p (t k e)")
        w2_raw = flat(prod)[0:HF1, 0:2 * D].rearrange("p (f n) -> p f n", f=2)
        gw_raw = flat(prod)[:, 2 * D:2 * D + KD * E1].rearrange("p (b n) -> p b n", b=KD)
        scores_t = flat(onehot)[0:E1, 0:2 * CH].rearrange("p (c t) -> p c t", c=2)
        sel = sb("sel", [P, NT * E1], BF16)
        upper, ones = sb("upper", [P, P], BF16), sb("ones", [P, P], BF16)
        tot, run_b = biased, scores
        run_a = top_in_group[:, :, :].rearrange("p (t g) e -> p t (g e)", g=G1)
        wsum = sb("wsum", [P, NT])
        posk, valid = sb("posk", [P, NT, K1]), sb("valid", [P, NT, K1])
        iota_e, iota_c = sb("iota_e", [P, E1]), sb("iota_c", [P, CAP])
        tok = sb("tok", [P, NT])
        at_row = [xt_hi[:, n, 0:K1 * CAP].rearrange("p (k s) -> p k s", k=K1) for n in range(2)]
        at_col = sb("at_col", [P, 2, K1, E1], F32R)

        sem = lambda n: k.sem("s1_" + n)
        s_gw, s_w1, s_w2, s_b = sem("gate_w_loaded"), sem("w1_loaded"), sem("w2_loaded"), sem("bias_loaded")
        s_whi, s_wlo = sem("weight_hi"), sem("weight_split")
        s_tps, s_thi, s_tlo = sem("turned"), sem("turned_hi"), sem("turned_lo")
        s_gwz, s_lg, s_sig, s_back, s_sc = sem("gate_w_zeroed"), sem("logits"), sem("sigmoid"), sem("turned_back"), sem("scores")
        s_gu, s_act, s_h, s_hh, s_hlo = sem("gate_up"), sem("gate_up_read"), sem("hidden"), sem("hidden_hi"), sem("hidden_split")
        s_dn, s_ys, s_res = sem("down"), sem("down_copied"), sem("residual")
        s_const, s_r = sem("constants"), sem("route_chain")
        s_sel, s_pre, s_tot = sem("selected"), sem("prefix"), sem("totals_copied")
        s_row, s_col, s_used = sem("rows_made"), sem("cols_made"), sem("rows_used")
        s_tab = sem("table_made")
        NU = 2 * NC

        def schedule(gate_up, down, ahead=0):
            gate_up(0)
            gate_up(1)
            for c in range(NC):
                if ahead and c + 1 < NC:
                    gate_up(2 * c + 2)
                down(c)
                for u in range(2 * c + 2 + ahead, min(2 * c + 4, NU)):
                    gate_up(u)

        with nc.Block() as block:
            @block.sync
            def _(sp):
                sp.dma_start(gw_raw[:, :, :], io["gate_w"].rearrange("(b p) n -> p b n", p=P)).then_inc(s_gw, 16)
                sp.dma_start(bias[:, :], io["bias"].partition_broadcast(P)).then_inc(s_b, 16)
                for a, name in enumerate(("ws_gate", "ws_up")):
                    sp.dma_start(w1_raw[:, :, a * F1:(a + 1) * F1], io[name].rearrange("(b p) n -> p b n", p=P)).then_inc(s_w1, 16)
                sp.dma_start(w2_raw[:, :, :], io["ws_down"].rearrange("(f p) n -> p f n", p=HF1)).then_inc(s_w2, 16)

                sp.wait_ge(s_wlo, 2)
                sp.dma_start(w1_raw[:, :, :].rearrange("p b n -> p (b n)"), io["w_gate_up"][0]).then_inc(k.s_w1_first, 16)
                sp.wait_ge(k.s_rows, 2 * 16 * NC)

            @block.gpsimd
            def _(pool):
                pool.memset(gw_hi[:, :, :].bitcast(F32), 0.0).then_inc(s_gwz, 1)
                pool.memset(gw_lo[:, :, :].bitcast(F32), 0.0).then_inc(s_gwz, 1)
                pool.memset(upper[:, :], 1.0).then_inc(s_const, 1)
                pool.memset(ones[:, :], 1.0).then_inc(s_const, 1)
                pool.memset(lower[:, :, :], 1.0).then_inc(s_const, 1)
                for a, n in ((iota_e, E1), (iota_c, CAP)):
                    pool.iota(a[:, :], [[1, n]], base=0, channel_multiplier=0,
                              allow_small_or_imprecise_dtypes=True).then_inc(s_const, 1)
                pool.iota(tok[:, :], [[P, NT]], base=0, channel_multiplier=1,
                          allow_small_or_imprecise_dtypes=True).then_inc(s_const, 1)
                pool.wait_ge(s_const, 6)
                pool.affine_select(out=upper[:, :], in_=upper[:, :], compare_op=ALU.is_gt, fill=0.0,
                                   base=0, pattern=[[1, P]], channel_multiplier=-1).then_inc(s_const, 1)
                pool.affine_select(out=lower[:, :, :], in_=lower[:, :, :], compare_op=ALU.is_gt, fill=0.0,
                                   base=0, pattern=[[1, G1], [-1, G1]], channel_multiplier=0).then_inc(s_const, 1)

                def gate_up(u):
                    if u >= 2:
                        pool.wait_ge(s_hlo, u - 1)
                    pool.wait_ge(s_act, u + 1)
                    pool.tensor_tensor(hf[:, u % 2, :], si[:, :], up[:, :], ALU.mult).then_inc(s_h, 1)
                    pool.wait_ge(s_hh, u + 1)
                    if u >= 2:
                        pool.wait_ge(s_dn, TC * (u // 2))
                    pool.tensor_tensor(h_lo[:, u % 2, :], hf[:, u % 2, :], h_hi[:, u % 2, :].bitcast(F32), ALU.subtract).then_inc(s_hlo, 1)

                def down(c):
                    if c == 0:
                        pool.wait_ge(k.s_rows, 2 * 16 * NC)
                    for i in range(c * TC, c * TC + TC):
                        pool.wait_ge(s_ys, i + 1)
                        pool.tensor_tensor(k.x[:, i, :], ys[:, :], k.x[:, i, :], ALU.add).then_inc(s_res, 1)

                schedule(gate_up, down)

            @block.tensor
            def _(pe):
                def turn(c):
                    for b in range(KD):
                        n = 4 * c + b
                        if n >= 2:
                            pe.wait_ge(s_tlo, n - 1)
                        for j in range(TC):
                            mm = pe.transpose(bank[n % 2][:, j * P:(j + 1) * P], k.x[:, c * TC + j, b * P:(b + 1) * P], k.ident[:, :])
                        mm.then_inc(s_tps, 1)

                def logits(c):
                    pe.wait_ge(s_tlo, 4 * c + 4)
                    if c >= 2:
                        pe.wait_ge(s_sig, c - 1)
                    for b in range(KD):
                        t = slice(c * CH, (c + 1) * CH)
                        mm = mm3(pe, bank[6 + c % 2][:, :], gw_hi[:, b, :], gw_lo[:, b, :], xt_hi[:, b, t], xt_lo[:, b, t], b == 0, b == KD - 1)
                    mm.then_inc(s_lg, 1)

                def scores_back(c):
                    pe.wait_ge(s_sig, c + 1)
                    for j in range(TC):
                        o = (c % 2 * TC + j) * E1
                        mm = pe.transpose(bank[4 + c // 2][:, o:o + E1], scores_t[:, c % 2, j * P:(j + 1) * P], k.ident[0:E1, 0:E1])
                    mm.then_inc(s_back, 1)

                def gate_up(u):
                    c, f = u // 2, u % 2
                    if u == 0:
                        pe.wait_ge(s_wlo, 2)
                        pe.wait_ge(s_sc, 2)
                    if u >= 2:
                        pe.wait_ge(s_act, u - 1)
                    t = slice(c * CH, (c + 1) * CH)
                    for a in range(2):
                        fs = slice(a * F1 + f * HF1, a * F1 + (f + 1) * HF1)
                        for b in range(KD):
                            mm = mm3(pe, bank[2 + 2 * a + f][0:HF1, :], w1_hi[:, b, fs], w1_lo[:, b, fs],
                                     xt_hi[:, b, t], xt_lo[:, b, t], b == 0, b == KD - 1)
                    mm.then_inc(s_gu, 1)

                def down(c):
                    if c == 0:
                        pe.wait_ge(s_wlo, 3)
                    if c == NC - 2:
                        prefix()
                    pe.wait_ge(s_hlo, 2 * c + 2)
                    for i in range(4 * c, 4 * c + 4):
                        if i:
                            pe.wait_ge(s_ys, i)
                        t = slice(i % 4 * P, (i % 4 + 1) * P)
                        for f in range(2):
                            mm = mm3(pe, bank[6][:, :], h_hi[:, f, t], h_lo[:, f, t], w2_hi[:, f, :], w2_lo[:, f, :],
                                     f == 0, f == 1)
                        mm.then_inc(s_dn, 1)

                def prefix():
                    pe.wait_ge(s_sel, 1)
                    pe.wait_ge(s_const, 8)
                    for a in range(2):
                        half = sel[:, a * 512:(a + 1) * 512]
                        if a:
                            pe.wait_ge(s_tot, 1)
                        pe.matmul(bank[7][:, :], ones[:, :], half, start=True, stop=True)
                        pe.matmul(bank[a][:, :], upper[:, :], half, start=True, stop=True).then_inc(s_pre, 1)

                def table():
                    pe.wait_ge(s_tot, 2)
                    for n in range(NT * K1):
                        if n % K1 == 0:
                            pe.wait_ge(s_col, n // K1 + 1)
                            pe.wait_ge(s_row, n // K1 + 1)
                        mm = pe.matmul(bank[7][0:CAP, 0:E1], at_row[n // K1 % 2][:, n % K1, :], at_col[:, n // K1 % 2, n % K1, :],
                                       start=(n == 0), stop=(n == NT * K1 - 1))
                        if n % K1 == K1 - 1:
                            mm.then_inc(s_used, 1)

                turn(0)
                pe.wait_ge(s_wlo, 1)
                for c in range(NC):
                    if c + 1 < NC:
                        turn(c + 1)
                    logits(c)
                    if c:
                        scores_back(c - 1)
                scores_back(NC - 1)
                schedule(gate_up, down, ahead=1)
                table()

            @block.scalar
            def _(act):
                act.wait_ge(s_gw, 16)
                act.wait_ge(s_gwz, 2)
                act.activation(gw_hi[:, :, 0:E1], gw_raw[:, :, :], ACT.Copy).then_inc(s_whi, 1)

                def sigmoid(c):
                    act.wait_ge(s_lg, c + 1)
                    if c >= 2:
                        act.wait_ge(s_back, c - 1)
                    act.activation(scores_t[:, c % 2, :], bank[6 + c % 2][0:E1, :], ACT.Sigmoid).then_inc(s_sig, 1)

                for n in range(4 * NC):
                    act.wait_ge(s_tps, n + 1)
                    act.activation(xt_hi[:, n % 4, n // 4 * CH:(n // 4 + 1) * CH], bank[n % 2][:, :], ACT.Copy).then_inc(s_thi, 1)
                    if n == 3:
                        act.wait_ge(s_w1, 32)
                        act.activation(w1_hi[:, :, :], w1_raw[:, :, :], ACT.Copy).then_inc(s_whi, 1)
                    if n == 7:
                        act.wait_ge(s_w2, 16)
                        act.activation(w2_hi[:, :, :], w2_raw[:, :, :], ACT.Copy).then_inc(s_whi, 1)
                    if n % 4 == 3 and n > 3:
                        sigmoid(n // 4 - 1)
                sigmoid(NC - 1)
                for a in range(2):
                    act.wait_ge(s_back, 2 * a + 2)
                    act.activation(scores[:, 8 * a:8 * a + 8, :].rearrange("p t e -> p (t e)"), bank[4 + a][:, :], ACT.Copy).then_inc(s_sc, 1)

                def gate_up(u):
                    act.wait_ge(s_gu, u + 1)
                    if u:
                        act.wait_ge(s_h, u)
                    act.activation(si[:, :], bank[2 + u % 2][0:HF1, :], ACT.Silu)
                    act.activation(up[:, :], bank[4 + u % 2][0:HF1, :], ACT.Copy).then_inc(s_act, 1)
                    act.wait_ge(s_h, u + 1)
                    if u >= 2:
                        act.wait_ge(s_dn, TC * (u // 2))
                    act.activation(h_hi[:, u % 2, :], hf[:, u % 2, :], ACT.Copy).then_inc(s_hh, 1)

                def down(c):
                    for i in range(c * TC, c * TC + TC):
                        act.wait_ge(s_dn, i + 1)
                        if i:
                            act.wait_ge(s_res, i)
                        act.activation(ys[:, :], bank[6][:, :], ACT.Copy).then_inc(s_ys, 1)

                schedule(gate_up, down)

            @block.vector
            def _(vec):
                done = [0]

                def step(ins):
                    ins.then_inc(s_r, 1)
                    done[0] += 1

                def sync():
                    vec.wait_ge(s_r, done[0])

                def split_lo(n, lo, raw, hi):
                    vec.wait_ge(s_whi, n + 1)
                    vec.tensor_tensor(lo, raw, hi, ALU.subtract).then_inc(s_wlo, 1)

                def choose():
                    vec.wait_ge(s_b, 16)
                    vec.wait_ge(s_sc, 2)
                    step(vec.tensor_tensor(biased[:, :, :], scores[:, :, :], bias[:, :].unsqueeze(1).to_broadcast([P, NT, E1]), ALU.add))
                    sync()
                    by_group = biased[:, :, :].rearrange("p t (g e) -> p (t g) e", g=G1)
                    for n in range(NT * G1):
                        last = vec.max(top_in_group[:, n, :], by_group[:, n, :])
                    step(last)
                    sync()
                    best = top_in_group[:, :, :].rearrange("p (t g) e -> p t g e", g=G1)
                    step(vec.tensor_tensor(gscore[:, :, :], best[:, :, :, 0], best[:, :, :, 1], ALU.add))
                    sync()
                    shape = [P, NT, G1, G1]
                    pairs = lambda n: prod[:, :, :, :].rearrange("p t k e -> p (t k e)")[:, n * NT * G1 * G1:(n + 1) * NT * G1 * G1].rearrange(
                        "p (t g h) -> p t g h", g=G1, h=G1)
                    mine = gscore[:, :, :].unsqueeze(3).to_broadcast(shape)
                    other = gscore[:, :, :].unsqueeze(2).to_broadcast(shape)
                    step(vec.tensor_tensor(pairs(0), other, mine, ALU.is_gt))
                    step(vec.tensor_tensor(pairs(1), other, mine, ALU.is_equal))
                    vec.wait_ge(s_const, 8)
                    sync()
                    step(vec.tensor_tensor(pairs(1), pairs(1), lower[:, :, :].unsqueeze(1).to_broadcast(shape), ALU.mult))
                    sync()
                    step(vec.tensor_tensor(pairs(0), pairs(0), pairs(1), ALU.add))
                    sync()
                    step(vec.tensor_reduce(rank[:, :, :], pairs(0), AX.X, ALU.add))
                    sync()
                    step(vec.tensor_scalar(rank[:, :, :], rank[:, :, :], float(KG1), -BIG, ALU.is_ge, ALU.mult))
                    sync()
                    step(vec.tensor_tensor(biased[:, :, :].rearrange("p t (g e) -> p t g e", g=G1),
                                           biased[:, :, :].rearrange("p t (g e) -> p t g e", g=G1),
                                           rank[:, :, :].unsqueeze(3).to_broadcast([P, NT, G1, EG]), ALU.add))
                    sync()
                    for i in range(NT):
                        step(vec.max(top[:, i, :], biased[:, i, :]))
                    sync()
                    for i in range(NT):
                        step(vec.max_index(arg[:, i, :], top[:, i, :], biased[:, i, :]))
                    sync()
                    step(vec.tensor_copy(argf[:, :, :], arg[:, :, 0:K1]))
                    sync()
                    step(vec.tensor_tensor(onehot[:, :, :, :], iota_e[:, :].unsqueeze(1).unsqueeze(1).to_broadcast([P, NT, K1, E1]),
                                           argf[:, :, :].unsqueeze(3).to_broadcast([P, NT, K1, E1]), ALU.is_equal))
                    sync()
                    with nc.allow_low_precision("counts of 0 or 1"):
                        vec.tensor_reduce(sel[:, :].rearrange("p (t e) -> p t e", e=E1), onehot[:, :, :, :].rearrange("p t k e -> p t e k"),
                                          AX.X, ALU.add).then_inc(s_sel, 1)
                    for half in range(2):
                        t = slice(half * NT // 2, (half + 1) * NT // 2)
                        sync()
                        step(vec.tensor_tensor(prod[:, :, :, :], onehot[:, t, :, :],
                                               scores[:, t, :].unsqueeze(2).to_broadcast([P, NT // 2, K1, E1]), ALU.mult))
                        sync()
                        step(vec.tensor_reduce(k.weight[:, t, :], prod[:, :, :, :], AX.X, ALU.add))
                    sync()
                    step(vec.tensor_reduce(wsum[:, :], k.weight[:, :, :], AX.X, ALU.add))
                    sync()
                    step(vec.reciprocal(wsum[:, :], wsum[:, :]))
                    sync()
                    step(vec.tensor_scalar(wsum[:, :], wsum[:, :], ROUTED_SCALE, None, ALU.mult))
                    sync()
                    step(vec.tensor_tensor(k.weight[:, :, :], k.weight[:, :, :], wsum[:, :].unsqueeze(2).to_broadcast([P, NT, K1]), ALU.mult))

                def positions():
                    for a in range(2):
                        t = slice(8 * a, 8 * a + 8)
                        vec.wait_ge(s_pre, a + 1)
                        whole = bank[7][:, :].rearrange("p (t e) -> p t e", e=E1)
                        step(vec.tensor_copy(run_a[:, t, :], whole))
                        vec.tensor_copy(tot[:, t, :], whole).then_inc(s_tot, 1)
                    a, b = run_a, run_b[:, :, :]
                    for d in (1, 2, 4, 8):
                        sync()
                        step(vec.tensor_tensor(b[:, d:, :], a[:, d:, :], a[:, :NT - d, :], ALU.add))
                        step(vec.tensor_copy(b[:, :d, :], a[:, :d, :]))
                        a, b = b, a
                    vec.wait_ge(s_tot, 2)
                    sync()
                    step(vec.tensor_tensor(b, a, tot[:, :, :], ALU.subtract))
                    sync()
                    for h in range(2):
                        t = slice(8 * h, 8 * h + 8)
                        step(vec.tensor_tensor(b[:, t, :], bank[h][:, :].rearrange("p (t e) -> p t e", e=E1), b[:, t, :], ALU.add))
                    for half in range(2):
                        t = slice(half * NT // 2, (half + 1) * NT // 2)
                        sync()
                        step(vec.tensor_tensor(prod[:, :, :, :], onehot[:, t, :, :],
                                               b[:, t, :].unsqueeze(2).to_broadcast([P, NT // 2, K1, E1]), ALU.mult))
                        sync()
                        step(vec.tensor_reduce(posk[:, t, :], prod[:, :, :, :], AX.X, ALU.add))
                    sync()
                    step(vec.tensor_scalar(valid[:, :, :], posk[:, :, :], float(CAP), None, ALU.is_lt))
                    step(vec.tensor_scalar(argf[:, :, :], argf[:, :, :], float(CAP), None, ALU.mult))
                    sync()
                    step(vec.tensor_tensor(k.weight[:, :, :], k.weight[:, :, :], valid[:, :, :], ALU.mult))
                    step(vec.scalar_tensor_tensor(k.slot[:, :, :], posk[:, :, :], float(CAP - 1), argf[:, :, :], ALU.min, ALU.add))

                def table():
                    vec.wait_ge(s_gu, NU)
                    shape = [P, K1, CAP]
                    for i in range(NT):
                        if i >= 2:
                            vec.wait_ge(s_used, i - 1)
                        vec.tensor_tensor(at_row[i % 2], iota_c[:, :].unsqueeze(1).to_broadcast(shape),
                                          posk[:, i, :].unsqueeze(2).to_broadcast(shape), ALU.is_equal).then_inc(s_row, 1)
                        vec.tensor_scalar(at_col[:, i % 2, :, :], onehot[:, i, :, :], tok[:, i:i + 1], None, ALU.mult).then_inc(s_col, 1)
                    vec.wait_ge(s_used, NT)
                    vec.tensor_copy(k.token_of[:, :], bank[7][0:CAP, 0:E1]).then_inc(s_tab, 1)

                split_lo(0, gw_lo[:, :, 0:E1], gw_raw[:, :, :], gw_hi[:, :, 0:E1])
                for n in range(4 * NC):
                    vec.wait_ge(s_thi, n + 1)
                    t = slice(n // 4 * CH, (n // 4 + 1) * CH)
                    vec.tensor_tensor(xt_lo[:, n % 4, t], bank[n % 2][:, :], xt_hi[:, n % 4, t], ALU.subtract).then_inc(s_tlo, 1)
                    if n == 7:
                        split_lo(1, w1_lo[:, :, :], w1_raw[:, :, :], w1_hi[:, :, :])
                    if n == 11:
                        split_lo(2, w2_lo[:, :, :], w2_raw[:, :, :], w2_hi[:, :, :])
                choose()
                positions()
                table()


def experts1_routed(k):
    nc, bank, io = k.nc, k.bank, k.io
    with ExitStack() as ctx:
        U = 4
        two = lambda name, shape, dt=F32: [k.sb(f"e1_{name}{p}", shape, dt, ctx) for p in range(2)] * 2
        four = lambda name, shape, dt=F32: [k.sb(f"e1_{name}{p}", shape, dt, ctx) for p in range(U)]
        w1_raw = [k.w1_first] + [k.sb(f"e1_w1_raw{p}", [P, KD, 2 * F1], F32, ctx) for p in range(1, U)]
        w1_hi, w1_lo = two("w1_hi", [P, KD, 2 * F1], F32R), two("w1_lo", [P, KD, 2 * F1], F32R)
        w2_raw, w2_hi, w2_lo = four("w2_raw", [HF1, 2, D]), two("w2_hi", [HF1, 2, D], F32R), two("w2_lo", [HF1, 2, D], F32R)
        index = four("index", [CAP, 1], I32)
        xg = four("xg", [CAP, D])
        xt_hi, xt_lo = two("xt_hi", [P, KD * CAP], F32R), two("xt_lo", [P, KD * CAP], F32R)
        si, hf = two("si", [CAP, F1]), two("hf", [CAP, F1])
        ht_hi, ht_lo = two("ht_hi", [HF1, 2 * CAP], F32R), two("ht_lo", [HF1, 2 * CAP], F32R)
        y = four("y", [CAP, D])

        each = lambda name: [k.sem(f"e1_{name}{p}") for p in range(U)]
        sem = lambda n: k.sem("e1_" + n)
        s_w = [k.s_w1_first] + [sem(f"gate_up_loaded{p}") for p in range(1, U)]
        s_v, s_g, s_y = each("down_loaded"), each("rows_gathered"), each("results_stored")
        s_ix, s_go = sem("index"), sem("index_seen")
        s_whi, s_wlo, s_vhi, s_vlo = sem("gate_up_hi"), sem("gate_up_lo"), sem("down_hi"), sem("down_lo")
        s_tps, s_thi, s_tlo = sem("turned"), sem("turned_hi"), sem("turned_lo")
        s_gu, s_si, s_h = sem("gate_up"), sem("silu"), sem("hidden")
        s_ht, s_hh, s_hlo = sem("hidden_turned"), sem("hidden_hi"), sem("hidden_lo")
        s_dn, s_ysb = sem("down"), sem("results")
        nothing = lambda h, p: None
        past = lambda h, p, n: not (isinstance(h, int) and U * h + p < n)
        y_rows = k.y1.rearrange("(e s) d -> e s d", s=CAP)

        with nc.Block() as block:
            @block.sync
            def _(sp):
                def load(h, p):
                    e = U * h + p
                    if past(h, p, U):
                        sp.wait_ge(s_wlo, e - U + 1)
                    if past(h, p, 1):
                        sp.dma_start(w1_raw[p][:, :, :].rearrange("p b n -> p (b n)"),
                                     io["w_gate_up"][bass.ds(e, 1)].rearrange("e p n -> p (e n)")).then_inc(s_w[p], 16)
                    if past(h, p, U):
                        sp.wait_ge(s_vlo, e - U + 1)
                    sp.dma_start(w2_raw[p][:, :, :].rearrange("p f n -> p (f n)"),
                                 io["w_down"][bass.ds(e, 1)].rearrange("e p n -> p (e n)")).then_inc(s_v[p], 16)

                def store(h, p):
                    e = U * h + p
                    sp.wait_ge(s_ysb, e + 1)
                    sp.dma_start(y_rows[bass.ds(e, 1)].rearrange("e s d -> s (e d)"), y[p][:, :]).then_inc(s_y[p], 16)

                three_stages(sp, E1, nothing, nothing, store, ahead=load, unroll=U)
                for p in range(U):
                    sp.wait_ge(s_y[p], 16 * (E1 // U))

            @block.gpsimd
            def _(pool):
                def gather(h, p):
                    e = U * h + p
                    if past(h, p, U):
                        pool.wait_ge(s_g[p], 16 * h)
                        pool.wait_ge(s_tps, e - U + 1)
                    pool.tensor_copy(index[p][:, :], k.token_of[:, bass.ds(e, 1)]).then_inc(s_ix, 1)
                    pool.wait_ge(s_ix, e + 1)
                    pool.sem_inc(s_go, 1)
                    pool.indirect_dma_start(xg[p][:, :], None, k.rows, bass.IndirectOffsetOnAxis(index[p][:, 0:1], 0)
                                            ).then_inc(s_g[p], 16)

                def down_lo(h, p):
                    e = U * h + p
                    pool.wait_ge(s_vhi, e + 1)
                    pool.tensor_tensor(w2_lo[p][:, :, :], w2_raw[p][:, :, :], w2_hi[p][:, :, :].bitcast(F32), ALU.subtract).then_inc(s_vlo, 1)

                three_stages(pool, E1, nothing, down_lo, nothing, ahead=gather, unroll=U)

            @block.tensor
            def _(pe):
                def turn(h, p):
                    pe.wait_ge(s_g[p], 16 * (h + 1))
                    if past(h, p, 2):
                        pe.wait_ge(s_tlo, U * h + p - 1)
                    for b in range(KD):
                        mm = pe.transpose(bank[p % 2][:, b * CAP:(b + 1) * CAP], xg[p][:, b * P:(b + 1) * P], k.ident[0:CAP, 0:CAP])
                    mm.then_inc(s_tps, 1)

                def gate_up(h, p):
                    e = U * h + p
                    pe.wait_ge(s_wlo, e + 1)
                    pe.wait_ge(s_tlo, e + 1)
                    if past(h, p, 2):
                        pe.wait_ge(s_h, e - 1)
                    for b in range(KD):
                        c = slice(b * CAP, (b + 1) * CAP)
                        mm = mm3(pe, bank[2 + p % 2][0:CAP, 0:2 * F1], xt_hi[p][:, c], xt_lo[p][:, c], w1_hi[p][:, b, :], w1_lo[p][:, b, :],
                                 b == 0, b == KD - 1)
                    mm.then_inc(s_gu, 1)

                def turn_hidden(h, p):
                    pe.wait_ge(s_h, U * h + p + 1)
                    if past(h, p, 2):
                        pe.wait_ge(s_hlo, U * h + p - 1)
                    for f in range(2):
                        mm = pe.transpose(bank[4 + p % 2][0:HF1, f * CAP:(f + 1) * CAP], hf[p][:, f * HF1:(f + 1) * HF1], k.ident[0:CAP, 0:CAP])
                    mm.then_inc(s_ht, 1)

                def down(h, p):
                    e = U * h + p
                    pe.wait_ge(s_hlo, e + 1)
                    pe.wait_ge(s_vlo, e + 1)
                    if past(h, p, 2):
                        pe.wait_ge(s_ysb, e - 1)
                    for f in range(2):
                        c = slice(f * CAP, (f + 1) * CAP)
                        mm = mm3(pe, bank[6 + p % 2][0:CAP, :], ht_hi[p][:, c], ht_lo[p][:, c], w2_hi[p][:, f, :], w2_lo[p][:, f, :],
                                 f == 0, f == 1)
                    mm.then_inc(s_dn, 1)

                three_stages(pe, E1, turn, gate_up, down, between=turn_hidden, unroll=U)

            @block.scalar
            def _(act):
                def turned_hi(h, p):
                    e = U * h + p
                    act.wait_ge(s_tps, e + 1)
                    act.activation(xt_hi[p][:, :], bank[p % 2][:, 0:KD * CAP], ACT.Copy).then_inc(s_thi, 1)

                def weights_hi(h, p):
                    e = U * h + p
                    act.wait_ge(s_w[p], 16 * (h + 1))
                    if past(h, p, 2):
                        act.wait_ge(s_gu, e - 1)
                    act.activation(w1_hi[p][:, :, :], w1_raw[p][:, :, :], ACT.Copy).then_inc(s_whi, 1)

                def hidden_hi(h, p):
                    e = U * h + p
                    act.wait_ge(s_ht, e + 1)
                    if past(h, p, 2):
                        act.wait_ge(s_dn, e - 1)
                    act.activation(ht_hi[p][:, :], bank[4 + p % 2][0:HF1, 0:2 * CAP], ACT.Copy).then_inc(s_hh, 1)

                def silu(h, p):
                    e = U * h + p
                    act.wait_ge(s_v[p], 16 * (h + 1))
                    if past(h, p, 2):
                        act.wait_ge(s_dn, e - 1)
                    act.activation(w2_hi[p][:, :, :], w2_raw[p][:, :, :], ACT.Copy).then_inc(s_vhi, 1)
                    act.wait_ge(s_gu, e + 1)
                    if past(h, p, 2):
                        act.wait_ge(s_h, e - 1)
                    act.activation(si[p][:, :], bank[2 + p % 2][0:CAP, 0:F1], ACT.Silu).then_inc(s_si, 1)

                def results(h, p):
                    e = U * h + p
                    act.wait_ge(s_dn, e + 1)
                    if past(h, p, U):
                        act.wait_ge(s_y[p], 16 * h)
                    act.activation(y[p][:, :], bank[6 + p % 2][0:CAP, :], ACT.Copy).then_inc(s_ysb, 1)

                three_stages(act, E1, turned_hi, silu, results, between=hidden_hi, prepare=weights_hi, unroll=U)

            @block.vector
            def _(vec):
                def weights_lo(h, p):
                    e = U * h + p
                    vec.wait_ge(s_whi, e + 1)
                    vec.tensor_tensor(w1_lo[p][:, :, :], w1_raw[p][:, :, :], w1_hi[p][:, :, :], ALU.subtract).then_inc(s_wlo, 1)

                def turned_lo(h, p):
                    e = U * h + p
                    vec.wait_ge(s_thi, e + 1)
                    vec.tensor_tensor(xt_lo[p][:, :], bank[p % 2][:, 0:KD * CAP], xt_hi[p][:, :], ALU.subtract).then_inc(s_tlo, 1)

                def hidden_lo(h, p):
                    vec.wait_ge(s_hh, U * h + p + 1)
                    vec.tensor_tensor(ht_lo[p][:, :], bank[4 + p % 2][0:HF1, 0:2 * CAP], ht_hi[p][:, :], ALU.subtract).then_inc(s_hlo, 1)

                def hidden(h, p):
                    e = U * h + p
                    vec.wait_ge(s_si, e + 1)
                    if past(h, p, 2):
                        vec.wait_ge(s_ht, e - 1)
                    vec.tensor_tensor(hf[p][:, :], si[p][:, :], bank[2 + p % 2][0:CAP, F1:2 * F1], ALU.mult).then_inc(s_h, 1)

                three_stages(vec, E1, turned_lo, hidden, nothing, between=hidden_lo, prepare=weights_lo, unroll=U)


def combine1(k):
    nc, io = k.nc, k.io
    NB = 3
    NL = 2
    with ExitStack() as ctx:
        yg = [k.sb(f"c1_yg{n}", [P, K1, D], F32, ctx) for n in range(NB)]
        s_g = [[k.sem(f"c1_gathered{n}_{kk}") for kk in range(K1)] for n in range(NB)]
        s_sum, s_used = k.sem("c1_summed"), k.sem("c1_gathered_used")
        s_stat, s_var, s_rstd, s_ln, s_st = (k.sem("c1_" + n) for n in ("stats", "var", "rstd", "normed", "stored"))
        with nc.Block() as block:
            @block.sync
            def _(sp):
                for c in range(NT // NL):
                    sp.wait_ge(s_ln, NL * (c + 1))
                    sp.dma_start(io["out"].rearrange("(c j p) d -> c p j d", p=P, j=NL)[c],
                                 k.x[:, c * NL:(c + 1) * NL, :]).then_inc(s_st, 16)
                sp.wait_ge(s_st, 16 * (NT // NL))

            @block.gpsimd
            def _(pool):
                def rstd(c):
                    pool.wait_ge(s_stat, 2 * NL * (c + 1))
                    ln_rstd(k, pool, c * NL, NL, s_var, s_rstd, c)

                for i in range(NT):
                    if i >= NB:
                        pool.wait_ge(s_used, i - NB + 1)
                    for kk in range(K1):
                        pool.indirect_dma_start(yg[i % NB][:, kk, :], None, k.y1, bass.IndirectOffsetOnAxis(k.slot[:, i, kk:kk + 1], 0)
                                                ).then_inc(s_g[i % NB][kk], 16)
                    if i >= 2 * NL + 1 and i % NL == 1:
                        rstd(i // NL - 2)
                rstd(NT // NL - 2)
                rstd(NT // NL - 1)

            @block.vector
            def _(vec):
                def apply(c):
                    vec.wait_ge(s_rstd, c + 1)
                    for i in range(c * NL, c * NL + NL):
                        ln_apply(k, vec, i).then_inc(s_ln, 1)

                for i in range(NT):
                    xi = k.x[:, i, :]
                    for kk in range(K1):
                        vec.wait_ge(s_g[i % NB][kk], 16 * (i // NB + 1))
                        vec.scalar_tensor_tensor(xi, yg[i % NB][:, kk, :], k.weight[:, i, kk:kk + 1], xi, ALU.mult, ALU.add).then_inc(s_sum, 1)
                        vec.wait_ge(s_sum, K1 * i + kk + 1)
                    vec.sem_inc(s_used, 1)
                    ln_stats(k, vec, i, s_stat, i)
                    if i >= 3 * NL + 1 and i % NL == 1:
                        apply(i // NL - 3)
                for c in range(NT // NL - 3, NT // NL):
                    apply(c)


def two_layers(nc, io):
    with ExitStack() as ctx:
        k = Core(nc, ctx, io)
        k.rows = nc.dram_tensor("rows", (T, D), F32, kind="Internal").ap()
        k.y0 = nc.dram_tensor("results0", (NG0 * GRP, D), F32, kind="Internal").ap()
        k.y1 = nc.dram_tensor("results1", (E1 * CAP, D), F32, kind="Internal").ap()
        setup(k)
        attention0(k)
        with ExitStack() as k.table_ctx:
            with ExitStack() as k.moe_ctx:
                experts0_shared(k)
                experts0_routed(k)
            k.clear_semaphores()
            attention1(k)
        k.clear_semaphores()
        with ExitStack() as k.moe_ctx:
            experts1_shared(k)
            experts1_routed(k)
            combine1(k)


def layouts(inputs):
    a = {name: np.asarray(v) for name, v in inputs.items()}
    l0 = lambda n: a["L0_ffn_" + n]
    l1 = lambda n: a["L1_attn_" + n]
    m1 = lambda n: a["L1_ffn_" + n]
    blocks = lambda v: v.reshape(-1, P).T
    expert_blocks = lambda v: v.reshape(E0, F0 // P, P).transpose(2, 1, 0).reshape(P, -1)
    by_row = lambda w, n: w.reshape(E1, -1, n, w.shape[-1])
    names = {
        "x": a["L0_attn_hidden_states"].reshape(T, D),
        "wq_t": a["L0_attn_Wq"].T, "wo_t": a["L0_attn_Wo"].T,
        "mem": a["L0_attn_memories"].reshape(4, 4, 4, 32, 32).transpose(2, 3, 1, 0, 4).reshape(P, -1),
        "nrm": a["L0_attn_memory_norms"].reshape(4, 4, 4, 32).transpose(2, 3, 1, 0).reshape(P, -1),
        "bank_w": a["L0_attn_bank_weights"].reshape(4, 4, 4).transpose(0, 2, 1).reshape(-1),
        "sgb_t": blocks(l0("sgb")), "sb1_t": blocks(l0("sb1")),
        "rgb_t": expert_blocks(l0("rgb")), "rb1_t": expert_blocks(l0("rb1")),
        "b2": np.concatenate([l0("rb2"), l0("sb2")], 0),
        "kb_t": blocks(l1("kb")), "qb_t": blocks(l1("qb")), "fw2_t": l1("fw2").T,
        "w_gate_up": np.concatenate([by_row(m1("w_gate"), P), by_row(m1("w_up"), P)], 3).transpose(0, 2, 1, 3).reshape(E1, P, -1),
        "w_down": by_row(m1("w_down"), HF1).transpose(0, 2, 1, 3).reshape(E1, HF1, -1),
    }
    for n in ("wa", "sg", "sw1", "sw2", "rg", "rw1", "rw2"):
        names[n] = l0(n)
    for n in ("qw", "kw", "vw", "ow", "vb", "ob", "fw1", "fb1", "fw2", "fb2"):
        names[n] = l1(n)
    for n in ("gate_w", "bias", "ws_gate", "ws_up", "ws_down"):
        names[n] = m1(n)
    return {n: np.ascontiguousarray(v) for n, v in names.items()}


def kernel(**inputs):
    import concourse.bacc as bacc
    from concourse.bass_utils import run_bass_kernel_spmd

    nc = bacc.Bacc("TRN2", target_bir_lowering=False, num_devices=1)
    arrays = {"in_" + n: v for n, v in layouts(inputs).items()}
    io = {n[3:]: nc.dram_tensor(n, v.shape, mybir.dt.from_np(v.dtype), kind="ExternalInput").ap() for n, v in arrays.items()}
    io["out"] = nc.dram_tensor("out", (T, D), F32, kind="ExternalOutput").ap()
    two_layers(nc, io)
    r = run_bass_kernel_spmd(nc, [arrays], core_ids=[0])
    return r.results[0]["out"].reshape(1, T, D)
```
